# Optimizing a Trainium2 kernel written in Bass

```python
import numpy as np
import jax
import jax.numpy as jnp

def _softmax(x, axis=-1):
    return jax.nn.softmax(x, axis=axis)

def _gelu(x):
    return jax.nn.gelu(x, approximate=True)

def _silu(x):
    return jax.nn.silu(x)

def _sigmoid(x):
    return jax.nn.sigmoid(x)

def _layernorm(x, axis=-1, eps=1e-05):
    m = jnp.mean(x, axis=axis, keepdims=True)
    v = jnp.var(x, axis=axis, keepdims=True)
    return (x - m) / jnp.sqrt(v + eps)

def _scatter_add(tgt, idx, src, axis=0):
    return tgt.at[idx].add(src)

def _segment_sum(src, seg, n):
    return jax.ops.segment_sum(src, seg, n)
kernel_name = 'mk_hybrid_d2_jaxref_r8_55f35b'

def setup_inputs(seed: int=0):
    np.random.seed(seed)
    _w = jnp.asarray

    def _L0_attn_a_setup():
        import jax, jax.numpy as jnp
        import numpy as np
        B_SZ, L, D_MODEL = (2, 128, 128)
        D_INNER, D_STATE, D_CONV = (256, 16, 4)
        EPS = 1e-06

        def _selective_scan(xc, delta, A, Bm, Cm, D_skip):
            dA = jnp.exp(delta[..., None] * A)
            dBx = (delta * xc)[..., None] * Bm[:, :, None, :]
            h0 = jnp.zeros((xc.shape[0], xc.shape[2], A.shape[1]), xc.dtype)

            def step(h, inp):
                dA_t, dBx_t, C_t = inp
                h = dA_t * h + dBx_t
                y_t = jnp.einsum('bds,bs->bd', h, C_t)
                return (h, y_t)
            _, ys = jax.lax.scan(step, h0, (dA.transpose(1, 0, 2, 3), dBx.transpose(1, 0, 2, 3), Cm.transpose(1, 0, 2)))
            y = ys.transpose(1, 0, 2)
            return y + D_skip * xc

        def _layernorm(r, alpha, beta):
            mean = jnp.mean(r, axis=-1, keepdims=True)
            diff = r - mean
            var_unb = jnp.sum(diff * diff, axis=-1, keepdims=True) / (r.shape[-1] - 1)
            std = jnp.sqrt(var_unb)
            return alpha * diff / (std + EPS) + beta
        key = jax.random.key(seed)
        ks = jax.random.split(key, 8)

        def n(k, shape, scale=0.02):
            return jax.random.normal(k, shape, jnp.float32) * scale
        return {'x': jax.random.normal(ks[0], (B_SZ, L, D_MODEL), jnp.float32), 'W_in': n(ks[1], (D_MODEL, 2 * D_INNER)), 'b_in': jnp.zeros((2 * D_INNER,), jnp.float32), 'conv_w': n(ks[2], (D_INNER, 1, D_CONV), 0.2), 'conv_b': jnp.zeros((D_INNER,), jnp.float32), 'W_xp': n(ks[3], (D_INNER, 2 * D_STATE)), 'b_xp': jnp.zeros((2 * D_STATE,), jnp.float32), 'W_dt': n(ks[4], (D_INNER, D_INNER)), 'b_dt': jnp.full((D_INNER,), -1.0, jnp.float32), 'A_log': jnp.log(jax.random.uniform(ks[5], (D_INNER, D_STATE), jnp.float32, 0.5, 1.5)), 'D_skip': jnp.ones((D_INNER,), jnp.float32), 'W_out': n(ks[6], (D_INNER, D_MODEL)), 'b_out': jnp.zeros((D_MODEL,), jnp.float32), 'alpha': jnp.ones((D_MODEL,), jnp.float32), 'beta': jnp.zeros((D_MODEL,), jnp.float32)}
    _L0_attn_a_in = _L0_attn_a_setup()

    def _L0_attn_b_setup():
        import jax, jax.numpy as jnp
        import numpy as np
        B, S, HID = (2, 256, 128)
        H, DH = (16, 64)
        RAMP = 32
        NEG = -1000000000.0

        def _split_heads(x):
            b, s, _ = x.shape
            return x.reshape(b, s, H, DH).transpose(0, 2, 1, 3)
        key = jax.random.key(seed)
        ks = jax.random.split(key, 6)
        sc = 1.0 / np.sqrt(HID)
        return {'query': jax.random.normal(ks[0], (B, S, HID), dtype=jnp.float32), 'Wq': jax.random.normal(ks[1], (HID, H * DH), dtype=jnp.float32) * sc, 'Wk': jax.random.normal(ks[2], (HID, H * DH), dtype=jnp.float32) * sc, 'Wv': jax.random.normal(ks[3], (HID, H * DH), dtype=jnp.float32) * sc, 'Wo': jax.random.normal(ks[4], (H * DH, HID), dtype=jnp.float32) * sc, 'span_val': jax.random.uniform(ks[5], (1, H, 1, 1), dtype=jnp.float32, minval=0.0, maxval=0.2)}
    _L0_attn_b_in = _L0_attn_b_setup()

    def _L0_ffn_setup():
        import jax, jax.numpy as jnp
        import numpy as np
        IN_DIM = 128
        HIDDEN = 128
        OUT_DIM = 128
        NUM_EXPERTS = 16
        TOP_K = 2
        ROUTER_TEMP = 1.0
        LN_EPS = 1e-05

        def _layernorm(h, g, b):
            mu = jnp.mean(h, axis=-1, keepdims=True)
            var = jnp.mean(jnp.square(h - mu), axis=-1, keepdims=True)
            return (h - mu) * jax.lax.rsqrt(var + LN_EPS) * g + b
        key = jax.random.key(seed)
        ks = jax.random.split(key, 8)
        s_in = 1.0 / np.sqrt(IN_DIM)
        s_h = 1.0 / np.sqrt(HIDDEN)
        x = jax.random.normal(ks[0], (4, 256, IN_DIM), dtype=jnp.float32)
        Wr = jax.random.uniform(ks[1], (IN_DIM, NUM_EXPERTS), jnp.float32, -s_in, s_in)
        br = jax.random.uniform(ks[2], (NUM_EXPERTS,), jnp.float32, -s_in, s_in)
        W1 = jax.random.uniform(ks[3], (NUM_EXPERTS, IN_DIM, HIDDEN), jnp.float32, -s_in, s_in)
        b1 = jax.random.uniform(ks[4], (NUM_EXPERTS, HIDDEN), jnp.float32, -s_in, s_in)
        g1 = jnp.ones((NUM_EXPERTS, HIDDEN), jnp.float32)
        be1 = jnp.zeros((NUM_EXPERTS, HIDDEN), jnp.float32)
        W2 = jax.random.uniform(ks[5], (NUM_EXPERTS, HIDDEN, OUT_DIM), jnp.float32, -s_h, s_h)
        b2 = jax.random.uniform(ks[6], (NUM_EXPERTS, OUT_DIM), jnp.float32, -s_h, s_h)
        return {'x': x, 'Wr': Wr, 'br': br, 'W1': W1, 'b1': b1, 'g1': g1, 'be1': be1, 'W2': W2, 'b2': b2}
    _L0_ffn_in = _L0_ffn_setup()

    def _L1_attn_a_setup():
        import jax, jax.numpy as jnp
        import numpy as np
        D_MODEL = 128
        NUM_HEADS = 16
        HEAD_DIM = D_MODEL // NUM_HEADS
        THETA = 10000.0
        B, T = (4, 256)

        def _cos_sin(seq_len, head_dim, theta):
            freqs = 1.0 / theta ** (jnp.arange(0, head_dim, 2, dtype=jnp.float32) / head_dim)
            t = jnp.arange(seq_len, dtype=jnp.float32)
            angles = jnp.outer(t, freqs)
            return jnp.concatenate([jnp.cos(angles), jnp.sin(angles)], axis=-1)

        def _apply_rope(x, cos_sin):
            x1 = x[..., 0::2]
            x2 = x[..., 1::2]
            half = x.shape[-1] // 2
            cos = cos_sin[:, :half]
            sin = cos_sin[:, half:]
            out = jnp.stack([x1 * cos - x2 * sin, x1 * sin + x2 * cos], axis=-1)
            return out.reshape(x.shape)
        key = jax.random.key(seed)
        k1, k2, k3 = jax.random.split(key, 3)
        x = jax.random.normal(k1, (B, T, D_MODEL), dtype=jnp.float32)
        W_qkv = jax.random.normal(k2, (3 * D_MODEL, D_MODEL), dtype=jnp.float32) * D_MODEL ** (-0.5)
        W_out = jax.random.normal(k3, (D_MODEL, D_MODEL), dtype=jnp.float32) * D_MODEL ** (-0.5)
        return {'x': x, 'W_qkv': W_qkv, 'W_out': W_out}
    _L1_attn_a_in = _L1_attn_a_setup()

    def _L1_attn_b_setup():
        import jax, jax.numpy as jnp
        import numpy as np
        N_HEAD = 8
        HEAD = 64
        RATIO = 2
        DEG = 2
        N_EMBD = 128
        QKV = (RATIO + 2) * N_HEAD * HEAD

        def _rope(t):
            B, T, h, d = t.shape
            div = 2.0 * np.pi / float(T) ** (np.arange(0, d, 2, dtype=np.float32) / d)
            ang = jnp.arange(T, dtype=jnp.float32)[:, None] * jnp.asarray(div)[None, :]
            sin = jnp.repeat(jnp.sin(ang), 2, axis=-1)[None, :, None, :]
            cos = jnp.repeat(jnp.cos(ang), 2, axis=-1)[None, :, None, :]
            x1 = t[..., ::2]
            x2 = t[..., 1::2]
            rot = jnp.stack((-x2, x1), axis=-1).reshape(t.shape)
            return t * cos + rot * sin
        key = jax.random.key(seed)
        k1, k2, k3 = jax.random.split(key, 3)
        B, T = (1, 256)
        x = jax.random.normal(k1, (B, T, N_EMBD), dtype=jnp.float32)
        w_attn = jax.random.normal(k2, (N_EMBD, QKV + N_HEAD), dtype=jnp.float32) * N_EMBD ** (-0.5)
        w_proj = jax.random.normal(k3, (RATIO * N_HEAD * HEAD, N_EMBD), dtype=jnp.float32) * (RATIO * N_HEAD * HEAD) ** (-0.5)
        ln_w = jnp.ones((HEAD,), dtype=jnp.float32)
        return {'x': x, 'w_attn': w_attn, 'w_proj': w_proj, 'ln_w': ln_w}
    _L1_attn_b_in = _L1_attn_b_setup()

    def _L1_ffn_setup():
        import jax, jax.numpy as jnp
        import numpy as np
        NUM_EXPERTS = 8
        TOP_K = 2
        CAPACITY_FACTOR = 1.25
        key = jax.random.key(seed)
        ks = jax.random.split(key, 5)
        B, S, D, H, E = (4, 256, 128, 256, NUM_EXPERTS)
        scale = 0.02
        return {'x': jax.random.normal(ks[0], (B, S, D), dtype=jnp.float32), 'gate_w': jax.random.normal(ks[1], (E, D), dtype=jnp.float32) * scale, 'gate_proj_w': jax.random.normal(ks[2], (E, H, D), dtype=jnp.float32) * scale, 'up_proj_w': jax.random.normal(ks[3], (E, H, D), dtype=jnp.float32) * scale, 'down_proj_w': jax.random.normal(ks[4], (E, D, H), dtype=jnp.float32) * scale}
    _L1_ffn_in = _L1_ffn_setup()
    _d = {'L0_attn_a_x': _L0_attn_a_in['x'], 'L0_attn_a_W_in': _L0_attn_a_in['W_in'], 'L0_attn_a_b_in': _L0_attn_a_in['b_in'], 'L0_attn_a_conv_w': _L0_attn_a_in['conv_w'], 'L0_attn_a_conv_b': _L0_attn_a_in['conv_b'], 'L0_attn_a_W_xp': _L0_attn_a_in['W_xp'], 'L0_attn_a_b_xp': _L0_attn_a_in['b_xp'], 'L0_attn_a_W_dt': _L0_attn_a_in['W_dt'], 'L0_attn_a_b_dt': _L0_attn_a_in['b_dt'], 'L0_attn_a_A_log': _L0_attn_a_in['A_log'], 'L0_attn_a_D_skip': _L0_attn_a_in['D_skip'], 'L0_attn_a_W_out': _L0_attn_a_in['W_out'], 'L0_attn_a_b_out': _L0_attn_a_in['b_out'], 'L0_attn_a_alpha': _L0_attn_a_in['alpha'], 'L0_attn_a_beta': _L0_attn_a_in['beta'], 'L0_attn_b_Wq': _L0_attn_b_in['Wq'], 'L0_attn_b_Wk': _L0_attn_b_in['Wk'], 'L0_attn_b_Wv': _L0_attn_b_in['Wv'], 'L0_attn_b_Wo': _L0_attn_b_in['Wo'], 'L0_attn_b_span_val': _L0_attn_b_in['span_val'], 'L0_ffn_Wr': _L0_ffn_in['Wr'], 'L0_ffn_br': _L0_ffn_in['br'], 'L0_ffn_W1': _L0_ffn_in['W1'], 'L0_ffn_b1': _L0_ffn_in['b1'], 'L0_ffn_g1': _L0_ffn_in['g1'], 'L0_ffn_be1': _L0_ffn_in['be1'], 'L0_ffn_W2': _L0_ffn_in['W2'], 'L0_ffn_b2': _L0_ffn_in['b2'], 'L1_attn_a_W_qkv': _L1_attn_a_in['W_qkv'], 'L1_attn_a_W_out': _L1_attn_a_in['W_out'], 'L1_attn_b_w_attn': _L1_attn_b_in['w_attn'], 'L1_attn_b_w_proj': _L1_attn_b_in['w_proj'], 'L1_attn_b_ln_w': _L1_attn_b_in['ln_w'], 'L1_ffn_gate_w': _L1_ffn_in['gate_w'], 'L1_ffn_gate_proj_w': _L1_ffn_in['gate_proj_w'], 'L1_ffn_up_proj_w': _L1_ffn_in['up_proj_w'], 'L1_ffn_down_proj_w': _L1_ffn_in['down_proj_w']}
    _x0 = _d['L0_attn_a_x']
    _d['L0_attn_a_x'] = jax.random.normal(jax.random.fold_in(jax.random.key(seed), 1), (1, 2048, 128), dtype=_x0.dtype)
    del _x0
    return _d

def reference(L0_attn_a_x, L0_attn_a_W_in, L0_attn_a_b_in, L0_attn_a_conv_w, L0_attn_a_conv_b, L0_attn_a_W_xp, L0_attn_a_b_xp, L0_attn_a_W_dt, L0_attn_a_b_dt, L0_attn_a_A_log, L0_attn_a_D_skip, L0_attn_a_W_out, L0_attn_a_b_out, L0_attn_a_alpha, L0_attn_a_beta, L0_attn_b_Wq, L0_attn_b_Wk, L0_attn_b_Wv, L0_attn_b_Wo, L0_attn_b_span_val, L0_ffn_Wr, L0_ffn_br, L0_ffn_W1, L0_ffn_b1, L0_ffn_g1, L0_ffn_be1, L0_ffn_W2, L0_ffn_b2, L1_attn_a_W_qkv, L1_attn_a_W_out, L1_attn_b_w_attn, L1_attn_b_w_proj, L1_attn_b_ln_w, L1_ffn_gate_w, L1_ffn_gate_proj_w, L1_ffn_up_proj_w, L1_ffn_down_proj_w):

    def _L0_attn_a_ref(x, W_in, b_in, conv_w, conv_b, W_xp, b_xp, W_dt, b_dt, A_log, D_skip, W_out, b_out, alpha, beta):
        import jax, jax.numpy as jnp
        import numpy as np
        B_SZ, L, D_MODEL = (2, 128, 128)
        D_INNER, D_STATE, D_CONV = (256, 16, 4)
        EPS = 1e-06

        def _selective_scan(xc, delta, A, Bm, Cm, D_skip):
            dA = jnp.exp(delta[..., None] * A)
            dBx = (delta * xc)[..., None] * Bm[:, :, None, :]
            h0 = jnp.zeros((xc.shape[0], xc.shape[2], A.shape[1]), xc.dtype)

            def step(h, inp):
                dA_t, dBx_t, C_t = inp
                h = dA_t * h + dBx_t
                y_t = jnp.einsum('bds,bs->bd', h, C_t)
                return (h, y_t)
            _, ys = jax.lax.scan(step, h0, (dA.transpose(1, 0, 2, 3), dBx.transpose(1, 0, 2, 3), Cm.transpose(1, 0, 2)))
            y = ys.transpose(1, 0, 2)
            return y + D_skip * xc

        def _layernorm(r, alpha, beta):
            mean = jnp.mean(r, axis=-1, keepdims=True)
            diff = r - mean
            var_unb = jnp.sum(diff * diff, axis=-1, keepdims=True) / (r.shape[-1] - 1)
            std = jnp.sqrt(var_unb)
            return alpha * diff / (std + EPS) + beta
        residual = x
        xz = x @ W_in + b_in
        x_in, z = jnp.split(xz, 2, axis=-1)
        xt = x_in.transpose(0, 2, 1)
        xt = jax.lax.conv_general_dilated(xt, conv_w, window_strides=(1,), padding=[(D_CONV - 1, 0)], feature_group_count=D_INNER, dimension_numbers=('NCH', 'OIH', 'NCH'))
        xt = xt + conv_b[None, :, None]
        x_conv = jax.nn.silu(xt.transpose(0, 2, 1))
        x_proj_out = x_conv @ W_xp + b_xp
        Bm, Cm = jnp.split(x_proj_out, 2, axis=-1)
        delta = jax.nn.softplus(x_conv @ W_dt + b_dt)
        A = -jnp.exp(A_log)
        y = _selective_scan(x_conv, delta, A, Bm, Cm, D_skip)
        y = y * jax.nn.silu(z)
        out = y @ W_out + b_out
        return _layernorm(residual + out, alpha, beta)

    def _L0_attn_b_ref(query, Wq, Wk, Wv, Wo, span_val):
        import jax, jax.numpy as jnp
        import numpy as np
        B, S, HID = (2, 256, 128)
        H, DH = (16, 64)
        RAMP = 32
        NEG = -1000000000.0

        def _split_heads(x):
            b, s, _ = x.shape
            return x.reshape(b, s, H, DH).transpose(0, 2, 1, 3)
        q = _split_heads(query @ Wq)
        k = _split_heads(query @ Wk)
        v = _split_heads(query @ Wv)
        w = jnp.einsum('bhqd,bhkd->bhqk', q, k) / DH
        s = q.shape[2]
        causal = jnp.triu(jnp.full((s, s), NEG, dtype=w.dtype), k=1)
        w = w + causal[None, None]
        w = jax.nn.softmax(w, axis=-1)
        attn_span = jnp.float32(s)
        tmpl = jnp.arange(s, dtype=jnp.float32).reshape(1, 1, 1, s)
        mask = jnp.clip((tmpl + span_val * attn_span) / (RAMP + 1), 0.0, 1.0)
        w = w * mask
        w = w / (jnp.sum(w, axis=-1, keepdims=True) + 1e-08)
        out = jnp.einsum('bhqk,bhkd->bhqd', w, v)
        out = out.transpose(0, 2, 1, 3).reshape(out.shape[0], s, H * DH)
        return out @ Wo

    def _L0_ffn_ref(x, Wr, br, W1, b1, g1, be1, W2, b2):
        import jax, jax.numpy as jnp
        import numpy as np
        IN_DIM = 128
        HIDDEN = 128
        OUT_DIM = 128
        NUM_EXPERTS = 16
        TOP_K = 2
        ROUTER_TEMP = 1.0
        LN_EPS = 1e-05

        def _layernorm(h, g, b):
            mu = jnp.mean(h, axis=-1, keepdims=True)
            var = jnp.mean(jnp.square(h - mu), axis=-1, keepdims=True)
            return (h - mu) * jax.lax.rsqrt(var + LN_EPS) * g + b
        orig_shape = x.shape[:-1]
        x_flat = x.reshape(-1, x.shape[-1])
        logits = (x_flat @ Wr + br) / max(ROUTER_TEMP, 1e-06)
        probs = jax.nn.softmax(logits, axis=-1)
        topk_w, topk_idx = jax.lax.top_k(probs, TOP_K)
        topk_w = topk_w / jnp.clip(jnp.sum(topk_w, axis=-1, keepdims=True), 1e-09)
        h = jnp.einsum('nc,ech->neh', x_flat, W1) + b1
        h = _layernorm(h, g1, be1)
        h = jax.nn.gelu(h, approximate=False)
        expert_out = jnp.einsum('neh,eho->neo', h, W2) + b2
        sel = jnp.take_along_axis(expert_out, topk_idx[:, :, None], axis=1)
        y_flat = jnp.sum(sel * topk_w[:, :, None], axis=1)
        return y_flat.reshape(*orig_shape, y_flat.shape[-1])

    def _L1_attn_a_ref(x, W_qkv, W_out):
        import jax, jax.numpy as jnp
        import numpy as np
        D_MODEL = 128
        NUM_HEADS = 16
        HEAD_DIM = D_MODEL // NUM_HEADS
        THETA = 10000.0
        B, T = (4, 256)

        def _cos_sin(seq_len, head_dim, theta):
            freqs = 1.0 / theta ** (jnp.arange(0, head_dim, 2, dtype=jnp.float32) / head_dim)
            t = jnp.arange(seq_len, dtype=jnp.float32)
            angles = jnp.outer(t, freqs)
            return jnp.concatenate([jnp.cos(angles), jnp.sin(angles)], axis=-1)

        def _apply_rope(x, cos_sin):
            x1 = x[..., 0::2]
            x2 = x[..., 1::2]
            half = x.shape[-1] // 2
            cos = cos_sin[:, :half]
            sin = cos_sin[:, half:]
            out = jnp.stack([x1 * cos - x2 * sin, x1 * sin + x2 * cos], axis=-1)
            return out.reshape(x.shape)
        Bsz, Tlen, _ = x.shape
        qkv = jnp.einsum('bti,oi->bto', x, W_qkv)
        qkv = qkv.reshape(Bsz, Tlen, 3 * NUM_HEADS, HEAD_DIM).transpose(0, 2, 1, 3)
        q, k, v = jnp.split(qkv, 3, axis=1)
        cos_sin = _cos_sin(Tlen, HEAD_DIM, THETA)
        q = _apply_rope(q, cos_sin)
        k = _apply_rope(k, cos_sin)
        scores = jnp.einsum('bhqd,bhkd->bhqk', q, k) / np.sqrt(HEAD_DIM).astype(np.float32)
        causal = jnp.tril(jnp.ones((Tlen, Tlen), dtype=bool))
        scores = jnp.where(causal[None, None], scores, -jnp.inf)
        attn = jax.nn.softmax(scores, axis=-1)
        o = jnp.einsum('bhqk,bhkd->bhqd', attn, v)
        o = o.transpose(0, 2, 1, 3).reshape(Bsz, Tlen, D_MODEL)
        return jnp.einsum('bti,oi->bto', o, W_out)

    def _L1_attn_b_ref(x, w_attn, w_proj, ln_w):
        import jax, jax.numpy as jnp
        import numpy as np
        N_HEAD = 8
        HEAD = 64
        RATIO = 2
        DEG = 2
        N_EMBD = 128
        QKV = (RATIO + 2) * N_HEAD * HEAD

        def _rope(t):
            B, T, h, d = t.shape
            div = 2.0 * np.pi / float(T) ** (np.arange(0, d, 2, dtype=np.float32) / d)
            ang = jnp.arange(T, dtype=jnp.float32)[:, None] * jnp.asarray(div)[None, :]
            sin = jnp.repeat(jnp.sin(ang), 2, axis=-1)[None, :, None, :]
            cos = jnp.repeat(jnp.cos(ang), 2, axis=-1)[None, :, None, :]
            x1 = t[..., ::2]
            x2 = t[..., 1::2]
            rot = jnp.stack((-x2, x1), axis=-1).reshape(t.shape)
            return t * cos + rot * sin
        B, T, C = x.shape
        h, d, r = (N_HEAD, HEAD, RATIO)
        hq = r * h
        qkvg = x @ w_attn
        q = qkvg[..., :hq * d].reshape(B, T, hq, d)
        k = qkvg[..., hq * d:(hq + h) * d].reshape(B, T, h, d)
        v = qkvg[..., (hq + h) * d:QKV].reshape(B, T, h, d)
        log_g = jax.nn.log_sigmoid(6.906768 + qkvg[..., QKV:])
        q = _rope(q)
        k = _rope(k)
        k = jnp.repeat(k, r, axis=2)
        v = jnp.repeat(v, r, axis=2)
        log_G = jnp.repeat(jnp.cumsum(log_g, axis=1), r, axis=2).transpose(0, 2, 1)
        scale = 1.0 / d ** 0.5
        s = jnp.einsum('bthd,bshd->bhts', q, k) * scale
        logits = DEG * jnp.log(jnp.abs(s) + 1e-30) + log_G[:, :, :, None] - log_G[:, :, None, :]
        mask = jnp.tril(jnp.ones((T, T), dtype=bool))
        logits = jnp.where(mask, logits, -jnp.inf)
        m = jax.lax.stop_gradient(jnp.max(logits, axis=-1, keepdims=True))
        a = jnp.exp(logits - m)
        if DEG % 2 == 1:
            a = a * jnp.sign(s)
        a = jnp.where(mask, a, 0.0)
        num = jnp.einsum('bhts,bshd->bthd', a, v)
        den = jnp.sum(a, axis=-1).transpose(0, 2, 1)
        y = num / (den[..., None] + 1e-06)
        mu = jnp.mean(y, axis=-1, keepdims=True)
        var = jnp.mean((y - mu) ** 2, axis=-1, keepdims=True)
        y = (y - mu) / jnp.sqrt(var + 1e-09) * ln_w
        return y.reshape(B, T, hq * d) @ w_proj

    def _L1_ffn_ref(x, gate_w, gate_proj_w, up_proj_w, down_proj_w):
        import jax, jax.numpy as jnp
        import numpy as np
        NUM_EXPERTS = 8
        TOP_K = 2
        CAPACITY_FACTOR = 1.25
        B, S, D = x.shape
        E, K = (NUM_EXPERTS, TOP_K)
        T = B * S
        xf = x.reshape(T, D)
        logits = xf @ gate_w.T
        probs = jax.nn.softmax(logits, axis=-1)
        top_p, top_i = jax.lax.top_k(probs, K)
        w = top_p / (jnp.sum(top_p, axis=-1, keepdims=True) + 1e-09)
        capacity = int(CAPACITY_FACTOR * T / E)
        oh = jax.nn.one_hot(top_i, E, dtype=jnp.int32)
        rank = jnp.cumsum(oh, axis=0) - 1
        my_rank = jnp.sum(rank * oh, axis=-1)
        keep = (my_rank < capacity).astype(w.dtype)
        comb = jnp.einsum('tk,tke->te', w * keep, oh.astype(w.dtype))
        out = jnp.zeros_like(xf)
        for e in range(E):
            g = jax.nn.silu(xf @ gate_proj_w[e].T)
            u = xf @ up_proj_w[e].T
            y = g * u @ down_proj_w[e].T
            out = out + comb[:, e:e + 1] * y
        return out.reshape(B, S, D)
    x = L0_attn_a_x
    x = x + _L0_attn_a_ref(_layernorm(x, axis=-1), L0_attn_a_W_in, L0_attn_a_b_in, L0_attn_a_conv_w, L0_attn_a_conv_b, L0_attn_a_W_xp, L0_attn_a_b_xp, L0_attn_a_W_dt, L0_attn_a_b_dt, L0_attn_a_A_log, L0_attn_a_D_skip, L0_attn_a_W_out, L0_attn_a_b_out, L0_attn_a_alpha, L0_attn_a_beta)
    x = x + _L0_ffn_ref(_layernorm(x, axis=-1), L0_ffn_Wr, L0_ffn_br, L0_ffn_W1, L0_ffn_b1, L0_ffn_g1, L0_ffn_be1, L0_ffn_W2, L0_ffn_b2)
    x = x + _L0_attn_b_ref(_layernorm(x, axis=-1), L0_attn_b_Wq, L0_attn_b_Wk, L0_attn_b_Wv, L0_attn_b_Wo, L0_attn_b_span_val)
    x = x + _L0_ffn_ref(_layernorm(x, axis=-1), L0_ffn_Wr, L0_ffn_br, L0_ffn_W1, L0_ffn_b1, L0_ffn_g1, L0_ffn_be1, L0_ffn_W2, L0_ffn_b2)
    x = x + _L1_attn_a_ref(_layernorm(x, axis=-1), L1_attn_a_W_qkv, L1_attn_a_W_out)
    x = x + _L1_ffn_ref(_layernorm(x, axis=-1), L1_ffn_gate_w, L1_ffn_gate_proj_w, L1_ffn_up_proj_w, L1_ffn_down_proj_w)
    x = x + _L1_attn_b_ref(_layernorm(x, axis=-1), L1_attn_b_w_attn, L1_attn_b_w_proj, L1_attn_b_ln_w)
    x = x + _L1_ffn_ref(_layernorm(x, axis=-1), L1_ffn_gate_w, L1_ffn_gate_proj_w, L1_ffn_up_proj_w, L1_ffn_down_proj_w)
    return x

_drawn_inputs = setup_inputs


def setup_inputs(seed=0):
    import zlib

    import numpy as np

    out = dict(_drawn_inputs(seed))
    spreads = {'L0_attn_a_b_in': (0.0, 0.8),
     'L0_attn_a_conv_b': (0.0, 0.8),
     'L0_attn_a_b_xp': (0.0, 0.8),
     'L0_attn_a_b_dt': (-1.0, 0.6),
     'L0_attn_a_D_skip': (1.0, 0.6),
     'L0_attn_a_b_out': (0.0, 0.1),
     'L0_attn_a_alpha': (1.0, 0.2),
     'L0_attn_a_beta': (0.0, 0.1),
     'L0_ffn_g1': (1.0, 0.2),
     'L0_ffn_be1': (0.0, 0.1),
     'L1_attn_b_ln_w': (1.0, 0.2)}
    factors = {'L0_attn_a_W_in': 8.0,
     'L0_attn_a_conv_w': 7.093,
     'L0_attn_a_W_xp': 8.0,
     'L0_attn_a_W_dt': 8.0,
     'L0_attn_a_A_log': 8.0,
     'L0_attn_a_W_out': 7.263,
     'L0_attn_b_span_val': 3.393,
     'L1_ffn_gate_w': 8.0,
     'L1_ffn_gate_proj_w': 8.0,
     'L1_ffn_up_proj_w': 8.0,
     'L1_ffn_down_proj_w': 8.0}
    for name, (base, spread) in spreads.items():
        noise = np.random.default_rng([zlib.crc32(name.encode()), seed]).standard_normal(out[name].shape)
        drawn = base * np.exp(spread * noise) if base else spread * noise
        out[name] = jnp.asarray(drawn.astype(out[name].dtype))
    for name, factor in factors.items():
        out[name] = (out[name] * factor).astype(out[name].dtype)
    return out
```

```python
import concourse.bass as bass
from concourse import mybir
from concourse.alu_op_type import AluOpType as ALU
from contextlib import ExitStack

F32 = mybir.dt.float32
BF16 = mybir.dt.bfloat16
I32 = mybir.dt.int32
U32 = mybir.dt.uint32
ACT = mybir.ActivationFunctionType
AX = mybir.AxisListType

P = 128
T = 2048
D = 128
NT = T // P
CH = 512
NCH = T // CH
TPC = CH // P
MASKED = -1.0e30


class Steps:

    def __init__(self, eng, sem, base=0):
        self.eng, self.sem, self.base, self.n = eng, sem, base, 0

    def add(self, ins):
        ins.then_inc(self.sem, 1)
        self.n += 1
        return self.n

    def wait(self, n=None):
        self.eng.wait_ge(self.sem, self.base + (self.n if n is None else n))

    def run(self, ins):
        self.add(ins)
        self.wait()


class Core:

    def __init__(self, nc, ctx):
        self.nc = nc
        sb = lambda name, shape, dt: ctx.enter_context(nc.sbuf_tensor(name, shape, dt))
        self.x = sb("x_residual", [P, NT, D], F32)
        self.xT = sb("x_norm_T", [P, T], F32)
        self.ident = sb("ident", [P, P], F32)
        self.ident_b = sb("ident_b", [P, P], BF16)
        self.hide = sb("hide_qk", [P, P], BF16)
        self.hideT = sb("hide_kq", [P, P], BF16)
        self.ones_b = sb("ones_b", [P, P], BF16)


class Stage:

    def __init__(self, nc, tag):
        self.nc, self.tag, self.ctx, self.sems = nc, tag, ExitStack(), []

    def sb(self, name, shape, dt=F32):
        return self.ctx.enter_context(self.nc.sbuf_tensor(f"{self.tag}_{name}", shape, dt))

    def ps(self, name, shape, dt=F32):
        return self.ctx.enter_context(self.nc.psum_tensor(f"{self.tag}_{name}", shape, dt))

    def sem(self, name):
        self.sems.append(self.ctx.enter_context(self.nc.semaphore(f"{self.tag}_{name}")))
        return self.sems[-1]

    def restart(self):
        with self.nc.Block() as block:
            @block.gpsimd
            def _(pool):
                for sem in self.sems:
                    pool.sem_clear(sem)

    def __enter__(self):
        return self

    def __exit__(self, kind, *rest):
        if kind is None:
            self.restart()
        self.ctx.close()


def stage_constants(nc, core, x_in):
    with Stage(nc, "setup") as s:
        x_loaded = s.sem("x_loaded")
        pool_step = s.sem("pool_step")
        with nc.Block() as block:
            @block.sync
            def _(sp):
                sp.dma_start(core.x[:, :, :], x_in.rearrange("b (t p) d -> p (b t) d", p=P)).then_inc(x_loaded, 16)
                sp.wait_ge(x_loaded, 16)

            @block.gpsimd
            def _(pool):
                st = Steps(pool, pool_step)
                for m, value in ((core.ident, 0.0), (core.ident_b, 0.0), (core.hide, 0.0), (core.hideT, 0.0), (core.ones_b, 1.0)):
                    st.add(nc.gpsimd.memset(m[:, :], value))
                st.wait()
                for m in (core.ident, core.ident_b):
                    st.add(nc.gpsimd.affine_select(out=m[:, :], in_=m[:, :], compare_op=ALU.not_equal, fill=1.0,
                                                   base=0, pattern=[[-1, P]], channel_multiplier=1))
                st.add(nc.gpsimd.affine_select(out=core.hide[:, :], in_=core.hide[:, :], compare_op=ALU.is_ge, fill=MASKED,
                                               base=0, pattern=[[-1, P]], channel_multiplier=1))
                st.add(nc.gpsimd.affine_select(out=core.hideT[:, :], in_=core.hideT[:, :], compare_op=ALU.is_ge, fill=MASKED,
                                               base=0, pattern=[[1, P]], channel_multiplier=-1))
                st.wait()


def stage_norm(nc, core, tag, xn=None):
    with Stage(nc, tag) as s:
        stats = s.sb("stats", [P, NT, 6])
        mean = s.sb("mean", [P, NT])
        var = s.sb("var", [P, NT])
        dif = s.sb("dif", [P, NT])
        rstd = s.sb("rstd", [P, NT])
        keep = xn if xn is not None else s.sb("xn", [P, NT, D])
        psT = s.ps("psT", [P, T])
        dve_step, var_ready, std_ready = s.sem("dve_step"), s.sem("var_ready"), s.sem("std_ready")
        norm_ready, transposed, xT_ready = s.sem("norm_ready"), s.sem("transposed"), s.sem("xT_ready")
        with nc.Block() as block:
            @block.vector
            def _(dve):
                st = Steps(dve, dve_step)
                for t in range(NT):
                    st.add(nc.vector.bn_stats(stats[:, t, :], core.x[:, t, :]))
                st.wait()
                st.add(nc.vector.tensor_tensor(mean[:, :], stats[:, :, 1], stats[:, :, 4], ALU.add))
                st.add(nc.vector.tensor_tensor(dif[:, :], stats[:, :, 1], stats[:, :, 4], ALU.subtract))
                st.run(nc.vector.tensor_tensor(var[:, :], stats[:, :, 2], stats[:, :, 5], ALU.add))
                st.add(nc.vector.tensor_scalar(mean[:, :], mean[:, :], 0.5, None, ALU.mult))
                st.add(nc.vector.tensor_scalar(var[:, :], var[:, :], 1.0 / D, 1e-5, ALU.mult, ALU.add))
                st.run(nc.vector.scalar_tensor_tensor(out=dif[:, :], in0=dif[:, :], scalar=0.25, in1=dif[:, :],
                                                      op0=ALU.mult, op1=ALU.mult))
                nc.vector.tensor_tensor(var[:, :], var[:, :], dif[:, :], ALU.add).then_inc(var_ready, 1)
                dve.wait_ge(std_ready, 1)
                st.run(nc.vector.reciprocal(rstd[:, :], var[:, :]))
                for t in range(NT):
                    nc.vector.tensor_scalar(keep[:, t, :], core.x[:, t, :], mean[:, t:t + 1], rstd[:, t:t + 1],
                                            ALU.subtract, ALU.mult).then_inc(norm_ready, 1)

            @block.tensor
            def _(pe):
                for t in range(NT):
                    pe.wait_ge(norm_ready, t + 1)
                    nc.tensor.transpose(psT[:, t * P:(t + 1) * P], keep[:, t, :], core.ident[:, :]).then_inc(transposed, 1)

            @block.scalar
            def _(act):
                act.wait_ge(var_ready, 1)
                nc.scalar.activation(var[:, :], var[:, :], ACT.Sqrt).then_inc(std_ready, 1)
                for c in range(NCH):
                    act.wait_ge(transposed, TPC * (c + 1))
                    nc.scalar.activation(core.xT[:, c * CH:(c + 1) * CH], psT[:, c * CH:(c + 1) * CH], ACT.Copy).then_inc(xT_ready, 1)
                act.wait_ge(xT_ready, NCH)


def stage_store(nc, core, out):
    with Stage(nc, "store") as s:
        stored = s.sem("stored")
        with nc.Block() as block:
            @block.sync
            def _(sp):
                sp.dma_start(out.rearrange("b (t p) d -> p (b t) d", p=P), core.x[:, :, :]).then_inc(stored, 16)
                sp.wait_ge(stored, 16)


def stage_mamba(nc, core, tag, xn, w):
    NS, NHALF, NCONV, DI = 16, 2, 4, 256
    NB = 2 * NS
    with Stage(nc, tag) as s:
        sz, xc, delta, dx = (s.sb(n, [P, NHALF, T]) for n in ("silu_z", "x_conv", "delta", "delta_x"))
        bc = s.sb("bc_parts", [P, T], BF16)
        sel = s.sb("select", [P, NB, P], BF16)
        A = s.sb("A", [P, NHALF, NS])
        d_skip = s.sb("d_skip", [P, NHALF])
        w_out = s.sb("w_out", [P, NHALF, D])
        h_last = s.sb("h_last", [P, NHALF, NS])
        loaded = s.sem("loaded")
        with Stage(nc, tag + "_in") as q:
            w_in, w_dt = q.sb("w_in", [P, 2 * DI]), q.sb("w_dt", [P, NHALF, DI])
            w_xp = q.sb("w_xp", [P, NHALF, 3, NB])
            b_in, conv_w, conv_b = q.sb("b_in", [P, 4]), q.sb("conv_w", [P, NHALF, NCONV]), q.sb("conv_b", [P, NHALF])
            b_dt, b_xp = q.sb("b_dt", [P, NHALF]), q.sb("b_xp", [3 * NB, 1])
            xin = q.sb("x_in", [P, NHALF, T + NCONV - 1])
            conv = q.sb("conv", [P, NHALF, T])
            bcf, bcr = q.sb("bc", [3 * NB, T]), q.sb("bc_rest", [3 * NB, T])
            pick = q.sb("pick", [P, NB])
            ps = q.ps("ps", [P, 4, CH])
            dve_step, zeroed = q.sem("dve_step"), q.sem("zeroed")
            proj, ev_act, conv_done, xc_ready = q.sem("projected"), q.sem("in_evacuated"), q.sem("conv_done"), q.sem("xc_ready")
            bc_done, bc_out, dt_done = q.sem("bc_done"), q.sem("bc_out"), q.sem("dt_done")
            dt_rd, abs_done, exp_done, ln_done = q.sem("dt_read"), q.sem("abs_done"), q.sem("exp_done"), q.sem("ln_done")
            a_done = q.sem("a_done")
            NLOAD = 15
            with nc.Block() as block:
                @block.sync
                def _(sp):
                    loads = [(w_in[:, :], w["W_in"]), (b_in[:, :], w["b_in"]), (conv_w[:, :, :], w["conv_w"]), (conv_b[:, :], w["conv_b"]),
                             (w_dt[:, :, :], w["W_dt"].rearrange("(k p) n -> p k n", p=P)), (b_dt[:, :], w["b_dt"]),
                             (A[:, :, :], w["A_log"].rearrange("(k p) n -> p k n", p=P)), (d_skip[:, :], w["D_skip"]),
                             (w_out[:, :, :], w["W_out"].rearrange("(k p) n -> p k n", p=P))]
                    for part in range(3):
                        loads.append((w_xp[:, :, part, :], w["W_xp"].rearrange("(k p) n -> p k n", p=P)))
                        loads.append((b_xp[part * NB:(part + 1) * NB, :], w["b_xp"]))
                    assert len(loads) == NLOAD
                    for dst, src in loads:
                        sp.dma_start(dst, src).then_inc(loaded, 16)
                    sp.wait_ge(loaded, 16 * NLOAD)

                @block.gpsimd
                def _(pool):
                    nc.gpsimd.memset(xin[:, :, 0:NCONV - 1], 0.0).then_inc(zeroed, 1)
                    nc.gpsimd.memset(bc[:, :], 0.0).then_inc(zeroed, 1)
                    nc.gpsimd.memset(h_last[:, :, :], 0.0).then_inc(zeroed, 1)

                @block.tensor
                def _(pe):
                    pe.wait_ge(loaded, 16 * NLOAD)
                    for n in range(4 * NCH):
                        if n >= 4:
                            pe.wait_ge(ev_act, n - 3)
                        j, c = n // NCH, n % NCH
                        nc.tensor.matmul(ps[:, n % 4, :], w_in[:, j * P:(j + 1) * P], core.xT[:, c * CH:(c + 1) * CH],
                                         start=True, stop=True).then_inc(proj, 1)
                    pe.wait_ge(xc_ready, NHALF)
                    for c in range(NCH):
                        for k in range(NHALF):
                            last = nc.tensor.matmul(ps[0:3 * NB, c, :], w_xp[:, k, :, :].rearrange("p a b -> p (a b)"),
                                                    xc[:, k, c * CH:(c + 1) * CH], start=k == 0, stop=k == NHALF - 1)
                        last.then_inc(bc_done, 1)
                    for n in range(NHALF * NCH):
                        m, c = n // NCH, n % NCH
                        if n < 4:
                            pe.wait_ge(bc_out, n + 1)
                        else:
                            pe.wait_ge(dt_rd, n - 3)
                        for k in range(NHALF):
                            last = nc.tensor.matmul(ps[:, n % 4, :], w_dt[:, k, m * P:(m + 1) * P], xc[:, k, c * CH:(c + 1) * CH],
                                                    start=k == 0, stop=k == NHALF - 1)
                        last.then_inc(dt_done, 1)

                @block.scalar
                def _(act):
                    act.wait_ge(loaded, 16 * NLOAD)
                    for n in range(4 * NCH):
                        j, c = n // NCH, n % NCH
                        act.wait_ge(proj, n + 1)
                        if j < NHALF:
                            nc.scalar.activation(xin[:, j, NCONV - 1 + c * CH:NCONV - 1 + (c + 1) * CH], ps[:, n % 4, :], ACT.Identity,
                                                 bias=b_in[:, j:j + 1]).then_inc(ev_act, 1)
                        else:
                            nc.scalar.activation(sz[:, j - NHALF, c * CH:(c + 1) * CH], ps[:, n % 4, :], ACT.Silu,
                                                 bias=b_in[:, j:j + 1]).then_inc(ev_act, 1)
                    for k in range(NHALF):
                        act.wait_ge(conv_done, k + 1)
                        nc.scalar.activation(xc[:, k, :], conv[:, k, :], ACT.Silu).then_inc(xc_ready, 1)
                    for m in range(NHALF):
                        act.wait_ge(dt_rd, (m + 1) * NCH)
                        nc.scalar.activation(delta[:, m, :], conv[:, m, :], ACT.Abs).then_inc(abs_done, 1)
                    act.wait_ge(abs_done, NHALF)
                    nc.scalar.activation(A[:, :, :], A[:, :, :], ACT.Exp).then_inc(a_done, 1)
                    for m in range(NHALF):
                        nc.scalar.activation(delta[:, m, :], delta[:, m, :], ACT.Exp, scale=-1.0).then_inc(exp_done, 1)
                    act.wait_ge(exp_done, NHALF)
                    for m in range(NHALF):
                        nc.scalar.activation(xin[:, m, 0:T], delta[:, m, :], ACT.Ln, bias=1.0).then_inc(ln_done, 1)

                @block.vector
                def _(dve):
                    st = Steps(dve, dve_step)
                    dve.wait_ge(loaded, 16 * NLOAD)
                    dve.wait_ge(zeroed, 3)
                    st.run(nc.vector.tensor_tensor(pick[:, :], core.ident[:, 0:NB], core.ident[:, NB:2 * NB], ALU.add))
                    st.run(nc.vector.tensor_tensor(pick[:, :], pick[:, :], core.ident[:, 2 * NB:3 * NB], ALU.add))
                    st.add(nc.vector.tensor_copy(sel[:, :, :], pick[:, :].unsqueeze(2).to_broadcast([P, NB, P])))
                    for k in range(NHALF):
                        dve.wait_ge(ev_act, (k + 1) * NCH)
                        st.run(nc.vector.tensor_scalar(conv[:, k, :], xin[:, k, 0:T], conv_w[:, k, 0:1], conv_b[:, k:k + 1], ALU.mult, ALU.add))
                        for tap in range(1, NCONV):
                            last = nc.vector.scalar_tensor_tensor(out=conv[:, k, :], in0=xin[:, k, tap:tap + T], scalar=conv_w[:, k, tap:tap + 1],
                                                                  in1=conv[:, k, :], op0=ALU.mult, op1=ALU.add)
                            if tap < NCONV - 1:
                                st.run(last)
                        last.then_inc(conv_done, 1)
                    for c in range(NCH):
                        dve.wait_ge(bc_done, c + 1)
                        nc.vector.tensor_scalar(bcf[:, c * CH:(c + 1) * CH], ps[0:3 * NB, c, :], b_xp[:, 0:1], None, ALU.add).then_inc(bc_out, 1)
                    dve.wait_ge(bc_out, NCH)
                    st.run(nc.vector.tensor_copy(bc[0:3 * NB, :], bcf[:, :]))
                    st.run(nc.vector.tensor_tensor(bcr[:, :], bcf[:, :], bc[0:3 * NB, :], ALU.subtract))
                    for lo in (NB, 2 * NB):
                        st.run(nc.vector.tensor_copy(bc[lo:lo + NB, :], bcr[lo:lo + NB, :]))
                    st.run(nc.vector.tensor_tensor(bcr[2 * NB:3 * NB, :], bcr[2 * NB:3 * NB, :], bc[2 * NB:3 * NB, :], ALU.subtract))
                    st.add(nc.vector.tensor_copy(bc[2 * NB:3 * NB, :], bcr[2 * NB:3 * NB, :]))
                    dve.wait_ge(xc_ready, NHALF)
                    for n in range(NHALF * NCH):
                        m, c = n // NCH, n % NCH
                        dve.wait_ge(dt_done, n + 1)
                        nc.vector.tensor_scalar(conv[:, m, c * CH:(c + 1) * CH], ps[:, n % 4, :], b_dt[:, m:m + 1], None, ALU.add).then_inc(dt_rd, 1)
                    dve.wait_ge(dt_rd, NHALF * NCH)
                    dve.wait_ge(a_done, 1)
                    st.add(nc.vector.tensor_scalar(A[:, :, :], A[:, :, :], -1.0, None, ALU.mult))
                    for m in range(NHALF):
                        dve.wait_ge(exp_done, NHALF)
                        st.run(nc.vector.tensor_scalar(dx[:, m, :], delta[:, m, :], 1.0, -1.0, ALU.add, ALU.add))
                        st.run(nc.vector.tensor_tensor(dx[:, m, :], delta[:, m, :], dx[:, m, :], ALU.subtract))
                        st.run(nc.vector.scalar_tensor_tensor(out=conv[:, m, :], in0=conv[:, m, :], scalar=0.0, in1=dx[:, m, :],
                                                              op0=ALU.max, op1=ALU.add))
                        dve.wait_ge(ln_done, m + 1)
                        st.run(nc.vector.tensor_tensor(delta[:, m, :], xin[:, m, 0:T], conv[:, m, :], ALU.add))
                        st.run(nc.vector.tensor_tensor(dx[:, m, :], delta[:, m, :], xc[:, m, :], ALU.mult))

        NI = NS * NHALF
        NBUF = 3
        dA, dbx, hc = (s.sb(n, [P, NBUF, CH]) for n in ("dA", "dB_x", "h_C"))
        hs = s.sb("h", [P, 2, CH])
        b_all = s.sb("b_spread", [P, 2, CH])
        yz = s.sb("y_gated", [P, NHALF, T])
        with Stage(nc, tag + "_scan") as q:
            ps_b, ps_c, ps_y = q.ps("ps_b", [P, 2, CH]), q.ps("ps_c", [P, 2, CH]), q.ps("ps_y", [P, NHALF, CH])
            spread, b_out, dA_done, dbx_done = q.sem("spread"), q.sem("b_evacuated"), q.sem("dA_done"), q.sem("dbx_done")
            scanned, kept, hc_done, summed = q.sem("scanned"), q.sem("h_kept"), q.sem("hC_done"), q.sem("summed")
            skip_done, gated = q.sem("skip_added"), q.sem("gated")
            with nc.Fori(0, NCH) as c:
                q.restart()
                cols = bass.ds(c * CH, CH)
                with nc.Block() as block:
                    @block.tensor
                    def _(pe):
                        def spread_bc(n):
                            if n >= 2:
                                pe.wait_ge(b_out, n - 1)
                                pe.wait_ge(hc_done, NHALF * (n - 1))
                            nc.tensor.matmul(ps_b[:, n % 2, :], sel[:, n, :], bc[:, cols], start=True, stop=True)
                            nc.tensor.matmul(ps_c[:, n % 2, :], sel[:, NS + n, :], bc[:, cols], start=True, stop=True).then_inc(spread, 1)

                        spread_bc(0)
                        spread_bc(1)
                        for n in range(NI):
                            st_, k = n // NHALF, n % NHALF
                            pe.wait_ge(hc_done, n + 1)
                            nc.tensor.matmul(ps_y[:, k, :], core.ident[:, :], hc[:, n % NBUF, :], start=st_ == 0, stop=st_ == NS - 1).then_inc(summed, 1)
                            if k == NHALF - 1 and st_ + 2 < NS:
                                spread_bc(st_ + 2)

                    @block.scalar
                    def _(act):
                        for n in range(NI):
                            st_, k = n // NHALF, n % NHALF
                            if k == 0:
                                act.wait_ge(spread, st_ + 1)
                                if st_ >= 2:
                                    act.wait_ge(dbx_done, NHALF * (st_ - 1))
                                nc.scalar.activation(b_all[:, st_ % 2, :], ps_b[:, st_ % 2, :], ACT.Copy).then_inc(b_out, 1)
                            if n >= NBUF:
                                act.wait_ge(scanned, n - NBUF + 1)
                            nc.scalar.activation(dA[:, n % NBUF, :], delta[:, k, cols], ACT.Exp, scale=A[:, k, st_:st_ + 1]).then_inc(dA_done, 1)

                    @block.gpsimd
                    def _(pool):
                        for n in range(NI):
                            st_, k = n // NHALF, n % NHALF
                            pool.wait_ge(b_out, st_ + 1)
                            if n >= NBUF:
                                pool.wait_ge(scanned, n - NBUF + 1)
                            if n >= 1:
                                pool.wait_ge(dbx_done, n)
                            nc.gpsimd.tensor_tensor(dbx[:, n % NBUF, :], dx[:, k, cols], b_all[:, st_ % 2, :], ALU.mult).then_inc(dbx_done, 1)

                    @block.vector
                    def _(dve):
                        def scan(n):
                            st_, k = n // NHALF, n % NHALF
                            dve.wait_ge(dA_done, n + 1)
                            dve.wait_ge(dbx_done, n + 1)
                            if n >= 2:
                                dve.wait_ge(hc_done, n - 1)
                                dve.wait_ge(kept, n - 1)
                            nc.vector.tensor_tensor_scan(hs[:, n % 2, :], dA[:, n % NBUF, :], dbx[:, n % NBUF, :],
                                                         h_last[:, k, st_:st_ + 1], ALU.mult, ALU.add).then_inc(scanned, 1)

                        scan(0)
                        for n in range(NI):
                            st_, k = n // NHALF, n % NHALF
                            if n + 1 < NI:
                                scan(n + 1)
                            dve.wait_ge(scanned, n + 1)
                            if n >= NBUF:
                                dve.wait_ge(summed, n - NBUF + 1)
                            nc.vector.tensor_tensor(hc[:, n % NBUF, :], hs[:, n % 2, :], ps_c[:, st_ % 2, :], ALU.mult).then_inc(hc_done, 1)
                            nc.vector.tensor_copy(h_last[:, k, st_:st_ + 1], hs[:, n % 2, CH - 1:CH]).then_inc(kept, 1)
                        dve.wait_ge(summed, NI)
                        for k in range(NHALF):
                            nc.vector.scalar_tensor_tensor(out=yz[:, k, cols], in0=xc[:, k, cols], scalar=d_skip[:, k:k + 1],
                                                           in1=ps_y[:, k, :], op0=ALU.mult, op1=ALU.add).then_inc(skip_done, 1)
                        for k in range(NHALF):
                            dve.wait_ge(skip_done, k + 1)
                            nc.vector.tensor_tensor(yz[:, k, cols], yz[:, k, cols], sz[:, k, cols], ALU.mult).then_inc(gated, 1)

        with Stage(nc, tag + "_out") as q:
            b_out, alpha, beta = q.sb("b_out", [P, D]), q.sb("alpha", [P, D]), q.sb("beta", [P, D])
            r = q.sb("sum", [P, NT, D])
            stats = q.sb("stats", [P, NT, 6])
            mean, var, dif = (q.sb(n, [P, NT]) for n in ("mean", "var", "dif"))
            ps = q.ps("ps", [P, 2, TPC, D])
            vec_loaded, done, dve_step = q.sem("vectors_loaded"), q.sem("out_done"), q.sem("dve_step")
            summed, var_ready, std_ready = q.sem("summed"), q.sem("var_ready"), q.sem("std_ready")
            with nc.Block() as block:
                @block.sync
                def _(sp):
                    for dst, src in ((b_out, w["b_out"]), (alpha, w["alpha"]), (beta, w["beta"])):
                        sp.dma_start(dst[:, :], src.partition_broadcast(P)).then_inc(vec_loaded, 16)
                    sp.wait_ge(vec_loaded, 48)

                @block.tensor
                def _(pe):
                    for c in range(NCH):
                        if c >= 2:
                            pe.wait_ge(summed, c - 1)
                        for j in range(TPC):
                            t = c * TPC + j
                            for k in range(NHALF):
                                last = nc.tensor.matmul(ps[:, c % 2, j, :], yz[:, k, t * P:(t + 1) * P], w_out[:, k, :],
                                                        start=k == 0, stop=k == NHALF - 1)
                        last.then_inc(done, 1)

                @block.scalar
                def _(act):
                    act.wait_ge(var_ready, 1)
                    nc.scalar.activation(var[:, :], var[:, :], ACT.Sqrt).then_inc(std_ready, 1)

                @block.vector
                def _(dve):
                    st = Steps(dve, dve_step)
                    wide = [P, TPC, D]
                    dve.wait_ge(vec_loaded, 48)
                    for c in range(NCH):
                        tiles = slice(c * TPC, (c + 1) * TPC)
                        st.run(nc.vector.tensor_tensor(r[:, tiles, :], xn[:, tiles, :], b_out[:, :].unsqueeze(1).to_broadcast(wide), ALU.add))
                        dve.wait_ge(done, c + 1)
                        nc.vector.tensor_tensor(r[:, tiles, :], r[:, tiles, :], ps[:, c % 2, :, :], ALU.add).then_inc(summed, 1)
                    dve.wait_ge(summed, NCH)
                    for t in range(NT):
                        st.add(nc.vector.bn_stats(stats[:, t, :], r[:, t, :]))
                    st.wait()
                    st.add(nc.vector.tensor_tensor(mean[:, :], stats[:, :, 1], stats[:, :, 4], ALU.add))
                    st.add(nc.vector.tensor_tensor(dif[:, :], stats[:, :, 1], stats[:, :, 4], ALU.subtract))
                    st.run(nc.vector.tensor_tensor(var[:, :], stats[:, :, 2], stats[:, :, 5], ALU.add))
                    st.add(nc.vector.tensor_scalar(mean[:, :], mean[:, :], 0.5, None, ALU.mult))
                    st.run(nc.vector.scalar_tensor_tensor(out=dif[:, :], in0=dif[:, :], scalar=0.25 * D, in1=dif[:, :],
                                                          op0=ALU.mult, op1=ALU.mult))
                    st.run(nc.vector.tensor_tensor(var[:, :], var[:, :], dif[:, :], ALU.add))
                    nc.vector.tensor_scalar(var[:, :], var[:, :], 1.0 / (D - 1), None, ALU.mult).then_inc(var_ready, 1)
                    dve.wait_ge(std_ready, 1)
                    st.run(nc.vector.tensor_scalar(var[:, :], var[:, :], 1e-6, None, ALU.add))
                    st.run(nc.vector.reciprocal(dif[:, :], var[:, :]))
                    for t in range(NT):
                        st.add(nc.vector.tensor_scalar(r[:, t, :], r[:, t, :], mean[:, t:t + 1], dif[:, t:t + 1], ALU.subtract, ALU.mult))
                    st.wait()
                    full = [P, NT, D]
                    st.run(nc.vector.tensor_tensor(r[:, :, :], r[:, :, :], alpha[:, :].unsqueeze(1).to_broadcast(full), ALU.mult))
                    st.run(nc.vector.tensor_tensor(r[:, :, :], r[:, :, :], beta[:, :].unsqueeze(1).to_broadcast(full), ALU.add))
                    st.run(nc.vector.tensor_tensor(core.x[:, :, :], core.x[:, :, :], r[:, :, :], ALU.add))


def stage_route(nc, core, tag, E, Wr, br, comb, capacity=None):
    with Stage(nc, tag) as s:
        wr = s.sb("wr", [P, E])
        brb = s.sb("br", [P, E])
        lg = s.sb("logits", [P, NT, E])
        top, idx = s.sb("top", [P, NT, 8]), s.sb("idx", [P, NT, 8], U32)
        idxf, iota = s.sb("idxf", [P, NT, 2]), s.sb("iota", [P, E])
        mx, tot, w = s.sb("row_max", [P, NT]), s.sb("row_sum", [P, NT]), s.sb("weights", [P, 2, NT])
        hot = s.sb("one_hot", [P, 2, NT, E])
        hot_b = s.sb("one_hot_b", [P, 2, NT, E], BF16)
        tri = s.sb("tri_b", [P, P], BF16)
        before = s.sb("count_before", [P, 2, NT, E])
        total = s.sb("count_in_tile", [P, 2, NT, E])
        rank = s.sb("rank", [P, 2, NT])
        ps = s.ps("ps", [P, NT, E])
        ps_cum, ps_tot = s.ps("ps_cum", [P, 2, NT, E]), s.ps("ps_tot", [P, 2, NT, E])
        loaded, consts, scored, exps = s.sem("loaded"), s.sem("consts"), s.sem("scored"), s.sem("exp_done")
        shifted, dve_step, hot_ready, counted = s.sem("shifted"), s.sem("dve_step"), s.sem("hot_ready"), s.sem("counted")
        nload = 16 if br is None else 32
        with nc.Block() as block:
            @block.sync
            def _(sp):
                sp.dma_start(wr[:, :], Wr).then_inc(loaded, 16)
                if br is not None:
                    sp.dma_start(brb[:, :], br.partition_broadcast(P)).then_inc(loaded, 16)
                sp.wait_ge(loaded, nload)

            @block.gpsimd
            def _(pool):
                nc.gpsimd.iota(iota[:, :], pattern=[[1, E]], base=0, channel_multiplier=0,
                               allow_small_or_imprecise_dtypes=True).then_inc(consts, 1)
                nc.gpsimd.memset(tri[:, :], 1.0).then_inc(consts, 1)
                pool.wait_ge(consts, 2)
                nc.gpsimd.affine_select(out=tri[:, :], in_=tri[:, :], compare_op=ALU.is_ge, fill=0.0,
                                        base=0, pattern=[[1, P]], channel_multiplier=-1).then_inc(consts, 1)
                pool.wait_ge(consts, 3)

            @block.tensor
            def _(pe):
                pe.wait_ge(loaded, nload)
                for t in range(NT):
                    last = nc.tensor.matmul(ps[:, t, :], core.xT[:, t * P:(t + 1) * P], wr[:, :], start=True, stop=True)
                last.then_inc(scored, 1)
                if capacity is not None:
                    pe.wait_ge(consts, 3)
                    pe.wait_ge(hot_ready, 1)
                    flat = hot_b[:, :, :, :].rearrange("p k t e -> p (k t e)")
                    nc.tensor.matmul(ps_cum[:, :, :, :].rearrange("p k t e -> p (k t e)"), tri[:, :], flat, start=True, stop=True)
                    nc.tensor.matmul(ps_tot[:, :, :, :].rearrange("p k t e -> p (k t e)"), core.ones_b[:, :], flat,
                                     start=True, stop=True).then_inc(counted, 1)

            @block.scalar
            def _(act):
                act.wait_ge(shifted, 1)
                nc.scalar.activation(lg[:, :, :], lg[:, :, :], ACT.Exp).then_inc(exps, 1)

            @block.vector
            def _(dve):
                st = Steps(dve, dve_step)
                wide = [P, NT, E]
                dve.wait_ge(loaded, nload)
                dve.wait_ge(consts, 3)
                dve.wait_ge(scored, 1)
                if br is None:
                    st.run(nc.vector.tensor_copy(lg[:, :, :], ps[:, :, :]))
                else:
                    st.run(nc.vector.tensor_tensor(lg[:, :, :], ps[:, :, :], brb[:, :].unsqueeze(1).to_broadcast(wide), ALU.add))
                st.run(nc.vector.tensor_reduce(mx[:, :], lg[:, :, :], axis=AX.X, op=ALU.max))
                nc.vector.tensor_tensor(lg[:, :, :], lg[:, :, :], mx[:, :].unsqueeze(2).to_broadcast(wide), ALU.subtract).then_inc(shifted, 1)
                dve.wait_ge(exps, 1)
                st.run(nc.vector.tensor_reduce(tot[:, :], lg[:, :, :], axis=AX.X, op=ALU.add))
                st.run(nc.vector.reciprocal(mx[:, :], tot[:, :]))
                st.run(nc.vector.tensor_tensor(lg[:, :, :], lg[:, :, :], mx[:, :].unsqueeze(2).to_broadcast(wide), ALU.mult))
                for t in range(NT):
                    st.add(nc.vector.max(top[:, t, :], lg[:, t, :]))
                st.wait()
                for t in range(NT):
                    st.add(nc.vector.max_index(idx[:, t, :], top[:, t, :], lg[:, t, :]))
                st.wait()
                st.add(nc.vector.tensor_copy(idxf[:, :, :], idx[:, :, 0:2]))
                st.run(nc.vector.tensor_tensor(tot[:, :], top[:, :, 0], top[:, :, 1], ALU.add))
                for k in range(2):
                    st.add(nc.vector.tensor_tensor(hot[:, k, :, :], iota[:, :].unsqueeze(1).to_broadcast(wide),
                                                   idxf[:, :, k:k + 1].to_broadcast(wide), ALU.is_equal))
                if capacity is None:
                    st.run(nc.vector.tensor_scalar(tot[:, :], tot[:, :], 1e-9, None, ALU.max))
                else:
                    st.run(nc.vector.tensor_scalar(tot[:, :], tot[:, :], 1e-9, None, ALU.add))
                st.run(nc.vector.reciprocal(mx[:, :], tot[:, :]))
                for k in range(2):
                    st.add(nc.vector.tensor_tensor(w[:, k, :], top[:, :, k], mx[:, :], ALU.mult))
                st.wait()
                if capacity is not None:
                    nc.vector.tensor_copy(hot_b[:, :, :, :], hot[:, :, :, :]).then_inc(hot_ready, 1)
                    dve.wait_ge(counted, 1)
                    st.add(nc.vector.tensor_copy(total[:, :, :, :], ps_tot[:, :, :, :]))
                    st.add(nc.vector.memset(before[:, :, 0, :], 0.0))
                    st.wait()
                    for t in range(1, NT):
                        st.run(nc.vector.tensor_tensor(before[:, :, t, :], before[:, :, t - 1, :], total[:, :, t - 1, :], ALU.add))
                    st.run(nc.vector.tensor_tensor(before[:, :, :, :], before[:, :, :, :], ps_cum[:, :, :, :], ALU.add))
                    st.run(nc.vector.tensor_tensor(before[:, :, :, :], before[:, :, :, :], hot[:, :, :, :], ALU.mult))
                    st.run(nc.vector.tensor_reduce(rank[:, :, :], before[:, :, :, :], axis=AX.X, op=ALU.add))
                    st.run(nc.vector.tensor_scalar(rank[:, :, :], rank[:, :, :], capacity + 0.5, None, ALU.is_lt))
                    st.run(nc.vector.tensor_tensor(w[:, :, :], w[:, :, :], rank[:, :, :], ALU.mult))
                for k in range(2):
                    st.add(nc.vector.tensor_tensor(hot[:, k, :, :], hot[:, k, :, :], w[:, k, :].unsqueeze(2).to_broadcast(wide), ALU.mult))
                st.wait()
                st.run(nc.vector.tensor_tensor(comb[:, :, :], hot[:, 0, :, :], hot[:, 1, :, :], ALU.add))


def stage_gelu_experts(nc, core, tag, comb, W1, b1, g1T, be1T, W2, b2):
    E, HID, Q = 16, 128, 4
    NQ = E // Q
    with Stage(nc, tag) as s:
        w1, w2 = s.sb("w1", [P, E * HID]), s.sb("w2", [P, E, D])
        b2s = s.sb("b2", [E, D])
        g, be = s.sb("g1", [P, E]), s.sb("be1", [P, E])
        b_rows, b_rest = s.sb("b1_rows", [3, E * HID]), s.sb("b1_rest", [3, E * HID])
        b_part = s.sb("b1_part", [3, E * HID], BF16)
        b_sum = s.sb("b1_sum", [P, E * HID], BF16)
        combT = s.sb("comb_T", [E, T])
        g_q, be_q, comb_q = s.sb("g1_quad", [P, Q]), s.sb("be1_quad", [P, Q]), s.sb("comb_quad", [P, NT, Q])
        h = s.sb("hidden", [P, NT, Q, HID])
        stats = s.sb("stats", [P, NT * Q, 6])
        mean, var, dif, rstd = (s.sb(n, [P, NT * Q]) for n in ("mean", "var", "dif", "rstd"))
        hn = s.sb("hidden_norm", [P, 2, TPC, HID])
        gT = s.sb("gelu_T", [P, 2, CH])
        ps_h, ps_t = s.ps("ps_hidden", [P, 2, CH]), s.ps("ps_turned", [P, 2, CH])
        ps_y = s.ps("ps_y", [P, 2, TPC, D])
        loaded, dve_step, zeroed = s.sem("loaded"), s.sem("dve_step"), s.sem("b1_zeroed")
        b_ready, turned, combT_ready = s.sem("b1_ready"), s.sem("comb_turned"), s.sem("comb_T_ready")
        y_done, added = s.sem("y_done"), s.sem("x_added")
        hid_done, hid_out, quad_ready = s.sem("hidden_done"), s.sem("hidden_evacuated"), s.sem("quad_ready")
        var_ready, std_ready, normed = s.sem("var_ready"), s.sem("std_ready"), s.sem("normalised")
        gelu_done = s.sem("gelu_done")
        with nc.Block() as block:
            @block.sync
            def _(sp):
                sp.dma_start(b_rows[:, :], b1.rearrange("e h -> (e h)").partition_broadcast(3)).then_inc(loaded, 16)
                sp.dma_start(b2s[:, :], b2).then_inc(loaded, 16)
                sp.dma_start(g[:, :], g1T).then_inc(loaded, 16)
                sp.dma_start(be[:, :], be1T).then_inc(loaded, 16)
                sp.dma_start(w1[:, :].rearrange("c (e h) -> c e h", e=E), W1.rearrange("e c h -> c e h")).then_inc(loaded, 16)
                sp.dma_start(w2[:, :, :], W2.rearrange("e h o -> h e o")).then_inc(loaded, 16)
                sp.wait_ge(loaded, 96)

            @block.gpsimd
            def _(pool):
                nc.gpsimd.memset(b_sum[:, :], 0.0).then_inc(zeroed, 1)

            @block.tensor
            def _(pe):
                for t in range(NT):
                    if t % TPC == 0 and t >= 2 * TPC:
                        pe.wait_ge(combT_ready, t // TPC - 1)
                    last = nc.tensor.transpose(ps_t[0:E, (t // TPC) % 2, (t % TPC) * P:(t % TPC + 1) * P], comb[:, t, :], core.ident[:, :])
                    if t % TPC == TPC - 1:
                        last.then_inc(turned, 1)
                pe.wait_ge(loaded, 96)
                for c in range(NCH):
                    pe.wait_ge(combT_ready, c + 1)
                    if c >= 2:
                        pe.wait_ge(added, c - 1)
                    for j in range(TPC):
                        t = c * TPC + j
                        last = nc.tensor.matmul(ps_y[:, c % 2, j, :], combT[:, t * P:(t + 1) * P], b2s[:, :], start=True, stop=True)
                    last.then_inc(y_done, 1)

            @block.scalar
            def _(act):
                for c in range(NCH):
                    act.wait_ge(turned, c + 1)
                    nc.scalar.activation(combT[:, c * CH:(c + 1) * CH], ps_t[0:E, c % 2, :], ACT.Copy).then_inc(combT_ready, 1)

            @block.vector
            def _(dve):
                st = Steps(dve, dve_step)
                dve.wait_ge(loaded, 96)
                dve.wait_ge(zeroed, 1)
                for k in range(3):
                    st.run(nc.vector.tensor_copy(b_part[:, :], b_rows[:, :]))
                    if k < 2:
                        st.run(nc.vector.tensor_tensor(b_rows[:, :], b_rows[:, :], b_part[:, :], ALU.subtract))
                    if k == 0:
                        st.run(nc.vector.tensor_scalar(b_sum[0:3, :], b_part[:, :], core.ident[0:3, 0:1], None, ALU.mult))
                    else:
                        st.run(nc.vector.tensor_scalar(b_rest[:, :], b_part[:, :], core.ident[0:3, k:k + 1], None, ALU.mult))
                        st.run(nc.vector.tensor_tensor(b_sum[0:3, :], b_sum[0:3, :], b_rest[:, :], ALU.add))
                for c in range(NCH):
                    dve.wait_ge(y_done, c + 1)
                    tiles = slice(c * TPC, (c + 1) * TPC)
                    nc.vector.tensor_tensor(core.x[:, tiles, :], core.x[:, tiles, :], ps_y[:, c % 2, :, :], ALU.add).then_inc(added, 1)
                dve.wait_ge(added, NCH)

        with nc.Fori(0, NQ) as i:
            s.restart()
            with nc.Block() as block:
                @block.gpsimd
                def _(pool):
                    nc.gpsimd.tensor_copy(g_q[:, :], g[:, bass.ds(i * Q, Q)]).then_inc(quad_ready, 1)
                    nc.gpsimd.tensor_copy(be_q[:, :], be[:, bass.ds(i * Q, Q)]).then_inc(quad_ready, 1)
                    nc.gpsimd.tensor_copy(comb_q[:, :, :], comb[:, :, bass.ds(i * Q, Q)]).then_inc(quad_ready, 1)

                @block.tensor
                def _(pe):
                    for t in range(NT):
                        if t >= 2:
                            pe.wait_ge(hid_out, t - 1)
                        nc.tensor.matmul(ps_h[:, t % 2, :], core.xT[:, t * P:(t + 1) * P], w1[:, bass.ds(i * Q * HID, Q * HID)], start=True, stop=False)
                        nc.tensor.matmul(ps_h[:, t % 2, :], core.ones_b[:, :], b_sum[:, bass.ds(i * Q * HID, Q * HID)], start=False, stop=True).then_inc(hid_done, 1)

                    def turn(n):
                        pe.wait_ge(normed, n + 1)
                        if n >= 2:
                            pe.wait_ge(gelu_done, n - 1)
                        for j in range(TPC):
                            last = nc.tensor.transpose(ps_t[:, n % 2, j * P:(j + 1) * P], hn[:, n % 2, j, :], core.ident[:, :])
                        last.then_inc(turned, 1)

                    turn(0)
                    for n in range(NCH * Q):
                        if n + 1 < NCH * Q:
                            turn(n + 1)
                        pe.wait_ge(gelu_done, n + 1)
                        if n >= 2:
                            pe.wait_ge(added, n - 1)
                        for j in range(TPC):
                            last = nc.tensor.matmul(ps_y[:, n % 2, j, :], gT[:, n % 2, j * P:(j + 1) * P],
                                                    w2[:, bass.ds(i * Q + n % Q, 1), :], start=True, stop=True)
                        last.then_inc(y_done, 1)

                @block.scalar
                def _(act):
                    for t in range(NT):
                        act.wait_ge(hid_done, t + 1)
                        nc.scalar.activation(h[:, t, :, :], ps_h[:, t % 2, :].rearrange("p (e h) -> p e h", e=Q), ACT.Copy).then_inc(hid_out, 1)
                    act.wait_ge(var_ready, 1)
                    nc.scalar.activation(var[:, :], var[:, :], ACT.Sqrt).then_inc(std_ready, 1)
                    act.wait_ge(quad_ready, 3)
                    for n in range(NCH * Q):
                        act.wait_ge(turned, n + 1)
                        if n >= 2:
                            act.wait_ge(y_done, n - 1)
                        nc.scalar.activation(gT[:, n % 2, :], ps_t[:, n % 2, :], ACT.Gelu, scale=g_q[:, n % Q:n % Q + 1],
                                             bias=be_q[:, n % Q:n % Q + 1]).then_inc(gelu_done, 1)

                @block.vector
                def _(dve):
                    st = Steps(dve, dve_step)
                    for t in range(NT):
                        dve.wait_ge(hid_out, t + 1)
                        for e in range(Q):
                            st.add(nc.vector.bn_stats(stats[:, t * Q + e, :], h[:, t, e, :]))
                    st.wait()
                    st.add(nc.vector.tensor_tensor(mean[:, :], stats[:, :, 1], stats[:, :, 4], ALU.add))
                    st.add(nc.vector.tensor_tensor(dif[:, :], stats[:, :, 1], stats[:, :, 4], ALU.subtract))
                    st.run(nc.vector.tensor_tensor(var[:, :], stats[:, :, 2], stats[:, :, 5], ALU.add))
                    st.add(nc.vector.tensor_scalar(mean[:, :], mean[:, :], 0.5, None, ALU.mult))
                    st.add(nc.vector.tensor_scalar(var[:, :], var[:, :], 1.0 / HID, 1e-5, ALU.mult, ALU.add))
                    st.run(nc.vector.scalar_tensor_tensor(out=dif[:, :], in0=dif[:, :], scalar=0.25, in1=dif[:, :],
                                                          op0=ALU.mult, op1=ALU.mult))
                    nc.vector.tensor_tensor(var[:, :], var[:, :], dif[:, :], ALU.add).then_inc(var_ready, 1)
                    dve.wait_ge(std_ready, 1)
                    st.run(nc.vector.reciprocal(rstd[:, :], var[:, :]))
                    dve.wait_ge(quad_ready, 3)

                    def normalise(n):
                        c, e = n // Q, n % Q
                        if n >= 2:
                            dve.wait_ge(turned, n - 1)
                        for j in range(TPC):
                            t = c * TPC + j
                            k = t * Q + e
                            last = nc.vector.tensor_scalar(hn[:, n % 2, j, :], h[:, t, e, :], mean[:, k:k + 1], rstd[:, k:k + 1],
                                                           ALU.subtract, ALU.mult)
                        last.then_inc(normed, 1)

                    normalise(0)
                    normalise(1)
                    for n in range(NCH * Q):
                        if n + 2 < NCH * Q:
                            normalise(n + 2)
                        dve.wait_ge(y_done, n + 1)
                        if n >= 1:
                            dve.wait_ge(added, n)
                        for j in range(TPC):
                            t = (n // Q) * TPC + j
                            last = nc.vector.scalar_tensor_tensor(out=core.x[:, t, :], in0=ps_y[:, n % 2, j, :],
                                                                  scalar=comb_q[:, t, n % Q:n % Q + 1], in1=core.x[:, t, :],
                                                                  op0=ALU.mult, op1=ALU.add)
                        last.then_inc(added, 1)


def stage_silu_experts(nc, core, tag, comb, WgT, WuT, WdT):
    E, HID = 8, 256
    NH = HID // P
    with Stage(nc, tag) as s:
        wg, wu = s.sb("wg", [P, E, HID]), s.sb("wu", [P, E, HID])
        wd = s.sb("wd", [P, NH, E, D])
        wg_e, wu_e, comb_e = s.sb("wg_expert", [P, HID]), s.sb("wu_expert", [P, HID]), s.sb("comb_expert", [P, NT])
        gate = s.sb("gate", [P, 2, CH])
        gu = s.sb("gate_up", [P, 2, NH, CH])
        ps_g, ps_u, ps_y = s.ps("ps_gate", [P, 2, CH]), s.ps("ps_up", [P, 2, CH]), s.ps("ps_y", [P, 2, TPC, D])
        loaded, expert_ready = s.sem("loaded"), s.sem("expert_ready")
        up_done, gated, gu_ready = s.sem("gate_up_done"), s.sem("silu_done"), s.sem("gu_ready")
        y_done, added = s.sem("y_done"), s.sem("x_added")
        with nc.Block() as block:
            @block.sync
            def _(sp):
                sp.dma_start(wg[:, :, :], WgT).then_inc(loaded, 16)
                sp.dma_start(wu[:, :, :], WuT).then_inc(loaded, 16)
                sp.dma_start(wd[:, :, :, :], WdT.rearrange("(k p) e o -> p k e o", p=P)).then_inc(loaded, 16)
                sp.wait_ge(loaded, 48)
        with nc.Fori(0, E) as i:
            s.restart()
            with nc.Block() as block:
                @block.tensor
                def _(pe):
                    pe.wait_ge(expert_ready, 3)

                    def gate_up(n):
                        c, k = n // NH, n % NH
                        if n >= 2:
                            pe.wait_ge(gu_ready, n - 1)
                        cols = core.xT[:, c * CH:(c + 1) * CH]
                        nc.tensor.matmul(ps_g[:, n % 2, :], wg_e[:, k * P:(k + 1) * P], cols, start=True, stop=True)
                        nc.tensor.matmul(ps_u[:, n % 2, :], wu_e[:, k * P:(k + 1) * P], cols, start=True, stop=True).then_inc(up_done, 1)

                    gate_up(0)
                    gate_up(1)
                    for c in range(NCH):
                        if c + 1 < NCH:
                            gate_up(2 * c + 2)
                            gate_up(2 * c + 3)
                        pe.wait_ge(gu_ready, NH * (c + 1))
                        if c >= 2:
                            pe.wait_ge(added, c - 1)
                        for j in range(TPC):
                            for k in range(NH):
                                last = nc.tensor.matmul(ps_y[:, c % 2, j, :], gu[:, c % 2, k, j * P:(j + 1) * P],
                                                        wd[:, k, bass.ds(i, 1), :], start=k == 0, stop=k == NH - 1)
                        last.then_inc(y_done, 1)

                @block.scalar
                def _(act):
                    for n in range(NCH * NH):
                        act.wait_ge(up_done, n + 1)
                        if n >= 2:
                            act.wait_ge(gu_ready, n - 1)
                        nc.scalar.activation(gate[:, n % 2, :], ps_g[:, n % 2, :], ACT.Silu).then_inc(gated, 1)

                @block.vector
                def _(dve):
                    nc.vector.tensor_copy(wg_e[:, :], wg[:, bass.ds(i, 1), :]).then_inc(expert_ready, 1)
                    nc.vector.tensor_copy(wu_e[:, :], wu[:, bass.ds(i, 1), :]).then_inc(expert_ready, 1)
                    nc.vector.tensor_copy(comb_e[:, :], comb[:, :, bass.ds(i, 1)]).then_inc(expert_ready, 1)
                    dve.wait_ge(expert_ready, 3)

                    def product(n):
                        c, k = n // NH, n % NH
                        dve.wait_ge(gated, n + 1)
                        if c >= 2:
                            dve.wait_ge(y_done, c - 1)
                        nc.vector.tensor_tensor(gu[:, c % 2, k, :], gate[:, n % 2, :], ps_u[:, n % 2, :], ALU.mult).then_inc(gu_ready, 1)

                    product(0)
                    product(1)
                    for c in range(NCH):
                        if c + 1 < NCH:
                            product(2 * c + 2)
                            product(2 * c + 3)
                        dve.wait_ge(y_done, c + 1)
                        for j in range(TPC):
                            t = c * TPC + j
                            last = nc.vector.scalar_tensor_tensor(out=core.x[:, t, :], in0=ps_y[:, c % 2, j, :], scalar=comb_e[:, t:t + 1],
                                                                  in1=core.x[:, t, :], op0=ALU.mult, op1=ALU.add)
                        last.then_inc(added, 1)


def stage_span_attention(nc, core, tag, Wq, Wk, Wv, Wo, span):
    H, DH, RAMP = 16, 64, 32
    NP_ = H // 2
    SC = 1.0 / DH
    M = DH + 2
    PASS1 = [(hh, qt, kc, min(CH, (qt + 1) * P - kc * CH), (qt // TPC) == kc)
             for hh in range(2) for qt in range(NT) for kc in range(qt // TPC + 1)]
    PASS2 = [(hh, qc, kb, max(0, kb * P - qc * CH))
             for hh in range(2) for qc in range(NCH) for kb in range(TPC * (qc + 1))]
    N1, N2 = len(PASS1), len(PASS2)
    NQK = 2 * NCH
    NPROJ = NQK + NCH
    NPB = 4
    with Stage(nc, tag) as s:
        wq, wk, wv = s.sb("wq", [P, H * DH]), s.sb("wk", [P, H * DH]), s.sb("wv", [P, H * DH])
        wo = s.sb("wo", [M, H, D + 1])
        wq_p, wk_p = s.sb("wq_pair", [P, P]), s.sb("wk_pair", [P, P])
        mask, mask_p = s.sb("mask", [P, H, NT]), s.sb("mask_pair", [P, 2, NT])
        pos, spans = s.sb("pos", [P, NT]), s.sb("spans", [P, H])
        qz = s.sb("q_padded", [P, 2, T])
        kT = s.sb("kT", [P, T])
        va = s.sb("v_aug", [P, 2, NT, M])
        m_part = s.sb("max_part", [P, NT, NCH])
        m_neg, m_rest = s.sb("max_neg", [P, NT]), s.sb("max_rest", [P, NT])
        m_split = s.sb("max_split", [P, 2, NT, 3], BF16)
        m_row = s.sb("max_row", [P, 2, T], BF16)
        probs = s.sb("probs", [P, NPB, CH])
        oT = s.sb("oT", [M, CH])
        rden = s.sb("rden", [P, TPC])
        ps1 = s.ps("ps_pass1", [P, 2, CH])
        ps2 = s.ps("ps_pass2", [P, 2, CH])
        psO = s.ps("ps_out", [P, CH])
        psF = s.ps("ps_final", [P, TPC, 256])
        psR = s.ps("ps_rows", [P, CH])
        loaded, wo_zero, consts = s.sem("loaded"), s.sem("wo_zeroed"), s.sem("consts")
        pool_step, dve_step = s.sem("pool_step"), s.sem("dve_step")
        pair_w, proj = s.sem("pair_weights"), s.sem("projected")
        qk_out, v_out = s.sem("qk_evacuated"), s.sem("v_evacuated")
        scored, max_done = s.sem("pass1_scored"), s.sem("pass1_max")
        split_ready, rows, row_ready = s.sem("max_split"), s.sem("rows_transposed"), s.sem("rows_ready")
        sc2, exped, pv = s.sem("pass2_scored"), s.sem("exp_done"), s.sem("pv_done")
        oT_ready, fin, recip, added = s.sem("oT_ready"), s.sem("final_ready"), s.sem("recip"), s.sem("x_added")
        with nc.Block() as block:
            @block.sync
            def _(sp):
                for dst, src in ((wq, Wq), (wk, Wk), (wv, Wv)):
                    sp.dma_start(dst[:, :], src).then_inc(loaded, 16)
                sp.dma_start(spans[:, :], span.rearrange("a h b c -> (a b c h)").partition_broadcast(P)).then_inc(loaded, 16)
                sp.wait_ge(wo_zero, 1)
                sp.dma_start(wo[0:DH, :, 0:D], Wo.rearrange("(h d) n -> d h n", d=DH)).then_inc(loaded, 16)
                sp.wait_ge(loaded, 80)

            @block.gpsimd
            def _(pool):
                st = Steps(pool, pool_step)
                st.run(nc.gpsimd.memset(wo[:, :, :], 0.0))
                nc.gpsimd.memset(wo[DH:M, :, D:D + 1], 1.0).then_inc(wo_zero, 1)
                pool.wait_ge(wo_zero, 1)
                st.add(nc.gpsimd.memset(m_row[:, :, :], 0.0))
                st.add(nc.gpsimd.memset(qz[:, :, :], 0.0))
                st.add(nc.gpsimd.memset(m_part[:, :, :], -3.0e38))
                st.add(nc.gpsimd.memset(va[:, :, :, DH + 1:M], 1e-8))
                st.add(nc.gpsimd.iota(pos[:, :], pattern=[[P, NT]], base=0, channel_multiplier=1,
                                      allow_small_or_imprecise_dtypes=True))
                pool.wait_ge(loaded, 80)
                st.run(nc.gpsimd.tensor_scalar(spans[:, :], spans[:, :], float(T), None, ALU.mult))
                for h in range(H):
                    st.add(nc.gpsimd.tensor_scalar(mask[:, h, :], pos[:, :], spans[:, h:h + 1], 1.0 / (RAMP + 1), ALU.add, ALU.mult))
                st.wait()
                nc.gpsimd.tensor_scalar(mask[:, :, :], mask[:, :, :], 0.0, 1.0, ALU.max, ALU.min).then_inc(consts, 1)
                pool.wait_ge(consts, 1)

        with nc.Fori(0, NP_) as i:
            s.restart()
            with nc.Block() as block:
                @block.gpsimd
                def _(pool):
                    nc.gpsimd.tensor_copy(wq_p[:, :], wq[:, bass.ds(i * P, P)]).then_inc(pair_w, 1)
                    nc.gpsimd.tensor_copy(wk_p[:, :], wk[:, bass.ds(i * P, P)]).then_inc(pair_w, 1)
                    nc.gpsimd.tensor_copy(mask_p[:, :, :], mask[:, bass.ds(i * 2, 2), :]).then_inc(pair_w, 1)

                @block.tensor
                def _(pe):
                    pe.wait_ge(pair_w, 3)
                    for n in range(NQK):
                        if n >= 2:
                            pe.wait_ge(qk_out, n - 1)
                        w, c = (wq_p, wk_p)[n // NCH], n % NCH
                        nc.tensor.matmul(ps1[:, n % 2, :], w[:, :], core.xT[:, c * CH:(c + 1) * CH],
                                         start=True, stop=True).then_inc(proj, 1)
                    for c in range(NCH):
                        if c < 2:
                            pe.wait_ge(qk_out, NQK - 1 + c)
                        else:
                            pe.wait_ge(v_out, c - 1)
                        for j in range(TPC):
                            t = c * TPC + j
                            last = nc.tensor.matmul(ps1[:, c % 2, j * P:(j + 1) * P], core.xT[:, t * P:(t + 1) * P],
                                                    wv[:, bass.ds(i * P, P)], start=True, stop=True)
                        last.then_inc(proj, 1)

                    for n, (hh, qt, kc, w, diag) in enumerate(PASS1):
                        if n == 0:
                            pe.wait_ge(v_out, NCH)
                        if n >= 2:
                            pe.wait_ge(max_done, n - 1)
                        mm = nc.tensor.matmul(ps1[:, n % 2, 0:w], qz[:, hh, qt * P:(qt + 1) * P], kT[:, kc * CH:kc * CH + w],
                                              start=True, stop=not diag)
                        if diag:
                            mm = nc.tensor.matmul(ps1[:, n % 2, w - P:w], core.ident_b[:, :], core.hide[:, :], start=False, stop=True)
                        mm.then_inc(scored, 1)

                    def maxima_to_rows(hh):
                        pe.wait_ge(split_ready, hh + 1)
                        for c in range(NCH):
                            pe.wait_ge(row_ready, hh * NCH + c)
                            for j in range(TPC):
                                last = nc.tensor.matmul(psR[0:3, j * P:(j + 1) * P], m_split[:, hh, c * TPC + j, :],
                                                        core.ident_b[:, :], start=True, stop=True)
                            last.then_inc(rows, 1)

                    def scores(n):
                        hh, qc, kb, q0 = PASS2[n]
                        if n in (0, N2 // 2):
                            pe.wait_ge(row_ready, (hh + 1) * NCH)
                        if n >= 2:
                            pe.wait_ge(exped, n - 1)
                        q1, w = qc * CH + q0, CH - q0
                        diag = kb >= TPC * qc
                        nc.tensor.matmul(ps2[:, n % 2, 0:w], kT[:, kb * P:(kb + 1) * P], qz[:, hh, q1:q1 + w], start=True, stop=False)
                        mm = nc.tensor.matmul(ps2[:, n % 2, 0:w], core.ones_b[:, :], m_row[:, hh, q1:q1 + w], start=False, stop=not diag)
                        if diag:
                            mm = nc.tensor.matmul(ps2[:, n % 2, 0:P], core.ident_b[:, :], core.hideT[:, :], start=False, stop=True)
                        mm.then_inc(sc2, 1)

                    def values(n):
                        hh, qc, kb, q0 = PASS2[n]
                        if kb == 0:
                            pe.wait_ge(oT_ready, hh * NCH + qc)
                        pe.wait_ge(exped, n + 1)
                        nc.tensor.matmul(psO[0:M, q0:CH], va[:, hh, kb, :], probs[:, n % NPB, 0:CH - q0],
                                         start=kb == 0, stop=kb == TPC * (qc + 1) - 1).then_inc(pv, 1)

                    def project_out(g):
                        pe.wait_ge(oT_ready, g + 1)
                        pe.wait_ge(added, g)
                        for j in range(TPC):
                            last = nc.tensor.matmul(psF[:, j, 0:D + 1], oT[:, j * P:(j + 1) * P],
                                                    wo[:, bass.ds(i * 2 + g // NCH, 1), :], start=True, stop=True)
                        last.then_inc(fin, 1)

                    maxima_to_rows(0)
                    scores(0)
                    for n in range(N2):
                        if n == 2:
                            maxima_to_rows(1)
                        if n + 1 < N2:
                            scores(n + 1)
                        values(n)
                        hh, qc, kb, _ = PASS2[n]
                        if kb == 1 and n > 1:
                            project_out(hh * NCH + qc - 1)
                    project_out(2 * NCH - 1)

                @block.scalar
                def _(act):
                    for n in range(NQK):
                        c = n % NCH
                        act.wait_ge(proj, n + 1)
                        if n < NCH:
                            nc.scalar.activation(qz[0:DH, 0, c * CH:(c + 1) * CH], ps1[0:DH, n % 2, :], ACT.Copy)
                            nc.scalar.activation(qz[DH:P, 1, c * CH:(c + 1) * CH], ps1[DH:P, n % 2, :], ACT.Copy).then_inc(qk_out, 1)
                        else:
                            nc.scalar.activation(kT[:, c * CH:(c + 1) * CH], ps1[:, n % 2, :], ACT.Copy).then_inc(qk_out, 1)

                    def output(n):
                        act.wait_ge(pv, n + 1)
                        nc.scalar.activation(oT[:, :], psO[0:M, :], ACT.Copy).then_inc(oT_ready, 1)

                    for n, (hh, qc, kb, q0) in enumerate(PASS2):
                        act.wait_ge(sc2, n + 1)
                        if n >= NPB:
                            act.wait_ge(pv, n - NPB + 1)
                        nc.scalar.activation(probs[:, n % NPB, 0:CH - q0], ps2[:, n % 2, 0:CH - q0], ACT.Exp, scale=SC).then_inc(exped, 1)
                        if kb == 0 and n > 0:
                            output(n - 1)
                    output(N2 - 1)

                @block.vector
                def _(dve):
                    dve.wait_ge(pair_w, 3)
                    for c in range(NCH):
                        dve.wait_ge(proj, NQK + c + 1)
                        tiles = slice(c * TPC, (c + 1) * TPC)
                        for hh in range(2):
                            m4 = mask_p[:, hh, tiles].unsqueeze(2)
                            nc.vector.tensor_copy(va[:, hh, tiles, DH:DH + 1], m4)
                            last = nc.vector.tensor_tensor(
                                va[:, hh, tiles, 0:DH],
                                ps1[:, c % 2, :].rearrange("p (t h d) -> p t h d", t=TPC, h=2)[:, :, hh, :],
                                m4.to_broadcast([P, TPC, DH]), ALU.mult)
                        last.then_inc(v_out, 1)

                    st = Steps(dve, dve_step)
                    for hh in range(2):
                        for n, (h1, qt, kc, w, _) in enumerate(PASS1):
                            if h1 == hh:
                                dve.wait_ge(scored, n + 1)
                                nc.vector.tensor_reduce(m_part[:, qt, kc:kc + 1], ps1[:, n % 2, 0:w], axis=AX.X, op=ALU.max).then_inc(max_done, 1)
                        dve.wait_ge(max_done, (hh + 1) * N1 // 2)
                        st.run(nc.vector.tensor_reduce(m_neg[:, :], m_part[:, :, :], axis=AX.X, op=ALU.max, negate=True))
                        st.run(nc.vector.tensor_copy(m_split[:, hh, :, 0], m_neg[:, :]))
                        st.run(nc.vector.tensor_tensor(m_rest[:, :], m_neg[:, :], m_split[:, hh, :, 0], ALU.subtract))
                        st.run(nc.vector.tensor_copy(m_split[:, hh, :, 1], m_rest[:, :]))
                        st.run(nc.vector.tensor_tensor(m_neg[:, :], m_rest[:, :], m_split[:, hh, :, 1], ALU.subtract))
                        st.run(nc.vector.tensor_copy(m_split[:, hh, :, 2], m_neg[:, :]))
                        dve.sem_inc(split_ready, 1)
                    assert st.n == 12

                    for hh in range(2):
                        for c in range(NCH):
                            dve.wait_ge(rows, hh * NCH + c + 1)
                            nc.vector.tensor_copy(m_row[0:3, hh, c * CH:(c + 1) * CH], psR[0:3, :]).then_inc(row_ready, 1)

                    for g in range(2 * NCH):
                        dve.wait_ge(fin, g + 1)
                        dve.wait_ge(added, g)
                        nc.vector.reciprocal(rden[:, :].unsqueeze(2), psF[:, :, D:D + 1]).then_inc(recip, 1)
                        dve.wait_ge(recip, g + 1)
                        for j in range(TPC):
                            t = (g % NCH) * TPC + j
                            last = nc.vector.scalar_tensor_tensor(out=core.x[:, t, :], in0=psF[:, j, 0:D], scalar=rden[:, j:j + 1],
                                                                  in1=core.x[:, t, :], op0=ALU.mult, op1=ALU.add)
                        last.then_inc(added, 1)


def stage_rope_attention(nc, core, tag, WqkvT, WswapT, WoutT, cosT, sinT):
    H, DH, G, NPART = 16, 8, 4, 3
    NG = H // G
    SC = DH ** -0.5
    Q_ORDER, K_ORDER = (0, 1, 0, 1, 2, 0), (0, 0, 1, 1, 0, 2)
    PASS1 = [(g, qt, kc, min(CH, (qt + 1) * P - kc * CH), (qt // TPC) == kc)
             for g in range(G) for qt in range(NT) for kc in range(qt // TPC + 1)]
    PASS2 = [(g, qc, kb, max(0, kb * P - qc * CH))
             for qc in range(NCH) for kb in range(TPC * (qc + 1)) for g in range(G)]
    N1, N2 = len(PASS1), len(PASS2)
    N1H = N1 // G
    NPB, NS2, MR = 6, 3, 64
    with Stage(nc, tag) as s:
        o_all = s.sb("o_tokens", [P, NT, D])
        w_out = s.sb("w_out", [P, D])
        va = s.sb("v_aug", [P, NT, H, 32])
        scratch = {n: nc.dram_tensor(f"{tag}_{n}_parts", (NPART, P, T), BF16, kind="Internal").ap() for n in "qk"}
        with Stage(nc, tag + "_in") as q:
            w, ws = q.sb("w_qkv", [P, 3 * D]), q.sb("w_swapped", [P, 2 * D])
            cos, sin = q.sb("cos", [P, T]), q.sb("sin", [P, T])
            roped, rest = q.sb("roped", [P, T]), q.sb("rest", [P, T])
            parts = q.sb("parts", [P, 2, NPART, T], BF16)
            ps_a, ps_b = q.ps("ps_plain", [P, 2, CH]), q.ps("ps_swapped", [P, 2, CH])
            ps_v = q.ps("ps_v", [P, 2, TPC, D])
            loaded, stored, zeroed, dve_step = q.sem("loaded"), q.sem("stored"), q.sem("v_zeroed"), q.sem("dve_step")
            proj, a_used, b_used, v_done, v_out, split = (q.sem(n) for n in ("projected", "plain_used", "swapped_used", "v_done", "v_out", "split"))
            with nc.Block() as block:
                @block.sync
                def _(sp):
                    for dst, src in ((w, WqkvT), (ws, WswapT), (cos, cosT), (sin, sinT), (w_out, WoutT)):
                        sp.dma_start(dst[:, :], src).then_inc(loaded, 16)
                    for n, name in enumerate("qk"):
                        for part in range(NPART):
                            sp.wait_ge(split, n * NPART + part + 1)
                            sp.dma_start(scratch[name][part, :, :], parts[:, n, part, :]).then_inc(stored, 16)
                    sp.wait_ge(loaded, 80)
                    sp.wait_ge(stored, 16 * 2 * NPART)

                @block.gpsimd
                def _(pool):
                    nc.gpsimd.memset(va[:, :, :, :], 0.0).then_inc(zeroed, 1)
                    pool.wait_ge(zeroed, 1)
                    nc.gpsimd.memset(va[:, :, :, DH:DH + 1], 1.0).then_inc(zeroed, 1)

                @block.tensor
                def _(pe):
                    pe.wait_ge(loaded, 80)
                    for n in range(2 * NCH):
                        j, c = n // NCH, n % NCH
                        if n >= 2:
                            pe.wait_ge(a_used, n - 1)
                            pe.wait_ge(b_used, n - 1)
                        cols = core.xT[:, c * CH:(c + 1) * CH]
                        nc.tensor.matmul(ps_a[:, n % 2, :], w[:, j * D:(j + 1) * D], cols, start=True, stop=True)
                        nc.tensor.matmul(ps_b[:, n % 2, :], ws[:, j * D:(j + 1) * D], cols, start=True, stop=True).then_inc(proj, 1)
                    for c in range(NCH):
                        if c >= 2:
                            pe.wait_ge(v_out, c - 1)
                        for j in range(TPC):
                            t = c * TPC + j
                            last = nc.tensor.matmul(ps_v[:, c % 2, j, :], core.xT[:, t * P:(t + 1) * P], w[:, 2 * D:3 * D], start=True, stop=True)
                        last.then_inc(v_done, 1)

                @block.scalar
                def _(act):
                    act.wait_ge(zeroed, 2)
                    for c in range(NCH):
                        act.wait_ge(v_done, c + 1)
                        nc.scalar.activation(va[:, c * TPC:(c + 1) * TPC, :, 0:DH].rearrange("p t h d -> p (t h) d"),
                                             ps_v[:, c % 2, :, :].rearrange("p t (h d) -> p (t h) d", d=DH), ACT.Copy).then_inc(v_out, 1)

                @block.vector
                def _(dve):
                    st = Steps(dve, dve_step)
                    dve.wait_ge(loaded, 80)
                    for j in range(2):
                        for c in range(NCH):
                            n = j * NCH + c
                            cs = slice(c * CH, (c + 1) * CH)
                            dve.wait_ge(proj, n + 1)
                            nc.vector.tensor_tensor(roped[:, cs], ps_a[:, n % 2, :], cos[:, cs], ALU.mult).then_inc(a_used, 1)
                            nc.vector.tensor_tensor(rest[:, cs], ps_b[:, n % 2, :], sin[:, cs], ALU.mult).then_inc(b_used, 1)
                        dve.wait_ge(a_used, (j + 1) * NCH)
                        dve.wait_ge(b_used, (j + 1) * NCH)
                        st.run(nc.vector.tensor_tensor(roped[:, :], roped[:, :], rest[:, :], ALU.add))
                        for part in range(NPART):
                            nc.vector.tensor_copy(parts[:, j, part, :], roped[:, :]).then_inc(split, 1)
                            dve.wait_ge(split, j * NPART + part + 1)
                            if part < NPART - 1:
                                st.run(nc.vector.tensor_tensor(roped[:, :], roped[:, :], parts[:, j, part, :], ALU.subtract))

        with Stage(nc, tag + "_heads") as q:
            qs, ks = q.sb("q_stack", [P, G, T], BF16), q.sb("k_stack", [P, G, T], BF16)
            vg = q.sb("v_group", [P, NT, G, 32])
            m_part = q.sb("max_part", [P, NT, NCH])
            m_neg, m_rest = q.sb("max_neg", [P, NT]), q.sb("max_rest", [P, NT])
            m_split = q.sb("max_split", [P, G, NT, 3], BF16)
            probs = q.sb("probs", [P, NPB, CH])
            oT, rden = q.sb("oT", [P, CH]), q.sb("rden", [P, TPC, G])
            ps1, ps2 = q.ps("ps_pass1", [P, 2, CH]), q.ps("ps_pass2", [P, NS2, CH])
            ps_o, ps_r, ps_t = q.ps("ps_out", [P, CH]), q.ps("ps_rows", [P, CH]), q.ps("ps_turned", [P, TPC, G, 32])
            zeroed, dve_step = q.sem("zeroed"), q.sem("dve_step")
            q_in, k_in, v_ready, cleared = q.sem("q_in"), q.sem("k_in"), q.sem("v_ready"), q.sem("max_rows_cleared")
            scored, max_done, split_ready = q.sem("pass1_scored"), q.sem("pass1_max"), q.sem("max_split")
            rows, row_ready = q.sem("rows_transposed"), q.sem("rows_ready")
            sc2, exped, pv, oT_ready = q.sem("pass2_scored"), q.sem("exp_done"), q.sem("pv_done"), q.sem("oT_ready")
            turned, recip, o_out = q.sem("o_turned"), q.sem("recip"), q.sem("o_out")
            with nc.Block() as block:
                @block.gpsimd
                def _(pool):
                    nc.gpsimd.memset(qs[:, :, :], 0.0).then_inc(zeroed, 1)
                    nc.gpsimd.memset(m_part[:, :, :], -3.0e38).then_inc(zeroed, 1)
                    nc.gpsimd.memset(ks[:, :, :], 0.0).then_inc(zeroed, 1)
                    pool.wait_ge(zeroed, 3)
                    nc.gpsimd.memset(ks[MR:MR + 3, :, :], 1.0).then_inc(zeroed, 1)
            with nc.Fori(0, NG) as i:
                q.restart()
                with nc.Block() as block:
                    @block.sync
                    def _(sp):
                        for g in range(G):
                            for r in range(6):
                                src = bass.ds(i * (G * DH) + g * DH, DH)
                                sp.dma_start(qs[r * DH:(r + 1) * DH, g, :], scratch["q"][Q_ORDER[r], src, :]).then_inc(q_in, 16)
                                sp.dma_start(ks[r * DH:(r + 1) * DH, g, :], scratch["k"][K_ORDER[r], src, :]).then_inc(k_in, 16)
                        sp.wait_ge(q_in, 16 * 6 * G)
                        sp.wait_ge(k_in, 16 * 6 * G)

                    @block.gpsimd
                    def _(pool):
                        nc.gpsimd.tensor_copy(vg[:, :, :, :], va[:, :, bass.ds(i * G, G), :]).then_inc(v_ready, 1)

                    @block.tensor
                    def _(pe):
                        pe.wait_ge(cleared, 1)
                        pe.wait_ge(q_in, 16 * 6 * G)
                        pe.wait_ge(k_in, 16 * 6 * G)
                        for n, (g, qt, kc, w_, diag) in enumerate(PASS1):
                            if n >= 2:
                                pe.wait_ge(max_done, n - 1)
                            mm = nc.tensor.matmul(ps1[:, n % 2, 0:w_], qs[:, g, qt * P:(qt + 1) * P], ks[:, g, kc * CH:kc * CH + w_],
                                                  start=True, stop=not diag)
                            if diag:
                                mm = nc.tensor.matmul(ps1[:, n % 2, w_ - P:w_], core.ident_b[:, :], core.hide[:, :], start=False, stop=True)
                            mm.then_inc(scored, 1)
                        for g in range(G):
                            pe.wait_ge(split_ready, g + 1)
                            for c in range(NCH):
                                pe.wait_ge(row_ready, g * NCH + c)
                                for j in range(TPC):
                                    last = nc.tensor.matmul(ps_r[MR:MR + 3, j * P:(j + 1) * P], m_split[:, g, c * TPC + j, :],
                                                            core.ident_b[:, :], start=True, stop=True)
                                last.then_inc(rows, 1)

                        def scores(n):
                            g, qc, kb, q0 = PASS2[n]
                            if n >= NS2:
                                pe.wait_ge(exped, n - NS2 + 1)
                            q1, w_ = qc * CH + q0, CH - q0
                            diag = kb >= TPC * qc
                            mm = nc.tensor.matmul(ps2[:, n % NS2, 0:w_], ks[:, g, kb * P:(kb + 1) * P], qs[:, g, q1:q1 + w_],
                                                  start=True, stop=not diag)
                            if diag:
                                mm = nc.tensor.matmul(ps2[:, n % NS2, 0:P], core.ident_b[:, :], core.hideT[:, :], start=False, stop=True)
                            mm.then_inc(sc2, 1)

                        def turn(qc):
                            pe.wait_ge(oT_ready, qc + 1)
                            pe.wait_ge(o_out, qc)
                            for j in range(TPC):
                                last = nc.tensor.transpose(ps_t[:, j, :, :].rearrange("p g d -> p (g d)"), oT[:, j * P:(j + 1) * P], core.ident[:, :])
                            last.then_inc(turned, 1)

                        pe.wait_ge(row_ready, G * NCH)
                        pe.wait_ge(v_ready, 1)
                        scores(0)
                        scores(1)
                        for n, (g, qc, kb, q0) in enumerate(PASS2):
                            if n + 2 < N2:
                                scores(n + 2)
                            if kb == 0 and g == 0:
                                pe.wait_ge(oT_ready, qc)
                            pe.wait_ge(exped, n + 1)
                            nc.tensor.matmul(ps_o[32 * g:32 * g + 32, q0:CH], vg[:, kb, g, :], probs[:, n % NPB, 0:CH - q0],
                                             start=kb == 0, stop=kb == TPC * (qc + 1) - 1).then_inc(pv, 1)
                            if kb == 1 and g == G - 1 and qc > 0:
                                turn(qc - 1)
                        turn(NCH - 1)

                    @block.scalar
                    def _(act):
                        def output(n):
                            act.wait_ge(pv, n + 1)
                            nc.scalar.activation(oT[:, :], ps_o[:, :], ACT.Copy).then_inc(oT_ready, 1)

                        for n, (g, qc, kb, q0) in enumerate(PASS2):
                            act.wait_ge(sc2, n + 1)
                            if n >= NPB:
                                act.wait_ge(pv, n - NPB + 1)
                            nc.scalar.activation(probs[:, n % NPB, 0:CH - q0], ps2[:, n % NS2, 0:CH - q0], ACT.Exp, scale=SC).then_inc(exped, 1)
                            if kb == 0 and g == 1 and n > G:
                                output(n - 2)
                        output(N2 - 1)

                    @block.vector
                    def _(dve):
                        nc.vector.memset(qs[MR:MR + 3, :, :], 0.0).then_inc(cleared, 1)
                        st = Steps(dve, dve_step)
                        for g in range(G):
                            for n in range(g * N1H, (g + 1) * N1H):
                                _, qt, kc, w_, _ = PASS1[n]
                                dve.wait_ge(scored, n + 1)
                                nc.vector.tensor_reduce(m_part[:, qt, kc:kc + 1], ps1[:, n % 2, 0:w_], axis=AX.X, op=ALU.max).then_inc(max_done, 1)
                            dve.wait_ge(max_done, (g + 1) * N1H)
                            st.run(nc.vector.tensor_reduce(m_neg[:, :], m_part[:, :, :], axis=AX.X, op=ALU.max, negate=True))
                            st.run(nc.vector.tensor_copy(m_split[:, g, :, 0], m_neg[:, :]))
                            st.run(nc.vector.tensor_tensor(m_rest[:, :], m_neg[:, :], m_split[:, g, :, 0], ALU.subtract))
                            st.run(nc.vector.tensor_copy(m_split[:, g, :, 1], m_rest[:, :]))
                            st.run(nc.vector.tensor_tensor(m_neg[:, :], m_rest[:, :], m_split[:, g, :, 1], ALU.subtract))
                            st.run(nc.vector.tensor_copy(m_split[:, g, :, 2], m_neg[:, :]))
                            dve.sem_inc(split_ready, 1)
                        for g in range(G):
                            for c in range(NCH):
                                dve.wait_ge(rows, g * NCH + c + 1)
                                nc.vector.tensor_copy(qs[MR:MR + 3, g, c * CH:(c + 1) * CH], ps_r[MR:MR + 3, :]).then_inc(row_ready, 1)
                        for qc in range(NCH):
                            dve.wait_ge(turned, qc + 1)
                            dve.wait_ge(o_out, qc)
                            nc.vector.reciprocal(rden[:, :, :].unsqueeze(3), ps_t[:, :, :, DH:DH + 1]).then_inc(recip, 1)
                            dve.wait_ge(recip, qc + 1)
                            dst = o_all[:, qc * TPC:(qc + 1) * TPC, bass.ds(i * (G * DH), G * DH)].rearrange("p t (g d) -> p t g d", g=G)
                            nc.vector.tensor_tensor(dst, ps_t[:, :, :, 0:DH], rden[:, :, :].unsqueeze(3).to_broadcast([P, TPC, G, DH]), ALU.mult).then_inc(o_out, 1)

        stage_project(nc, core, tag + "_out", o_all, w_out)


def stage_project(nc, core, tag, o_all, w_out):
    with Stage(nc, tag) as s:
        oT = s.sb("oT", [P, 2, CH])
        ps_t, ps_y = s.ps("ps_turned", [P, 2, CH]), s.ps("ps_y", [P, 2, TPC, D])
        turned, ready, done, added = s.sem("turned"), s.sem("oT_ready"), s.sem("y_done"), s.sem("x_added")
        with nc.Block() as block:
            @block.tensor
            def _(pe):
                def turn(c):
                    if c >= 2:
                        pe.wait_ge(ready, c - 1)
                    for j in range(TPC):
                        last = nc.tensor.transpose(ps_t[:, c % 2, j * P:(j + 1) * P], o_all[:, c * TPC + j, :], core.ident[:, :])
                    last.then_inc(turned, 1)

                turn(0)
                for c in range(NCH):
                    if c + 1 < NCH:
                        turn(c + 1)
                    pe.wait_ge(ready, c + 1)
                    if c >= 2:
                        pe.wait_ge(added, c - 1)
                    for j in range(TPC):
                        last = nc.tensor.matmul(ps_y[:, c % 2, j, :], oT[:, c % 2, j * P:(j + 1) * P], w_out[:, :], start=True, stop=True)
                    last.then_inc(done, 1)

            @block.scalar
            def _(act):
                for c in range(NCH):
                    act.wait_ge(turned, c + 1)
                    if c >= 2:
                        act.wait_ge(done, c - 1)
                    nc.scalar.activation(oT[:, c % 2, :], ps_t[:, c % 2, :], ACT.Copy).then_inc(ready, 1)

            @block.vector
            def _(dve):
                for c in range(NCH):
                    dve.wait_ge(done, c + 1)
                    tiles = slice(c * TPC, (c + 1) * TPC)
                    nc.vector.tensor_tensor(core.x[:, tiles, :], core.x[:, tiles, :], ps_y[:, c % 2, :, :], ALU.add).then_inc(added, 1)
                dve.wait_ge(added, NCH)


def stage_power_attention(nc, core, tag, Wq, WqS, Wk, WkS, Wv, Wg, Wp, lnw, cosT, sinT):
    HK, R, DH = 8, 2, 64
    SC = DH ** -0.5
    M = DH + 1
    TINY = 2.0 ** -60
    PASS1 = [(hh, qt, kc, min(CH, (qt + 1) * P - kc * CH), (qt // TPC) == kc)
             for hh in range(R) for qt in range(NT) for kc in range(qt // TPC + 1)]
    PASS2 = [(hh, qc, kb, max(0, kb * P - qc * CH))
             for hh in range(R) for qc in range(NCH) for kb in range(TPC * (qc + 1))]
    N1, N2 = len(PASS1), len(PASS2)
    N1H = N1 // R
    NG = R * NCH
    ENDS = {n: hh * NCH + qc for n, (hh, qc, kb, _) in enumerate(PASS2) if kb == TPC * (qc + 1) - 1}
    NPB = 3

    def due(n, lag):
        return ENDS.get(n - lag)

    with Stage(nc, tag) as s:
        wq, wqs = s.sb("wq", [P, HK * R * DH]), s.sb("wq_swapped", [P, HK * R * DH])
        wk, wks, wv = s.sb("wk", [P, HK * DH]), s.sb("wk_swapped", [P, HK * DH]), s.sb("wv", [P, HK * DH])
        wp = s.sb("w_proj", [DH + 1, HK * R, D])
        lw = s.sb("ln_w", [DH, 1])
        cos, sin = s.sb("cos", [P, T]), s.sb("sin", [P, T])
        gcol, gend = s.sb("gate_col", [P, NT, HK]), s.sb("gate_tile_end", [P, NT, HK])
        later = s.sb("later_tiles", [P, NT, NT])
        tri = s.sb("tri_qk", [P, P])
        center = s.sb("center", [M, M])
        mean_col, den_col = s.sb("mean_col", [DH, 1]), s.sb("den_col", [M, 1])
        f_dram = nc.dram_tensor(f"{tag}_decay", (HK, T), F32, kind="Internal").ap()
        with Stage(nc, tag + "_in") as q:
            wg = q.sb("wg", [P, HK])
            v, e, l, g = (q.sb(n, [HK, T]) for n in ("v", "e", "l", "g"))
            one, last_row = q.sb("one", [HK, T]), q.sb("last_row", [P, P])
            ps_z, ps_g, ps_e = q.ps("ps_z", [HK, 2, CH]), q.ps("ps_g", [P, NT, HK]), q.ps("ps_e", [P, NT, HK])
            loaded, dve_step, pool_step = q.sem("loaded"), q.sem("dve_step"), q.sem("pool_step")
            z_done, z_out, v_ready, abs_done, exp_done, ln_done = (q.sem(n) for n in ("z_done", "z_out", "v_ready", "abs_done", "exp_done", "ln_done"))
            g_ready, f_ready, f_exp, stored, g_turned, gcol_ready, e_done = (q.sem(n) for n in ("g_ready", "f_ready", "f_exp", "stored", "g_turned", "gcol_ready", "e_done"))
            NLOAD = 10
            with nc.Block() as block:
                @block.sync
                def _(sp):
                    sp.wait_ge(pool_step, 1)
                    for dst, src in ((wq, Wq), (wqs, WqS), (wk, Wk), (wks, WkS), (wv, Wv), (wg, Wg), (cos, cosT), (sin, sinT), (lw, lnw)):
                        sp.dma_start(dst[:, :], src).then_inc(loaded, 16)
                    sp.dma_start(wp[0:DH, :, :], Wp.rearrange("(h d) n -> d h n", d=DH)).then_inc(loaded, 16)
                    sp.wait_ge(loaded, 16 * NLOAD)
                    sp.wait_ge(f_exp, 1)
                    sp.dma_start(f_dram, e[:, :]).then_inc(stored, 16)
                    sp.wait_ge(stored, 16)

                @block.gpsimd
                def _(pool):
                    st = Steps(pool, pool_step)
                    st.run(nc.gpsimd.memset(wp[:, :, :], 0.0))
                    st.run(nc.gpsimd.memset(one[:, :], 1.0))
                    st.run(nc.gpsimd.memset(later[:, :, :], 0.0))
                    st.run(nc.gpsimd.affine_select(out=later[:, :, :], in_=later[:, :, :], compare_op=ALU.is_ge, fill=MASKED, base=0,
                                                   pattern=[[1, NT], [-1, NT]], channel_multiplier=0))
                    st.run(nc.gpsimd.memset(tri[:, :], 1.0))
                    st.run(nc.gpsimd.affine_select(out=tri[:, :], in_=tri[:, :], compare_op=ALU.is_ge, fill=0.0, base=0,
                                                   pattern=[[-1, P]], channel_multiplier=1))
                    st.run(nc.gpsimd.memset(mean_col[:, :], 1.0 / DH))

                @block.tensor
                def _(pe):
                    pe.wait_ge(loaded, 16 * NLOAD)
                    for c in range(NCH):
                        if c >= 2:
                            pe.wait_ge(z_out, c - 1)
                        nc.tensor.matmul(ps_z[:, c % 2, :], wg[:, :], core.xT[:, c * CH:(c + 1) * CH], start=True, stop=True).then_inc(z_done, 1)
                    pe.wait_ge(g_ready, 1)
                    for t in range(NT):
                        last = nc.tensor.transpose(ps_g[:, t, :], g[:, t * P:(t + 1) * P], core.ident[0:HK, 0:HK])
                    last.then_inc(g_turned, 1)
                    pe.wait_ge(gcol_ready, 1)
                    nc.tensor.matmul(ps_e[:, :, :].rearrange("p t h -> p (t h)"), last_row[:, :], gcol[:, :, :].rearrange("p t h -> p (t h)"),
                                     start=True, stop=True).then_inc(e_done, 1)

                @block.scalar
                def _(act):
                    act.wait_ge(v_ready, 1)
                    nc.scalar.activation(l[:, :], v[:, :], ACT.Abs).then_inc(abs_done, 1)
                    act.wait_ge(abs_done, 1)
                    nc.scalar.activation(e[:, :], l[:, :], ACT.Exp, scale=-1.0).then_inc(exp_done, 1)
                    act.wait_ge(exp_done, 1)
                    nc.scalar.activation(l[:, :], e[:, :], ACT.Ln, bias=1.0).then_inc(ln_done, 1)
                    act.wait_ge(f_ready, 1)
                    nc.scalar.activation(e[:, :], e[:, :], ACT.Exp).then_inc(f_exp, 1)

                @block.vector
                def _(dve):
                    st = Steps(dve, dve_step)
                    dve.wait_ge(loaded, 16 * NLOAD)
                    dve.wait_ge(pool_step, 7)
                    st.add(nc.vector.tensor_scalar(wp[0:DH, :, :], wp[0:DH, :, :], lw[:, 0:1], None, ALU.mult))
                    st.add(nc.vector.tensor_copy(last_row[:, :], core.ident[:, P - 1:P].to_broadcast([P, P])))
                    st.add(nc.vector.tensor_copy(den_col[:, :], core.ident[0:M, DH:M]))
                    st.run(nc.vector.tensor_copy(center[:, :], core.ident[0:M, 0:M]))
                    st.add(nc.vector.tensor_scalar(center[0:DH, 0:DH], center[0:DH, 0:DH], -1.0 / DH, None, ALU.add))
                    for c in range(NCH):
                        dve.wait_ge(z_done, c + 1)
                        nc.vector.tensor_scalar(v[:, c * CH:(c + 1) * CH], ps_z[:, c % 2, :], 6.906768, None, ALU.add).then_inc(z_out, 1)
                    dve.wait_ge(z_out, NCH)
                    dve.sem_inc(v_ready, 1)
                    dve.wait_ge(exp_done, 1)
                    st.run(nc.vector.tensor_scalar(g[:, :], e[:, :], 1.0, -1.0, ALU.add, ALU.add))
                    st.run(nc.vector.tensor_tensor(g[:, :], e[:, :], g[:, :], ALU.subtract))
                    dve.wait_ge(ln_done, 1)
                    st.run(nc.vector.tensor_tensor(g[:, :], g[:, :], l[:, :], ALU.add))
                    st.run(nc.vector.scalar_tensor_tensor(out=v[:, :], in0=v[:, :], scalar=0.0, in1=g[:, :], op0=ALU.min, op1=ALU.subtract))
                    st.run(nc.vector.tensor_tensor_scan(l[:, :], one[:, :], v[:, :], 0.0, ALU.mult, ALU.add))
                    st.run(nc.vector.tensor_scalar(g[:, :], l[:, :], 0.5, None, ALU.mult))
                    dve.sem_inc(g_ready, 1)
                    by_tile = g[:, :].rearrange("h (t p) -> h t p", p=P)
                    nc.vector.tensor_tensor(e[:, :].rearrange("h (t p) -> h t p", p=P), by_tile[:, :, P - 1:P].to_broadcast([HK, NT, P]), by_tile,
                                            ALU.subtract).then_inc(f_ready, 1)
                    dve.wait_ge(g_turned, 1)
                    nc.vector.tensor_copy(gcol[:, :, :], ps_g[:, :, :]).then_inc(gcol_ready, 1)
                    dve.wait_ge(e_done, 1)
                    st.run(nc.vector.tensor_copy(gend[:, :, :], ps_e[:, :, :]))

        with Stage(nc, tag + "_heads") as q:
            wq_h, wqs_h, wk_h, wks_h = (q.sb(n, [P, P]) for n in ("wq_head", "wq_swapped_head", "wk_head", "wk_swapped_head"))
            ngk, ge = q.sb("minus_gate", [P, NT]), q.sb("gate_end", [P, NT])
            decay = q.sb("decay", [P, T])
            qz = q.sb("q_padded", [P, R, T])
            kT, kd = q.sb("kT", [P, T]), q.sb("k_decayed", [P, T])
            va = q.sb("v_aug", [P, NT, M])
            t1, t2 = q.sb("rope_plain", [P, 2, CH]), q.sb("rope_swapped", [P, 2, CH])
            m_abs = q.sb("max_abs", [P, NT, NT])
            l1, l2 = q.sb("log_a", [P, NT, NT]), q.sb("log_b", [P, NT, NT])
            scrap = q.sb("masked_scores", [P, P])
            m_neg, m_rest = q.sb("max_neg", [P, NT]), q.sb("max_rest", [P, NT])
            m_split = q.sb("max_split", [P, R, NT, 3], BF16)
            m_row = q.sb("max_row", [P, R, T], BF16)
            wexp, sabs, probs = (q.sb(n, [P, NPB, CH]) for n in ("weights", "scores_abs", "probs"))
            oT, cT, sq = q.sb("oT", [M, CH]), q.sb("centered_T", [M, CH]), q.sb("squares_T", [DH, CH])
            rd, uu = q.sb("rden", [P, TPC]), q.sb("var", [P, TPC])
            ps1, psS = q.ps("ps_pass1_gate", [P, 2, CH]), q.ps("ps_scores", [P, 2, CH])
            psO, psR, psF = q.ps("ps_out", [P, CH]), q.ps("ps_rows_center", [P, CH]), q.ps("ps_final", [P, TPC, D])
            psV = q.ps("ps_columns", [P, TPC, 2])
            zeroed, dve_step = q.sem("zeroed"), q.sem("dve_step")
            w_ready, decay_in, proj, t_done, q_out, k_out = (q.sem(n) for n in ("weights_ready", "decay_in", "projected", "rope_products", "q_out", "k_out"))
            kd_out, v_done, v_out, scored, max_done = (q.sem(n) for n in ("k_decayed", "v_done", "v_out", "pass1_scored", "pass1_max"))
            ln_in, ln_out, split_ready, rows, row_ready = (q.sem(n) for n in ("ln_in", "ln_out", "max_split", "rows_transposed", "rows_ready"))
            sc2, wexp_done, abs_done, b_done, a_done, pv = (q.sem(n) for n in ("pass2_scored", "gate_exp", "scores_abs", "product", "squared", "pv_done"))
            oT_ready, centered, cT_ready, fin, u_ready, rs_ready, added = (q.sem(n) for n in ("oT_ready", "centered", "cT_ready", "final", "var_ready", "rstd_ready", "x_added"))
            recip = q.sem("recip")
            act_step = q.sem("act_step")
            with nc.Block() as block:
                @block.gpsimd
                def _(pool):
                    for n, (buf, val) in enumerate(((qz[:, :, :], 0.0), (m_row[:, :, :], 0.0), (m_abs[:, :, :], 0.0), (va[:, :, DH:M], 1.0))):
                        nc.gpsimd.memset(buf, val).then_inc(zeroed, 1)
                        pool.wait_ge(zeroed, n + 1)
            with nc.Fori(0, HK) as i:
                q.restart()
                with nc.Block() as block:
                    @block.sync
                    def _(sp):
                        sp.dma_start(decay[:, :], f_dram[bass.ds(i, 1), :].partition_broadcast(P)).then_inc(decay_in, 16)
                        sp.wait_ge(decay_in, 16)

                    @block.gpsimd
                    def _(pool):
                        nc.gpsimd.tensor_copy(wq_h[:, :], wq[:, bass.ds(i * P, P)]).then_inc(w_ready, 1)
                        nc.gpsimd.tensor_copy(wqs_h[:, :], wqs[:, bass.ds(i * P, P)]).then_inc(w_ready, 1)
                        for half in range(2):
                            nc.gpsimd.tensor_copy(wk_h[:, half * DH:(half + 1) * DH], wk[:, bass.ds(i * DH, DH)]).then_inc(w_ready, 1)
                            nc.gpsimd.tensor_copy(wks_h[:, half * DH:(half + 1) * DH], wks[:, bass.ds(i * DH, DH)]).then_inc(w_ready, 1)
                        pool.wait_ge(decay_in, 16)
                        for c in range(NCH):
                            cs = slice(c * CH, (c + 1) * CH)
                            pool.wait_ge(k_out, c + 1)
                            nc.gpsimd.tensor_tensor(kd[:, cs], kT[:, cs], decay[:, cs], ALU.mult).then_inc(kd_out, 1)

                    @block.tensor
                    def _(pe):
                        for c in range(NCH):
                            if c >= 2:
                                pe.wait_ge(v_out, c - 1)
                            for j in range(TPC):
                                t = c * TPC + j
                                last = nc.tensor.matmul(psO[:, j * DH:(j + 1) * DH] if c % 2 == 0 else psR[:, j * DH:(j + 1) * DH],
                                                        core.xT[:, t * P:(t + 1) * P], wv[:, bass.ds(i * DH, DH)], start=True, stop=True)
                            last.then_inc(v_done, 1)
                        pe.wait_ge(w_ready, 6)
                        for n in range(2 * NCH):
                            c = n % NCH
                            a, b = ((wk_h, wks_h), (wq_h, wqs_h))[n // NCH]
                            if n >= 2:
                                pe.wait_ge(t_done, 2 * (n - 1))
                            cols = core.xT[:, c * CH:(c + 1) * CH]
                            nc.tensor.matmul(ps1[:, n % 2, :], a[:, :], cols, start=True, stop=True)
                            nc.tensor.matmul(psS[:, n % 2, :], b[:, :], cols, start=True, stop=True).then_inc(proj, 1)
                        pe.wait_ge(t_done, 4 * NCH)
                        pe.wait_ge(q_out, NCH)
                        pe.wait_ge(kd_out, NCH)
                        for n, (hh, qt, kc, w_, diag) in enumerate(PASS1):
                            if n >= 2:
                                pe.wait_ge(max_done, n - 1)
                            nc.tensor.matmul(ps1[:, n % 2, 0:w_], qz[:, hh, qt * P:(qt + 1) * P], kd[:, kc * CH:kc * CH + w_],
                                             start=True, stop=True).then_inc(scored, 1)
                        pe.wait_ge(v_out, NCH)

                        def maxima_to_rows(hh):
                            pe.wait_ge(split_ready, hh + 1)
                            for c in range(NCH):
                                pe.wait_ge(row_ready, hh * NCH + c)
                                for j in range(TPC):
                                    last = nc.tensor.matmul(psR[0:3, j * P:(j + 1) * P], m_split[:, hh, c * TPC + j, :],
                                                            core.ident_b[:, :], start=True, stop=True)
                                last.then_inc(rows, 1)

                        def scores(n):
                            hh, qc, kb, q0 = PASS2[n]
                            if n in (0, N2 // 2):
                                pe.wait_ge(row_ready, (hh + 1) * NCH)
                            if n >= 2:
                                pe.wait_ge(wexp_done, n - 1)
                                pe.wait_ge(abs_done, n - 1)
                            q1, w_ = qc * CH + q0, CH - q0
                            diag = kb >= TPC * qc
                            mm = nc.tensor.matmul(ps1[:, n % 2, 0:w_], core.ones_b[:, :], m_row[:, hh, q1:q1 + w_], start=True, stop=not diag)
                            if diag:
                                mm = nc.tensor.matmul(ps1[:, n % 2, 0:P], core.ident_b[:, :], core.hideT[:, :], start=False, stop=True)
                            nc.tensor.matmul(psS[:, n % 2, 0:w_], kT[:, kb * P:(kb + 1) * P], qz[:, hh, q1:q1 + w_],
                                             start=True, stop=True).then_inc(sc2, 1)

                        def values(n):
                            hh, qc, kb, q0 = PASS2[n]
                            if kb == 0:
                                pe.wait_ge(oT_ready, hh * NCH + qc)
                            pe.wait_ge(a_done, n + 1)
                            nc.tensor.matmul(psO[0:M, q0:CH], va[:, kb, :], probs[:, n % NPB, 0:CH - q0],
                                             start=kb == 0, stop=kb == TPC * (qc + 1) - 1).then_inc(pv, 1)

                        def center_values(g):
                            pe.wait_ge(oT_ready, g + 1)
                            nc.tensor.matmul(psR[0:M, :], center[:, :], oT[:, :], start=True, stop=True).then_inc(centered, 1)

                        def final(g):
                            pe.wait_ge(cT_ready, 2 * g + 2)
                            pe.wait_ge(added, g)
                            for j in range(TPC):
                                js = slice(j * P, (j + 1) * P)
                                nc.tensor.matmul(psF[:, j, :], cT[:, js], wp[:, bass.ds(i * R + g // NCH, 1), :], start=True, stop=True)
                                nc.tensor.matmul(psV[:, j, 0:1], cT[:, js], den_col[:, :], start=True, stop=True)
                                last = nc.tensor.matmul(psV[:, j, 1:2], sq[:, js], mean_col[:, :], start=True, stop=True)
                            last.then_inc(fin, 1)

                        maxima_to_rows(0)
                        maxima_to_rows(1)
                        scores(0)
                        scores(1)
                        for n in range(N2 + 4):
                            if n < N2:
                                if 2 <= n + 1 < N2:
                                    scores(n + 1)
                                values(n)
                            if (g := due(n, 1)) is not None:
                                center_values(g)
                            if (g := due(n, 3)) is not None:
                                final(g)

                    @block.scalar
                    def _(act):
                        for c in range(NCH):
                            act.wait_ge(v_done, c + 1)
                            src = (psO, psR)[c % 2][:, 0:TPC * DH].rearrange("p (t d) -> p t d", d=DH)
                            nc.scalar.activation(va[:, c * TPC:(c + 1) * TPC, 0:DH], src, ACT.Copy).then_inc(v_out, 1)
                        for hh in range(R):
                            act.wait_ge(ln_in, 2 * hh + 1)
                            nc.scalar.activation(l1[:, :, :], l1[:, :, :], ACT.Ln).then_inc(ln_out, 1)
                            act.wait_ge(ln_in, 2 * hh + 2)
                            nc.scalar.activation(l2[:, :, :], l2[:, :, :], ACT.Ln).then_inc(ln_out, 1)

                        def gate_exp(n):
                            hh, qc, kb, q0 = PASS2[n]
                            w_ = CH - q0
                            act.wait_ge(sc2, n + 1)
                            if n >= NPB:
                                act.wait_ge(b_done, n - NPB + 1)
                            nc.scalar.activation(wexp[:, n % NPB, 0:w_], ps1[:, n % 2, 0:w_], ACT.Exp, bias=ngk[:, kb:kb + 1]).then_inc(wexp_done, 1)
                            nc.scalar.activation(sabs[:, n % NPB, 0:w_], psS[:, n % 2, 0:w_], ACT.Abs, scale=SC).then_inc(abs_done, 1)

                        gate_exp(0)
                        for n in range(N2 + 8):
                            if n < N2:
                                if n + 1 < N2:
                                    gate_exp(n + 1)
                                hh, qc, kb, q0 = PASS2[n]
                                act.wait_ge(b_done, n + 1)
                                if n >= NPB:
                                    act.wait_ge(pv, n - NPB + 1)
                                nc.scalar.activation(probs[:, n % NPB, 0:CH - q0], sabs[:, n % NPB, 0:CH - q0], ACT.Square).then_inc(a_done, 1)
                            if (g := due(n, 0)) is not None:
                                act.wait_ge(pv, n + 1)
                                act.wait_ge(centered, g)
                                nc.scalar.activation(oT[:, :], psO[0:M, :], ACT.Copy).then_inc(oT_ready, 1)
                            if (g := due(n, 2)) is not None:
                                act.wait_ge(centered, g + 1)
                                act.wait_ge(fin, g)
                                nc.scalar.activation(cT[:, :], psR[0:M, :], ACT.Copy).then_inc(cT_ready, 1)
                                nc.scalar.activation(sq[:, :], psR[0:DH, :], ACT.Square).then_inc(cT_ready, 1)
                            if (g := due(n, 4)) is not None:
                                act.wait_ge(u_ready, g + 1)
                                st = Steps(act, act_step, g)
                                st.run(nc.scalar.activation(uu[:, :], uu[:, :], ACT.Ln))
                                nc.scalar.activation(uu[:, :], uu[:, :], ACT.Exp, scale=-0.5).then_inc(rs_ready, 1)

                    @block.vector
                    def _(dve):
                        st = Steps(dve, dve_step)
                        st.add(nc.vector.tensor_scalar(ngk[:, :], gcol[:, :, bass.ds(i, 1)].rearrange("p t h -> p (t h)"), -1.0, None, ALU.mult))
                        st.add(nc.vector.tensor_copy(ge[:, :], gend[:, :, bass.ds(i, 1)].rearrange("p t h -> p (t h)")))
                        for n in range(2 * NCH):
                            c = n % NCH
                            cs = slice(c * CH, (c + 1) * CH)
                            dve.wait_ge(proj, n + 1)
                            if n >= 2:
                                if n - 2 < NCH:
                                    dve.wait_ge(k_out, n - 1)
                                else:
                                    dve.wait_ge(q_out, n - 1 - NCH)
                            nc.vector.tensor_tensor(t1[:, n % 2, :], ps1[:, n % 2, :], cos[:, cs], ALU.mult).then_inc(t_done, 1)
                            nc.vector.tensor_tensor(t2[:, n % 2, :], psS[:, n % 2, :], sin[:, cs], ALU.mult).then_inc(t_done, 1)
                            dve.wait_ge(t_done, 2 * n + 2)
                            if n < NCH:
                                nc.vector.tensor_tensor(kT[:, cs], t1[:, n % 2, :], t2[:, n % 2, :], ALU.add).then_inc(k_out, 1)
                            else:
                                nc.vector.tensor_tensor(qz[0:DH, 0, cs], t1[0:DH, n % 2, :], t2[0:DH, n % 2, :], ALU.add)
                                nc.vector.tensor_tensor(qz[DH:P, 1, cs], t1[DH:P, n % 2, :], t2[DH:P, n % 2, :], ALU.add).then_inc(q_out, 1)
                        for hh in range(R):
                            for n in range(hh * N1H, (hh + 1) * N1H):
                                _, qt, kc, w_, diag = PASS1[n]
                                dve.wait_ge(scored, n + 1)
                                nb = w_ // P - (1 if diag else 0)
                                if nb:
                                    last = nc.vector.tensor_reduce(m_abs[:, qt, kc * TPC:kc * TPC + nb],
                                                                   ps1[:, n % 2, 0:nb * P].rearrange("p (b k) -> p b k", k=P),
                                                                   axis=AX.X, op=ALU.max, apply_absolute_value=True)
                                if diag:
                                    st.run(nc.vector.tensor_tensor(scrap[:, :], ps1[:, n % 2, w_ - P:w_], tri[:, :], ALU.mult))
                                    last = nc.vector.tensor_reduce(m_abs[:, qt, qt:qt + 1], scrap[:, :], axis=AX.X, op=ALU.max, apply_absolute_value=True)
                                last.then_inc(max_done, 1)
                                if diag:
                                    dve.wait_ge(max_done, n + 1)
                            dve.wait_ge(max_done, (hh + 1) * N1H)
                            st.run(nc.vector.tensor_scalar(l2[:, :, :], m_abs[:, :, :], SC, 1e-30, ALU.mult, ALU.add))
                            nc.vector.tensor_scalar(l1[:, :, :], l2[:, :, :], TINY, None, ALU.max).then_inc(ln_in, 1)
                            dve.wait_ge(ln_in, 2 * hh + 1)
                            nc.vector.tensor_scalar(l2[:, :, :], l2[:, :, :], TINY, 1.0 / TINY, ALU.min, ALU.mult).then_inc(ln_in, 1)
                            dve.wait_ge(ln_out, 2 * hh + 2)
                            st.run(nc.vector.tensor_tensor(l1[:, :, :], l1[:, :, :], l2[:, :, :], ALU.add))
                            st.run(nc.vector.tensor_tensor(l1[:, :, :], l1[:, :, :], ge[:, :].unsqueeze(1).to_broadcast([P, NT, NT]), ALU.subtract))
                            st.run(nc.vector.tensor_tensor(l1[:, :, :], l1[:, :, :], later[:, :, :], ALU.add))
                            st.run(nc.vector.tensor_reduce(m_neg[:, :], l1[:, :, :], axis=AX.X, op=ALU.max, negate=True))
                            st.run(nc.vector.tensor_copy(m_split[:, hh, :, 0], m_neg[:, :]))
                            st.run(nc.vector.tensor_tensor(m_rest[:, :], m_neg[:, :], m_split[:, hh, :, 0], ALU.subtract))
                            st.run(nc.vector.tensor_copy(m_split[:, hh, :, 1], m_rest[:, :]))
                            st.run(nc.vector.tensor_tensor(m_neg[:, :], m_rest[:, :], m_split[:, hh, :, 1], ALU.subtract))
                            st.run(nc.vector.tensor_copy(m_split[:, hh, :, 2], m_neg[:, :]))
                            dve.sem_inc(split_ready, 1)
                        for hh in range(R):
                            for c in range(NCH):
                                dve.wait_ge(rows, hh * NCH + c + 1)
                                nc.vector.tensor_copy(m_row[0:3, hh, c * CH:(c + 1) * CH], psR[0:3, :]).then_inc(row_ready, 1)
                        for n in range(N2 + 8):
                            if n < N2:
                                hh, qc, kb, q0 = PASS2[n]
                                w_ = CH - q0
                                dve.wait_ge(wexp_done, n + 1)
                                dve.wait_ge(abs_done, n + 1)
                                nc.vector.scalar_tensor_tensor(out=sabs[:, n % NPB, 0:w_], in0=sabs[:, n % NPB, 0:w_], scalar=1e-30,
                                                               in1=wexp[:, n % NPB, 0:w_], op0=ALU.add, op1=ALU.mult).then_inc(b_done, 1)
                            if (g := due(n, 3)) is not None:
                                dve.wait_ge(fin, g + 1)
                                st.run(nc.vector.tensor_scalar(rd[:, :], psV[:, :, 0], 1e-6, None, ALU.add))
                                st.run(nc.vector.reciprocal(rd[:, :], rd[:, :]))
                                st.run(nc.vector.tensor_tensor(uu[:, :], psV[:, :, 1], rd[:, :], ALU.mult))
                                st.run(nc.vector.tensor_tensor(uu[:, :], uu[:, :], rd[:, :], ALU.mult))
                                nc.vector.tensor_scalar(uu[:, :], uu[:, :], 1e-9, None, ALU.add).then_inc(u_ready, 1)
                            if (g := due(n, 4)) is not None:
                                dve.wait_ge(rs_ready, g + 1)
                                st.run(nc.vector.tensor_tensor(rd[:, :], rd[:, :], uu[:, :], ALU.mult))
                                for j in range(TPC):
                                    t = (g % NCH) * TPC + j
                                    last = nc.vector.scalar_tensor_tensor(out=core.x[:, t, :], in0=psF[:, j, :], scalar=rd[:, j:j + 1],
                                                                          in1=core.x[:, t, :], op0=ALU.mult, op1=ALU.add)
                                last.then_inc(added, 1)
                                dve.wait_ge(added, g + 1)


def hybrid_kernel(nc, a, out):
    with ExitStack() as ctx:
        core = Core(nc, ctx)
        stage_constants(nc, core, a["x"])
        with nc.sbuf_tensor("x_norm", [P, NT, D], F32) as xn:
            stage_norm(nc, core, "n0", xn)
            stage_mamba(nc, core, "mamba", xn, a)

        def gelu_ffn(tag):
            stage_norm(nc, core, tag + "_n")
            with nc.sbuf_tensor(tag + "_comb", [P, NT, 16], F32) as comb:
                stage_route(nc, core, tag + "_r", 16, a["Wr"], a["br"], comb)
                stage_gelu_experts(nc, core, tag, comb, a["W1"], a["b1"], a["g1T"], a["be1T"], a["W2"], a["b2"])

        def silu_ffn(tag):
            stage_norm(nc, core, tag + "_n")
            with nc.sbuf_tensor(tag + "_comb", [P, NT, 8], F32) as comb:
                stage_route(nc, core, tag + "_r", 8, a["gate_wT"], None, comb, capacity=int(1.25 * T / 8))
                stage_silu_experts(nc, core, tag, comb, a["gate_projT"], a["up_projT"], a["down_projT"])

        gelu_ffn("ffn0")
        stage_norm(nc, core, "n2")
        stage_span_attention(nc, core, "span", a["Wq"], a["Wk"], a["Wv"], a["Wo"], a["span_val"])
        gelu_ffn("ffn1")
        stage_norm(nc, core, "n4")
        stage_rope_attention(nc, core, "rope", a["W_qkvT"], a["W_qk_swapT"], a["W_outT"], a["cos8"], a["sin8"])
        silu_ffn("moe0")
        stage_norm(nc, core, "n6")
        stage_power_attention(nc, core, "power", a["pq"], a["pq_swap"], a["pk"], a["pk_swap"], a["pv"], a["pg"], a["w_proj"], a["ln_w"],
                              a["cos64"], a["sin64"])
        silu_ffn("moe1")
        stage_store(nc, core, out)


def _rotary_tables(np, angles, heads):
    cos, sin = np.cos(angles).astype(np.float32), np.sin(angles).astype(np.float32)
    pairs, t = angles.shape
    cos = np.tile(np.repeat(cos, 2, axis=0), (heads, 1))
    sin = np.tile(np.stack([-sin, sin], axis=1).reshape(2 * pairs, t), (heads, 1))
    return cos, sin


def kernel(**inputs):
    import numpy as np
    import concourse.bacc as bacc
    from concourse.bass_utils import run_bass_kernel_spmd

    w = {k: np.asarray(v) for k, v in inputs.items()}
    m = lambda name: w["L0_attn_a_" + name]
    halves = lambda v: v.reshape(-1, 128).T
    swapped = lambda v: v.reshape(v.shape[0], -1, 2)[:, :, ::-1].reshape(v.shape)
    times = np.arange(2048, dtype=np.float32)
    f8 = (1.0 / np.float32(10000.0) ** (np.arange(0, 8, 2, dtype=np.float32) / np.float32(8))).astype(np.float32)
    f64 = (2.0 * np.pi / float(2048) ** (np.arange(0, 64, 2, dtype=np.float32) / np.float32(64))).astype(np.float32)
    cos8, sin8 = _rotary_tables(np, np.outer(f8, times).astype(np.float32), 16)
    cos64, sin64 = _rotary_tables(np, np.outer(f64, times).astype(np.float32), 2)
    qkv, pa = w["L1_attn_a_W_qkv"], w["L1_attn_b_w_attn"]
    arrays = {
        "x": m("x"), "W_in": m("W_in"), "b_in": halves(m("b_in")), "conv_w": m("conv_w").reshape(2, 128, 4).transpose(1, 0, 2),
        "conv_b": halves(m("conv_b")), "W_xp": m("W_xp"), "b_xp": m("b_xp").reshape(32, 1), "W_dt": m("W_dt"), "b_dt": halves(m("b_dt")),
        "A_log": m("A_log"), "D_skip": halves(m("D_skip")), "W_out": m("W_out"), "b_out": m("b_out"), "alpha": m("alpha"), "beta": m("beta"),
        "Wq": w["L0_attn_b_Wq"], "Wk": w["L0_attn_b_Wk"], "Wv": w["L0_attn_b_Wv"], "Wo": w["L0_attn_b_Wo"], "span_val": w["L0_attn_b_span_val"],
        "Wr": w["L0_ffn_Wr"], "br": w["L0_ffn_br"], "W1": w["L0_ffn_W1"], "b1": w["L0_ffn_b1"], "g1T": w["L0_ffn_g1"].T, "be1T": w["L0_ffn_be1"].T,
        "W2": w["L0_ffn_W2"], "b2": w["L0_ffn_b2"],
        "W_qkvT": qkv.T, "W_qk_swapT": swapped(qkv[:256].T), "W_outT": w["L1_attn_a_W_out"].T, "cos8": cos8, "sin8": sin8,
        "pq": pa[:, :1024], "pq_swap": swapped(pa[:, :1024]), "pk": pa[:, 1024:1536], "pk_swap": swapped(pa[:, 1024:1536]),
        "pv": pa[:, 1536:2048], "pg": pa[:, 2048:], "w_proj": w["L1_attn_b_w_proj"], "ln_w": w["L1_attn_b_ln_w"].reshape(64, 1),
        "cos64": cos64, "sin64": sin64,
        "gate_wT": w["L1_ffn_gate_w"].T, "gate_projT": w["L1_ffn_gate_proj_w"].transpose(2, 0, 1),
        "up_projT": w["L1_ffn_up_proj_w"].transpose(2, 0, 1), "down_projT": w["L1_ffn_down_proj_w"].transpose(2, 0, 1),
    }
    arrays = {f"in_{k}": np.ascontiguousarray(v) for k, v in arrays.items()}
    nc = bacc.Bacc("TRN2", target_bir_lowering=False, num_devices=1)
    dram = {k[3:]: nc.dram_tensor(k, v.shape, mybir.dt.from_np(v.dtype), kind="ExternalInput").ap() for k, v in arrays.items()}
    out = nc.dram_tensor("out", (1, 2048, 128), F32, kind="ExternalOutput").ap()
    hybrid_kernel(nc, dram, out)
    return run_bass_kernel_spmd(nc, [arrays], core_ids=[0]).results[0]["out"]
```

```python
import concourse.bass as bass
from concourse import mybir
from concourse.alu_op_type import AluOpType as ALU
from contextlib import ExitStack

F32 = mybir.dt.float32
BF16 = mybir.dt.bfloat16
I32 = mybir.dt.int32
U32 = mybir.dt.uint32
ACT = mybir.ActivationFunctionType
AX = mybir.AxisListType

P = 128
T = 2048
D = 128
NT = T // P
CH = 512
NCH = T // CH
TPC = CH // P
MASKED = -1.0e30


class Steps:

    def __init__(self, eng, sem, base=0):
        self.eng, self.sem, self.base, self.n = eng, sem, base, 0

    def add(self, ins):
        ins.then_inc(self.sem, 1)
        self.n += 1
        return self.n

    def wait(self, n=None):
        self.eng.wait_ge(self.sem, self.base + (self.n if n is None else n))

    def run(self, ins):
        self.add(ins)
        self.wait()


class Core:

    def __init__(self, nc, ctx):
        self.nc = nc
        sb = lambda name, shape, dt: ctx.enter_context(nc.sbuf_tensor(name, shape, dt))
        self.x = sb("x_residual", [P, NT, D], F32)
        self.xT = sb("x_norm_T", [P, T], F32)
        self.ident = sb("ident", [P, P], F32)
        self.ident_b = sb("ident_b", [P, P], BF16)
        self.hide = sb("hide_qk", [P, P], BF16)
        self.hideT = sb("hide_kq", [P, P], BF16)
        self.ones_b = sb("ones_b", [P, P], BF16)


class Stage:

    def __init__(self, nc, tag):
        self.nc, self.tag, self.ctx, self.sems = nc, tag, ExitStack(), []

    def sb(self, name, shape, dt=F32):
        return self.ctx.enter_context(self.nc.sbuf_tensor(f"{self.tag}_{name}", shape, dt))

    def ps(self, name, shape, dt=F32):
        return self.ctx.enter_context(self.nc.psum_tensor(f"{self.tag}_{name}", shape, dt))

    def sem(self, name):
        self.sems.append(self.ctx.enter_context(self.nc.semaphore(f"{self.tag}_{name}")))
        return self.sems[-1]

    def restart(self):
        with self.nc.Block() as block:
            @block.gpsimd
            def _(pool):
                for sem in self.sems:
                    pool.sem_clear(sem)

    def __enter__(self):
        return self

    def __exit__(self, kind, *rest):
        if kind is None:
            self.restart()
        self.ctx.close()


def stage_constants(nc, core, x_in):
    with Stage(nc, "setup") as s:
        x_loaded = s.sem("x_loaded")
        pool_step = s.sem("pool_step")
        with nc.Block() as block:
            @block.sync
            def _(sp):
                sp.dma_start(core.x[:, :, :], x_in.rearrange("b (t p) d -> p (b t) d", p=P)).then_inc(x_loaded, 16)
                sp.wait_ge(x_loaded, 16)

            @block.gpsimd
            def _(pool):
                st = Steps(pool, pool_step)
                for m, value in ((core.ident, 0.0), (core.ident_b, 0.0), (core.hide, 0.0), (core.hideT, 0.0), (core.ones_b, 1.0)):
                    st.add(nc.gpsimd.memset(m[:, :], value))
                st.wait()
                for m in (core.ident, core.ident_b):
                    st.add(nc.gpsimd.affine_select(out=m[:, :], in_=m[:, :], compare_op=ALU.not_equal, fill=1.0,
                                                   base=0, pattern=[[-1, P]], channel_multiplier=1))
                st.add(nc.gpsimd.affine_select(out=core.hide[:, :], in_=core.hide[:, :], compare_op=ALU.is_ge, fill=MASKED,
                                               base=0, pattern=[[-1, P]], channel_multiplier=1))
                st.add(nc.gpsimd.affine_select(out=core.hideT[:, :], in_=core.hideT[:, :], compare_op=ALU.is_ge, fill=MASKED,
                                               base=0, pattern=[[1, P]], channel_multiplier=-1))
                st.wait()


def stage_norm(nc, core, tag, xn=None):
    with Stage(nc, tag) as s:
        stats = s.sb("stats", [P, NT, 6])
        mean = s.sb("mean", [P, NT])
        var = s.sb("var", [P, NT])
        dif = s.sb("dif", [P, NT])
        rstd = s.sb("rstd", [P, NT])
        keep = xn if xn is not None else s.sb("xn", [P, NT, D])
        psT = s.ps("psT", [P, T])
        dve_step, var_ready, std_ready = s.sem("dve_step"), s.sem("var_ready"), s.sem("std_ready")
        norm_ready, transposed, xT_ready = s.sem("norm_ready"), s.sem("transposed"), s.sem("xT_ready")
        with nc.Block() as block:
            @block.vector
            def _(dve):
                st = Steps(dve, dve_step)
                for t in range(NT):
                    st.add(nc.vector.bn_stats(stats[:, t, :], core.x[:, t, :]))
                st.wait()
                st.add(nc.vector.tensor_tensor(mean[:, :], stats[:, :, 1], stats[:, :, 4], ALU.add))
                st.add(nc.vector.tensor_tensor(dif[:, :], stats[:, :, 1], stats[:, :, 4], ALU.subtract))
                st.run(nc.vector.tensor_tensor(var[:, :], stats[:, :, 2], stats[:, :, 5], ALU.add))
                st.add(nc.vector.tensor_scalar(mean[:, :], mean[:, :], 0.5, None, ALU.mult))
                st.add(nc.vector.tensor_scalar(var[:, :], var[:, :], 1.0 / D, 1e-5, ALU.mult, ALU.add))
                st.run(nc.vector.scalar_tensor_tensor(out=dif[:, :], in0=dif[:, :], scalar=0.25, in1=dif[:, :],
                                                      op0=ALU.mult, op1=ALU.mult))
                nc.vector.tensor_tensor(var[:, :], var[:, :], dif[:, :], ALU.add).then_inc(var_ready, 1)
                dve.wait_ge(std_ready, 1)
                st.run(nc.vector.reciprocal(rstd[:, :], var[:, :]))
                for t in range(NT):
                    nc.vector.tensor_scalar(keep[:, t, :], core.x[:, t, :], mean[:, t:t + 1], rstd[:, t:t + 1],
                                            ALU.subtract, ALU.mult).then_inc(norm_ready, 1)

            @block.tensor
            def _(pe):
                for t in range(NT):
                    pe.wait_ge(norm_ready, t + 1)
                    nc.tensor.transpose(psT[:, t * P:(t + 1) * P], keep[:, t, :], core.ident[:, :]).then_inc(transposed, 1)

            @block.scalar
            def _(act):
                act.wait_ge(var_ready, 1)
                nc.scalar.activation(var[:, :], var[:, :], ACT.Sqrt).then_inc(std_ready, 1)
                for c in range(NCH):
                    act.wait_ge(transposed, TPC * (c + 1))
                    nc.scalar.activation(core.xT[:, c * CH:(c + 1) * CH], psT[:, c * CH:(c + 1) * CH], ACT.Copy).then_inc(xT_ready, 1)
                act.wait_ge(xT_ready, NCH)


def stage_store(nc, core, out):
    with Stage(nc, "store") as s:
        stored = s.sem("stored")
        with nc.Block() as block:
            @block.sync
            def _(sp):
                sp.dma_start(out.rearrange("b (t p) d -> p (b t) d", p=P), core.x[:, :, :]).then_inc(stored, 16)
                sp.wait_ge(stored, 16)


def stage_mamba(nc, core, tag, xn, w):
    NS, NHALF, NCONV, DI = 16, 2, 4, 256
    NB = 2 * NS
    with Stage(nc, tag) as s:
        sz, xc, delta, dx = (s.sb(n, [P, NHALF, T]) for n in ("silu_z", "x_conv", "delta", "delta_x"))
        bc = s.sb("bc_parts", [P, T], BF16)
        sel = s.sb("select", [P, NB, P], BF16)
        A = s.sb("A", [P, NHALF, NS])
        d_skip = s.sb("d_skip", [P, NHALF])
        w_out = s.sb("w_out", [P, NHALF, D])
        h_last = s.sb("h_last", [P, NHALF, NS])
        loaded = s.sem("loaded")
        with Stage(nc, tag + "_in") as q:
            w_in, w_dt = q.sb("w_in", [P, 2 * DI]), q.sb("w_dt", [P, NHALF, DI])
            w_xp = q.sb("w_xp", [P, NHALF, 3, NB])
            b_in, conv_w, conv_b = q.sb("b_in", [P, 4]), q.sb("conv_w", [P, NHALF, NCONV]), q.sb("conv_b", [P, NHALF])
            b_dt, b_xp = q.sb("b_dt", [P, NHALF]), q.sb("b_xp", [3 * NB, 1])
            xin = q.sb("x_in", [P, NHALF, T + NCONV - 1])
            conv = q.sb("conv", [P, NHALF, T])
            bcf, bcr = q.sb("bc", [3 * NB, T]), q.sb("bc_rest", [3 * NB, T])
            pick = q.sb("pick", [P, NB])
            ps = q.ps("ps", [P, 4, CH])
            dve_step, zeroed = q.sem("dve_step"), q.sem("zeroed")
            proj, ev_act, conv_done, xc_ready = q.sem("projected"), q.sem("in_evacuated"), q.sem("conv_done"), q.sem("xc_ready")
            bc_done, bc_out, dt_done = q.sem("bc_done"), q.sem("bc_out"), q.sem("dt_done")
            dt_rd, abs_done, exp_done, ln_done = q.sem("dt_read"), q.sem("abs_done"), q.sem("exp_done"), q.sem("ln_done")
            a_done = q.sem("a_done")
            NLOAD = 15
            with nc.Block() as block:
                @block.sync
                def _(sp):
                    loads = [(w_in[:, :], w["W_in"]), (b_in[:, :], w["b_in"]), (conv_w[:, :, :], w["conv_w"]), (conv_b[:, :], w["conv_b"]),
                             (w_dt[:, :, :], w["W_dt"].rearrange("(k p) n -> p k n", p=P)), (b_dt[:, :], w["b_dt"]),
                             (A[:, :, :], w["A_log"].rearrange("(k p) n -> p k n", p=P)), (d_skip[:, :], w["D_skip"]),
                             (w_out[:, :, :], w["W_out"].rearrange("(k p) n -> p k n", p=P))]
                    for part in range(3):
                        loads.append((w_xp[:, :, part, :], w["W_xp"].rearrange("(k p) n -> p k n", p=P)))
                        loads.append((b_xp[part * NB:(part + 1) * NB, :], w["b_xp"]))
                    assert len(loads) == NLOAD
                    for dst, src in loads:
                        sp.dma_start(dst, src).then_inc(loaded, 16)
                    sp.wait_ge(loaded, 16 * NLOAD)

                @block.gpsimd
                def _(pool):
                    nc.gpsimd.memset(xin[:, :, 0:NCONV - 1], 0.0).then_inc(zeroed, 1)
                    nc.gpsimd.memset(bc[:, :], 0.0).then_inc(zeroed, 1)
                    nc.gpsimd.memset(h_last[:, :, :], 0.0).then_inc(zeroed, 1)

                @block.tensor
                def _(pe):
                    pe.wait_ge(loaded, 16 * NLOAD)
                    for n in range(4 * NCH):
                        if n >= 4:
                            pe.wait_ge(ev_act, n - 3)
                        j, c = n // NCH, n % NCH
                        nc.tensor.matmul(ps[:, n % 4, :], w_in[:, j * P:(j + 1) * P], core.xT[:, c * CH:(c + 1) * CH],
                                         start=True, stop=True).then_inc(proj, 1)
                    pe.wait_ge(xc_ready, NHALF)
                    for c in range(NCH):
                        for k in range(NHALF):
                            last = nc.tensor.matmul(ps[0:3 * NB, c, :], w_xp[:, k, :, :].rearrange("p a b -> p (a b)"),
                                                    xc[:, k, c * CH:(c + 1) * CH], start=k == 0, stop=k == NHALF - 1)
                        last.then_inc(bc_done, 1)
                    for n in range(NHALF * NCH):
                        m, c = n // NCH, n % NCH
                        if n < 4:
                            pe.wait_ge(bc_out, n + 1)
                        else:
                            pe.wait_ge(dt_rd, n - 3)
                        for k in range(NHALF):
                            last = nc.tensor.matmul(ps[:, n % 4, :], w_dt[:, k, m * P:(m + 1) * P], xc[:, k, c * CH:(c + 1) * CH],
                                                    start=k == 0, stop=k == NHALF - 1)
                        last.then_inc(dt_done, 1)

                @block.scalar
                def _(act):
                    act.wait_ge(loaded, 16 * NLOAD)
                    for n in range(4 * NCH):
                        j, c = n // NCH, n % NCH
                        act.wait_ge(proj, n + 1)
                        if j < NHALF:
                            nc.scalar.activation(xin[:, j, NCONV - 1 + c * CH:NCONV - 1 + (c + 1) * CH], ps[:, n % 4, :], ACT.Identity,
                                                 bias=b_in[:, j:j + 1]).then_inc(ev_act, 1)
                        else:
                            nc.scalar.activation(sz[:, j - NHALF, c * CH:(c + 1) * CH], ps[:, n % 4, :], ACT.Silu,
                                                 bias=b_in[:, j:j + 1]).then_inc(ev_act, 1)
                    for k in range(NHALF):
                        act.wait_ge(conv_done, k + 1)
                        nc.scalar.activation(xc[:, k, :], conv[:, k, :], ACT.Silu).then_inc(xc_ready, 1)
                    for m in range(NHALF):
                        act.wait_ge(dt_rd, (m + 1) * NCH)
                        nc.scalar.activation(delta[:, m, :], conv[:, m, :], ACT.Abs).then_inc(abs_done, 1)
                    act.wait_ge(abs_done, NHALF)
                    nc.scalar.activation(A[:, :, :], A[:, :, :], ACT.Exp).then_inc(a_done, 1)
                    for m in range(NHALF):
                        nc.scalar.activation(delta[:, m, :], delta[:, m, :], ACT.Exp, scale=-1.0).then_inc(exp_done, 1)
                    act.wait_ge(exp_done, NHALF)
                    for m in range(NHALF):
                        nc.scalar.activation(xin[:, m, 0:T], delta[:, m, :], ACT.Ln, bias=1.0).then_inc(ln_done, 1)

                @block.vector
                def _(dve):
                    st = Steps(dve, dve_step)
                    dve.wait_ge(loaded, 16 * NLOAD)
                    dve.wait_ge(zeroed, 3)
                    st.run(nc.vector.tensor_tensor(pick[:, :], core.ident[:, 0:NB], core.ident[:, NB:2 * NB], ALU.add))
                    st.run(nc.vector.tensor_tensor(pick[:, :], pick[:, :], core.ident[:, 2 * NB:3 * NB], ALU.add))
                    st.add(nc.vector.tensor_copy(sel[:, :, :], pick[:, :].unsqueeze(2).to_broadcast([P, NB, P])))
                    for k in range(NHALF):
                        dve.wait_ge(ev_act, (k + 1) * NCH)
                        st.run(nc.vector.tensor_scalar(conv[:, k, :], xin[:, k, 0:T], conv_w[:, k, 0:1], conv_b[:, k:k + 1], ALU.mult, ALU.add))
                        for tap in range(1, NCONV):
                            last = nc.vector.scalar_tensor_tensor(out=conv[:, k, :], in0=xin[:, k, tap:tap + T], scalar=conv_w[:, k, tap:tap + 1],
                                                                  in1=conv[:, k, :], op0=ALU.mult, op1=ALU.add)
                            if tap < NCONV - 1:
                                st.run(last)
                        last.then_inc(conv_done, 1)
                    for c in range(NCH):
                        dve.wait_ge(bc_done, c + 1)
                        nc.vector.tensor_scalar(bcf[:, c * CH:(c + 1) * CH], ps[0:3 * NB, c, :], b_xp[:, 0:1], None, ALU.add).then_inc(bc_out, 1)
                    dve.wait_ge(bc_out, NCH)
                    st.run(nc.vector.tensor_copy(bc[0:3 * NB, :], bcf[:, :]))
                    st.run(nc.vector.tensor_tensor(bcr[:, :], bcf[:, :], bc[0:3 * NB, :], ALU.subtract))
                    for lo in (NB, 2 * NB):
                        st.run(nc.vector.tensor_copy(bc[lo:lo + NB, :], bcr[lo:lo + NB, :]))
                    st.run(nc.vector.tensor_tensor(bcr[2 * NB:3 * NB, :], bcr[2 * NB:3 * NB, :], bc[2 * NB:3 * NB, :], ALU.subtract))
                    st.add(nc.vector.tensor_copy(bc[2 * NB:3 * NB, :], bcr[2 * NB:3 * NB, :]))
                    dve.wait_ge(xc_ready, NHALF)
                    for n in range(NHALF * NCH):
                        m, c = n // NCH, n % NCH
                        dve.wait_ge(dt_done, n + 1)
                        nc.vector.tensor_scalar(conv[:, m, c * CH:(c + 1) * CH], ps[:, n % 4, :], b_dt[:, m:m + 1], None, ALU.add).then_inc(dt_rd, 1)
                    dve.wait_ge(dt_rd, NHALF * NCH)
                    dve.wait_ge(a_done, 1)
                    st.add(nc.vector.tensor_scalar(A[:, :, :], A[:, :, :], -1.0, None, ALU.mult))
                    for m in range(NHALF):
                        dve.wait_ge(exp_done, NHALF)
                        st.run(nc.vector.tensor_scalar(dx[:, m, :], delta[:, m, :], 1.0, -1.0, ALU.add, ALU.add))
                        st.run(nc.vector.tensor_tensor(dx[:, m, :], delta[:, m, :], dx[:, m, :], ALU.subtract))
                        st.run(nc.vector.scalar_tensor_tensor(out=conv[:, m, :], in0=conv[:, m, :], scalar=0.0, in1=dx[:, m, :],
                                                              op0=ALU.max, op1=ALU.add))
                        dve.wait_ge(ln_done, m + 1)
                        st.run(nc.vector.tensor_tensor(delta[:, m, :], xin[:, m, 0:T], conv[:, m, :], ALU.add))
                        st.run(nc.vector.tensor_tensor(dx[:, m, :], delta[:, m, :], xc[:, m, :], ALU.mult))

        NI = NS * NHALF
        NBUF = 3
        dA, dbx, hc = (s.sb(n, [P, NBUF, CH]) for n in ("dA", "dB_x", "h_C"))
        hs = s.sb("h", [P, 2, CH])
        b_all = s.sb("b_spread", [P, 2, CH])
        yz = s.sb("y_gated", [P, NHALF, T])
        with Stage(nc, tag + "_scan") as q:
            ps_b, ps_c, ps_y = q.ps("ps_b", [P, 2, CH]), q.ps("ps_c", [P, 2, CH]), q.ps("ps_y", [P, NHALF, CH])
            spread, b_out, dA_done, dbx_done = q.sem("spread"), q.sem("b_evacuated"), q.sem("dA_done"), q.sem("dbx_done")
            scanned, kept, hc_done, summed = q.sem("scanned"), q.sem("h_kept"), q.sem("hC_done"), q.sem("summed")
            skip_done, gated = q.sem("skip_added"), q.sem("gated")
            with nc.Fori(0, NCH) as c:
                q.restart()
                cols = bass.ds(c * CH, CH)
                with nc.Block() as block:
                    @block.tensor
                    def _(pe):
                        def spread_bc(n):
                            if n >= 2:
                                pe.wait_ge(b_out, n - 1)
                                pe.wait_ge(hc_done, NHALF * (n - 1))
                            nc.tensor.matmul(ps_b[:, n % 2, :], sel[:, n, :], bc[:, cols], start=True, stop=True)
                            nc.tensor.matmul(ps_c[:, n % 2, :], sel[:, NS + n, :], bc[:, cols], start=True, stop=True).then_inc(spread, 1)

                        spread_bc(0)
                        spread_bc(1)
                        for n in range(NI):
                            st_, k = n // NHALF, n % NHALF
                            pe.wait_ge(hc_done, n + 1)
                            nc.tensor.matmul(ps_y[:, k, :], core.ident[:, :], hc[:, n % NBUF, :], start=st_ == 0, stop=st_ == NS - 1).then_inc(summed, 1)
                            if k == NHALF - 1 and st_ + 2 < NS:
                                spread_bc(st_ + 2)

                    @block.scalar
                    def _(act):
                        for n in range(NI):
                            st_, k = n // NHALF, n % NHALF
                            if k == 0:
                                act.wait_ge(spread, st_ + 1)
                                if st_ >= 2:
                                    act.wait_ge(dbx_done, NHALF * (st_ - 1))
                                nc.scalar.activation(b_all[:, st_ % 2, :], ps_b[:, st_ % 2, :], ACT.Copy).then_inc(b_out, 1)
                            if n >= NBUF:
                                act.wait_ge(scanned, n - NBUF + 1)
                            nc.scalar.activation(dA[:, n % NBUF, :], delta[:, k, cols], ACT.Exp, scale=A[:, k, st_:st_ + 1]).then_inc(dA_done, 1)

                    @block.gpsimd
                    def _(pool):
                        for n in range(NI):
                            st_, k = n // NHALF, n % NHALF
                            pool.wait_ge(b_out, st_ + 1)
                            if n >= NBUF:
                                pool.wait_ge(scanned, n - NBUF + 1)
                            if n >= 1:
                                pool.wait_ge(dbx_done, n)
                            nc.gpsimd.tensor_tensor(dbx[:, n % NBUF, :], dx[:, k, cols], b_all[:, st_ % 2, :], ALU.mult).then_inc(dbx_done, 1)

                    @block.vector
                    def _(dve):
                        def scan(n):
                            st_, k = n // NHALF, n % NHALF
                            dve.wait_ge(dA_done, n + 1)
                            dve.wait_ge(dbx_done, n + 1)
                            if n >= 2:
                                dve.wait_ge(hc_done, n - 1)
                                dve.wait_ge(kept, n - 1)
                            nc.vector.tensor_tensor_scan(hs[:, n % 2, :], dA[:, n % NBUF, :], dbx[:, n % NBUF, :],
                                                         h_last[:, k, st_:st_ + 1], ALU.mult, ALU.add).then_inc(scanned, 1)

                        scan(0)
                        for n in range(NI):
                            st_, k = n // NHALF, n % NHALF
                            if n + 1 < NI:
                                scan(n + 1)
                            dve.wait_ge(scanned, n + 1)
                            if n >= NBUF:
                                dve.wait_ge(summed, n - NBUF + 1)
                            nc.vector.tensor_tensor(hc[:, n % NBUF, :], hs[:, n % 2, :], ps_c[:, st_ % 2, :], ALU.mult).then_inc(hc_done, 1)
                            nc.vector.tensor_copy(h_last[:, k, st_:st_ + 1], hs[:, n % 2, CH - 1:CH]).then_inc(kept, 1)
                        dve.wait_ge(summed, NI)
                        for k in range(NHALF):
                            nc.vector.scalar_tensor_tensor(out=yz[:, k, cols], in0=xc[:, k, cols], scalar=d_skip[:, k:k + 1],
                                                           in1=ps_y[:, k, :], op0=ALU.mult, op1=ALU.add).then_inc(skip_done, 1)
                        for k in range(NHALF):
                            dve.wait_ge(skip_done, k + 1)
                            nc.vector.tensor_tensor(yz[:, k, cols], yz[:, k, cols], sz[:, k, cols], ALU.mult).then_inc(gated, 1)

        with Stage(nc, tag + "_out") as q:
            b_out, alpha, beta = q.sb("b_out", [P, D]), q.sb("alpha", [P, D]), q.sb("beta", [P, D])
            r = q.sb("sum", [P, NT, D])
            stats = q.sb("stats", [P, NT, 6])
            mean, var, dif = (q.sb(n, [P, NT]) for n in ("mean", "var", "dif"))
            ps = q.ps("ps", [P, 2, TPC, D])
            vec_loaded, done, dve_step = q.sem("vectors_loaded"), q.sem("out_done"), q.sem("dve_step")
            summed, var_ready, std_ready = q.sem("summed"), q.sem("var_ready"), q.sem("std_ready")
            with nc.Block() as block:
                @block.sync
                def _(sp):
                    for dst, src in ((b_out, w["b_out"]), (alpha, w["alpha"]), (beta, w["beta"])):
                        sp.dma_start(dst[:, :], src.partition_broadcast(P)).then_inc(vec_loaded, 16)
                    sp.wait_ge(vec_loaded, 48)

                @block.tensor
                def _(pe):
                    for c in range(NCH):
                        if c >= 2:
                            pe.wait_ge(summed, c - 1)
                        for j in range(TPC):
                            t = c * TPC + j
                            for k in range(NHALF):
                                last = nc.tensor.matmul(ps[:, c % 2, j, :], yz[:, k, t * P:(t + 1) * P], w_out[:, k, :],
                                                        start=k == 0, stop=k == NHALF - 1)
                        last.then_inc(done, 1)

                @block.scalar
                def _(act):
                    act.wait_ge(var_ready, 1)
                    nc.scalar.activation(var[:, :], var[:, :], ACT.Sqrt).then_inc(std_ready, 1)

                @block.vector
                def _(dve):
                    st = Steps(dve, dve_step)
                    wide = [P, TPC, D]
                    dve.wait_ge(vec_loaded, 48)
                    for c in range(NCH):
                        tiles = slice(c * TPC, (c + 1) * TPC)
                        st.run(nc.vector.tensor_tensor(r[:, tiles, :], xn[:, tiles, :], b_out[:, :].unsqueeze(1).to_broadcast(wide), ALU.add))
                        dve.wait_ge(done, c + 1)
                        nc.vector.tensor_tensor(r[:, tiles, :], r[:, tiles, :], ps[:, c % 2, :, :], ALU.add).then_inc(summed, 1)
                    dve.wait_ge(summed, NCH)
                    for t in range(NT):
                        st.add(nc.vector.bn_stats(stats[:, t, :], r[:, t, :]))
                    st.wait()
                    st.add(nc.vector.tensor_tensor(mean[:, :], stats[:, :, 1], stats[:, :, 4], ALU.add))
                    st.add(nc.vector.tensor_tensor(dif[:, :], stats[:, :, 1], stats[:, :, 4], ALU.subtract))
                    st.run(nc.vector.tensor_tensor(var[:, :], stats[:, :, 2], stats[:, :, 5], ALU.add))
                    st.add(nc.vector.tensor_scalar(mean[:, :], mean[:, :], 0.5, None, ALU.mult))
                    st.run(nc.vector.scalar_tensor_tensor(out=dif[:, :], in0=dif[:, :], scalar=0.25 * D, in1=dif[:, :],
                                                          op0=ALU.mult, op1=ALU.mult))
                    st.run(nc.vector.tensor_tensor(var[:, :], var[:, :], dif[:, :], ALU.add))
                    nc.vector.tensor_scalar(var[:, :], var[:, :], 1.0 / (D - 1), None, ALU.mult).then_inc(var_ready, 1)
                    dve.wait_ge(std_ready, 1)
                    st.run(nc.vector.tensor_scalar(var[:, :], var[:, :], 1e-6, None, ALU.add))
                    st.run(nc.vector.reciprocal(dif[:, :], var[:, :]))
                    for t in range(NT):
                        st.add(nc.vector.tensor_scalar(r[:, t, :], r[:, t, :], mean[:, t:t + 1], dif[:, t:t + 1], ALU.subtract, ALU.mult))
                    st.wait()
                    full = [P, NT, D]
                    st.run(nc.vector.tensor_tensor(r[:, :, :], r[:, :, :], alpha[:, :].unsqueeze(1).to_broadcast(full), ALU.mult))
                    st.run(nc.vector.tensor_tensor(r[:, :, :], r[:, :, :], beta[:, :].unsqueeze(1).to_broadcast(full), ALU.add))
                    st.run(nc.vector.tensor_tensor(core.x[:, :, :], core.x[:, :, :], r[:, :, :], ALU.add))


def stage_route(nc, core, tag, E, Wr, br, comb, capacity=None):
    with Stage(nc, tag) as s:
        wr = s.sb("wr", [P, E])
        brb = s.sb("br", [P, E])
        lg = s.sb("logits", [P, NT, E])
        top, idx = s.sb("top", [P, NT, 8]), s.sb("idx", [P, NT, 8], U32)
        idxf, iota = s.sb("idxf", [P, NT, 2]), s.sb("iota", [P, E])
        mx, tot, w = s.sb("row_max", [P, NT]), s.sb("row_sum", [P, NT]), s.sb("weights", [P, 2, NT])
        hot = s.sb("one_hot", [P, 2, NT, E])
        hot_b = s.sb("one_hot_b", [P, 2, NT, E], BF16)
        tri = s.sb("tri_b", [P, P], BF16)
        before = s.sb("count_before", [P, 2, NT, E])
        total = s.sb("count_in_tile", [P, 2, NT, E])
        rank = s.sb("rank", [P, 2, NT])
        ps = s.ps("ps", [P, NT, E])
        ps_cum, ps_tot = s.ps("ps_cum", [P, 2, NT, E]), s.ps("ps_tot", [P, 2, NT, E])
        loaded, consts, scored, exps = s.sem("loaded"), s.sem("consts"), s.sem("scored"), s.sem("exp_done")
        shifted, dve_step, hot_ready, counted = s.sem("shifted"), s.sem("dve_step"), s.sem("hot_ready"), s.sem("counted")
        nload = 16 if br is None else 32
        with nc.Block() as block:
            @block.sync
            def _(sp):
                sp.dma_start(wr[:, :], Wr).then_inc(loaded, 16)
                if br is not None:
                    sp.dma_start(brb[:, :], br.partition_broadcast(P)).then_inc(loaded, 16)
                sp.wait_ge(loaded, nload)

            @block.gpsimd
            def _(pool):
                nc.gpsimd.iota(iota[:, :], pattern=[[1, E]], base=0, channel_multiplier=0,
                               allow_small_or_imprecise_dtypes=True).then_inc(consts, 1)
                nc.gpsimd.memset(tri[:, :], 1.0).then_inc(consts, 1)
                pool.wait_ge(consts, 2)
                nc.gpsimd.affine_select(out=tri[:, :], in_=tri[:, :], compare_op=ALU.is_ge, fill=0.0,
                                        base=0, pattern=[[1, P]], channel_multiplier=-1).then_inc(consts, 1)
                pool.wait_ge(consts, 3)

            @block.tensor
            def _(pe):
                pe.wait_ge(loaded, nload)
                for t in range(NT):
                    last = nc.tensor.matmul(ps[:, t, :], core.xT[:, t * P:(t + 1) * P], wr[:, :], start=True, stop=True)
                last.then_inc(scored, 1)
                if capacity is not None:
                    pe.wait_ge(consts, 3)
                    pe.wait_ge(hot_ready, 1)
                    flat = hot_b[:, :, :, :].rearrange("p k t e -> p (k t e)")
                    nc.tensor.matmul(ps_cum[:, :, :, :].rearrange("p k t e -> p (k t e)"), tri[:, :], flat, start=True, stop=True)
                    nc.tensor.matmul(ps_tot[:, :, :, :].rearrange("p k t e -> p (k t e)"), core.ones_b[:, :], flat,
                                     start=True, stop=True).then_inc(counted, 1)

            @block.scalar
            def _(act):
                act.wait_ge(shifted, 1)
                nc.scalar.activation(lg[:, :, :], lg[:, :, :], ACT.Exp).then_inc(exps, 1)

            @block.vector
            def _(dve):
                st = Steps(dve, dve_step)
                wide = [P, NT, E]
                dve.wait_ge(loaded, nload)
                dve.wait_ge(consts, 3)
                dve.wait_ge(scored, 1)
                if br is None:
                    st.run(nc.vector.tensor_copy(lg[:, :, :], ps[:, :, :]))
                else:
                    st.run(nc.vector.tensor_tensor(lg[:, :, :], ps[:, :, :], brb[:, :].unsqueeze(1).to_broadcast(wide), ALU.add))
                st.run(nc.vector.tensor_reduce(mx[:, :], lg[:, :, :], axis=AX.X, op=ALU.max))
                nc.vector.tensor_tensor(lg[:, :, :], lg[:, :, :], mx[:, :].unsqueeze(2).to_broadcast(wide), ALU.subtract).then_inc(shifted, 1)
                dve.wait_ge(exps, 1)
                st.run(nc.vector.tensor_reduce(tot[:, :], lg[:, :, :], axis=AX.X, op=ALU.add))
                st.run(nc.vector.reciprocal(mx[:, :], tot[:, :]))
                st.run(nc.vector.tensor_tensor(lg[:, :, :], lg[:, :, :], mx[:, :].unsqueeze(2).to_broadcast(wide), ALU.mult))
                for t in range(NT):
                    st.add(nc.vector.max(top[:, t, :], lg[:, t, :]))
                st.wait()
                for t in range(NT):
                    st.add(nc.vector.max_index(idx[:, t, :], top[:, t, :], lg[:, t, :]))
                st.wait()
                st.add(nc.vector.tensor_copy(idxf[:, :, :], idx[:, :, 0:2]))
                st.run(nc.vector.tensor_tensor(tot[:, :], top[:, :, 0], top[:, :, 1], ALU.add))
                for k in range(2):
                    st.add(nc.vector.tensor_tensor(hot[:, k, :, :], iota[:, :].unsqueeze(1).to_broadcast(wide),
                                                   idxf[:, :, k:k + 1].to_broadcast(wide), ALU.is_equal))
                if capacity is None:
                    st.run(nc.vector.tensor_scalar(tot[:, :], tot[:, :], 1e-9, None, ALU.max))
                else:
                    st.run(nc.vector.tensor_scalar(tot[:, :], tot[:, :], 1e-9, None, ALU.add))
                st.run(nc.vector.reciprocal(mx[:, :], tot[:, :]))
                for k in range(2):
                    st.add(nc.vector.tensor_tensor(w[:, k, :], top[:, :, k], mx[:, :], ALU.mult))
                st.wait()
                if capacity is not None:
                    nc.vector.tensor_copy(hot_b[:, :, :, :], hot[:, :, :, :]).then_inc(hot_ready, 1)
                    dve.wait_ge(counted, 1)
                    st.add(nc.vector.tensor_copy(total[:, :, :, :], ps_tot[:, :, :, :]))
                    st.add(nc.vector.memset(before[:, :, 0, :], 0.0))
                    st.wait()
                    for t in range(1, NT):
                        st.run(nc.vector.tensor_tensor(before[:, :, t, :], before[:, :, t - 1, :], total[:, :, t - 1, :], ALU.add))
                    st.run(nc.vector.tensor_tensor(before[:, :, :, :], before[:, :, :, :], ps_cum[:, :, :, :], ALU.add))
                    st.run(nc.vector.tensor_tensor(before[:, :, :, :], before[:, :, :, :], hot[:, :, :, :], ALU.mult))
                    st.run(nc.vector.tensor_reduce(rank[:, :, :], before[:, :, :, :], axis=AX.X, op=ALU.add))
                    st.run(nc.vector.tensor_scalar(rank[:, :, :], rank[:, :, :], capacity + 0.5, None, ALU.is_lt))
                    st.run(nc.vector.tensor_tensor(w[:, :, :], w[:, :, :], rank[:, :, :], ALU.mult))
                for k in range(2):
                    st.add(nc.vector.tensor_tensor(hot[:, k, :, :], hot[:, k, :, :], w[:, k, :].unsqueeze(2).to_broadcast(wide), ALU.mult))
                st.wait()
                st.run(nc.vector.tensor_tensor(comb[:, :, :], hot[:, 0, :, :], hot[:, 1, :, :], ALU.add))


def stage_gelu_experts(nc, core, tag, comb, W1, b1, g1T, be1T, W2, b2):
    E, HID, Q = 16, 128, 4
    NQ = E // Q
    with Stage(nc, tag) as s:
        w1, w2 = s.sb("w1", [P, E * HID]), s.sb("w2", [P, E, D])
        b2s = s.sb("b2", [E, D])
        g, be = s.sb("g1", [P, E]), s.sb("be1", [P, E])
        b_rows, b_rest = s.sb("b1_rows", [3, E * HID]), s.sb("b1_rest", [3, E * HID])
        b_part = s.sb("b1_part", [3, E * HID], BF16)
        b_sum = s.sb("b1_sum", [P, E * HID], BF16)
        combT = s.sb("comb_T", [E, T])
        g_q, be_q, comb_q = s.sb("g1_quad", [P, Q]), s.sb("be1_quad", [P, Q]), s.sb("comb_quad", [P, NT, Q])
        h = s.sb("hidden", [P, NT, Q, HID])
        stats = s.sb("stats", [P, NT * Q, 6])
        mean, var, dif, rstd = (s.sb(n, [P, NT * Q]) for n in ("mean", "var", "dif", "rstd"))
        hn = s.sb("hidden_norm", [P, 2, TPC, HID])
        gT = s.sb("gelu_T", [P, 2, CH])
        ps_h, ps_t = s.ps("ps_hidden", [P, 2, CH]), s.ps("ps_turned", [P, 2, CH])
        ps_y = s.ps("ps_y", [P, 2, TPC, D])
        loaded, dve_step, zeroed = s.sem("loaded"), s.sem("dve_step"), s.sem("b1_zeroed")
        b_ready, turned, combT_ready = s.sem("b1_ready"), s.sem("comb_turned"), s.sem("comb_T_ready")
        y_done, added = s.sem("y_done"), s.sem("x_added")
        hid_done, hid_out, quad_ready = s.sem("hidden_done"), s.sem("hidden_evacuated"), s.sem("quad_ready")
        var_ready, std_ready, normed = s.sem("var_ready"), s.sem("std_ready"), s.sem("normalised")
        gelu_done = s.sem("gelu_done")
        with nc.Block() as block:
            @block.sync
            def _(sp):
                sp.dma_start(b_rows[:, :], b1.rearrange("e h -> (e h)").partition_broadcast(3)).then_inc(loaded, 16)
                sp.dma_start(b2s[:, :], b2).then_inc(loaded, 16)
                sp.dma_start(g[:, :], g1T).then_inc(loaded, 16)
                sp.dma_start(be[:, :], be1T).then_inc(loaded, 16)
                sp.dma_start(w1[:, :].rearrange("c (e h) -> c e h", e=E), W1.rearrange("e c h -> c e h")).then_inc(loaded, 16)
                sp.dma_start(w2[:, :, :], W2.rearrange("e h o -> h e o")).then_inc(loaded, 16)
                sp.wait_ge(loaded, 96)

            @block.gpsimd
            def _(pool):
                nc.gpsimd.memset(b_sum[:, :], 0.0).then_inc(zeroed, 1)

            @block.tensor
            def _(pe):
                for t in range(NT):
                    if t % TPC == 0 and t >= 2 * TPC:
                        pe.wait_ge(combT_ready, t // TPC - 1)
                    last = nc.tensor.transpose(ps_t[0:E, (t // TPC) % 2, (t % TPC) * P:(t % TPC + 1) * P], comb[:, t, :], core.ident[:, :])
                    if t % TPC == TPC - 1:
                        last.then_inc(turned, 1)
                pe.wait_ge(loaded, 96)
                for c in range(NCH):
                    pe.wait_ge(combT_ready, c + 1)
                    if c >= 2:
                        pe.wait_ge(added, c - 1)
                    for j in range(TPC):
                        t = c * TPC + j
                        last = nc.tensor.matmul(ps_y[:, c % 2, j, :], combT[:, t * P:(t + 1) * P], b2s[:, :], start=True, stop=True)
                    last.then_inc(y_done, 1)

            @block.scalar
            def _(act):
                for c in range(NCH):
                    act.wait_ge(turned, c + 1)
                    nc.scalar.activation(combT[:, c * CH:(c + 1) * CH], ps_t[0:E, c % 2, :], ACT.Copy).then_inc(combT_ready, 1)

            @block.vector
            def _(dve):
                st = Steps(dve, dve_step)
                dve.wait_ge(loaded, 96)
                dve.wait_ge(zeroed, 1)
                for k in range(3):
                    st.run(nc.vector.tensor_copy(b_part[:, :], b_rows[:, :]))
                    if k < 2:
                        st.run(nc.vector.tensor_tensor(b_rows[:, :], b_rows[:, :], b_part[:, :], ALU.subtract))
                    if k == 0:
                        st.run(nc.vector.tensor_scalar(b_sum[0:3, :], b_part[:, :], core.ident[0:3, 0:1], None, ALU.mult))
                    else:
                        st.run(nc.vector.tensor_scalar(b_rest[:, :], b_part[:, :], core.ident[0:3, k:k + 1], None, ALU.mult))
                        st.run(nc.vector.tensor_tensor(b_sum[0:3, :], b_sum[0:3, :], b_rest[:, :], ALU.add))
                for c in range(NCH):
                    dve.wait_ge(y_done, c + 1)
                    tiles = slice(c * TPC, (c + 1) * TPC)
                    nc.vector.tensor_tensor(core.x[:, tiles, :], core.x[:, tiles, :], ps_y[:, c % 2, :, :], ALU.add).then_inc(added, 1)
                dve.wait_ge(added, NCH)

        with nc.Fori(0, NQ) as i:
            s.restart()
            with nc.Block() as block:
                @block.gpsimd
                def _(pool):
                    nc.gpsimd.tensor_copy(g_q[:, :], g[:, bass.ds(i * Q, Q)]).then_inc(quad_ready, 1)
                    nc.gpsimd.tensor_copy(be_q[:, :], be[:, bass.ds(i * Q, Q)]).then_inc(quad_ready, 1)
                    nc.gpsimd.tensor_copy(comb_q[:, :, :], comb[:, :, bass.ds(i * Q, Q)]).then_inc(quad_ready, 1)

                @block.tensor
                def _(pe):
                    for t in range(NT):
                        if t >= 2:
                            pe.wait_ge(hid_out, t - 1)
                        nc.tensor.matmul(ps_h[:, t % 2, :], core.xT[:, t * P:(t + 1) * P], w1[:, bass.ds(i * Q * HID, Q * HID)], start=True, stop=False)
                        nc.tensor.matmul(ps_h[:, t % 2, :], core.ones_b[:, :], b_sum[:, bass.ds(i * Q * HID, Q * HID)], start=False, stop=True).then_inc(hid_done, 1)

                    def turn(n):
                        pe.wait_ge(normed, n + 1)
                        if n >= 2:
                            pe.wait_ge(gelu_done, n - 1)
                        for j in range(TPC):
                            last = nc.tensor.transpose(ps_t[:, n % 2, j * P:(j + 1) * P], hn[:, n % 2, j, :], core.ident[:, :])
                        last.then_inc(turned, 1)

                    turn(0)
                    for n in range(NCH * Q):
                        if n + 1 < NCH * Q:
                            turn(n + 1)
                        pe.wait_ge(gelu_done, n + 1)
                        if n >= 2:
                            pe.wait_ge(added, n - 1)
                        for j in range(TPC):
                            last = nc.tensor.matmul(ps_y[:, n % 2, j, :], gT[:, n % 2, j * P:(j + 1) * P],
                                                    w2[:, bass.ds(i * Q + n % Q, 1), :], start=True, stop=True)
                        last.then_inc(y_done, 1)

                @block.scalar
                def _(act):
                    for t in range(NT):
                        act.wait_ge(hid_done, t + 1)
                        nc.scalar.activation(h[:, t, :, :], ps_h[:, t % 2, :].rearrange("p (e h) -> p e h", e=Q), ACT.Copy).then_inc(hid_out, 1)
                    act.wait_ge(var_ready, 1)
                    nc.scalar.activation(var[:, :], var[:, :], ACT.Sqrt).then_inc(std_ready, 1)
                    act.wait_ge(quad_ready, 3)
                    for n in range(NCH * Q):
                        act.wait_ge(turned, n + 1)
                        if n >= 2:
                            act.wait_ge(y_done, n - 1)
                        nc.scalar.activation(gT[:, n % 2, :], ps_t[:, n % 2, :], ACT.Gelu, scale=g_q[:, n % Q:n % Q + 1],
                                             bias=be_q[:, n % Q:n % Q + 1]).then_inc(gelu_done, 1)

                @block.vector
                def _(dve):
                    st = Steps(dve, dve_step)
                    for t in range(NT):
                        dve.wait_ge(hid_out, t + 1)
                        for e in range(Q):
                            st.add(nc.vector.bn_stats(stats[:, t * Q + e, :], h[:, t, e, :]))
                    st.wait()
                    st.add(nc.vector.tensor_tensor(mean[:, :], stats[:, :, 1], stats[:, :, 4], ALU.add))
                    st.add(nc.vector.tensor_tensor(dif[:, :], stats[:, :, 1], stats[:, :, 4], ALU.subtract))
                    st.run(nc.vector.tensor_tensor(var[:, :], stats[:, :, 2], stats[:, :, 5], ALU.add))
                    st.add(nc.vector.tensor_scalar(mean[:, :], mean[:, :], 0.5, None, ALU.mult))
                    st.add(nc.vector.tensor_scalar(var[:, :], var[:, :], 1.0 / HID, 1e-5, ALU.mult, ALU.add))
                    st.run(nc.vector.scalar_tensor_tensor(out=dif[:, :], in0=dif[:, :], scalar=0.25, in1=dif[:, :],
                                                          op0=ALU.mult, op1=ALU.mult))
                    nc.vector.tensor_tensor(var[:, :], var[:, :], dif[:, :], ALU.add).then_inc(var_ready, 1)
                    dve.wait_ge(std_ready, 1)
                    st.run(nc.vector.reciprocal(rstd[:, :], var[:, :]))
                    dve.wait_ge(quad_ready, 3)

                    def normalise(n):
                        c, e = n // Q, n % Q
                        if n >= 2:
                            dve.wait_ge(turned, n - 1)
                        for j in range(TPC):
                            t = c * TPC + j
                            k = t * Q + e
                            last = nc.vector.tensor_scalar(hn[:, n % 2, j, :], h[:, t, e, :], mean[:, k:k + 1], rstd[:, k:k + 1],
                                                           ALU.subtract, ALU.mult)
                        last.then_inc(normed, 1)

                    normalise(0)
                    normalise(1)
                    for n in range(NCH * Q):
                        if n + 2 < NCH * Q:
                            normalise(n + 2)
                        dve.wait_ge(y_done, n + 1)
                        if n >= 1:
                            dve.wait_ge(added, n)
                        for j in range(TPC):
                            t = (n // Q) * TPC + j
                            last = nc.vector.scalar_tensor_tensor(out=core.x[:, t, :], in0=ps_y[:, n % 2, j, :],
                                                                  scalar=comb_q[:, t, n % Q:n % Q + 1], in1=core.x[:, t, :],
                                                                  op0=ALU.mult, op1=ALU.add)
                        last.then_inc(added, 1)


def stage_silu_experts(nc, core, tag, comb, WgT, WuT, WdT):
    E, HID = 8, 256
    NH = HID // P
    with Stage(nc, tag) as s:
        wg, wu = s.sb("wg", [P, E, HID]), s.sb("wu", [P, E, HID])
        wd = s.sb("wd", [P, NH, E, D])
        wg_e, wu_e, comb_e = s.sb("wg_expert", [P, HID]), s.sb("wu_expert", [P, HID]), s.sb("comb_expert", [P, NT])
        gate = s.sb("gate", [P, 2, CH])
        gu = s.sb("gate_up", [P, 2, NH, CH])
        ps_g, ps_u, ps_y = s.ps("ps_gate", [P, 2, CH]), s.ps("ps_up", [P, 2, CH]), s.ps("ps_y", [P, 2, TPC, D])
        loaded, expert_ready = s.sem("loaded"), s.sem("expert_ready")
        up_done, gated, gu_ready = s.sem("gate_up_done"), s.sem("silu_done"), s.sem("gu_ready")
        y_done, added = s.sem("y_done"), s.sem("x_added")
        with nc.Block() as block:
            @block.sync
            def _(sp):
                sp.dma_start(wg[:, :, :], WgT).then_inc(loaded, 16)
                sp.dma_start(wu[:, :, :], WuT).then_inc(loaded, 16)
                sp.dma_start(wd[:, :, :, :], WdT.rearrange("(k p) e o -> p k e o", p=P)).then_inc(loaded, 16)
                sp.wait_ge(loaded, 48)
        with nc.Fori(0, E) as i:
            s.restart()
            with nc.Block() as block:
                @block.tensor
                def _(pe):
                    pe.wait_ge(expert_ready, 3)

                    def gate_up(n):
                        c, k = n // NH, n % NH
                        if n >= 2:
                            pe.wait_ge(gu_ready, n - 1)
                        cols = core.xT[:, c * CH:(c + 1) * CH]
                        nc.tensor.matmul(ps_g[:, n % 2, :], wg_e[:, k * P:(k + 1) * P], cols, start=True, stop=True)
                        nc.tensor.matmul(ps_u[:, n % 2, :], wu_e[:, k * P:(k + 1) * P], cols, start=True, stop=True).then_inc(up_done, 1)

                    gate_up(0)
                    gate_up(1)
                    for c in range(NCH):
                        if c + 1 < NCH:
                            gate_up(2 * c + 2)
                            gate_up(2 * c + 3)
                        pe.wait_ge(gu_ready, NH * (c + 1))
                        if c >= 2:
                            pe.wait_ge(added, c - 1)
                        for j in range(TPC):
                            for k in range(NH):
                                last = nc.tensor.matmul(ps_y[:, c % 2, j, :], gu[:, c % 2, k, j * P:(j + 1) * P],
                                                        wd[:, k, bass.ds(i, 1), :], start=k == 0, stop=k == NH - 1)
                        last.then_inc(y_done, 1)

                @block.scalar
                def _(act):
                    for n in range(NCH * NH):
                        act.wait_ge(up_done, n + 1)
                        if n >= 2:
                            act.wait_ge(gu_ready, n - 1)
                        nc.scalar.activation(gate[:, n % 2, :], ps_g[:, n % 2, :], ACT.Silu).then_inc(gated, 1)

                @block.vector
                def _(dve):
                    nc.vector.tensor_copy(wg_e[:, :], wg[:, bass.ds(i, 1), :]).then_inc(expert_ready, 1)
                    nc.vector.tensor_copy(wu_e[:, :], wu[:, bass.ds(i, 1), :]).then_inc(expert_ready, 1)
                    nc.vector.tensor_copy(comb_e[:, :], comb[:, :, bass.ds(i, 1)]).then_inc(expert_ready, 1)
                    dve.wait_ge(expert_ready, 3)

                    def product(n):
                        c, k = n // NH, n % NH
                        dve.wait_ge(gated, n + 1)
                        if c >= 2:
                            dve.wait_ge(y_done, c - 1)
                        nc.vector.tensor_tensor(gu[:, c % 2, k, :], gate[:, n % 2, :], ps_u[:, n % 2, :], ALU.mult).then_inc(gu_ready, 1)

                    product(0)
                    product(1)
                    for c in range(NCH):
                        if c + 1 < NCH:
                            product(2 * c + 2)
                            product(2 * c + 3)
                        dve.wait_ge(y_done, c + 1)
                        for j in range(TPC):
                            t = c * TPC + j
                            last = nc.vector.scalar_tensor_tensor(out=core.x[:, t, :], in0=ps_y[:, c % 2, j, :], scalar=comb_e[:, t:t + 1],
                                                                  in1=core.x[:, t, :], op0=ALU.mult, op1=ALU.add)
                        last.then_inc(added, 1)


def stage_span_attention(nc, core, tag, Wq, Wk, Wv, Wo, span):
    H, DH, RAMP = 16, 64, 32
    HP = H + 1
    SC = 1.0 / DH
    M = DH + 2
    F32R = mybir.dt.float32r
    PASS1 = [(qt, kc, min(CH, (qt + 1) * P - kc * CH), (qt // TPC) == kc) for qt in range(NT) for kc in range(qt // TPC + 1)]
    HEAD2 = [(qc, kb, max(0, kb * P - qc * CH)) for qc in range(NCH) for kb in range(TPC * (qc + 1))]
    N1, NH = len(PASS1), len(HEAD2)
    HB = 4
    NPB = 4
    LAG = 4
    with Stage(nc, tag) as s:
        wq, wk, wv = s.sb("wq", [P, HP * DH]), s.sb("wk", [P, HP * DH]), s.sb("wv", [P, HP * DH])
        wo = s.sb("wo", [M, H, D + 1])
        wq_h, wk_h = s.sb("wq_head", [P, 2, DH]), s.sb("wk_head", [P, 2, DH])
        mask, mask_h = s.sb("mask", [P, HP, NT]), s.sb("mask_head", [P, NT])
        pos, spans = s.sb("pos", [P, NT]), s.sb("spans", [P, H])
        k_hl = s.sb("k_hi_lo", [P, 2, T], F32R)
        q_hi, q_lo = s.sb("q_hi", [P, 2, T], F32R), s.sb("q_lo", [P, 2, T], F32R)
        va = s.sb("v_aug", [P, 2, NT, M])
        m_row = s.sb("max_row", [P, 2, T], BF16)
        m_part = s.sb("max_part", [P, NT, NCH])
        m_neg, m_rest = s.sb("max_neg", [P, NT]), s.sb("max_rest", [P, NT])
        m_split = s.sb("max_split", [P, NT, 3], BF16)
        probs = s.sb("probs", [P, NPB, CH])
        oT = s.sb("oT", [M, CH])
        rden = s.sb("rden", [P, TPC])
        ring, psS, psO = s.ps("ps_ring", [P, 2, CH]), s.ps("ps_scores", [P, 2, CH]), s.ps("ps_out", [P, 2, CH])
        psF = s.ps("ps_final", [P, TPC, 256])
        loaded, wo_zero, consts = s.sem("loaded"), s.sem("wo_zeroed"), s.sem("consts")
        pool_step, dve_step = s.sem("pool_step"), s.sem("dve_step")
        w_ready, rounded = s.sem("weights_ready"), s.sem("rounded")
        filled, slot_free = s.sem("ring_filled"), [s.sem(f"ring_free{b}") for b in range(2)]
        split_ready = s.sem("max_split")
        sc2, exped, pv = s.sem("pass2_scored"), s.sem("exp_done"), s.sem("pv_done")
        oT_ready, fin, recip, added = s.sem("oT_ready"), s.sem("final_ready"), s.sem("recip"), s.sem("x_added")
        with nc.Block() as block:
            @block.sync
            def _(sp):
                for dst, src in ((wq, Wq), (wk, Wk), (wv, Wv)):
                    sp.dma_start(dst[:, 0:H * DH], src).then_inc(loaded, 16)
                sp.dma_start(spans[:, :], span.rearrange("a h b c -> (a b c h)").partition_broadcast(P)).then_inc(loaded, 16)
                sp.wait_ge(wo_zero, 1)
                sp.dma_start(wo[0:DH, :, 0:D], Wo.rearrange("(h d) n -> d h n", d=DH)).then_inc(loaded, 16)
                sp.wait_ge(loaded, 80)

            @block.gpsimd
            def _(pool):
                st = Steps(pool, pool_step)
                st.run(nc.gpsimd.memset(wo[:, :, :], 0.0))
                nc.gpsimd.memset(wo[DH:M, :, D:D + 1], 1.0).then_inc(wo_zero, 1)
                pool.wait_ge(wo_zero, 1)
                for w in (wq, wk, wv):
                    st.add(nc.gpsimd.memset(w[:, H * DH:HP * DH], 0.0))
                st.add(nc.gpsimd.memset(mask[:, H:HP, :], 0.0))
                st.add(nc.gpsimd.memset(m_row[:, :, :], 0.0))
                st.add(nc.gpsimd.memset(m_part[:, :, :], -3.0e38))
                st.add(nc.gpsimd.memset(va[:, :, :, DH + 1:M], 1e-8))
                st.add(nc.gpsimd.iota(pos[:, :], pattern=[[P, NT]], base=0, channel_multiplier=1,
                                      allow_small_or_imprecise_dtypes=True))
                pool.wait_ge(loaded, 80)
                st.run(nc.gpsimd.tensor_scalar(spans[:, :], spans[:, :], float(T), None, ALU.mult))
                for h in range(H):
                    st.add(nc.gpsimd.tensor_scalar(mask[:, h, :], pos[:, :], spans[:, h:h + 1], 1.0 / (RAMP + 1), ALU.add, ALU.mult))
                st.wait()
                nc.gpsimd.tensor_scalar(mask[:, 0:H, :], mask[:, 0:H, :], 0.0, 1.0, ALU.max, ALU.min).then_inc(consts, 1)
                pool.wait_ge(consts, 1)

        def heads(i, targets):
            main = i is not None
            steps = (0, HB * NH + LAG) if main else (-NH, 0)
            N2 = HB * NH if main else 0
            at = lambda L, size: bass.ds(i * (HB * size) + L * size, size) if main else slice(0, size)
            ENDS = {L * NH + n: L * NCH + qc for L in range(HB) for n, (qc, kb, _) in enumerate(HEAD2) if kb == TPC * (qc + 1) - 1} if main else {}
            items = []
            for L in targets:
                s0 = (L - 1) * NH
                for c in range(NCH):
                    items += [(s0 + 4 * c, "k", L, c), (s0 + 4 * c + 1, "q", L, c), (s0 + 4 * c + 3, "v", L, c)]
                items += [(s0 + max(3 + k * (NH - 9) // N1, 4 * (PASS1[k][0] // TPC) + 3), "max", L, k) for k in range(N1)]
                items += [(s0 + NH - 4, "row", L, c) for c in range(NCH)]
            items.sort(key=lambda item: item[0])
            AT = {}
            for r, item in enumerate(items):
                AT.setdefault(item[0], []).append(r)
            WHERE = {item[1:]: r for r, item in enumerate(items)}
            ROUNDED = {r: n + 1 for n, r in enumerate(r for r, it in enumerate(items) if it[1] in ("k", "q"))}

            def pass2(n):
                qc, kb, q0 = HEAD2[n % NH]
                return n // NH, n // NH * NCH + qc, qc, kb, q0

            def due(n, lag):
                return ENDS.get(n - lag)

            def wait_slot(eng, r):
                eng.wait_ge(slot_free[r % 2], r // 2 + 1)

            with nc.Block() as block:
                @block.gpsimd
                def _(pool):
                    for n, L in enumerate(targets):
                        if n:
                            pool.wait_ge(filled, WHERE["q", targets[n - 1], NCH - 1] + 1)
                            wait_slot(pool, WHERE["v", targets[n - 1], NCH - 1])
                        for dst, w in ((wk_h, wk), (wq_h, wq)):
                            nc.gpsimd.tensor_copy(dst[:, :, :], w[:, at(L, DH)].unsqueeze(1).to_broadcast([P, 2, DH])).then_inc(w_ready, 1)
                        nc.gpsimd.tensor_copy(mask_h[:, :], mask[:, at(L, 1), :].rearrange("p a t -> p (a t)")).then_inc(w_ready, 1)

                @block.tensor
                def _(pe):
                    def fill(r):
                        _, kind, L, k = items[r]
                        out, par = ring[:, r % 2, :], L % 2
                        if r >= 2:
                            pe.wait_ge(slot_free[r % 2], r // 2)
                        if kind in ("k", "q"):
                            pe.wait_ge(w_ready, 3 * (targets.index(L) + 1))
                            w = wk_h if kind == "k" else wq_h
                            last = nc.tensor.matmul(out, w[:, :, :].rearrange("p r d -> p (r d)"), core.xT[:, k * CH:(k + 1) * CH],
                                                    start=True, stop=True)
                        elif kind == "v":
                            for j in range(TPC):
                                t = k * TPC + j
                                last = nc.tensor.matmul(out[:, j * DH:(j + 1) * DH], core.xT[:, t * P:(t + 1) * P], wv[:, at(L, DH)],
                                                        start=True, stop=True)
                        elif kind == "max":
                            qt, kc, w_, diag = PASS1[k]
                            if kc == 0 and qt % TPC == 0:
                                wait_slot(pe, WHERE["k", L, qt // TPC])
                                wait_slot(pe, WHERE["q", L, qt // TPC])
                            last = nc.tensor.matmul(out[:, 0:w_], q_hi[:, par, qt * P:(qt + 1) * P], k_hl[:, par, kc * CH:kc * CH + w_],
                                                    start=True, stop=not diag)
                            if diag:
                                last = nc.tensor.matmul(out[:, w_ - P:w_], core.ident_b[:, :], core.hide[:, :], start=False, stop=True)
                        else:
                            pe.wait_ge(split_ready, targets.index(L) + 1)
                            for j in range(TPC):
                                last = nc.tensor.matmul(out[0:3, j * P:(j + 1) * P], m_split[:, k * TPC + j, :], core.ident_b[:, :],
                                                        start=True, stop=True)
                        last.then_inc(filled, 1)

                    def scores(n):
                        L, g, qc, kb, q0 = pass2(n)
                        par = L % 2
                        if n >= 2:
                            pe.wait_ge(exped, n - 1)
                        if n % NH == 0 and ("row", L, 0) in WHERE:
                            wait_slot(pe, WHERE["row", L, NCH - 2])
                            wait_slot(pe, WHERE["row", L, NCH - 1])
                        q1, w = qc * CH + q0, CH - q0
                        diag = kb >= TPC * qc
                        out, keys = psS[:, n % 2, 0:w], k_hl[:, par, kb * P:(kb + 1) * P]
                        nc.tensor.matmul(out, keys, q_hi[:, par, q1:q1 + w], start=True, stop=False)
                        nc.tensor.matmul(out, keys, q_lo[:, par, q1:q1 + w], start=False, stop=False)
                        mm = nc.tensor.matmul(out, core.ones_b[:, :], m_row[:, par, q1:q1 + w], start=False, stop=not diag)
                        if diag:
                            mm = nc.tensor.matmul(psS[:, n % 2, 0:P], core.ident_b[:, :], core.hideT[:, :], start=False, stop=True)
                        mm.then_inc(sc2, 1)

                    def values(n):
                        L, g, qc, kb, q0 = pass2(n)
                        if kb == 0 and g >= 2:
                            pe.wait_ge(oT_ready, g - 1)
                        if n % NH == 0 and ("v", L, 0) in WHERE:
                            wait_slot(pe, WHERE["v", L, NCH - 1])
                        pe.wait_ge(exped, n + 1)
                        nc.tensor.matmul(psO[0:M, g % 2, q0:CH], va[:, L % 2, kb, :], probs[:, n % NPB, 0:CH - q0],
                                         start=kb == 0, stop=kb == TPC * (qc + 1) - 1).then_inc(pv, 1)

                    def project_out(g):
                        pe.wait_ge(oT_ready, g + 1)
                        pe.wait_ge(added, g)
                        for j in range(TPC):
                            last = nc.tensor.matmul(psF[:, j, 0:D + 1], oT[:, j * P:(j + 1) * P], wo[:, at(g // NCH, 1), :], start=True, stop=True)
                        last.then_inc(fin, 1)

                    if main:
                        scores(0)
                        scores(1)
                    for n in range(*steps):
                        if main and n + 2 < N2:
                            scores(n + 2)
                        fills = AT.get(n, [])
                        for r in fills[:(len(fills) + 1) // 2]:
                            fill(r)
                        if main and n < N2:
                            values(n)
                        for r in fills[(len(fills) + 1) // 2:]:
                            fill(r)
                        if (g := due(n, 2)) is not None:
                            project_out(g)

                @block.scalar
                def _(act):
                    def high_half(r):
                        _, kind, L, c = items[r]
                        act.wait_ge(filled, r + 1)
                        dst = k_hl if kind == "k" else q_hi
                        nc.scalar.activation(dst[:, L % 2, c * CH:(c + 1) * CH], ring[:, r % 2, :], ACT.Copy).then_inc(rounded, 1)

                    def exponential(n):
                        q0 = pass2(n)[4]
                        act.wait_ge(sc2, n + 1)
                        if n >= NPB:
                            act.wait_ge(pv, n - NPB + 1)
                        nc.scalar.activation(probs[:, n % NPB, 0:CH - q0], psS[:, n % 2, 0:CH - q0], ACT.Exp, scale=SC).then_inc(exped, 1)

                    if main:
                        exponential(0)
                    for n in range(*steps):
                        if main and n + 1 < N2:
                            exponential(n + 1)
                        for r in AT.get(n, ()):
                            if items[r][1] in ("k", "q"):
                                high_half(r)
                        if (g := due(n, 1)) is not None:
                            act.wait_ge(pv, n)
                            act.wait_ge(fin, g)
                            nc.scalar.activation(oT[:, :], psO[0:M, g % 2, :], ACT.Copy).then_inc(oT_ready, 1)

                @block.vector
                def _(dve):
                    st = Steps(dve, dve_step)

                    def take(r):
                        _, kind, L, k = items[r]
                        par, bank, free = L % 2, ring[:, r % 2, :], slot_free[r % 2]
                        cs = slice(k * CH, (k + 1) * CH)
                        dve.wait_ge(filled, r + 1)
                        if kind == "k":
                            dve.wait_ge(rounded, ROUNDED[r])
                            nc.vector.tensor_tensor(k_hl[DH:P, par, cs], bank[DH:P, :], k_hl[DH:P, par, cs].bitcast(F32), ALU.subtract).then_inc(free, 1)
                        elif kind == "q":
                            dve.wait_ge(rounded, ROUNDED[r])
                            nc.vector.tensor_tensor(q_lo[:, par, cs], bank, q_hi[:, par, cs].bitcast(F32), ALU.subtract).then_inc(free, 1)
                        elif kind == "v":
                            tiles = slice(k * TPC, (k + 1) * TPC)
                            dve.wait_ge(w_ready, 3 * (targets.index(L) + 1))
                            m4 = mask_h[:, tiles].unsqueeze(2)
                            nc.vector.tensor_copy(va[:, par, tiles, DH:DH + 1], m4)
                            nc.vector.tensor_tensor(va[:, par, tiles, 0:DH], bank[:, 0:TPC * DH].rearrange("p (t d) -> p t d", d=DH),
                                                    m4.to_broadcast([P, TPC, DH]), ALU.mult).then_inc(free, 1)
                        elif kind == "max":
                            qt, kc, w_, _ = PASS1[k]
                            nc.vector.tensor_reduce(m_part[:, qt, kc:kc + 1], bank[:, 0:w_], axis=AX.X, op=ALU.max).then_inc(free, 1)
                            if k == N1 - 1:
                                wait_slot(dve, WHERE["max", L, N1 - 2])
                                wait_slot(dve, r)
                                maxima(L)
                        else:
                            nc.vector.tensor_copy(m_row[0:3, par, cs], ring[0:3, r % 2, :]).then_inc(free, 1)

                    def maxima(L):
                        st.run(nc.vector.tensor_reduce(m_neg[:, :], m_part[:, :, :], axis=AX.X, op=ALU.max, negate=True))
                        st.run(nc.vector.tensor_copy(m_split[:, :, 0], m_neg[:, :]))
                        st.run(nc.vector.tensor_tensor(m_rest[:, :], m_neg[:, :], m_split[:, :, 0], ALU.subtract))
                        st.run(nc.vector.tensor_copy(m_split[:, :, 1], m_rest[:, :]))
                        st.run(nc.vector.tensor_tensor(m_neg[:, :], m_rest[:, :], m_split[:, :, 1], ALU.subtract))
                        st.run(nc.vector.tensor_copy(m_split[:, :, 2], m_neg[:, :]))
                        dve.sem_inc(split_ready, 1)

                    def add_to_x(g):
                        dve.wait_ge(fin, g + 1)
                        nc.vector.reciprocal(rden[:, :].unsqueeze(2), psF[:, :, D:D + 1]).then_inc(recip, 1)
                        dve.wait_ge(recip, g + 1)
                        for j in range(TPC):
                            t = (g % NCH) * TPC + j
                            last = nc.vector.scalar_tensor_tensor(out=core.x[:, t, :], in0=psF[:, j, 0:D], scalar=rden[:, j:j + 1],
                                                                  in1=core.x[:, t, :], op0=ALU.mult, op1=ALU.add)
                        last.then_inc(added, 1)
                        dve.wait_ge(added, g + 1)

                    for n in range(*steps):
                        for r in AT.get(n, ()):
                            take(r)
                        if (g := due(n, 3)) is not None:
                            add_to_x(g)

        s.restart()
        heads(None, [0])
        with nc.Fori(0, H // HB) as i:
            s.restart()
            heads(i, list(range(1, HB + 1)))


def stage_rope_attention(nc, core, tag, WqkvT, WswapT, WoutT, cosT, sinT):
    H, DH, G, NPART = 16, 8, 4, 3
    NG = H // G
    SC = DH ** -0.5
    Q_ORDER, K_ORDER = (0, 1, 0, 1, 2, 0), (0, 0, 1, 1, 0, 2)
    PASS1 = [(qt, kc, min(CH, (qt + 1) * P - kc * CH), (qt // TPC) == kc) for qt in range(NT) for kc in range(qt // TPC + 1)]
    HEAD2 = [(qc, kb, max(0, kb * P - qc * CH)) for qc in range(NCH) for kb in range(TPC * (qc + 1))]
    N1, NH = len(PASS1), len(HEAD2)
    UNROLL = 2
    NPB, NR, MR = 2 * G, 3, 64
    LAG = 4
    with Stage(nc, tag) as s:
        o_all = s.sb("o_tokens", [P, NT, D])
        w_out = s.sb("w_out", [P, D])
        va = s.sb("v_aug", [P, NT, H + G, 32])
        qs, ks = s.sb("q_stack", [P, 2, G, T], BF16), s.sb("k_stack", [P, 2, G, T], BF16)
        scratch = {n: nc.dram_tensor(f"{tag}_{n}_parts", (NPART, P + G * DH, T), BF16, kind="Internal").ap() for n in "qk"}
        with Stage(nc, tag + "_in") as q:
            w, ws = q.sb("w_qkv", [P, 3 * D]), q.sb("w_swapped", [P, 2 * D])
            cos, sin = q.sb("cos", [P, T]), q.sb("sin", [P, T])
            roped, rest = q.sb("roped", [P, T]), q.sb("rest", [P, T])
            parts = q.sb("parts", [P, 2, NPART, T], BF16)
            ps_a, ps_b = q.ps("ps_plain", [P, 2, CH]), q.ps("ps_swapped", [P, 2, CH])
            ps_v = q.ps("ps_v", [P, 2, TPC, D])
            loaded, stored, zeroed, dve_step = q.sem("loaded"), q.sem("stored"), q.sem("v_zeroed"), q.sem("dve_step")
            proj, a_used, b_used, v_done, v_out, split = (q.sem(n) for n in ("projected", "plain_used", "swapped_used", "v_done", "v_out", "split"))
            with nc.Block() as block:
                @block.sync
                def _(sp):
                    for dst, src in ((w, WqkvT), (ws, WswapT), (cos, cosT), (sin, sinT), (w_out, WoutT)):
                        sp.dma_start(dst[:, :], src).then_inc(loaded, 16)
                    for n, name in enumerate("qk"):
                        for part in range(NPART):
                            sp.wait_ge(split, n * NPART + part + 1)
                            sp.dma_start(scratch[name][part, 0:P, :], parts[:, n, part, :]).then_inc(stored, 16)
                            sp.dma_start(scratch[name][part, P:P + G * DH, :], parts[0:G * DH, n, part, :]).then_inc(stored, 16)
                    sp.wait_ge(loaded, 80)
                    sp.wait_ge(stored, 16 * 4 * NPART)

                @block.gpsimd
                def _(pool):
                    nc.gpsimd.memset(va[:, :, :, :], 0.0).then_inc(zeroed, 1)
                    pool.wait_ge(zeroed, 1)
                    nc.gpsimd.memset(va[:, :, :, DH:DH + 1], 1.0).then_inc(zeroed, 1)
                    nc.gpsimd.memset(qs[:, :, :, :], 0.0).then_inc(zeroed, 1)
                    pool.wait_ge(zeroed, 3)

                @block.tensor
                def _(pe):
                    pe.wait_ge(loaded, 80)
                    for n in range(2 * NCH):
                        j, c = n // NCH, n % NCH
                        if n >= 2:
                            pe.wait_ge(a_used, n - 1)
                            pe.wait_ge(b_used, n - 1)
                        cols = core.xT[:, c * CH:(c + 1) * CH]
                        nc.tensor.matmul(ps_a[:, n % 2, :], w[:, j * D:(j + 1) * D], cols, start=True, stop=True)
                        nc.tensor.matmul(ps_b[:, n % 2, :], ws[:, j * D:(j + 1) * D], cols, start=True, stop=True).then_inc(proj, 1)
                    for c in range(NCH):
                        if c >= 2:
                            pe.wait_ge(v_out, c - 1)
                        for j in range(TPC):
                            t = c * TPC + j
                            last = nc.tensor.matmul(ps_v[:, c % 2, j, :], core.xT[:, t * P:(t + 1) * P], w[:, 2 * D:3 * D], start=True, stop=True)
                        last.then_inc(v_done, 1)

                @block.scalar
                def _(act):
                    act.wait_ge(zeroed, 2)
                    for c in range(NCH):
                        act.wait_ge(v_done, c + 1)
                        nc.scalar.activation(va[:, c * TPC:(c + 1) * TPC, 0:H, 0:DH],
                                             ps_v[:, c % 2, :, :].rearrange("p t (h d) -> p t h d", d=DH), ACT.Copy).then_inc(v_out, 1)

                @block.vector
                def _(dve):
                    st = Steps(dve, dve_step)
                    dve.wait_ge(loaded, 80)
                    for j in range(2):
                        for c in range(NCH):
                            n = j * NCH + c
                            cs = slice(c * CH, (c + 1) * CH)
                            dve.wait_ge(proj, n + 1)
                            nc.vector.tensor_tensor(roped[:, cs], ps_a[:, n % 2, :], cos[:, cs], ALU.mult).then_inc(a_used, 1)
                            nc.vector.tensor_tensor(rest[:, cs], ps_b[:, n % 2, :], sin[:, cs], ALU.mult).then_inc(b_used, 1)
                        dve.wait_ge(a_used, (j + 1) * NCH)
                        dve.wait_ge(b_used, (j + 1) * NCH)
                        st.run(nc.vector.tensor_tensor(roped[:, :], roped[:, :], rest[:, :], ALU.add))
                        for part in range(NPART):
                            nc.vector.tensor_copy(parts[:, j, part, :], roped[:, :]).then_inc(split, 1)
                            dve.wait_ge(split, j * NPART + part + 1)
                            if part < NPART - 1:
                                st.run(nc.vector.tensor_tensor(roped[:, :], roped[:, :], parts[:, j, part, :], ALU.subtract))

        with Stage(nc, tag + "_heads") as q:
            vg = q.sb("v_group", [P, 2, NT, G, 32])
            m_part = q.sb("max_part", [P, NT, NCH])
            m_neg, m_rest = q.sb("max_neg", [P, NT]), q.sb("max_rest", [P, NT])
            m_split = q.sb("max_split", [P, G, NT, 3], BF16)
            probs = q.sb("probs", [P, NPB, CH])
            oT, rden = q.sb("oT", [P, CH]), q.sb("rden", [P, TPC, G])
            ring, psS = q.ps("ps_ring", [P, NR, CH]), q.ps("ps_scores", [P, G, CH])
            ps_o = q.ps("ps_out", [P, CH])
            zeroed, dve_step = q.sem("zeroed"), q.sem("dve_step")
            stack_in, v_ready, cleared = [q.sem(f"stack_in{g}") for g in range(G)], q.sem("v_ready"), q.sem("max_rows_cleared")
            filled, slot_free = q.sem("ring_filled"), [q.sem(f"ring_free{b}") for b in range(NR)]
            split_ready = q.sem("max_split")
            sc2, exped, pv, oT_ready = q.sem("pass2_scored"), q.sem("exp_done"), q.sem("pv_done"), q.sem("oT_ready")
            recip = q.sem("recip")

            def groups(i, targets):
                main = i is not None
                steps = (0, UNROLL * NH + LAG) if main else (-NH, 0)
                NS = UNROLL * NH if main else 0
                at = lambda L, size, off=0, n=None: (bass.ds(i * (UNROLL * size) + (L * size + off), n or size) if main
                                                     else slice(off, off + (n or size)))
                ENDS = {L * NH + n: L * NCH + qc for L in range(UNROLL) for n, (qc, kb, _) in enumerate(HEAD2)
                        if kb == TPC * (qc + 1) - 1} if main else {}
                items = []
                for L in targets:
                    s0 = (L - 1) * NH
                    for g in range(G):
                        put = [s0 + 3 + (g * N1 + k) * (NH - 8) // (G * N1) for k in range(N1)]
                        items += [(put[k], "max", L, g, k) for k in range(N1)]
                        items += [(put[-1] + 2, "row", L, g, c) for c in range(NCH)]
                items += [(e + 2, "turn", chunk // NCH, 0, chunk) for e, chunk in ENDS.items()]
                items.sort(key=lambda item: item[0])
                AT = {}
                for r, item in enumerate(items):
                    AT.setdefault(item[0], []).append(r)
                TURNS = {it[4]: r for r, it in enumerate(items) if it[1] == "turn"}
                WHERE = {item[1:]: r for r, item in enumerate(items)}

                def pass2(n):
                    qc, kb, q0 = HEAD2[n % NH]
                    return n // NH, n // NH * NCH + qc, qc, kb, q0

                def due(n, lag):
                    return ENDS.get(n - lag)

                def wait_slot(eng, r):
                    eng.wait_ge(slot_free[r % NR], r // NR + 1)

                with nc.Block() as block:
                    @block.sync
                    def _(sp):
                        for n, L in enumerate(targets):
                            if L >= 2:
                                sp.wait_ge(pv, G * (L - 1) * NH)
                            for g in range(G):
                                for r in range(6):
                                    src, dst = at(L, G * DH, g * DH, DH), slice(r * DH, (r + 1) * DH)
                                    sp.dma_start(qs[dst, L % 2, g, :], scratch["q"][Q_ORDER[r], src, :]).then_inc(stack_in[g], 16)
                                    sp.dma_start(ks[dst, L % 2, g, :], scratch["k"][K_ORDER[r], src, :]).then_inc(stack_in[g], 16)
                            for g in range(G):
                                sp.wait_ge(stack_in[g], 16 * 12 * (n + 1))

                    @block.gpsimd
                    def _(pool):
                        for n, L in enumerate(targets):
                            if L >= 2:
                                pool.wait_ge(pv, G * (L - 1) * NH)
                            for g in range(G):
                                nc.gpsimd.memset(qs[MR:MR + 3, L % 2, g, :], 0.0).then_inc(cleared, 1)
                            pool.wait_ge(cleared, G * (n + 1))
                            nc.gpsimd.tensor_copy(vg[:, L % 2, :, :, :], va[:, :, at(L, G), :]).then_inc(v_ready, 1)
                            pool.wait_ge(v_ready, n + 1)

                    @block.tensor
                    def _(pe):
                        def fill(r):
                            _, kind, L, g, k = items[r]
                            n, par = (targets.index(L) if L in targets else 0), L % 2
                            if r >= NR:
                                pe.wait_ge(slot_free[r % NR], r // NR)
                            if kind == "max":
                                if k == 0:
                                    pe.wait_ge(cleared, G * n + g + 1)
                                    pe.wait_ge(stack_in[g], 16 * 12 * (n + 1))
                                qt, kc, w_, diag = PASS1[k]
                                last = nc.tensor.matmul(ring[:, r % NR, 0:w_], qs[:, par, g, qt * P:(qt + 1) * P],
                                                        ks[:, par, g, kc * CH:kc * CH + w_], start=True, stop=not diag)
                                if diag:
                                    last = nc.tensor.matmul(ring[:, r % NR, w_ - P:w_], core.ident_b[:, :], core.hide[:, :], start=False, stop=True)
                            elif kind == "turn":
                                pe.wait_ge(oT_ready, k + 1)
                                for j in range(TPC):
                                    last = nc.tensor.transpose(ring[:, r % NR, j * P:(j + 1) * P], oT[:, j * P:(j + 1) * P], core.ident[:, :])
                            else:
                                pe.wait_ge(split_ready, n * G + g + 1)
                                for j in range(TPC):
                                    last = nc.tensor.matmul(ring[MR:MR + 3, r % NR, j * P:(j + 1) * P], m_split[:, g, k * TPC + j, :],
                                                            core.ident_b[:, :], start=True, stop=True)
                            last.then_inc(filled, 1)

                        def scores(n, g):
                            L, _, qc, kb, q0 = pass2(n)
                            if n % NH == 0 and L in targets:
                                for c in range(NCH - NR, NCH - 1):
                                    wait_slot(pe, WHERE["row", L, g, c])
                                wait_slot(pe, WHERE["row", L, g, NCH - 1])
                            if n:
                                pe.wait_ge(exped, G * (n - 1) + g + 1)
                            q1, w_ = qc * CH + q0, CH - q0
                            diag = kb >= TPC * qc
                            mm = nc.tensor.matmul(psS[:, g, 0:w_], ks[:, L % 2, g, kb * P:(kb + 1) * P], qs[:, L % 2, g, q1:q1 + w_],
                                                  start=True, stop=not diag)
                            if diag:
                                mm = nc.tensor.matmul(psS[:, g, 0:P], core.ident_b[:, :], core.hideT[:, :], start=False, stop=True)
                            mm.then_inc(sc2, 1)

                        def values(n):
                            L, chunk, qc, kb, q0 = pass2(n)
                            if kb == 0 and chunk:
                                pe.wait_ge(oT_ready, chunk)
                            if n % NH == 0 and L in targets:
                                pe.wait_ge(v_ready, targets.index(L) + 1)
                            for g in range(G):
                                pe.wait_ge(exped, G * n + g + 1)
                                nc.tensor.matmul(ps_o[32 * g:32 * g + 32, q0:CH], vg[:, L % 2, kb, g, :], probs[:, (G * n + g) % NPB, 0:CH - q0],
                                                 start=kb == 0, stop=kb == TPC * (qc + 1) - 1).then_inc(pv, 1)

                        if main:
                            for g in range(G):
                                scores(0, g)
                        for n in range(*steps):
                            fills = AT.get(n, [])
                            for g in range(G):
                                if main and n + 1 < NS:
                                    scores(n + 1, g)
                                for r in fills[g * len(fills) // G:(g + 1) * len(fills) // G]:
                                    fill(r)
                            if main and n < NS:
                                values(n)

                    @block.scalar
                    def _(act):
                        def exponentials(n):
                            q0 = pass2(n)[4]
                            for g in range(G):
                                m = G * n + g
                                act.wait_ge(sc2, m + 1)
                                if m >= NPB:
                                    act.wait_ge(pv, m - NPB + 1)
                                nc.scalar.activation(probs[:, m % NPB, 0:CH - q0], psS[:, g, 0:CH - q0], ACT.Exp, scale=SC).then_inc(exped, 1)

                        if main:
                            exponentials(0)
                        for n in range(*steps):
                            if (chunk := due(n, 1)) is not None:
                                act.wait_ge(pv, G * n)
                                if chunk:
                                    act.wait_ge(filled, TURNS[chunk - 1] + 1)
                                nc.scalar.activation(oT[:, :], ps_o[:, :], ACT.Copy).then_inc(oT_ready, 1)
                            if main and n + 1 < NS:
                                exponentials(n + 1)

                    @block.vector
                    def _(dve):
                        st = Steps(dve, dve_step)

                        def maxima(g):
                            st.run(nc.vector.tensor_reduce(m_neg[:, :], m_part[:, :, :], axis=AX.X, op=ALU.max, negate=True))
                            st.run(nc.vector.tensor_copy(m_split[:, g, :, 0], m_neg[:, :]))
                            st.run(nc.vector.tensor_tensor(m_rest[:, :], m_neg[:, :], m_split[:, g, :, 0], ALU.subtract))
                            st.run(nc.vector.tensor_copy(m_split[:, g, :, 1], m_rest[:, :]))
                            st.run(nc.vector.tensor_tensor(m_neg[:, :], m_rest[:, :], m_split[:, g, :, 1], ALU.subtract))
                            st.run(nc.vector.tensor_copy(m_split[:, g, :, 2], m_neg[:, :]))
                            dve.sem_inc(split_ready, 1)

                        def take(r):
                            _, kind, L, g, k = items[r]
                            dve.wait_ge(filled, r + 1)
                            if kind == "turn":
                                output(r)
                                return
                            if kind == "row":
                                nc.vector.tensor_copy(qs[MR:MR + 3, L % 2, g, k * CH:(k + 1) * CH], ring[MR:MR + 3, r % NR, :]).then_inc(slot_free[r % NR], 1)
                                return
                            qt, kc, w_, _ = PASS1[k]
                            nc.vector.tensor_reduce(m_part[:, qt, kc:kc + 1], ring[:, r % NR, 0:w_], axis=AX.X, op=ALU.max).then_inc(slot_free[r % NR], 1)
                            if k == N1 - 1:
                                for kk in range(N1 - NR, N1 - 1):
                                    wait_slot(dve, WHERE["max", L, g, kk])
                                wait_slot(dve, r)
                                maxima(g)

                        def output(r):
                            _, _, L, _, chunk = items[r]
                            qc, turned = chunk % NCH, ring[:, r % NR, :].rearrange("p (t g d) -> p t g d", t=TPC, g=G)
                            nc.vector.reciprocal(rden[:, :, :].unsqueeze(3), turned[:, :, :, DH:DH + 1]).then_inc(recip, 1)
                            dve.wait_ge(recip, chunk + 1)
                            dst = o_all[:, qc * TPC:(qc + 1) * TPC, at(L, G * DH)].rearrange("p t (g d) -> p t g d", g=G)
                            nc.vector.tensor_tensor(dst, turned[:, :, :, 0:DH], rden[:, :, :].unsqueeze(3).to_broadcast([P, TPC, G, DH]), ALU.mult).then_inc(slot_free[r % NR], 1)
                            wait_slot(dve, r)

                        for n in range(*steps):
                            for r in AT.get(n, ()):
                                take(r)

            with nc.Block() as block:
                @block.gpsimd
                def _(pool):
                    nc.gpsimd.memset(ks[:, 1, :, :], 0.0).then_inc(zeroed, 1)
                    nc.gpsimd.memset(m_part[:, :, :], -3.0e38).then_inc(zeroed, 1)
                    pool.wait_ge(zeroed, 2)
                    nc.gpsimd.memset(ks[MR:MR + 3, 1, :, :], 1.0).then_inc(zeroed, 1)

                @block.vector
                def _(dve):
                    st = Steps(dve, dve_step)
                    st.run(nc.vector.memset(ks[:, 0, :, :], 0.0))
                    st.run(nc.vector.memset(ks[MR:MR + 3, 0, :, :], 1.0))
            q.restart()
            groups(None, [0])
            with nc.Fori(0, NG // UNROLL) as i:
                q.restart()
                groups(i, list(range(1, UNROLL + 1)))

        stage_project(nc, core, tag + "_out", o_all, w_out)


def stage_project(nc, core, tag, o_all, w_out):
    with Stage(nc, tag) as s:
        oT = s.sb("oT", [P, 2, CH])
        ps_t, ps_y = s.ps("ps_turned", [P, 2, CH]), s.ps("ps_y", [P, 2, TPC, D])
        turned, ready, done, added = s.sem("turned"), s.sem("oT_ready"), s.sem("y_done"), s.sem("x_added")
        with nc.Block() as block:
            @block.tensor
            def _(pe):
                def turn(c):
                    if c >= 2:
                        pe.wait_ge(ready, c - 1)
                    for j in range(TPC):
                        last = nc.tensor.transpose(ps_t[:, c % 2, j * P:(j + 1) * P], o_all[:, c * TPC + j, :], core.ident[:, :])
                    last.then_inc(turned, 1)

                turn(0)
                for c in range(NCH):
                    if c + 1 < NCH:
                        turn(c + 1)
                    pe.wait_ge(ready, c + 1)
                    if c >= 2:
                        pe.wait_ge(added, c - 1)
                    for j in range(TPC):
                        last = nc.tensor.matmul(ps_y[:, c % 2, j, :], oT[:, c % 2, j * P:(j + 1) * P], w_out[:, :], start=True, stop=True)
                    last.then_inc(done, 1)

            @block.scalar
            def _(act):
                for c in range(NCH):
                    act.wait_ge(turned, c + 1)
                    if c >= 2:
                        act.wait_ge(done, c - 1)
                    nc.scalar.activation(oT[:, c % 2, :], ps_t[:, c % 2, :], ACT.Copy).then_inc(ready, 1)

            @block.vector
            def _(dve):
                for c in range(NCH):
                    dve.wait_ge(done, c + 1)
                    tiles = slice(c * TPC, (c + 1) * TPC)
                    nc.vector.tensor_tensor(core.x[:, tiles, :], core.x[:, tiles, :], ps_y[:, c % 2, :, :], ALU.add).then_inc(added, 1)
                dve.wait_ge(added, NCH)


def stage_power_attention(nc, core, tag, Wq, WqS, Wk, WkS, Wv, Wg, Wp, lnw, cosT, sinT):
    HK, R, DH = 8, 2, 64
    SC = DH ** -0.5
    M = DH + 1
    TINY = 2.0 ** -60
    PASS1 = [(qt, kc, min(CH, (qt + 1) * P - kc * CH), (qt // TPC) == kc) for qt in range(NT) for kc in range(qt // TPC + 1)]
    HEAD2 = [(qc, kb, max(0, kb * P - qc * CH)) for qc in range(NCH) for kb in range(TPC * (qc + 1))]
    N1, NH = len(PASS1), len(HEAD2)
    NPB = 6
    NR, NS = 2, 3
    LAG = 8
    FOFF = [0] + [CH + sum(CH - jj * P for jj in range(j)) for j in range(TPC)]
    FLEN = CH + sum(CH - j * P for j in range(TPC))
    NEXP = lambda g: TPC + (1 if g % NCH else 0)
    UNROLL = 2
    HB = UNROLL * R

    with Stage(nc, tag) as s:
        HP = HK + 1
        wq, wqs = s.sb("wq", [P, HP * R * DH]), s.sb("wq_swapped", [P, HP * R * DH])
        wk, wks, wv = s.sb("wk", [P, HP * DH]), s.sb("wk_swapped", [P, HP * DH]), s.sb("wv", [P, HP * DH])
        wp = s.sb("w_proj", [DH + 1, HK * R, D])
        lw = s.sb("ln_w", [DH, 1])
        cos, sin = s.sb("cos", [P, T]), s.sb("sin", [P, T])
        gcol, gend = s.sb("gate_col", [P, NT, HP]), s.sb("gate_tile_end", [P, NT, HP])
        later = s.sb("later_tiles", [P, NT, NT])
        tri = s.sb("tri_qk", [P, P])
        eps_col = s.sb("eps_decayed", [P, NT, HP])
        center = s.sb("center", [M, M])
        mean_col, den_bias = s.sb("mean_col", [M, 1]), s.sb("den_bias", [M, 1])
        f_dram = nc.dram_tensor(f"{tag}_decay", (HK + 1, T), F32, kind="Internal").ap()
        with Stage(nc, tag + "_in") as q:
            wg = q.sb("wg", [P, HK])
            v, e, l, g = (q.sb(n, [HK, T]) for n in ("v", "e", "l", "g"))
            one, last_row = q.sb("one", [HK, T]), q.sb("last_row", [P, P])
            ps_z, ps_g, ps_e = q.ps("ps_z", [HK, 2, CH]), q.ps("ps_g", [P, NT, HK]), q.ps("ps_e", [P, NT, HP])
            loaded, dve_step, pool_step = q.sem("loaded"), q.sem("dve_step"), q.sem("pool_step")
            z_done, z_out, v_ready, abs_done, exp_done, ln_done = (q.sem(n) for n in ("z_done", "z_out", "v_ready", "abs_done", "exp_done", "ln_done"))
            g_ready, f_ready, f_exp, stored, g_turned, gcol_ready, e_done = (q.sem(n) for n in ("g_ready", "f_ready", "f_exp", "stored", "g_turned", "gcol_ready", "e_done"))
            eps_in, eps_exp = q.sem("eps_in"), q.sem("eps_exp")
            NLOAD = 10
            with nc.Block() as block:
                @block.sync
                def _(sp):
                    sp.wait_ge(pool_step, 1)
                    for dst, src in ((wq, Wq), (wqs, WqS), (wk, Wk), (wks, WkS), (wv, Wv), (wg, Wg), (cos, cosT), (sin, sinT), (lw, lnw)):
                        sp.dma_start(dst[:, 0:src.shape[1]], src).then_inc(loaded, 16)
                    sp.dma_start(wp[0:DH, :, :], Wp.rearrange("(h d) n -> d h n", d=DH)).then_inc(loaded, 16)
                    sp.wait_ge(loaded, 16 * NLOAD)
                    sp.wait_ge(f_exp, 1)
                    sp.dma_start(f_dram[0:HK, :], e[:, :]).then_inc(stored, 16)
                    sp.dma_start(f_dram[HK:HK + 1, :], e[0:1, :]).then_inc(stored, 16)
                    sp.wait_ge(stored, 32)

                @block.gpsimd
                def _(pool):
                    st = Steps(pool, pool_step)
                    st.run(nc.gpsimd.memset(wp[:, :, :], 0.0))
                    st.run(nc.gpsimd.memset(one[:, :], 1.0))
                    st.run(nc.gpsimd.memset(later[:, :, :], 0.0))
                    st.run(nc.gpsimd.affine_select(out=later[:, :, :], in_=later[:, :, :], compare_op=ALU.is_ge, fill=MASKED, base=0,
                                                   pattern=[[1, NT], [-1, NT]], channel_multiplier=0))
                    st.run(nc.gpsimd.memset(tri[:, :], 1.0))
                    st.run(nc.gpsimd.affine_select(out=tri[:, :], in_=tri[:, :], compare_op=ALU.is_ge, fill=0.0, base=0,
                                                   pattern=[[-1, P]], channel_multiplier=1))
                    st.run(nc.gpsimd.memset(mean_col[0:DH, :], 1.0 / DH))
                    st.run(nc.gpsimd.memset(mean_col[DH:M, :], 1e-9))
                    for w, n in ((wq, R * DH), (wqs, R * DH), (wk, DH), (wks, DH), (wv, DH)):
                        st.run(nc.gpsimd.memset(w[:, HK * n:HP * n], 0.0))
                    st.run(nc.gpsimd.memset(gcol[:, :, HK:HP], 0.0))

                @block.tensor
                def _(pe):
                    pe.wait_ge(loaded, 16 * NLOAD)
                    for c in range(NCH):
                        if c >= 2:
                            pe.wait_ge(z_out, c - 1)
                        nc.tensor.matmul(ps_z[:, c % 2, :], wg[:, :], core.xT[:, c * CH:(c + 1) * CH], start=True, stop=True).then_inc(z_done, 1)
                    pe.wait_ge(g_ready, 1)
                    for t in range(NT):
                        last = nc.tensor.transpose(ps_g[:, t, :], g[:, t * P:(t + 1) * P], core.ident[0:HK, 0:HK])
                    last.then_inc(g_turned, 1)
                    pe.wait_ge(gcol_ready, 1)
                    nc.tensor.matmul(ps_e[:, :, :].rearrange("p t h -> p (t h)"), last_row[:, :], gcol[:, :, :].rearrange("p t h -> p (t h)"),
                                     start=True, stop=True).then_inc(e_done, 1)

                @block.scalar
                def _(act):
                    act.wait_ge(v_ready, 1)
                    nc.scalar.activation(l[:, :], v[:, :], ACT.Abs).then_inc(abs_done, 1)
                    act.wait_ge(abs_done, 1)
                    nc.scalar.activation(e[:, :], l[:, :], ACT.Exp, scale=-1.0).then_inc(exp_done, 1)
                    act.wait_ge(exp_done, 1)
                    nc.scalar.activation(l[:, :], e[:, :], ACT.Ln, bias=1.0).then_inc(ln_done, 1)
                    act.wait_ge(f_ready, 1)
                    nc.scalar.activation(e[:, :], e[:, :], ACT.Exp).then_inc(f_exp, 1)
                    act.wait_ge(eps_in, 1)
                    nc.scalar.activation(eps_col[:, :, :], eps_col[:, :, :], ACT.Exp).then_inc(eps_exp, 1)

                @block.vector
                def _(dve):
                    st = Steps(dve, dve_step)
                    dve.wait_ge(loaded, 16 * NLOAD)
                    dve.wait_ge(pool_step, 14)
                    st.add(nc.vector.tensor_scalar(wp[0:DH, :, :], wp[0:DH, :, :], lw[:, 0:1], None, ALU.mult))
                    st.add(nc.vector.tensor_copy(last_row[:, :], core.ident[:, P - 1:P].to_broadcast([P, P])))
                    st.add(nc.vector.tensor_scalar(den_bias[:, :], core.ident[0:M, DH:M], 1e-6, None, ALU.mult))
                    st.run(nc.vector.tensor_copy(center[:, :], core.ident[0:M, 0:M]))
                    st.add(nc.vector.tensor_scalar(center[0:DH, 0:DH], center[0:DH, 0:DH], -1.0 / DH, None, ALU.add))
                    for c in range(NCH):
                        dve.wait_ge(z_done, c + 1)
                        nc.vector.tensor_scalar(v[:, c * CH:(c + 1) * CH], ps_z[:, c % 2, :], 6.906768, None, ALU.add).then_inc(z_out, 1)
                    dve.wait_ge(z_out, NCH)
                    dve.sem_inc(v_ready, 1)
                    dve.wait_ge(exp_done, 1)
                    st.run(nc.vector.tensor_scalar(g[:, :], e[:, :], 1.0, -1.0, ALU.add, ALU.add))
                    st.run(nc.vector.tensor_tensor(g[:, :], e[:, :], g[:, :], ALU.subtract))
                    dve.wait_ge(ln_done, 1)
                    st.run(nc.vector.tensor_tensor(g[:, :], g[:, :], l[:, :], ALU.add))
                    st.run(nc.vector.scalar_tensor_tensor(out=v[:, :], in0=v[:, :], scalar=0.0, in1=g[:, :], op0=ALU.min, op1=ALU.subtract))
                    st.run(nc.vector.tensor_tensor_scan(l[:, :], one[:, :], v[:, :], 0.0, ALU.mult, ALU.add))
                    st.run(nc.vector.tensor_scalar(g[:, :], l[:, :], 0.5, None, ALU.mult))
                    dve.sem_inc(g_ready, 1)
                    by_tile = g[:, :].rearrange("h (t p) -> h t p", p=P)
                    nc.vector.tensor_tensor(e[:, :].rearrange("h (t p) -> h t p", p=P), by_tile[:, :, P - 1:P].to_broadcast([HK, NT, P]), by_tile,
                                            ALU.subtract).then_inc(f_ready, 1)
                    dve.wait_ge(g_turned, 1)
                    nc.vector.tensor_copy(gcol[:, :, 0:HK], ps_g[:, :, :]).then_inc(gcol_ready, 1)
                    dve.wait_ge(e_done, 1)
                    st.run(nc.vector.tensor_copy(gend[:, :, :], ps_e[:, :, :]))
                    nc.vector.tensor_tensor(eps_col[:, :, :], gend[:, :, :], gcol[:, :, :], ALU.subtract).then_inc(eps_in, 1)
                    dve.wait_ge(eps_exp, 1)
                    st.run(nc.vector.tensor_scalar(eps_col[:, :, :], eps_col[:, :, :], 1e-30, None, ALU.mult))

        with Stage(nc, tag + "_heads") as q:
            F32R = mybir.dt.float32r
            wq_h = [q.sb(f"wq_head{hh}", [P, 2, DH]) for hh in range(R)]
            wqs_h = [q.sb(f"wq_swapped_head{hh}", [P, 2, DH]) for hh in range(R)]
            wk_h, wks_h = q.sb("wk_head", [P, 2, DH]), q.sb("wk_swapped_head", [P, 2, DH])
            ge, nge, eps_d = (q.sb(n, [P, 2, NT]) for n in ("gate_end", "minus_gate_end", "eps_decayed_head"))
            c_col = q.sb("earlier_factor", [P, 2, NCH - 1, NT])
            c_eps = q.sb("earlier_eps", [P, 2, NCH - 1, NT])
            k_hl = q.sb("k_hi_lo", [P, 2, T], F32R)
            va = q.sb("v_aug", [P, 2, NT, M])
            decay, kd, k_hi = q.sb("decay", [P, T]), q.sb("k_decayed", [P, 2, CH]), q.sb("k_hi", [P, 2, CH], F32R)
            q_hi, q_lo = q.sb("q_hi", [P, R, T], F32R), q.sb("q_lo", [P, R, T], F32R)
            m_row = q.sb("max_row", [P, R, T], BF16)
            t1, t2, rot = (q.sb(n, [P, 2, CH]) for n in ("rope_plain", "rope_swapped", "rotated"))
            m_abs = q.sb("max_abs", [P, NT, NT])
            l1, l2 = q.sb("log_a", [P, NT, NT]), q.sb("log_b", [P, NT, NT])
            scrap = q.sb("masked_scores", [P, P])
            m_neg, m_rest = q.sb("max_neg", [P, NT]), q.sb("max_rest", [P, NT])
            m_split = q.sb("max_split", [P, NT, 3], BF16)
            fac = q.sb("factors", [P, 2, FLEN])
            sabs, probs = (q.sb(n, [P, NPB, CH]) for n in ("scores_abs", "probs"))
            oT, cT, sq = q.sb("oT", [M, CH]), q.sb("centered_T", [M, CH]), q.sb("squares_T", [M, CH])
            uu, rs, yy = (q.sb(n, [P, TPC]) for n in ("var", "rstd", "newton_term"))
            ring, psS, psO = q.ps("ps_ring", [P, NR, CH]), q.ps("ps_scores", [P, NS, CH]), q.ps("ps_out", [P, 2, CH])
            psC = q.ps("ps_center_final", [P, TPC, D])
            zeroed, dve_step, newton = q.sem("zeroed"), q.sem("dve_step"), q.sem("newton_step")
            w_ready, decay_in, t_done, rotated = (q.sem(n) for n in ("weights_ready", "decay_in", "rope_products", "rotated"))
            kd_out, rounded, split = (q.sem(n) for n in ("k_decayed", "rounded", "operand_split"))
            cols_in, c_exp, cols_ready = (q.sem(n) for n in ("cols_in", "c_exp", "cols_ready"))
            filled, slot_free = q.sem("ring_filled"), [q.sem(f"ring_free{b}") for b in range(NR)]
            max_done, ln_in, ln_out, split_ready = (q.sem(n) for n in ("pass1_max", "ln_in", "ln_out", "max_split"))
            f_done, f_masked = q.sem("factor_exp"), q.sem("factor_masked")
            sc2, abs_done, b_done, a_done, pv = (q.sem(n) for n in ("pass2_scored", "scores_abs", "product", "squared", "pv_done"))
            oT_ready, centered, cT_ready, added = (q.sem(n) for n in ("oT_ready", "centered", "cT_ready", "x_added"))
            u_ready, rs_ready = q.sem("var_ready"), q.sem("rstd_ready")

            def heads(i, targets):
                main = i is not None
                steps = (0, HB * NH + LAG) if main else (-NH, 0)
                N2 = HB * NH if main else 0
                at = lambda u, size, off=0, n=None: (bass.ds(i * (UNROLL * size) + (u * size + off), n or size) if main
                                                     else slice(off, off + (n or size)))
                START = {g: (g // NCH) * NH + HEAD2.index((g % NCH, 0, 0)) for g in range(-NCH, (HB + 1) * NCH)}
                ENDS = {START[g + 1] - 1: g for g in range(HB * NCH)} if main else {}
                cast_at = lambda g: max(steps[0], START[g] - (5 if g % NCH == 0 else 6))
                items, pairs = [], []
                for L in targets:
                    s0 = (L - 1) * NH
                    new_k = L % R == 0
                    todo = [(kind, c) for c in range(NCH) for kind in ("kq" if new_k else "q")]
                    for d, (kind, c) in enumerate(todo):
                        step = s0 + d * 12 // len(todo)
                        pairs.append((step, kind, L, c))
                        items += [(step, kind, L, c, 0), (step, kind, L, c, 1)]
                    if new_k:
                        items += [(s0 + 15 + 4 * c, "v", L, c, 0) for c in range(NCH)]
                    ready = {p[3]: p[0] + 4 for p in pairs if p[1:3] == ("q", L)}
                    items += [(max(s0 + 4 + k * (NH - 16) // N1, ready[PASS1[k][0] // TPC]), "max", L, k, 0) for k in range(N1)]
                    items += [(s0 + NH - 8, "row", L, c, 0) for c in range(NCH)]
                    items += [(cast_at(L * NCH), "bcast", L, 0, 0)]
                    if L < HB and main:
                        items += [(cast_at(L * NCH + c), "bcast", L, c, 0) for c in range(1, NCH)]
                if main:
                    items += [(cast_at(c), "bcast", 0, c, 0) for c in range(1, NCH)]
                items += [(e + 5, "fin", g // NCH, g, 0) for e, g in ENDS.items()]
                items.sort(key=lambda item: item[0])
                AT = {}
                for r, item in enumerate(items):
                    AT.setdefault(item[0], []).append(r)
                PAIR = {p[1:]: j for j, p in enumerate(pairs)}
                ROUNDS = [0]
                for p in pairs:
                    ROUNDS.append(ROUNDS[-1] + (2 if p[1] == "k" else 1))
                FINS = {it[3]: r for r, it in enumerate(items) if it[1] == "fin"}
                new_ks = [L for L in targets if L % R == 0]
                chunks = [it[2] * NCH + it[3] for it in items if it[1] == "bcast"]
                diagonals = [r for r, it in enumerate(items) if it[1] == "max" and PASS1[it[3]][3]]

                def pass2(n):
                    qc, kb, q0 = HEAD2[n % NH]
                    return n // NH, n // NH * NCH + qc, qc, kb, q0, kb >= TPC * qc

                def due(n, lag):
                    return ENDS.get(n - lag)

                def exps(g):
                    return sum(NEXP(gg) for gg in chunks[:chunks.index(g)])

                with nc.Block() as block:
                    @block.sync
                    def _(sp):
                        for n, L in enumerate(new_ks):
                            if n:
                                sp.wait_ge(kd_out, n * NCH)
                            sp.dma_start(decay[:, :], f_dram[at(L // R, 1), :].partition_broadcast(P)).then_inc(decay_in, 16)
                            sp.wait_ge(decay_in, 16 * (n + 1))

                    @block.gpsimd
                    def _(pool):
                        def head_weights(L):
                            u, used = L // R, [r for r, it in enumerate(items) if it[1] in "kq" and it[2] < L]
                            if used:
                                pool.wait_ge(filled, used[-1] + 1)
                            twice = lambda w, cols: w[:, cols].unsqueeze(1).to_broadcast([P, 2, DH])
                            nc.gpsimd.tensor_copy(wk_h[:, :, :], twice(wk, at(u, DH))).then_inc(w_ready, 1)
                            nc.gpsimd.tensor_copy(wks_h[:, :, :], twice(wks, at(u, DH))).then_inc(w_ready, 1)
                            for hh in range(R):
                                nc.gpsimd.tensor_copy(wq_h[hh][:, :, :], twice(wq, at(u, P, hh * DH, DH))).then_inc(w_ready, 1)
                                nc.gpsimd.tensor_copy(wqs_h[hh][:, :, :], twice(wqs, at(u, P, hh * DH, DH))).then_inc(w_ready, 1)

                        def rotate(j):
                            _, kind, L, c = pairs[j]
                            cs = slice(c * CH, (c + 1) * CH)
                            pool.wait_ge(t_done, 2 * j + 2)
                            if j >= 2:
                                pool.wait_ge(split, j - 1)
                            nc.gpsimd.tensor_tensor(rot[:, j % 2, :], t1[:, j % 2, :], t2[:, j % 2, :], ALU.add).then_inc(rotated, 1)
                            if kind == "k":
                                pool.wait_ge(rotated, j + 1)
                                pool.wait_ge(decay_in, 16 * (new_ks.index(L) + 1))
                                nc.gpsimd.tensor_tensor(kd[:, c % 2, :], rot[:, j % 2, :], decay[:, cs], ALU.mult).then_inc(kd_out, 1)

                        def low_half(j):
                            _, kind, L, c = pairs[j]
                            cs = slice(c * CH, (c + 1) * CH)
                            pool.wait_ge(rounded, ROUNDS[j + 1])
                            if kind == "k":
                                later_k = pairs[j + 1][1] == "k"
                                pool.wait_ge(rotated, j + 2)
                                pool.wait_ge(kd_out, new_ks.index(L) * NCH + c + (2 if later_k else 1))
                                out, whole, hi = k_hl[DH:P, L // R % 2, cs], kd[DH:P, c % 2, :], k_hi[DH:P, c % 2, :]
                            else:
                                out, whole, hi = q_lo[:, L % R, cs], rot[:, j % 2, :], q_hi[:, L % R, cs]
                            nc.gpsimd.tensor_tensor(out, whole, hi.bitcast(F32), ALU.subtract).then_inc(split, 1)
                            if kind == "k":
                                pool.wait_ge(split, j + 1)

                        def mask_factors(g):
                            for j in range(TPC):
                                pool.wait_ge(f_done, exps(g) + (1 if g % NCH else 0) + j + 1)
                                part = fac[:, g % 2, FOFF[1 + j]:FOFF[1 + j] + P]
                                nc.gpsimd.affine_select(out=part, in_=part, compare_op=ALU.is_ge, fill=0.0, base=0,
                                                        pattern=[[1, P]], channel_multiplier=-1).then_inc(f_masked, 1)

                        def root(g):
                            pool.wait_ge(u_ready, g + 1)
                            st = Steps(pool, newton, g * 12)
                            for _ in range(3):
                                st.run(nc.gpsimd.tensor_tensor(yy[:, :], rs[:, :], rs[:, :], ALU.mult))
                                st.run(nc.gpsimd.tensor_tensor(yy[:, :], yy[:, :], uu[:, :], ALU.mult))
                                st.run(nc.gpsimd.tensor_scalar(yy[:, :], yy[:, :], -0.5, 1.5, ALU.mult, ALU.add))
                                st.run(nc.gpsimd.tensor_tensor(rs[:, :], rs[:, :], yy[:, :], ALU.mult))
                            pool.sem_inc(rs_ready, 1)

                        todo = [((L - 1) * NH - 2, 0, head_weights, L) for L in new_ks]
                        todo += [(p[0], 1, rotate, j) for j, p in enumerate(pairs)]
                        todo += [(p[0] + 1, 2, low_half, j) for j, p in enumerate(pairs)]
                        todo += [(cast_at(g), 3, mask_factors, g) for g in chunks]
                        todo += [(e + 5.5, 4, root, g) for e, g in ENDS.items()]
                        for _, _, task, arg in sorted(todo, key=lambda t: t[:2]):
                            task(arg)

                    @block.tensor
                    def _(pe):
                        def fill(r):
                            _, kind, L, k, twin = items[r]
                            hh, u = L % R, L // R
                            out = ring[:, r % NR, :]
                            if r >= NR:
                                pe.wait_ge(slot_free[r % NR], r // NR)
                            if kind in "kq":
                                if kind == "k" and k == 0:
                                    pe.wait_ge(w_ready, (2 + 2 * R) * (new_ks.index(L) + 1))
                                w = ((wk_h, wks_h) if kind == "k" else (wq_h[hh], wqs_h[hh]))[twin]
                                last = nc.tensor.matmul(out, w[:, :, :].rearrange("p r d -> p (r d)"), core.xT[:, k * CH:(k + 1) * CH],
                                                        start=True, stop=True)
                            elif kind == "v":
                                for j in range(TPC):
                                    t = k * TPC + j
                                    last = nc.tensor.matmul(out[:, j * DH:(j + 1) * DH], core.xT[:, t * P:(t + 1) * P], wv[:, at(u, DH)],
                                                            start=True, stop=True)
                            elif kind == "max":
                                qt, kc, w_, _ = PASS1[k]
                                pe.wait_ge(split, PAIR["q", L, qt // TPC] + 1)
                                keys = k_hl[:, u % 2, kc * CH:kc * CH + w_]
                                last = nc.tensor.matmul(out[:, 0:w_], q_hi[:, hh, qt * P:(qt + 1) * P], keys, start=True, stop=True)
                            elif kind == "row":
                                pe.wait_ge(split_ready, targets.index(L) + 1)
                                for j in range(TPC):
                                    last = nc.tensor.matmul(out[0:3, j * P:(j + 1) * P], m_split[:, k * TPC + j, :], core.ident_b[:, :],
                                                            start=True, stop=True)
                            elif kind == "fin":
                                last = final(k, out)
                            else:
                                rows = [rr for rr in range(r) if items[rr][1] == "row" and items[rr][2] == L]
                                for rr in rows[-NR:]:
                                    pe.wait_ge(slot_free[rr % NR], rr // NR + 1)
                                last = nc.tensor.matmul(out, core.ones_b[:, :], m_row[:, hh, k * CH:(k + 1) * CH], start=True, stop=True)
                            last.then_inc(filled, 1)

                        def scores(n):
                            L, g, qc, kb, q0, _ = pass2(n)
                            if n >= NS:
                                pe.wait_ge(abs_done, n - NS + 1)
                            q1, w_ = qc * CH + q0, CH - q0
                            keys = k_hl[:, L // R % 2, kb * P:(kb + 1) * P]
                            nc.tensor.matmul(psS[:, n % NS, 0:w_], keys, q_hi[:, L % R, q1:q1 + w_], start=True, stop=False)
                            nc.tensor.matmul(psS[:, n % NS, 0:w_], keys, q_lo[:, L % R, q1:q1 + w_], start=False, stop=True).then_inc(sc2, 1)

                        def values(n):
                            L, g, qc, kb, q0, _ = pass2(n)
                            if kb == 0 and g >= 2:
                                pe.wait_ge(oT_ready, g - 1)
                            pe.wait_ge(a_done, n + 1)
                            nc.tensor.matmul(psO[0:M, g % 2, q0:CH], va[:, L // R % 2, kb, :], probs[:, n % NPB, 0:CH - q0],
                                             start=kb == 0, stop=kb == TPC * (qc + 1) - 1).then_inc(pv, 1)

                        def center_values(g):
                            pe.wait_ge(oT_ready, g + 1)
                            pe.wait_ge(added, g)
                            nc.tensor.matmul(psC[0:M, :, :].rearrange("p t d -> p (t d)"), center[:, :], oT[:, :], start=True, stop=True).then_inc(centered, 1)

                        def final(g, columns):
                            pe.wait_ge(cT_ready, 2 * g + 2)
                            L = g // NCH
                            for j in range(TPC):
                                js = slice(j * P, (j + 1) * P)
                                nc.tensor.matmul(psC[:, j, :], cT[:, js], wp[:, at(L // R, R, L % R, 1), :], start=True, stop=True)
                                last = nc.tensor.matmul(columns[:, j:j + 1], sq[:, js], mean_col[:, :], start=True, stop=True)
                            return last

                        if main:
                            for n in range(NS):
                                scores(n)
                        for n in range(*steps):
                            if main and n + NS < N2:
                                scores(n + NS)
                            fills = AT.get(n, [])
                            for r in fills[:len(fills) // 2]:
                                fill(r)
                            if main and n < N2:
                                values(n)
                            for r in fills[len(fills) // 2:]:
                                fill(r)
                            if (g := due(n, 3)) is not None:
                                center_values(g)

                    @block.scalar
                    def _(act):
                        def key_factors(L):
                            kp = L // R % 2
                            act.wait_ge(cols_in, new_ks.index(L) + 1)
                            for qc in range(1, NCH):
                                nc.scalar.activation(c_col[:, kp, qc - 1, 0:qc * TPC], ge[:, kp, 0:qc * TPC], ACT.Exp, scale=-1.0,
                                                     bias=ge[:, kp, qc * TPC - 1:qc * TPC]).then_inc(c_exp, 1)

                        def high_half(j):
                            _, kind, L, c = pairs[j]
                            cs = slice(c * CH, (c + 1) * CH)
                            if kind == "k":
                                n = new_ks.index(L) * NCH + c
                                act.wait_ge(kd_out, n + 1)
                                if c >= 2:
                                    act.wait_ge(split, j - 1)
                                nc.scalar.activation(k_hi[:, c % 2, :], kd[:, c % 2, :], ACT.Copy).then_inc(rounded, 1)
                                nc.scalar.activation(k_hl[0:DH, L // R % 2, cs], kd[0:DH, c % 2, :], ACT.Copy).then_inc(rounded, 1)
                            else:
                                act.wait_ge(rotated, j + 1)
                                nc.scalar.activation(q_hi[:, L % R, cs], rot[:, j % 2, :], ACT.Copy).then_inc(rounded, 1)

                        def take_values(r):
                            _, _, L, c, _ = items[r]
                            act.wait_ge(filled, r + 1)
                            src = ring[:, r % NR, 0:TPC * DH].rearrange("p (t d) -> p t d", d=DH)
                            nc.scalar.activation(va[:, L // R % 2, c * TPC:(c + 1) * TPC, 0:DH], src, ACT.Copy).then_inc(slot_free[r % NR], 1)

                        def logarithms(L):
                            n = targets.index(L)
                            act.wait_ge(ln_in, 2 * n + 1)
                            nc.scalar.activation(l1[:, :, :], l1[:, :, :], ACT.Ln).then_inc(ln_out, 1)
                            act.wait_ge(ln_in, 2 * n + 2)
                            nc.scalar.activation(l2[:, :, :], l2[:, :, :], ACT.Ln).then_inc(ln_out, 1)

                        def factors(r):
                            _, _, L, qc, _ = items[r]
                            g, kp = L * NCH + qc, L // R % 2
                            act.wait_ge(filled, r + 1)
                            if main and g >= 2:
                                act.wait_ge(b_done, START[g - 1])
                                act.wait_ge(f_masked, TPC * chunks.index(g))
                            if qc:
                                nc.scalar.activation(fac[:, g % 2, 0:CH], ring[:, r % NR, :], ACT.Exp,
                                                     bias=nge[:, kp, qc * TPC - 1:qc * TPC]).then_inc(f_done, 1)
                            for j in range(TPC):
                                nc.scalar.activation(fac[:, g % 2, FOFF[1 + j]:FOFF[1 + j] + CH - j * P], ring[:, r % NR, j * P:CH], ACT.Exp,
                                                     bias=nge[:, kp, qc * TPC + j:qc * TPC + j + 1]).then_inc(f_done, 1)
                            act.wait_ge(f_done, exps(g) + NEXP(g))
                            act.sem_inc(slot_free[r % NR], 1)

                        def absolute(n):
                            L, g, qc, kb, q0, own = pass2(n)
                            w_, kp = CH - q0, L // R % 2
                            act.wait_ge(sc2, n + 1)
                            if L in new_ks and L < HB:
                                act.wait_ge(cols_ready, new_ks.index(L) + 1)
                            nc.scalar.activation(sabs[:, n % NPB, 0:w_], psS[:, n % NS, 0:w_], ACT.Abs,
                                                 scale=SC if own else c_col[:, kp, qc - 1, kb:kb + 1]).then_inc(abs_done, 1)

                        def square(n):
                            q0 = pass2(n)[4]
                            act.wait_ge(b_done, n + 1)
                            if n >= NPB:
                                act.wait_ge(pv, n - NPB + 1)
                            nc.scalar.activation(probs[:, n % NPB, 0:CH - q0], sabs[:, n % NPB, 0:CH - q0], ACT.Square).then_inc(a_done, 1)

                        if main:
                            for n in range(NS):
                                absolute(n)
                            square(0)
                        for n in range(*steps):
                            if main and n + 1 < N2:
                                square(n + 1)
                            if main and n + NS < N2:
                                absolute(n + NS)
                            for L in new_ks:
                                if n == (L - 1) * NH + 1:
                                    key_factors(L)
                            for j, p in enumerate(pairs):
                                if p[0] + 1 == n:
                                    high_half(j)
                            for L in targets:
                                if n == L * NH - 10:
                                    logarithms(L)
                            for r in AT.get(n, ()):
                                if items[r][1] == "v":
                                    take_values(r)
                                if items[r][1] == "bcast":
                                    factors(r)
                            if (g := due(n, 1)) is not None:
                                act.wait_ge(pv, n)
                                act.wait_ge(centered, g)
                                nc.scalar.activation(oT[:, :], psO[0:M, g % 2, :], ACT.Copy).then_inc(oT_ready, 1)
                            if (g := due(n, 4)) is not None:
                                act.wait_ge(centered, g + 1)
                                if g:
                                    act.wait_ge(filled, FINS[g - 1] + 1)
                                centred = psC[0:M, :, :].rearrange("p t d -> p (t d)")
                                nc.scalar.activation(cT[:, :], centred, ACT.Copy).then_inc(cT_ready, 1)
                                nc.scalar.activation(sq[:, :], centred, ACT.Square, bias=den_bias[:, :]).then_inc(cT_ready, 1)

                    @block.vector
                    def _(dve):
                        st = Steps(dve, dve_step)

                        def key_columns(L):
                            kp, col = L // R % 2, at(L // R, 1)
                            st.run(nc.vector.tensor_copy(ge[:, kp, :], gend[:, :, col].rearrange("p t h -> p (t h)")))
                            dve.sem_inc(cols_in, 1)
                            st.add(nc.vector.tensor_scalar(nge[:, kp, :], ge[:, kp, :], -1.0, None, ALU.mult))
                            st.run(nc.vector.tensor_copy(eps_d[:, kp, :], eps_col[:, :, col].rearrange("p t h -> p (t h)")))

                        def key_factor_columns(L):
                            kp = L // R % 2
                            dve.wait_ge(c_exp, (NCH - 1) * (new_ks.index(L) + 1))
                            for qc in range(1, NCH):
                                part = c_col[:, kp, qc - 1, 0:qc * TPC]
                                st.run(nc.vector.tensor_tensor(c_eps[:, kp, qc - 1, 0:qc * TPC], part, eps_d[:, kp, 0:qc * TPC], ALU.mult))
                                st.run(nc.vector.tensor_scalar(part, part, SC, None, ALU.mult))
                            dve.sem_inc(cols_ready, 1)

                        def rope_product(r):
                            _, kind, L, c, twin = items[r]
                            j = PAIR[kind, L, c]
                            if j >= 2:
                                dve.wait_ge(rotated, j - 1)
                            dve.wait_ge(filled, r + 1)
                            cs = slice(c * CH, (c + 1) * CH)
                            nc.vector.tensor_tensor((t1, t2)[twin][:, j % 2, :], ring[:, r % NR, :], (cos, sin)[twin][:, cs],
                                                    ALU.mult).then_inc(slot_free[r % NR], 1)
                            if twin:
                                for rr in (r - 1, r):
                                    dve.wait_ge(slot_free[rr % NR], rr // NR + 1)
                                dve.sem_inc(t_done, 2)

                        def take_max(r):
                            _, _, L, k, _ = items[r]
                            qt, kc, w_, diag = PASS1[k]
                            nb = w_ // P - (1 if diag else 0)
                            dve.wait_ge(filled, r + 1)
                            if diag:
                                nc.vector.tensor_tensor(scrap[:, :], ring[:, r % NR, w_ - P:w_], tri[:, :], ALU.mult).then_inc(max_done, 1)
                            if nb:
                                last = nc.vector.tensor_reduce(m_abs[:, qt, kc * TPC:kc * TPC + nb],
                                                               ring[:, r % NR, 0:nb * P].rearrange("p (b k) -> p b k", k=P),
                                                               axis=AX.X, op=ALU.max, apply_absolute_value=True)
                            if diag:
                                dve.wait_ge(max_done, diagonals.index(r) + 1)
                                last = nc.vector.tensor_reduce(m_abs[:, qt, qt:qt + 1], scrap[:, :], axis=AX.X, op=ALU.max, apply_absolute_value=True)
                            last.then_inc(slot_free[r % NR], 1)
                            if diag or k >= N1 - NR:
                                dve.wait_ge(slot_free[r % NR], r // NR + 1)

                        def take_row(r):
                            _, _, L, c, _ = items[r]
                            dve.wait_ge(filled, r + 1)
                            nc.vector.tensor_copy(m_row[0:3, L % R, c * CH:(c + 1) * CH], ring[0:3, r % NR, :]).then_inc(slot_free[r % NR], 1)

                        def logs_in(L):
                            n = targets.index(L)
                            st.run(nc.vector.tensor_scalar(l2[:, :, :], m_abs[:, :, :], SC, 1e-30, ALU.mult, ALU.add))
                            nc.vector.tensor_scalar(l1[:, :, :], l2[:, :, :], TINY, None, ALU.max).then_inc(ln_in, 1)
                            dve.wait_ge(ln_in, 2 * n + 1)
                            nc.vector.tensor_scalar(l2[:, :, :], l2[:, :, :], TINY, 1.0 / TINY, ALU.min, ALU.mult).then_inc(ln_in, 1)

                        def maxima(L):
                            n, kp = targets.index(L), L // R % 2
                            dve.wait_ge(ln_out, 2 * n + 2)
                            st.run(nc.vector.tensor_tensor(l1[:, :, :], l1[:, :, :], l2[:, :, :], ALU.add))
                            st.run(nc.vector.tensor_tensor(l1[:, :, :], l1[:, :, :], ge[:, kp, :].unsqueeze(1).to_broadcast([P, NT, NT]), ALU.subtract))
                            st.run(nc.vector.tensor_tensor(l1[:, :, :], l1[:, :, :], later[:, :, :], ALU.add))
                            st.run(nc.vector.tensor_reduce(m_neg[:, :], l1[:, :, :], axis=AX.X, op=ALU.max, negate=True))
                            st.run(nc.vector.tensor_copy(m_split[:, :, 0], m_neg[:, :]))
                            st.run(nc.vector.tensor_tensor(m_rest[:, :], m_neg[:, :], m_split[:, :, 0], ALU.subtract))
                            st.run(nc.vector.tensor_copy(m_split[:, :, 1], m_rest[:, :]))
                            st.run(nc.vector.tensor_tensor(m_neg[:, :], m_rest[:, :], m_split[:, :, 1], ALU.subtract))
                            st.run(nc.vector.tensor_copy(m_split[:, :, 2], m_neg[:, :]))
                            dve.sem_inc(split_ready, 1)

                        def product(n):
                            L, g, qc, kb, q0, own = pass2(n)
                            w_, kp = CH - q0, L // R % 2
                            if own:
                                j = kb - TPC * qc
                                f, eps = fac[:, g % 2, FOFF[1 + j]:FOFF[1 + j] + w_], eps_d[:, kp, kb:kb + 1]
                                if g in chunks:
                                    dve.wait_ge(f_masked, TPC * chunks.index(g) + j + 1)
                            else:
                                f, eps = fac[:, g % 2, 0:CH], c_eps[:, kp, qc - 1, kb:kb + 1]
                                if g in chunks:
                                    dve.wait_ge(f_done, exps(g) + 1)
                            dve.wait_ge(abs_done, n + 1)
                            nc.vector.scalar_tensor_tensor(out=sabs[:, n % NPB, 0:w_], in0=sabs[:, n % NPB, 0:w_], scalar=eps,
                                                           in1=f, op0=ALU.add, op1=ALU.mult).then_inc(b_done, 1)

                        def variance(r):
                            dve.wait_ge(filled, r + 1)
                            nc.vector.tensor_copy(uu[:, :], ring[:, r % NR, 0:TPC]).then_inc(slot_free[r % NR], 1)
                            dve.wait_ge(slot_free[r % NR], r // NR + 1)
                            nc.vector.tensor_scalar(rs[:, :].bitcast(I32), uu[:, :].bitcast(I32), -0.5, float(0x5F3759DF),
                                                    ALU.mult, ALU.add).then_inc(u_ready, 1)

                        def add_to_x(g):
                            dve.wait_ge(rs_ready, g + 1)
                            for j in range(TPC):
                                t = (g % NCH) * TPC + j
                                last = nc.vector.scalar_tensor_tensor(out=core.x[:, t, :], in0=psC[:, j, :], scalar=rs[:, j:j + 1],
                                                                      in1=core.x[:, t, :], op0=ALU.mult, op1=ALU.add)
                            last.then_inc(added, 1)
                            dve.wait_ge(added, g + 1)

                        if main:
                            product(0)
                            product(1)
                        for n in range(*steps):
                            if main and n + 2 < N2:
                                product(n + 2)
                            for L in new_ks:
                                if n == (L - 1) * NH:
                                    key_columns(L)
                                if n == (L - 1) * NH + 2:
                                    key_factor_columns(L)
                            for r in AT.get(n, ()):
                                kind, L, k = items[r][1:4]
                                if kind in ("k", "q"):
                                    rope_product(r)
                                if kind == "max":
                                    take_max(r)
                                if kind == "fin":
                                    variance(r)
                                if kind == "row":
                                    if k == 0:
                                        maxima(L)
                                    take_row(r)
                            for L in targets:
                                if n == L * NH - 11:
                                    logs_in(L)
                            if (g := due(n, 7)) is not None:
                                add_to_x(g)

            with nc.Block() as block:
                @block.gpsimd
                def _(pool):
                    for n, (buf, val) in enumerate(((m_row[:, :, :], 0.0), (m_abs[:, :, :], 0.0), (va[:, :, :, DH:M], 1.0))):
                        nc.gpsimd.memset(buf, val).then_inc(zeroed, 1)
                        pool.wait_ge(zeroed, n + 1)
            heads(None, [0])
            with nc.Fori(0, HK // UNROLL) as i:
                q.restart()
                heads(i, list(range(1, HB + 1)))


def hybrid_kernel(nc, a, out):
    with ExitStack() as ctx:
        core = Core(nc, ctx)
        stage_constants(nc, core, a["x"])
        with nc.sbuf_tensor("x_norm", [P, NT, D], F32) as xn:
            stage_norm(nc, core, "n0", xn)
            stage_mamba(nc, core, "mamba", xn, a)

        def gelu_ffn(tag):
            stage_norm(nc, core, tag + "_n")
            with nc.sbuf_tensor(tag + "_comb", [P, NT, 16], F32) as comb:
                stage_route(nc, core, tag + "_r", 16, a["Wr"], a["br"], comb)
                stage_gelu_experts(nc, core, tag, comb, a["W1"], a["b1"], a["g1T"], a["be1T"], a["W2"], a["b2"])

        def silu_ffn(tag):
            stage_norm(nc, core, tag + "_n")
            with nc.sbuf_tensor(tag + "_comb", [P, NT, 8], F32) as comb:
                stage_route(nc, core, tag + "_r", 8, a["gate_wT"], None, comb, capacity=int(1.25 * T / 8))
                stage_silu_experts(nc, core, tag, comb, a["gate_projT"], a["up_projT"], a["down_projT"])

        gelu_ffn("ffn0")
        stage_norm(nc, core, "n2")
        stage_span_attention(nc, core, "span", a["Wq"], a["Wk"], a["Wv"], a["Wo"], a["span_val"])
        gelu_ffn("ffn1")
        stage_norm(nc, core, "n4")
        stage_rope_attention(nc, core, "rope", a["W_qkvT"], a["W_qk_swapT"], a["W_outT"], a["cos8"], a["sin8"])
        silu_ffn("moe0")
        stage_norm(nc, core, "n6")
        stage_power_attention(nc, core, "power", a["pq"], a["pq_swap"], a["pk"], a["pk_swap"], a["pv"], a["pg"], a["w_proj"], a["ln_w"],
                              a["cos64"], a["sin64"])
        silu_ffn("moe1")
        stage_store(nc, core, out)


def _rotary_tables(np, angles, heads):
    cos, sin = np.cos(angles).astype(np.float32), np.sin(angles).astype(np.float32)
    pairs, t = angles.shape
    cos = np.tile(np.repeat(cos, 2, axis=0), (heads, 1))
    sin = np.tile(np.stack([-sin, sin], axis=1).reshape(2 * pairs, t), (heads, 1))
    return cos, sin


def kernel(**inputs):
    import numpy as np
    import concourse.bacc as bacc
    from concourse.bass_utils import run_bass_kernel_spmd

    w = {k: np.asarray(v) for k, v in inputs.items()}
    m = lambda name: w["L0_attn_a_" + name]
    halves = lambda v: v.reshape(-1, 128).T
    swapped = lambda v: v.reshape(v.shape[0], -1, 2)[:, :, ::-1].reshape(v.shape)
    times = np.arange(2048, dtype=np.float32)
    f8 = (1.0 / np.float32(10000.0) ** (np.arange(0, 8, 2, dtype=np.float32) / np.float32(8))).astype(np.float32)
    f64 = (2.0 * np.pi / float(2048) ** (np.arange(0, 64, 2, dtype=np.float32) / np.float32(64))).astype(np.float32)
    cos8, sin8 = _rotary_tables(np, np.outer(f8, times).astype(np.float32), 16)
    cos64, sin64 = _rotary_tables(np, np.outer(f64, times).astype(np.float32), 2)
    qkv, pa = w["L1_attn_a_W_qkv"], w["L1_attn_b_w_attn"]
    arrays = {
        "x": m("x"), "W_in": m("W_in"), "b_in": halves(m("b_in")), "conv_w": m("conv_w").reshape(2, 128, 4).transpose(1, 0, 2),
        "conv_b": halves(m("conv_b")), "W_xp": m("W_xp"), "b_xp": m("b_xp").reshape(32, 1), "W_dt": m("W_dt"), "b_dt": halves(m("b_dt")),
        "A_log": m("A_log"), "D_skip": halves(m("D_skip")), "W_out": m("W_out"), "b_out": m("b_out"), "alpha": m("alpha"), "beta": m("beta"),
        "Wq": w["L0_attn_b_Wq"], "Wk": w["L0_attn_b_Wk"], "Wv": w["L0_attn_b_Wv"], "Wo": w["L0_attn_b_Wo"], "span_val": w["L0_attn_b_span_val"],
        "Wr": w["L0_ffn_Wr"], "br": w["L0_ffn_br"], "W1": w["L0_ffn_W1"], "b1": w["L0_ffn_b1"], "g1T": w["L0_ffn_g1"].T, "be1T": w["L0_ffn_be1"].T,
        "W2": w["L0_ffn_W2"], "b2": w["L0_ffn_b2"],
        "W_qkvT": qkv.T, "W_qk_swapT": swapped(qkv[:256].T), "W_outT": w["L1_attn_a_W_out"].T, "cos8": cos8, "sin8": sin8,
        "pq": pa[:, :1024], "pq_swap": swapped(pa[:, :1024]), "pk": pa[:, 1024:1536], "pk_swap": swapped(pa[:, 1024:1536]),
        "pv": pa[:, 1536:2048], "pg": pa[:, 2048:], "w_proj": w["L1_attn_b_w_proj"], "ln_w": w["L1_attn_b_ln_w"].reshape(64, 1),
        "cos64": cos64, "sin64": sin64,
        "gate_wT": w["L1_ffn_gate_w"].T, "gate_projT": w["L1_ffn_gate_proj_w"].transpose(2, 0, 1),
        "up_projT": w["L1_ffn_up_proj_w"].transpose(2, 0, 1), "down_projT": w["L1_ffn_down_proj_w"].transpose(2, 0, 1),
    }
    arrays = {f"in_{k}": np.ascontiguousarray(v) for k, v in arrays.items()}
    nc = bacc.Bacc("TRN2", target_bir_lowering=False, num_devices=1)
    dram = {k[3:]: nc.dram_tensor(k, v.shape, mybir.dt.from_np(v.dtype), kind="ExternalInput").ap() for k, v in arrays.items()}
    out = nc.dram_tensor("out", (1, 2048, 128), F32, kind="ExternalOutput").ap()
    hybrid_kernel(nc, dram, out)
    return run_bass_kernel_spmd(nc, [arrays], core_ids=[0]).results[0]["out"]
```

```python
import concourse.bass as bass
from concourse import mybir
from concourse.alu_op_type import AluOpType as ALU
from contextlib import ExitStack

F32 = mybir.dt.float32
BF16 = mybir.dt.bfloat16
I32 = mybir.dt.int32
U32 = mybir.dt.uint32
ACT = mybir.ActivationFunctionType
AX = mybir.AxisListType

P = 128
T = 2048
D = 128
NT = T // P
CH = 512
NCH = T // CH
TPC = CH // P
MASKED = -1.0e30


class Steps:

    def __init__(self, eng, sem, base=0):
        self.eng, self.sem, self.base, self.n = eng, sem, base, 0

    def add(self, ins):
        ins.then_inc(self.sem, 1)
        self.n += 1
        return self.n

    def wait(self, n=None):
        self.eng.wait_ge(self.sem, self.base + (self.n if n is None else n))

    def run(self, ins):
        self.add(ins)
        self.wait()


class Core:

    def __init__(self, nc, ctx):
        self.nc = nc
        sb = lambda name, shape, dt: ctx.enter_context(nc.sbuf_tensor(name, shape, dt))
        self.x = sb("x_residual", [P, NT, D], F32)
        self.xT = sb("x_norm_T", [P, T], F32)
        self.ident = sb("ident", [P, P], F32)
        self.ident_b = sb("ident_b", [P, P], BF16)
        self.hide = sb("hide_qk", [P, P], BF16)
        self.hideT = sb("hide_kq", [P, P], BF16)
        self.ones_b = sb("ones_b", [P, P], BF16)


class Stage:

    def __init__(self, nc, tag):
        self.nc, self.tag, self.ctx, self.sems = nc, tag, ExitStack(), []

    def sb(self, name, shape, dt=F32):
        return self.ctx.enter_context(self.nc.sbuf_tensor(f"{self.tag}_{name}", shape, dt))

    def ps(self, name, shape, dt=F32):
        return self.ctx.enter_context(self.nc.psum_tensor(f"{self.tag}_{name}", shape, dt))

    def sem(self, name):
        self.sems.append(self.ctx.enter_context(self.nc.semaphore(f"{self.tag}_{name}")))
        return self.sems[-1]

    def restart(self):
        with self.nc.Block() as block:
            @block.gpsimd
            def _(pool):
                for sem in self.sems:
                    pool.sem_clear(sem)

    def __enter__(self):
        return self

    def __exit__(self, kind, *rest):
        if kind is None:
            self.restart()
        self.ctx.close()


def issue_loads(nc, loads, loaded):
    with nc.Block() as block:
        @block.sync
        def _(sp):
            for dst, src in loads:
                sp.dma_start(dst, src).then_inc(loaded, 16)


def stage_constants(nc, core, x_in):
    with Stage(nc, "setup") as s:
        x_loaded = s.sem("x_loaded")
        pool_step = s.sem("pool_step")
        with nc.Block() as block:
            @block.sync
            def _(sp):
                sp.dma_start(core.x[:, :, :], x_in.rearrange("b (t p) d -> p (b t) d", p=P)).then_inc(x_loaded, 16)
                sp.wait_ge(x_loaded, 16)

            @block.gpsimd
            def _(pool):
                st = Steps(pool, pool_step)
                for m, value in ((core.ident, 0.0), (core.ident_b, 0.0), (core.hide, 0.0), (core.hideT, 0.0), (core.ones_b, 1.0)):
                    st.add(nc.gpsimd.memset(m[:, :], value))
                st.wait()
                for m in (core.ident, core.ident_b):
                    st.add(nc.gpsimd.affine_select(out=m[:, :], in_=m[:, :], compare_op=ALU.not_equal, fill=1.0,
                                                   base=0, pattern=[[-1, P]], channel_multiplier=1))
                st.add(nc.gpsimd.affine_select(out=core.hide[:, :], in_=core.hide[:, :], compare_op=ALU.is_ge, fill=MASKED,
                                               base=0, pattern=[[-1, P]], channel_multiplier=1))
                st.add(nc.gpsimd.affine_select(out=core.hideT[:, :], in_=core.hideT[:, :], compare_op=ALU.is_ge, fill=MASKED,
                                               base=0, pattern=[[1, P]], channel_multiplier=-1))
                st.wait()


def stage_norm(nc, core, tag, xn=None):
    with Stage(nc, tag) as s:
        stats = s.sb("stats", [P, NT, 6])
        mean = s.sb("mean", [P, NT])
        var = s.sb("var", [P, NT])
        dif = s.sb("dif", [P, NT])
        rstd = s.sb("rstd", [P, NT])
        keep = xn if xn is not None else s.sb("xn", [P, NT, D])
        psT = s.ps("psT", [P, T])
        dve_step, var_ready, std_ready = s.sem("dve_step"), s.sem("var_ready"), s.sem("std_ready")
        norm_ready, transposed, xT_ready = s.sem("norm_ready"), s.sem("transposed"), s.sem("xT_ready")
        with nc.Block() as block:
            @block.vector
            def _(dve):
                st = Steps(dve, dve_step)
                for t in range(NT):
                    st.add(nc.vector.bn_stats(stats[:, t, :], core.x[:, t, :]))
                st.wait()
                st.add(nc.vector.tensor_tensor(mean[:, :], stats[:, :, 1], stats[:, :, 4], ALU.add))
                st.add(nc.vector.tensor_tensor(dif[:, :], stats[:, :, 1], stats[:, :, 4], ALU.subtract))
                st.run(nc.vector.tensor_tensor(var[:, :], stats[:, :, 2], stats[:, :, 5], ALU.add))
                st.add(nc.vector.tensor_scalar(mean[:, :], mean[:, :], 0.5, None, ALU.mult))
                st.add(nc.vector.tensor_scalar(var[:, :], var[:, :], 1.0 / D, 1e-5, ALU.mult, ALU.add))
                st.run(nc.vector.scalar_tensor_tensor(out=dif[:, :], in0=dif[:, :], scalar=0.25, in1=dif[:, :],
                                                      op0=ALU.mult, op1=ALU.mult))
                nc.vector.tensor_tensor(var[:, :], var[:, :], dif[:, :], ALU.add).then_inc(var_ready, 1)
                dve.wait_ge(std_ready, 1)
                st.run(nc.vector.reciprocal(rstd[:, :], var[:, :]))
                for t in range(NT):
                    nc.vector.tensor_scalar(keep[:, t, :], core.x[:, t, :], mean[:, t:t + 1], rstd[:, t:t + 1],
                                            ALU.subtract, ALU.mult).then_inc(norm_ready, 1)

            @block.tensor
            def _(pe):
                for t in range(NT):
                    pe.wait_ge(norm_ready, t + 1)
                    nc.tensor.transpose(psT[:, t * P:(t + 1) * P], keep[:, t, :], core.ident[:, :]).then_inc(transposed, 1)

            @block.scalar
            def _(act):
                act.wait_ge(var_ready, 1)
                nc.scalar.activation(var[:, :], var[:, :], ACT.Sqrt).then_inc(std_ready, 1)
                for c in range(NCH):
                    act.wait_ge(transposed, TPC * (c + 1))
                    nc.scalar.activation(core.xT[:, c * CH:(c + 1) * CH], psT[:, c * CH:(c + 1) * CH], ACT.Copy).then_inc(xT_ready, 1)
                act.wait_ge(xT_ready, NCH)


def stage_store(nc, core, out):
    with Stage(nc, "store") as s:
        stored = s.sem("stored")
        with nc.Block() as block:
            @block.sync
            def _(sp):
                sp.dma_start(out.rearrange("b (t p) d -> p (b t) d", p=P), core.x[:, :, :]).then_inc(stored, 16)
                sp.wait_ge(stored, 16)


def stage_mamba(nc, core, tag, xn, w, before):
    NS, NHALF, NCONV, DI = 16, 2, 4, 256
    NB = 2 * NS
    with Stage(nc, tag) as s:
        sz, xc, delta, dx = (s.sb(n, [P, NHALF, T]) for n in ("silu_z", "x_conv", "delta", "delta_x"))
        bc = s.sb("bc_parts", [P, T], BF16)
        sel = s.sb("select", [P, NB, P], BF16)
        A = s.sb("A", [P, NHALF, NS])
        d_skip = s.sb("d_skip", [P, NHALF])
        w_out = s.sb("w_out", [P, NHALF, D])
        h_last = s.sb("h_last", [P, NHALF, NS])
        loaded = s.sem("loaded")
        with Stage(nc, tag + "_in") as q:
            w_in, w_dt = q.sb("w_in", [P, 2 * DI]), q.sb("w_dt", [P, NHALF, DI])
            w_xp = q.sb("w_xp", [P, NHALF, 3, NB])
            b_in, conv_w, conv_b = q.sb("b_in", [P, 4]), q.sb("conv_w", [P, NHALF, NCONV]), q.sb("conv_b", [P, NHALF])
            b_dt, b_xp = q.sb("b_dt", [P, NHALF]), q.sb("b_xp", [3 * NB, 1])
            xin = q.sb("x_in", [P, NHALF, T + NCONV - 1])
            conv = q.sb("conv", [P, NHALF, T])
            bcf, bcr = q.sb("bc", [3 * NB, T]), q.sb("bc_rest", [3 * NB, T])
            pick = q.sb("pick", [P, NB])
            loads = [(w_in[:, :], w["W_in"]), (b_in[:, :], w["b_in"]), (conv_w[:, :, :], w["conv_w"]), (conv_b[:, :], w["conv_b"]),
                     (w_dt[:, :, :], w["W_dt"].rearrange("(k p) n -> p k n", p=P)), (b_dt[:, :], w["b_dt"]),
                     (A[:, :, :], w["A_log"].rearrange("(k p) n -> p k n", p=P)), (d_skip[:, :], w["D_skip"]),
                     (w_out[:, :, :], w["W_out"].rearrange("(k p) n -> p k n", p=P))]
            for part in range(3):
                loads.append((w_xp[:, :, part, :], w["W_xp"].rearrange("(k p) n -> p k n", p=P)))
                loads.append((b_xp[part * NB:(part + 1) * NB, :], w["b_xp"]))
            NLOAD = len(loads)
            issue_loads(nc, loads, loaded)
            before()
            ps = q.ps("ps", [P, 4, CH])
            dve_step, zeroed = q.sem("dve_step"), q.sem("zeroed")
            proj, ev_act, conv_done, xc_ready = q.sem("projected"), q.sem("in_evacuated"), q.sem("conv_done"), q.sem("xc_ready")
            bc_done, bc_out, dt_done = q.sem("bc_done"), q.sem("bc_out"), q.sem("dt_done")
            dt_rd, abs_done, exp_done, ln_done = q.sem("dt_read"), q.sem("abs_done"), q.sem("exp_done"), q.sem("ln_done")
            a_done = q.sem("a_done")
            with nc.Block() as block:
                @block.sync
                def _(sp):
                    sp.wait_ge(loaded, 16 * NLOAD)

                @block.gpsimd
                def _(pool):
                    nc.gpsimd.memset(xin[:, :, 0:NCONV - 1], 0.0).then_inc(zeroed, 1)
                    nc.gpsimd.memset(bc[:, :], 0.0).then_inc(zeroed, 1)
                    nc.gpsimd.memset(h_last[:, :, :], 0.0).then_inc(zeroed, 1)

                @block.tensor
                def _(pe):
                    pe.wait_ge(loaded, 16 * NLOAD)
                    for n in range(4 * NCH):
                        if n >= 4:
                            pe.wait_ge(ev_act, n - 3)
                        j, c = n // NCH, n % NCH
                        nc.tensor.matmul(ps[:, n % 4, :], w_in[:, j * P:(j + 1) * P], core.xT[:, c * CH:(c + 1) * CH],
                                         start=True, stop=True).then_inc(proj, 1)
                    pe.wait_ge(xc_ready, NHALF)
                    for c in range(NCH):
                        for k in range(NHALF):
                            last = nc.tensor.matmul(ps[0:3 * NB, c, :], w_xp[:, k, :, :].rearrange("p a b -> p (a b)"),
                                                    xc[:, k, c * CH:(c + 1) * CH], start=k == 0, stop=k == NHALF - 1)
                        last.then_inc(bc_done, 1)
                    for n in range(NHALF * NCH):
                        m, c = n // NCH, n % NCH
                        if n < 4:
                            pe.wait_ge(bc_out, n + 1)
                        else:
                            pe.wait_ge(dt_rd, n - 3)
                        for k in range(NHALF):
                            last = nc.tensor.matmul(ps[:, n % 4, :], w_dt[:, k, m * P:(m + 1) * P], xc[:, k, c * CH:(c + 1) * CH],
                                                    start=k == 0, stop=k == NHALF - 1)
                        last.then_inc(dt_done, 1)

                @block.scalar
                def _(act):
                    act.wait_ge(loaded, 16 * NLOAD)
                    for n in range(4 * NCH):
                        j, c = n // NCH, n % NCH
                        act.wait_ge(proj, n + 1)
                        if j < NHALF:
                            nc.scalar.activation(xin[:, j, NCONV - 1 + c * CH:NCONV - 1 + (c + 1) * CH], ps[:, n % 4, :], ACT.Identity,
                                                 bias=b_in[:, j:j + 1]).then_inc(ev_act, 1)
                        else:
                            nc.scalar.activation(sz[:, j - NHALF, c * CH:(c + 1) * CH], ps[:, n % 4, :], ACT.Silu,
                                                 bias=b_in[:, j:j + 1]).then_inc(ev_act, 1)
                    for k in range(NHALF):
                        act.wait_ge(conv_done, k + 1)
                        nc.scalar.activation(xc[:, k, :], conv[:, k, :], ACT.Silu).then_inc(xc_ready, 1)
                    for m in range(NHALF):
                        act.wait_ge(dt_rd, (m + 1) * NCH)
                        nc.scalar.activation(delta[:, m, :], conv[:, m, :], ACT.Abs).then_inc(abs_done, 1)
                    act.wait_ge(abs_done, NHALF)
                    nc.scalar.activation(A[:, :, :], A[:, :, :], ACT.Exp).then_inc(a_done, 1)
                    for m in range(NHALF):
                        nc.scalar.activation(delta[:, m, :], delta[:, m, :], ACT.Exp, scale=-1.0).then_inc(exp_done, 1)
                    act.wait_ge(exp_done, NHALF)
                    for m in range(NHALF):
                        nc.scalar.activation(xin[:, m, 0:T], delta[:, m, :], ACT.Ln, bias=1.0).then_inc(ln_done, 1)

                @block.vector
                def _(dve):
                    st = Steps(dve, dve_step)
                    dve.wait_ge(loaded, 16 * NLOAD)
                    dve.wait_ge(zeroed, 3)
                    st.run(nc.vector.tensor_tensor(pick[:, :], core.ident[:, 0:NB], core.ident[:, NB:2 * NB], ALU.add))
                    st.run(nc.vector.tensor_tensor(pick[:, :], pick[:, :], core.ident[:, 2 * NB:3 * NB], ALU.add))
                    st.add(nc.vector.tensor_copy(sel[:, :, :], pick[:, :].unsqueeze(2).to_broadcast([P, NB, P])))
                    for k in range(NHALF):
                        dve.wait_ge(ev_act, (k + 1) * NCH)
                        st.run(nc.vector.tensor_scalar(conv[:, k, :], xin[:, k, 0:T], conv_w[:, k, 0:1], conv_b[:, k:k + 1], ALU.mult, ALU.add))
                        for tap in range(1, NCONV):
                            last = nc.vector.scalar_tensor_tensor(out=conv[:, k, :], in0=xin[:, k, tap:tap + T], scalar=conv_w[:, k, tap:tap + 1],
                                                                  in1=conv[:, k, :], op0=ALU.mult, op1=ALU.add)
                            if tap < NCONV - 1:
                                st.run(last)
                        last.then_inc(conv_done, 1)
                    for c in range(NCH):
                        dve.wait_ge(bc_done, c + 1)
                        nc.vector.tensor_scalar(bcf[:, c * CH:(c + 1) * CH], ps[0:3 * NB, c, :], b_xp[:, 0:1], None, ALU.add).then_inc(bc_out, 1)
                    dve.wait_ge(bc_out, NCH)
                    st.run(nc.vector.tensor_copy(bc[0:3 * NB, :], bcf[:, :]))
                    st.run(nc.vector.tensor_tensor(bcr[:, :], bcf[:, :], bc[0:3 * NB, :], ALU.subtract))
                    for lo in (NB, 2 * NB):
                        st.run(nc.vector.tensor_copy(bc[lo:lo + NB, :], bcr[lo:lo + NB, :]))
                    st.run(nc.vector.tensor_tensor(bcr[2 * NB:3 * NB, :], bcr[2 * NB:3 * NB, :], bc[2 * NB:3 * NB, :], ALU.subtract))
                    st.add(nc.vector.tensor_copy(bc[2 * NB:3 * NB, :], bcr[2 * NB:3 * NB, :]))
                    dve.wait_ge(xc_ready, NHALF)
                    for n in range(NHALF * NCH):
                        m, c = n // NCH, n % NCH
                        dve.wait_ge(dt_done, n + 1)
                        nc.vector.tensor_scalar(conv[:, m, c * CH:(c + 1) * CH], ps[:, n % 4, :], b_dt[:, m:m + 1], None, ALU.add).then_inc(dt_rd, 1)
                    dve.wait_ge(dt_rd, NHALF * NCH)
                    dve.wait_ge(a_done, 1)
                    st.add(nc.vector.tensor_scalar(A[:, :, :], A[:, :, :], -1.0, None, ALU.mult))
                    for m in range(NHALF):
                        dve.wait_ge(exp_done, NHALF)
                        st.run(nc.vector.tensor_scalar(dx[:, m, :], delta[:, m, :], 1.0, -1.0, ALU.add, ALU.add))
                        st.run(nc.vector.tensor_tensor(dx[:, m, :], delta[:, m, :], dx[:, m, :], ALU.subtract))
                        st.run(nc.vector.scalar_tensor_tensor(out=conv[:, m, :], in0=conv[:, m, :], scalar=0.0, in1=dx[:, m, :],
                                                              op0=ALU.max, op1=ALU.add))
                        dve.wait_ge(ln_done, m + 1)
                        st.run(nc.vector.tensor_tensor(delta[:, m, :], xin[:, m, 0:T], conv[:, m, :], ALU.add))
                        st.run(nc.vector.tensor_tensor(dx[:, m, :], delta[:, m, :], xc[:, m, :], ALU.mult))

        NI = NS * NHALF
        NBUF, NCB, NHB = 5, 4, 3
        dA, dbx, hc = (s.sb(n, [P, NBUF, CH]) for n in ("dA", "dB_x", "h_C"))
        hs = s.sb("h", [P, NHB, CH])
        b_all = s.sb("b_spread", [P, NCB, CH])
        yz = s.sb("y_gated", [P, NHALF, T])
        with Stage(nc, tag + "_scan") as q:
            ps_b, ps_c, ps_y = q.ps("ps_b", [P, 2, CH]), q.ps("ps_c", [P, NCB, CH]), q.ps("ps_y", [P, NHALF, CH])
            spread, b_out, dA_done, dbx_done = q.sem("spread"), q.sem("b_evacuated"), q.sem("dA_done"), q.sem("dbx_done")
            scanned, kept, hc_done, summed = q.sem("scanned"), q.sem("h_kept"), q.sem("hC_done"), q.sem("summed")
            skip_done, gated = q.sem("skip_added"), q.sem("gated")
            with nc.Fori(0, NCH) as c:
                q.restart()
                cols = bass.ds(c * CH, CH)
                with nc.Block() as block:
                    @block.tensor
                    def _(pe):
                        def spread_bc(n):
                            if n >= 2:
                                pe.wait_ge(b_out, n - 1)
                            if n >= NCB:
                                pe.wait_ge(hc_done, NHALF * (n - NCB + 1))
                            nc.tensor.matmul(ps_b[:, n % 2, :], sel[:, n, :], bc[:, cols], start=True, stop=True)
                            nc.tensor.matmul(ps_c[:, n % NCB, :], sel[:, NS + n, :], bc[:, cols], start=True, stop=True).then_inc(spread, 1)

                        for n in range(NCB):
                            spread_bc(n)
                        for n in range(NI):
                            st_, k = n // NHALF, n % NHALF
                            pe.wait_ge(hc_done, n + 1)
                            nc.tensor.matmul(ps_y[:, k, :], core.ident[:, :], hc[:, n % NBUF, :], start=st_ == 0, stop=st_ == NS - 1).then_inc(summed, 1)
                            if k == NHALF - 1 and st_ + NCB < NS:
                                spread_bc(st_ + NCB)

                    @block.scalar
                    def _(act):
                        def take_b(m):
                            act.wait_ge(spread, m + 1)
                            if m >= NCB:
                                act.wait_ge(dbx_done, NHALF * (m - NCB + 1))
                            nc.scalar.activation(b_all[:, m % NCB, :], ps_b[:, m % 2, :], ACT.Copy).then_inc(b_out, 1)

                        take_b(0)
                        for n in range(NI):
                            st_, k = n // NHALF, n % NHALF
                            if k == 0 and st_ + 1 < NS:
                                take_b(st_ + 1)
                            if n >= NBUF:
                                act.wait_ge(scanned, n - NBUF + 1)
                            nc.scalar.activation(dA[:, n % NBUF, :], delta[:, k, cols], ACT.Exp, scale=A[:, k, st_:st_ + 1]).then_inc(dA_done, 1)

                    @block.gpsimd
                    def _(pool):
                        for n in range(NI):
                            st_, k = n // NHALF, n % NHALF
                            pool.wait_ge(b_out, st_ + 1)
                            if n >= NBUF:
                                pool.wait_ge(scanned, n - NBUF + 1)
                            if n >= 1:
                                pool.wait_ge(dbx_done, n)
                            nc.gpsimd.tensor_tensor(dbx[:, n % NBUF, :], dx[:, k, cols], b_all[:, st_ % NCB, :], ALU.mult).then_inc(dbx_done, 1)

                    @block.vector
                    def _(dve):
                        def scan(n):
                            st_, k = n // NHALF, n % NHALF
                            dve.wait_ge(dA_done, n + 1)
                            dve.wait_ge(dbx_done, n + 1)
                            if n >= NHB:
                                dve.wait_ge(hc_done, n - NHB + 1)
                                dve.wait_ge(kept, n - NHB + 1)
                            nc.vector.tensor_tensor_scan(hs[:, n % NHB, :], dA[:, n % NBUF, :], dbx[:, n % NBUF, :],
                                                         h_last[:, k, st_:st_ + 1], ALU.mult, ALU.add).then_inc(scanned, 1)

                        scan(0)
                        for n in range(NI):
                            st_, k = n // NHALF, n % NHALF
                            if n + 1 < NI:
                                scan(n + 1)
                            dve.wait_ge(scanned, n + 1)
                            if n >= NBUF:
                                dve.wait_ge(summed, n - NBUF + 1)
                            nc.vector.tensor_tensor(hc[:, n % NBUF, :], hs[:, n % NHB, :], ps_c[:, st_ % NCB, :], ALU.mult).then_inc(hc_done, 1)
                            nc.vector.tensor_copy(h_last[:, k, st_:st_ + 1], hs[:, n % NHB, CH - 1:CH]).then_inc(kept, 1)
                        dve.wait_ge(summed, NI)
                        for k in range(NHALF):
                            nc.vector.scalar_tensor_tensor(out=yz[:, k, cols], in0=xc[:, k, cols], scalar=d_skip[:, k:k + 1],
                                                           in1=ps_y[:, k, :], op0=ALU.mult, op1=ALU.add).then_inc(skip_done, 1)
                        for k in range(NHALF):
                            dve.wait_ge(skip_done, k + 1)
                            nc.vector.tensor_tensor(yz[:, k, cols], yz[:, k, cols], sz[:, k, cols], ALU.mult).then_inc(gated, 1)

        with Stage(nc, tag + "_out") as q:
            b_out, alpha, beta = q.sb("b_out", [P, D]), q.sb("alpha", [P, D]), q.sb("beta", [P, D])
            r = q.sb("sum", [P, NT, D])
            stats = q.sb("stats", [P, NT, 6])
            mean, var, dif = (q.sb(n, [P, NT]) for n in ("mean", "var", "dif"))
            ps = q.ps("ps", [P, 2, TPC, D])
            vec_loaded, done, dve_step = q.sem("vectors_loaded"), q.sem("out_done"), q.sem("dve_step")
            summed, var_ready, std_ready = q.sem("summed"), q.sem("var_ready"), q.sem("std_ready")
            with nc.Block() as block:
                @block.sync
                def _(sp):
                    for dst, src in ((b_out, w["b_out"]), (alpha, w["alpha"]), (beta, w["beta"])):
                        sp.dma_start(dst[:, :], src.partition_broadcast(P)).then_inc(vec_loaded, 16)
                    sp.wait_ge(vec_loaded, 48)

                @block.tensor
                def _(pe):
                    for c in range(NCH):
                        if c >= 2:
                            pe.wait_ge(summed, c - 1)
                        for j in range(TPC):
                            t = c * TPC + j
                            for k in range(NHALF):
                                last = nc.tensor.matmul(ps[:, c % 2, j, :], yz[:, k, t * P:(t + 1) * P], w_out[:, k, :],
                                                        start=k == 0, stop=k == NHALF - 1)
                        last.then_inc(done, 1)

                @block.scalar
                def _(act):
                    act.wait_ge(var_ready, 1)
                    nc.scalar.activation(var[:, :], var[:, :], ACT.Sqrt).then_inc(std_ready, 1)

                @block.vector
                def _(dve):
                    st = Steps(dve, dve_step)
                    wide = [P, TPC, D]
                    dve.wait_ge(vec_loaded, 48)
                    for c in range(NCH):
                        tiles = slice(c * TPC, (c + 1) * TPC)
                        st.run(nc.vector.tensor_tensor(r[:, tiles, :], xn[:, tiles, :], b_out[:, :].unsqueeze(1).to_broadcast(wide), ALU.add))
                        dve.wait_ge(done, c + 1)
                        nc.vector.tensor_tensor(r[:, tiles, :], r[:, tiles, :], ps[:, c % 2, :, :], ALU.add).then_inc(summed, 1)
                    dve.wait_ge(summed, NCH)
                    for t in range(NT):
                        st.add(nc.vector.bn_stats(stats[:, t, :], r[:, t, :]))
                    st.wait()
                    st.add(nc.vector.tensor_tensor(mean[:, :], stats[:, :, 1], stats[:, :, 4], ALU.add))
                    st.add(nc.vector.tensor_tensor(dif[:, :], stats[:, :, 1], stats[:, :, 4], ALU.subtract))
                    st.run(nc.vector.tensor_tensor(var[:, :], stats[:, :, 2], stats[:, :, 5], ALU.add))
                    st.add(nc.vector.tensor_scalar(mean[:, :], mean[:, :], 0.5, None, ALU.mult))
                    st.run(nc.vector.scalar_tensor_tensor(out=dif[:, :], in0=dif[:, :], scalar=0.25 * D, in1=dif[:, :],
                                                          op0=ALU.mult, op1=ALU.mult))
                    st.run(nc.vector.tensor_tensor(var[:, :], var[:, :], dif[:, :], ALU.add))
                    nc.vector.tensor_scalar(var[:, :], var[:, :], 1.0 / (D - 1), None, ALU.mult).then_inc(var_ready, 1)
                    dve.wait_ge(std_ready, 1)
                    st.run(nc.vector.tensor_scalar(var[:, :], var[:, :], 1e-6, None, ALU.add))
                    st.run(nc.vector.reciprocal(dif[:, :], var[:, :]))
                    for t in range(NT):
                        st.add(nc.vector.tensor_scalar(r[:, t, :], r[:, t, :], mean[:, t:t + 1], dif[:, t:t + 1], ALU.subtract, ALU.mult))
                    st.wait()
                    full = [P, NT, D]
                    st.run(nc.vector.tensor_tensor(r[:, :, :], r[:, :, :], alpha[:, :].unsqueeze(1).to_broadcast(full), ALU.mult))
                    st.run(nc.vector.tensor_tensor(r[:, :, :], r[:, :, :], beta[:, :].unsqueeze(1).to_broadcast(full), ALU.add))
                    st.run(nc.vector.tensor_tensor(core.x[:, :, :], core.x[:, :, :], r[:, :, :], ALU.add))


def stage_route(nc, core, tag, E, Wr, br, comb, capacity=None):
    with Stage(nc, tag) as s:
        wr = s.sb("wr", [P, E])
        brb = s.sb("br", [P, E])
        lg = s.sb("logits", [P, NT, E])
        top, idx = s.sb("top", [P, NT, 8]), s.sb("idx", [P, NT, 8], U32)
        idxf, iota = s.sb("idxf", [P, NT, 2]), s.sb("iota", [P, E])
        mx, tot, w = s.sb("row_max", [P, NT]), s.sb("row_sum", [P, NT]), s.sb("weights", [P, 2, NT])
        hot = s.sb("one_hot", [P, 2, NT, E])
        hot_b = s.sb("one_hot_b", [P, 2, NT, E], BF16)
        tri = s.sb("tri_b", [P, P], BF16)
        before = s.sb("count_before", [P, 2, NT, E])
        total = s.sb("count_in_tile", [P, 2, NT, E])
        rank = s.sb("rank", [P, 2, NT])
        ps = s.ps("ps", [P, NT, E])
        ps_cum, ps_tot = s.ps("ps_cum", [P, 2, NT, E]), s.ps("ps_tot", [P, 2, NT, E])
        loaded, consts, scored, exps = s.sem("loaded"), s.sem("consts"), s.sem("scored"), s.sem("exp_done")
        shifted, dve_step, hot_ready, counted = s.sem("shifted"), s.sem("dve_step"), s.sem("hot_ready"), s.sem("counted")
        nload = 16 if br is None else 32
        with nc.Block() as block:
            @block.sync
            def _(sp):
                sp.dma_start(wr[:, :], Wr).then_inc(loaded, 16)
                if br is not None:
                    sp.dma_start(brb[:, :], br.partition_broadcast(P)).then_inc(loaded, 16)
                sp.wait_ge(loaded, nload)

            @block.gpsimd
            def _(pool):
                nc.gpsimd.iota(iota[:, :], pattern=[[1, E]], base=0, channel_multiplier=0,
                               allow_small_or_imprecise_dtypes=True).then_inc(consts, 1)
                nc.gpsimd.memset(tri[:, :], 1.0).then_inc(consts, 1)
                pool.wait_ge(consts, 2)
                nc.gpsimd.affine_select(out=tri[:, :], in_=tri[:, :], compare_op=ALU.is_ge, fill=0.0,
                                        base=0, pattern=[[1, P]], channel_multiplier=-1).then_inc(consts, 1)
                pool.wait_ge(consts, 3)

            @block.tensor
            def _(pe):
                pe.wait_ge(loaded, nload)
                for t in range(NT):
                    last = nc.tensor.matmul(ps[:, t, :], core.xT[:, t * P:(t + 1) * P], wr[:, :], start=True, stop=True)
                last.then_inc(scored, 1)
                if capacity is not None:
                    pe.wait_ge(consts, 3)
                    pe.wait_ge(hot_ready, 1)
                    flat = hot_b[:, :, :, :].rearrange("p k t e -> p (k t e)")
                    nc.tensor.matmul(ps_cum[:, :, :, :].rearrange("p k t e -> p (k t e)"), tri[:, :], flat, start=True, stop=True)
                    nc.tensor.matmul(ps_tot[:, :, :, :].rearrange("p k t e -> p (k t e)"), core.ones_b[:, :], flat,
                                     start=True, stop=True).then_inc(counted, 1)

            @block.scalar
            def _(act):
                act.wait_ge(shifted, 1)
                nc.scalar.activation(lg[:, :, :], lg[:, :, :], ACT.Exp).then_inc(exps, 1)

            @block.vector
            def _(dve):
                st = Steps(dve, dve_step)
                wide = [P, NT, E]
                dve.wait_ge(loaded, nload)
                dve.wait_ge(consts, 3)
                dve.wait_ge(scored, 1)
                if br is None:
                    st.run(nc.vector.tensor_copy(lg[:, :, :], ps[:, :, :]))
                else:
                    st.run(nc.vector.tensor_tensor(lg[:, :, :], ps[:, :, :], brb[:, :].unsqueeze(1).to_broadcast(wide), ALU.add))
                st.run(nc.vector.tensor_reduce(mx[:, :], lg[:, :, :], axis=AX.X, op=ALU.max))
                nc.vector.tensor_tensor(lg[:, :, :], lg[:, :, :], mx[:, :].unsqueeze(2).to_broadcast(wide), ALU.subtract).then_inc(shifted, 1)
                dve.wait_ge(exps, 1)
                st.run(nc.vector.tensor_reduce(tot[:, :], lg[:, :, :], axis=AX.X, op=ALU.add))
                st.run(nc.vector.reciprocal(mx[:, :], tot[:, :]))
                st.run(nc.vector.tensor_tensor(lg[:, :, :], lg[:, :, :], mx[:, :].unsqueeze(2).to_broadcast(wide), ALU.mult))
                for t in range(NT):
                    st.add(nc.vector.max(top[:, t, :], lg[:, t, :]))
                st.wait()
                for t in range(NT):
                    st.add(nc.vector.max_index(idx[:, t, :], top[:, t, :], lg[:, t, :]))
                st.wait()
                st.add(nc.vector.tensor_copy(idxf[:, :, :], idx[:, :, 0:2]))
                st.run(nc.vector.tensor_tensor(tot[:, :], top[:, :, 0], top[:, :, 1], ALU.add))
                for k in range(2):
                    st.add(nc.vector.tensor_tensor(hot[:, k, :, :], iota[:, :].unsqueeze(1).to_broadcast(wide),
                                                   idxf[:, :, k:k + 1].to_broadcast(wide), ALU.is_equal))
                if capacity is None:
                    st.run(nc.vector.tensor_scalar(tot[:, :], tot[:, :], 1e-9, None, ALU.max))
                else:
                    st.run(nc.vector.tensor_scalar(tot[:, :], tot[:, :], 1e-9, None, ALU.add))
                st.run(nc.vector.reciprocal(mx[:, :], tot[:, :]))
                for k in range(2):
                    st.add(nc.vector.tensor_tensor(w[:, k, :], top[:, :, k], mx[:, :], ALU.mult))
                st.wait()
                if capacity is not None:
                    nc.vector.tensor_copy(hot_b[:, :, :, :], hot[:, :, :, :]).then_inc(hot_ready, 1)
                    dve.wait_ge(counted, 1)
                    st.add(nc.vector.tensor_copy(total[:, :, :, :], ps_tot[:, :, :, :]))
                    st.add(nc.vector.memset(before[:, :, 0, :], 0.0))
                    st.wait()
                    for t in range(1, NT):
                        st.run(nc.vector.tensor_tensor(before[:, :, t, :], before[:, :, t - 1, :], total[:, :, t - 1, :], ALU.add))
                    st.run(nc.vector.tensor_tensor(before[:, :, :, :], before[:, :, :, :], ps_cum[:, :, :, :], ALU.add))
                    st.run(nc.vector.tensor_tensor(before[:, :, :, :], before[:, :, :, :], hot[:, :, :, :], ALU.mult))
                    st.run(nc.vector.tensor_reduce(rank[:, :, :], before[:, :, :, :], axis=AX.X, op=ALU.add))
                    st.run(nc.vector.tensor_scalar(rank[:, :, :], rank[:, :, :], capacity + 0.5, None, ALU.is_lt))
                    st.run(nc.vector.tensor_tensor(w[:, :, :], w[:, :, :], rank[:, :, :], ALU.mult))
                for k in range(2):
                    st.add(nc.vector.tensor_tensor(hot[:, k, :, :], hot[:, k, :, :], w[:, k, :].unsqueeze(2).to_broadcast(wide), ALU.mult))
                st.wait()
                st.run(nc.vector.tensor_tensor(comb[:, :, 0:E], hot[:, 0, :, :], hot[:, 1, :, :], ALU.add))


def stage_gelu_experts(nc, core, tag, comb, W1, b1, g1T, be1T, W2, b2, before):
    E, HID, Q = 16, 128, 4
    NQ = E // Q
    EP = E + Q
    UNROLL = 2
    NB = NCH * Q
    NBUF = 3
    ON_DVE = 3
    with Stage(nc, tag) as s:
        w1, w2 = s.sb("w1", [P, EP * HID]), s.sb("w2", [P, E, D])
        b2s = s.sb("b2", [E, D])
        g, be = s.sb("g1", [P, EP]), s.sb("be1", [P, EP])
        b_rows, loaded = s.sb("b1_rows", [3, E * HID]), s.sem("loaded")
        issue_loads(nc, [(b_rows[:, :], b1.rearrange("e h -> (e h)").partition_broadcast(3)), (b2s[:, :], b2), (g[:, 0:E], g1T), (be[:, 0:E], be1T),
                         (w1[:, 0:E * HID].rearrange("c (e h) -> c e h", e=E), W1.rearrange("e c h -> c e h")),
                         (w2[:, :, :], W2.rearrange("e h o -> h e o"))], loaded)
        before()
        b_rest = s.sb("b1_rest", [3, E * HID])
        b_part = s.sb("b1_part", [3, E * HID], BF16)
        b_sum = s.sb("b1_sum", [P, EP * HID], BF16)
        combT = s.sb("comb_T", [E, T])
        g_q, be_q, comb_q = s.sb("g1_quad", [P, 2, Q]), s.sb("be1_quad", [P, 2, Q]), s.sb("comb_quad", [P, 2, NT, Q])
        h = s.sb("hidden", [P, 2, NT, Q, HID])
        mean, rstd = s.sb("mean", [P, 2, NT * Q]), s.sb("rstd", [P, 2, NT * Q])
        stats, var, dif = s.sb("stats", [P, NT * Q, 6]), s.sb("var", [P, NT * Q]), s.sb("dif", [P, NT * Q])
        hn = s.sb("hidden_norm", [P, NBUF, TPC, HID])
        gT = s.sb("gelu_T", [P, NBUF, CH])
        ps_h, ps_t = s.ps("ps_hidden", [P, 2, CH]), s.ps("ps_turned", [P, NBUF, CH])
        ps_y = s.ps("ps_y", [P, NBUF, TPC, D])
        dve_step, zeroed = s.sem("dve_step"), s.sem("b1_zeroed")
        turned, combT_ready = s.sem("turned"), s.sem("comb_T_ready")
        y_done, added = s.sem("y_done"), s.sem("x_added")
        hid_done, hid_out, quad_ready = s.sem("hidden_done"), s.sem("hidden_evacuated"), s.sem("quad_ready")
        var_ready, std_ready, rstd_ready = s.sem("var_ready"), s.sem("std_ready"), s.sem("rstd_ready")
        normed, normed_pool, gelu_done = s.sem("normalised"), s.sem("normalised_by_pool"), s.sem("gelu_done")
        with nc.Block() as block:
            @block.sync
            def _(sp):
                sp.wait_ge(loaded, 96)

            @block.gpsimd
            def _(pool):
                for n, buf in enumerate((b_sum[:, :], w1[:, E * HID:EP * HID], g[:, E:EP], be[:, E:EP], comb[:, :, E:EP])):
                    nc.gpsimd.memset(buf, 0.0).then_inc(zeroed, 1)
                    pool.wait_ge(zeroed, n + 1)

            @block.tensor
            def _(pe):
                for t in range(NT):
                    if t % TPC == 0 and t >= 2 * TPC:
                        pe.wait_ge(combT_ready, t // TPC - 1)
                    last = nc.tensor.transpose(ps_t[0:E, (t // TPC) % 2, (t % TPC) * P:(t % TPC + 1) * P], comb[:, t, 0:E], core.ident[:, :])
                    if t % TPC == TPC - 1:
                        last.then_inc(turned, 1)
                pe.wait_ge(loaded, 96)
                for c in range(NCH):
                    pe.wait_ge(combT_ready, c + 1)
                    if c >= 2:
                        pe.wait_ge(added, c - 1)
                    for j in range(TPC):
                        t = c * TPC + j
                        last = nc.tensor.matmul(ps_y[:, c % 2, j, :], combT[:, t * P:(t + 1) * P], b2s[:, :], start=True, stop=True)
                    last.then_inc(y_done, 1)

            @block.scalar
            def _(act):
                for c in range(NCH):
                    act.wait_ge(turned, c + 1)
                    nc.scalar.activation(combT[:, c * CH:(c + 1) * CH], ps_t[0:E, c % 2, :], ACT.Copy).then_inc(combT_ready, 1)

            @block.vector
            def _(dve):
                st = Steps(dve, dve_step)
                dve.wait_ge(loaded, 96)
                dve.wait_ge(zeroed, 5)
                for k in range(3):
                    st.run(nc.vector.tensor_copy(b_part[:, :], b_rows[:, :]))
                    if k < 2:
                        st.run(nc.vector.tensor_tensor(b_rows[:, :], b_rows[:, :], b_part[:, :], ALU.subtract))
                    if k == 0:
                        st.run(nc.vector.tensor_scalar(b_sum[0:3, 0:E * HID], b_part[:, :], core.ident[0:3, 0:1], None, ALU.mult))
                    else:
                        st.run(nc.vector.tensor_scalar(b_rest[:, :], b_part[:, :], core.ident[0:3, k:k + 1], None, ALU.mult))
                        st.run(nc.vector.tensor_tensor(b_sum[0:3, 0:E * HID], b_sum[0:3, 0:E * HID], b_rest[:, :], ALU.add))
                for c in range(NCH):
                    dve.wait_ge(y_done, c + 1)
                    tiles = slice(c * TPC, (c + 1) * TPC)
                    nc.vector.tensor_tensor(core.x[:, tiles, :], core.x[:, tiles, :], ps_y[:, c % 2, :, :], ALU.add).then_inc(added, 1)
                dve.wait_ge(added, NCH)

        def quads(i, targets):
            main = i is not None
            steps = (0, UNROLL * NB) if main else (-NB, 0)
            N = UNROLL * NB if main else 0
            at = lambda L, size: bass.ds(i * (UNROLL * size) + L * size, size) if main else slice(0, size)
            TILES = {(L - 1) * NB + t * (NB - 4) // NT: [] for L in targets for t in range(NT)}
            for L in targets:
                for t in range(NT):
                    TILES[(L - 1) * NB + t * (NB - 4) // NT].append((L, t))
            order = lambda L, t: targets.index(L) * NT + t
            last_step = lambda n, L: n == L * NB - 2

            with nc.Block() as block:
                def normalise(eng, n):
                    L, c, e = n // NB, n % NB // Q, n % Q
                    if n >= NBUF:
                        eng.wait_ge(turned, n - NBUF + 1)
                    if L in targets:
                        eng.wait_ge(rstd_ready, targets.index(L) + 1)
                    on_dve = eng is nc.vector
                    for j in range(ON_DVE) if on_dve else range(ON_DVE, TPC):
                        t = c * TPC + j
                        k = t * Q + e
                        last = eng.tensor_scalar(hn[:, n % NBUF, j, :], h[:, L % 2, t, e, :], mean[:, L % 2, k:k + 1], rstd[:, L % 2, k:k + 1],
                                                 ALU.subtract, ALU.mult)
                    last.then_inc(normed if on_dve else normed_pool, 1)

                @block.gpsimd
                def _(pool):
                    def quad_columns(L):
                        if L >= 2:
                            pool.wait_ge(added, NB * (L - 1))
                            pool.wait_ge(gelu_done, NB * (L - 1))
                        cols = at(L, Q)
                        nc.gpsimd.tensor_copy(g_q[:, L % 2, :], g[:, cols]).then_inc(quad_ready, 1)
                        nc.gpsimd.tensor_copy(be_q[:, L % 2, :], be[:, cols]).then_inc(quad_ready, 1)
                        nc.gpsimd.tensor_copy(comb_q[:, L % 2, :, :], comb[:, :, cols]).then_inc(quad_ready, 1)

                    if main:
                        normalise(nc.gpsimd, 0)
                        normalise(nc.gpsimd, 1)
                    for n in range(*steps):
                        for L in targets:
                            if n == (L - 1) * NB:
                                quad_columns(L)
                        if main and n + 2 < N:
                            normalise(nc.gpsimd, n + 2)

                @block.tensor
                def _(pe):
                    def hidden(L, t):
                        a = order(L, t)
                        if a >= 2:
                            pe.wait_ge(hid_out, a - 1)
                        nc.tensor.matmul(ps_h[:, a % 2, :], core.xT[:, t * P:(t + 1) * P], w1[:, at(L, Q * HID)], start=True, stop=False)
                        nc.tensor.matmul(ps_h[:, a % 2, :], core.ones_b[:, :], b_sum[:, at(L, Q * HID)], start=False, stop=True).then_inc(hid_done, 1)

                    def turn(n):
                        pe.wait_ge(normed, n + 1)
                        pe.wait_ge(normed_pool, n + 1)
                        if n >= NBUF:
                            pe.wait_ge(gelu_done, n - NBUF + 1)
                        for j in range(TPC):
                            last = nc.tensor.transpose(ps_t[:, n % NBUF, j * P:(j + 1) * P], hn[:, n % NBUF, j, :], core.ident[:, :])
                        last.then_inc(turned, 1)

                    def product(n):
                        pe.wait_ge(gelu_done, n + 1)
                        if n >= NBUF:
                            pe.wait_ge(added, n - NBUF + 1)
                        L, e = n // NB, n % Q
                        for j in range(TPC):
                            last = nc.tensor.matmul(ps_y[:, n % NBUF, j, :], gT[:, n % NBUF, j * P:(j + 1) * P],
                                                    w2[:, bass.ds(i * (UNROLL * Q) + (L * Q + e), 1), :], start=True, stop=True)
                        last.then_inc(y_done, 1)

                    if main:
                        turn(0)
                    for n in range(*steps):
                        if main and n + 1 < N:
                            turn(n + 1)
                        for L, t in TILES.get(n, ()):
                            hidden(L, t)
                        if main:
                            product(n)

                @block.scalar
                def _(act):
                    def gelu(n):
                        L, e = n // NB, n % Q
                        act.wait_ge(turned, n + 1)
                        if n >= NBUF:
                            act.wait_ge(y_done, n - NBUF + 1)
                        if L in targets:
                            act.wait_ge(quad_ready, 3 * (targets.index(L) + 1))
                        nc.scalar.activation(gT[:, n % NBUF, :], ps_t[:, n % NBUF, :], ACT.Gelu, scale=g_q[:, L % 2, e:e + 1],
                                             bias=be_q[:, L % 2, e:e + 1]).then_inc(gelu_done, 1)

                    if main:
                        gelu(0)
                    for n in range(*steps):
                        for L in targets:
                            if last_step(n, L):
                                act.wait_ge(var_ready, targets.index(L) + 1)
                                nc.scalar.activation(var[:, :], var[:, :], ACT.Sqrt).then_inc(std_ready, 1)
                        if main and n + 1 < N:
                            gelu(n + 1)
                        for L, t in TILES.get(n, ()):
                            a = order(L, t)
                            act.wait_ge(hid_done, a + 1)
                            if L >= 2 and t == 0:
                                act.wait_ge(normed, NB * (L - 1))
                                act.wait_ge(normed_pool, NB * (L - 1))
                            nc.scalar.activation(h[:, L % 2, t, :, :], ps_h[:, a % 2, :].rearrange("p (e h) -> p e h", e=Q), ACT.Copy).then_inc(hid_out, 1)

                @block.vector
                def _(dve):
                    st = Steps(dve, dve_step)

                    def statistics(L, t):
                        dve.wait_ge(hid_out, order(L, t) + 1)
                        for e in range(Q):
                            st.add(nc.vector.bn_stats(stats[:, t * Q + e, :], h[:, L % 2, t, e, :]))

                    def deviations(L):
                        par = L % 2
                        st.wait()
                        st.add(nc.vector.tensor_tensor(mean[:, par, :], stats[:, :, 1], stats[:, :, 4], ALU.add))
                        st.add(nc.vector.tensor_tensor(dif[:, :], stats[:, :, 1], stats[:, :, 4], ALU.subtract))
                        st.run(nc.vector.tensor_tensor(var[:, :], stats[:, :, 2], stats[:, :, 5], ALU.add))
                        st.add(nc.vector.tensor_scalar(mean[:, par, :], mean[:, par, :], 0.5, None, ALU.mult))
                        st.add(nc.vector.tensor_scalar(var[:, :], var[:, :], 1.0 / HID, 1e-5, ALU.mult, ALU.add))
                        st.run(nc.vector.scalar_tensor_tensor(out=dif[:, :], in0=dif[:, :], scalar=0.25, in1=dif[:, :],
                                                              op0=ALU.mult, op1=ALU.mult))
                        nc.vector.tensor_tensor(var[:, :], var[:, :], dif[:, :], ALU.add).then_inc(var_ready, 1)
                        dve.wait_ge(std_ready, targets.index(L) + 1)
                        nc.vector.reciprocal(rstd[:, par, :], var[:, :]).then_inc(rstd_ready, 1)

                    def add_to_x(n):
                        L, c, e = n // NB, n % NB // Q, n % Q
                        if L in targets:
                            dve.wait_ge(quad_ready, 3 * (targets.index(L) + 1))
                        dve.wait_ge(y_done, n + 1)
                        if n >= 1:
                            dve.wait_ge(added, n)
                        for j in range(TPC):
                            t = c * TPC + j
                            last = nc.vector.scalar_tensor_tensor(out=core.x[:, t, :], in0=ps_y[:, n % NBUF, j, :],
                                                                  scalar=comb_q[:, L % 2, t, e:e + 1], in1=core.x[:, t, :],
                                                                  op0=ALU.mult, op1=ALU.add)
                        last.then_inc(added, 1)

                    if main:
                        normalise(nc.vector, 0)
                        normalise(nc.vector, 1)
                    for n in range(*steps):
                        for L, t in TILES.get(n - 1, ()):
                            statistics(L, t)
                        for L in targets:
                            if last_step(n, L):
                                deviations(L)
                        if main and n + 2 < N:
                            normalise(nc.vector, n + 2)
                        if main and n >= 1:
                            add_to_x(n - 1)
                    if main:
                        add_to_x(N - 1)

        s.restart()
        quads(None, [0])
        with nc.Fori(0, NQ // UNROLL) as i:
            s.restart()
            quads(i, list(range(1, UNROLL + 1)))


def stage_silu_experts(nc, core, tag, comb, WgT, WuT, WdT, before):
    E, HID = 8, 256
    NH = HID // P
    EB = 4
    NS = EB * NCH
    with Stage(nc, tag) as s:
        wg, wu = s.sb("wg", [P, E, HID]), s.sb("wu", [P, E, HID])
        wd = s.sb("wd", [P, NH, E, D])
        loaded = s.sem("loaded")
        issue_loads(nc, [(wg[:, :, :], WgT), (wu[:, :, :], WuT), (wd[:, :, :, :], WdT.rearrange("(k p) e o -> p k e o", p=P))], loaded)
        before()
        wg_e, wu_e, comb_e = s.sb("wg_expert", [P, 2, HID]), s.sb("wu_expert", [P, 2, HID]), s.sb("comb_expert", [P, 2, NT])
        gate = s.sb("gate", [P, 2, CH])
        gu = s.sb("gate_up", [P, 2, NH, CH])
        ps_g, ps_u, ps_y = s.ps("ps_gate", [P, 2, CH]), s.ps("ps_up", [P, 2, CH]), s.ps("ps_y", [P, 2, TPC, D])
        expert_ready = s.sem("expert_ready")
        up_done, gated, gu_ready = s.sem("gate_up_done"), s.sem("silu_done"), s.sem("gu_ready")
        y_done, added = s.sem("y_done"), s.sem("x_added")
        with nc.Block() as block:
            @block.sync
            def _(sp):
                sp.wait_ge(loaded, 48)
        with nc.Fori(0, E // EB) as i:
            s.restart()
            with nc.Block() as block:
                @block.gpsimd
                def _(pool):
                    for e in range(EB):
                        if e >= 2:
                            pool.wait_ge(up_done, NH * NCH * (e - 1))
                            pool.wait_ge(added, NCH * (e - 1))
                        at = bass.ds(i * EB + e, 1)
                        nc.gpsimd.tensor_copy(wg_e[:, e % 2, :], wg[:, at, :].rearrange("p a h -> p (a h)")).then_inc(expert_ready, 1)
                        nc.gpsimd.tensor_copy(wu_e[:, e % 2, :], wu[:, at, :].rearrange("p a h -> p (a h)")).then_inc(expert_ready, 1)
                        nc.gpsimd.tensor_copy(comb_e[:, e % 2, :], comb[:, :, at].rearrange("p t a -> p (t a)")).then_inc(expert_ready, 1)

                @block.tensor
                def _(pe):
                    def gate_up(n):
                        m, k = n // NH, n % NH
                        e, c = m // NCH, m % NCH
                        if c == 0 and k == 0:
                            pe.wait_ge(expert_ready, 3 * (e + 1))
                        if n >= 2:
                            pe.wait_ge(gu_ready, n - 1)
                        cols = core.xT[:, c * CH:(c + 1) * CH]
                        nc.tensor.matmul(ps_g[:, n % 2, :], wg_e[:, e % 2, k * P:(k + 1) * P], cols, start=True, stop=True)
                        nc.tensor.matmul(ps_u[:, n % 2, :], wu_e[:, e % 2, k * P:(k + 1) * P], cols, start=True, stop=True).then_inc(up_done, 1)

                    gate_up(0)
                    gate_up(1)
                    for m in range(NS):
                        if m + 1 < NS:
                            gate_up(2 * m + 2)
                            gate_up(2 * m + 3)
                        pe.wait_ge(gu_ready, NH * (m + 1))
                        if m >= 2:
                            pe.wait_ge(added, m - 1)
                        for j in range(TPC):
                            for k in range(NH):
                                last = nc.tensor.matmul(ps_y[:, m % 2, j, :], gu[:, m % 2, k, j * P:(j + 1) * P],
                                                        wd[:, k, bass.ds(i * EB + m // NCH, 1), :], start=k == 0, stop=k == NH - 1)
                        last.then_inc(y_done, 1)

                @block.scalar
                def _(act):
                    for n in range(NS * NH):
                        act.wait_ge(up_done, n + 1)
                        if n >= 2:
                            act.wait_ge(gu_ready, n - 1)
                        nc.scalar.activation(gate[:, n % 2, :], ps_g[:, n % 2, :], ACT.Silu).then_inc(gated, 1)

                @block.vector
                def _(dve):
                    def product(n):
                        m, k = n // NH, n % NH
                        dve.wait_ge(gated, n + 1)
                        if m >= 2:
                            dve.wait_ge(y_done, m - 1)
                        nc.vector.tensor_tensor(gu[:, m % 2, k, :], gate[:, n % 2, :], ps_u[:, n % 2, :], ALU.mult).then_inc(gu_ready, 1)

                    product(0)
                    product(1)
                    for m in range(NS):
                        e, c = m // NCH, m % NCH
                        if m + 1 < NS:
                            product(2 * m + 2)
                            product(2 * m + 3)
                        dve.wait_ge(expert_ready, 3 * (e + 1))
                        dve.wait_ge(y_done, m + 1)
                        if m >= NCH:
                            dve.wait_ge(added, m - NCH + 1)
                        for j in range(TPC):
                            t = c * TPC + j
                            last = nc.vector.scalar_tensor_tensor(out=core.x[:, t, :], in0=ps_y[:, m % 2, j, :], scalar=comb_e[:, e % 2, t:t + 1],
                                                                  in1=core.x[:, t, :], op0=ALU.mult, op1=ALU.add)
                        last.then_inc(added, 1)


def stage_span_attention(nc, core, tag, Wq, Wk, Wv, Wo, span, before):
    H, DH, RAMP = 16, 64, 32
    HP = H + 1
    SC = 1.0 / DH
    M = DH + 2
    F32R = mybir.dt.float32r
    PASS1 = [(qt, kc, min(CH, (qt + 1) * P - kc * CH), (qt // TPC) == kc) for qt in range(NT) for kc in range(qt // TPC + 1)]
    HEAD2 = [(qc, kb, max(0, kb * P - qc * CH)) for qc in range(NCH) for kb in range(TPC * (qc + 1))]
    N1, NH = len(PASS1), len(HEAD2)
    HB = 4
    NPB = 4
    LAG = 4
    with Stage(nc, tag) as s:
        wq, wk, wv = s.sb("wq", [P, HP * DH]), s.sb("wk", [P, HP * DH]), s.sb("wv", [P, HP * DH])
        wo = s.sb("wo", [M, H, D + 1])
        wq_h, wk_h = s.sb("wq_head", [P, 2, DH]), s.sb("wk_head", [P, 2, DH])
        mask, mask_h = s.sb("mask", [P, HP, NT]), s.sb("mask_head", [P, NT])
        pos, spans = s.sb("pos", [P, NT]), s.sb("spans", [P, H])
        loaded = s.sem("loaded")
        issue_loads(nc, [(wq[:, 0:H * DH], Wq), (wk[:, 0:H * DH], Wk), (wv[:, 0:H * DH], Wv),
                         (spans[:, :], span.rearrange("a h b c -> (a b c h)").partition_broadcast(P))], loaded)
        before()
        k_hl = s.sb("k_hi_lo", [P, 2, T], F32R)
        q_hi, q_lo = s.sb("q_hi", [P, 2, T], F32R), s.sb("q_lo", [P, 2, T], F32R)
        va = s.sb("v_aug", [P, 2, NT, M])
        m_row = s.sb("max_row", [P, 2, T], BF16)
        m_part = s.sb("max_part", [P, NT, NCH])
        m_neg, m_rest = s.sb("max_neg", [P, NT]), s.sb("max_rest", [P, NT])
        m_split = s.sb("max_split", [P, NT, 3], BF16)
        probs = s.sb("probs", [P, NPB, CH])
        oT = s.sb("oT", [M, CH])
        rden = s.sb("rden", [P, TPC])
        ring, psS, psO = s.ps("ps_ring", [P, 2, CH]), s.ps("ps_scores", [P, 2, CH]), s.ps("ps_out", [P, 2, CH])
        psF = s.ps("ps_final", [P, TPC, 256])
        wo_zero, consts = s.sem("wo_zeroed"), s.sem("consts")
        pool_step, dve_step = s.sem("pool_step"), s.sem("dve_step")
        w_ready, rounded = s.sem("weights_ready"), s.sem("rounded")
        filled, slot_free = s.sem("ring_filled"), [s.sem(f"ring_free{b}") for b in range(2)]
        split_ready = s.sem("max_split")
        sc2, exped, pv = s.sem("pass2_scored"), s.sem("exp_done"), s.sem("pv_done")
        oT_ready, fin, recip, added = s.sem("oT_ready"), s.sem("final_ready"), s.sem("recip"), s.sem("x_added")
        with nc.Block() as block:
            @block.sync
            def _(sp):
                sp.wait_ge(wo_zero, 1)
                sp.dma_start(wo[0:DH, :, 0:D], Wo.rearrange("(h d) n -> d h n", d=DH)).then_inc(loaded, 16)
                sp.wait_ge(loaded, 80)

            @block.gpsimd
            def _(pool):
                st = Steps(pool, pool_step)
                st.run(nc.gpsimd.memset(wo[:, :, :], 0.0))
                nc.gpsimd.memset(wo[DH:M, :, D:D + 1], 1.0).then_inc(wo_zero, 1)
                pool.wait_ge(wo_zero, 1)
                for w in (wq, wk, wv):
                    st.add(nc.gpsimd.memset(w[:, H * DH:HP * DH], 0.0))
                st.add(nc.gpsimd.memset(mask[:, H:HP, :], 0.0))
                st.add(nc.gpsimd.memset(m_row[:, :, :], 0.0))
                st.add(nc.gpsimd.memset(m_part[:, :, :], -3.0e38))
                st.add(nc.gpsimd.memset(va[:, :, :, DH + 1:M], 1e-8))
                st.add(nc.gpsimd.iota(pos[:, :], pattern=[[P, NT]], base=0, channel_multiplier=1,
                                      allow_small_or_imprecise_dtypes=True))
                pool.wait_ge(loaded, 80)
                st.run(nc.gpsimd.tensor_scalar(spans[:, :], spans[:, :], float(T), None, ALU.mult))
                for h in range(H):
                    st.add(nc.gpsimd.tensor_scalar(mask[:, h, :], pos[:, :], spans[:, h:h + 1], 1.0 / (RAMP + 1), ALU.add, ALU.mult))
                st.wait()
                nc.gpsimd.tensor_scalar(mask[:, 0:H, :], mask[:, 0:H, :], 0.0, 1.0, ALU.max, ALU.min).then_inc(consts, 1)
                pool.wait_ge(consts, 1)

        def heads(i, targets):
            main = i is not None
            steps = (0, HB * NH + LAG) if main else (-NH, 0)
            N2 = HB * NH if main else 0
            at = lambda L, size: bass.ds(i * (HB * size) + L * size, size) if main else slice(0, size)
            ENDS = {L * NH + n: L * NCH + qc for L in range(HB) for n, (qc, kb, _) in enumerate(HEAD2) if kb == TPC * (qc + 1) - 1} if main else {}
            items = []
            for L in targets:
                s0 = (L - 1) * NH
                for c in range(NCH):
                    items += [(s0 + 4 * c, "k", L, c), (s0 + 4 * c + 1, "q", L, c), (s0 + 4 * c + 3, "v", L, c)]
                items += [(s0 + max(3 + k * (NH - 9) // N1, 4 * (PASS1[k][0] // TPC) + 3), "max", L, k) for k in range(N1)]
                items += [(s0 + NH - 4, "row", L, c) for c in range(NCH)]
            items.sort(key=lambda item: item[0])
            AT = {}
            for r, item in enumerate(items):
                AT.setdefault(item[0], []).append(r)
            WHERE = {item[1:]: r for r, item in enumerate(items)}
            ROUNDED = {r: n + 1 for n, r in enumerate(r for r, it in enumerate(items) if it[1] in ("k", "q"))}

            def pass2(n):
                qc, kb, q0 = HEAD2[n % NH]
                return n // NH, n // NH * NCH + qc, qc, kb, q0

            def due(n, lag):
                return ENDS.get(n - lag)

            def wait_slot(eng, r):
                eng.wait_ge(slot_free[r % 2], r // 2 + 1)

            with nc.Block() as block:
                @block.gpsimd
                def _(pool):
                    for n, L in enumerate(targets):
                        if n:
                            pool.wait_ge(filled, WHERE["q", targets[n - 1], NCH - 1] + 1)
                            wait_slot(pool, WHERE["v", targets[n - 1], NCH - 1])
                        for dst, w in ((wk_h, wk), (wq_h, wq)):
                            nc.gpsimd.tensor_copy(dst[:, :, :], w[:, at(L, DH)].unsqueeze(1).to_broadcast([P, 2, DH])).then_inc(w_ready, 1)
                        nc.gpsimd.tensor_copy(mask_h[:, :], mask[:, at(L, 1), :].rearrange("p a t -> p (a t)")).then_inc(w_ready, 1)

                @block.tensor
                def _(pe):
                    def fill(r):
                        _, kind, L, k = items[r]
                        out, par = ring[:, r % 2, :], L % 2
                        if r >= 2:
                            pe.wait_ge(slot_free[r % 2], r // 2)
                        if kind in ("k", "q"):
                            pe.wait_ge(w_ready, 3 * (targets.index(L) + 1))
                            w = wk_h if kind == "k" else wq_h
                            last = nc.tensor.matmul(out, w[:, :, :].rearrange("p r d -> p (r d)"), core.xT[:, k * CH:(k + 1) * CH],
                                                    start=True, stop=True)
                        elif kind == "v":
                            for j in range(TPC):
                                t = k * TPC + j
                                last = nc.tensor.matmul(out[:, j * DH:(j + 1) * DH], core.xT[:, t * P:(t + 1) * P], wv[:, at(L, DH)],
                                                        start=True, stop=True)
                        elif kind == "max":
                            qt, kc, w_, diag = PASS1[k]
                            if kc == 0 and qt % TPC == 0:
                                wait_slot(pe, WHERE["k", L, qt // TPC])
                                wait_slot(pe, WHERE["q", L, qt // TPC])
                            last = nc.tensor.matmul(out[:, 0:w_], q_hi[:, par, qt * P:(qt + 1) * P], k_hl[:, par, kc * CH:kc * CH + w_],
                                                    start=True, stop=not diag)
                            if diag:
                                last = nc.tensor.matmul(out[:, w_ - P:w_], core.ident_b[:, :], core.hide[:, :], start=False, stop=True)
                        else:
                            pe.wait_ge(split_ready, targets.index(L) + 1)
                            for j in range(TPC):
                                last = nc.tensor.matmul(out[0:3, j * P:(j + 1) * P], m_split[:, k * TPC + j, :], core.ident_b[:, :],
                                                        start=True, stop=True)
                        last.then_inc(filled, 1)

                    def scores(n):
                        L, g, qc, kb, q0 = pass2(n)
                        par = L % 2
                        if n >= 2:
                            pe.wait_ge(exped, n - 1)
                        if n % NH == 0 and ("row", L, 0) in WHERE:
                            wait_slot(pe, WHERE["row", L, NCH - 2])
                            wait_slot(pe, WHERE["row", L, NCH - 1])
                        q1, w = qc * CH + q0, CH - q0
                        diag = kb >= TPC * qc
                        out, keys = psS[:, n % 2, 0:w], k_hl[:, par, kb * P:(kb + 1) * P]
                        nc.tensor.matmul(out, keys, q_hi[:, par, q1:q1 + w], start=True, stop=False)
                        nc.tensor.matmul(out, keys, q_lo[:, par, q1:q1 + w], start=False, stop=False)
                        mm = nc.tensor.matmul(out, core.ones_b[:, :], m_row[:, par, q1:q1 + w], start=False, stop=not diag)
                        if diag:
                            mm = nc.tensor.matmul(psS[:, n % 2, 0:P], core.ident_b[:, :], core.hideT[:, :], start=False, stop=True)
                        mm.then_inc(sc2, 1)

                    def values(n):
                        L, g, qc, kb, q0 = pass2(n)
                        if kb == 0 and g >= 2:
                            pe.wait_ge(oT_ready, g - 1)
                        if n % NH == 0 and ("v", L, 0) in WHERE:
                            wait_slot(pe, WHERE["v", L, NCH - 1])
                        pe.wait_ge(exped, n + 1)
                        nc.tensor.matmul(psO[0:M, g % 2, q0:CH], va[:, L % 2, kb, :], probs[:, n % NPB, 0:CH - q0],
                                         start=kb == 0, stop=kb == TPC * (qc + 1) - 1).then_inc(pv, 1)

                    def project_out(g):
                        pe.wait_ge(oT_ready, g + 1)
                        pe.wait_ge(added, g)
                        for j in range(TPC):
                            last = nc.tensor.matmul(psF[:, j, 0:D + 1], oT[:, j * P:(j + 1) * P], wo[:, at(g // NCH, 1), :], start=True, stop=True)
                        last.then_inc(fin, 1)

                    if main:
                        scores(0)
                        scores(1)
                    for n in range(*steps):
                        if main and n + 2 < N2:
                            scores(n + 2)
                        fills = AT.get(n, [])
                        for r in fills[:(len(fills) + 1) // 2]:
                            fill(r)
                        if main and n < N2:
                            values(n)
                        for r in fills[(len(fills) + 1) // 2:]:
                            fill(r)
                        if (g := due(n, 2)) is not None:
                            project_out(g)

                @block.scalar
                def _(act):
                    def high_half(r):
                        _, kind, L, c = items[r]
                        act.wait_ge(filled, r + 1)
                        dst = k_hl if kind == "k" else q_hi
                        nc.scalar.activation(dst[:, L % 2, c * CH:(c + 1) * CH], ring[:, r % 2, :], ACT.Copy).then_inc(rounded, 1)

                    def exponential(n):
                        q0 = pass2(n)[4]
                        act.wait_ge(sc2, n + 1)
                        if n >= NPB:
                            act.wait_ge(pv, n - NPB + 1)
                        nc.scalar.activation(probs[:, n % NPB, 0:CH - q0], psS[:, n % 2, 0:CH - q0], ACT.Exp, scale=SC).then_inc(exped, 1)

                    if main:
                        exponential(0)
                    for n in range(*steps):
                        if main and n + 1 < N2:
                            exponential(n + 1)
                        for r in AT.get(n, ()):
                            if items[r][1] in ("k", "q"):
                                high_half(r)
                        if (g := due(n, 1)) is not None:
                            act.wait_ge(pv, n)
                            act.wait_ge(fin, g)
                            nc.scalar.activation(oT[:, :], psO[0:M, g % 2, :], ACT.Copy).then_inc(oT_ready, 1)

                @block.vector
                def _(dve):
                    st = Steps(dve, dve_step)

                    def take(r):
                        _, kind, L, k = items[r]
                        par, bank, free = L % 2, ring[:, r % 2, :], slot_free[r % 2]
                        cs = slice(k * CH, (k + 1) * CH)
                        dve.wait_ge(filled, r + 1)
                        if kind == "k":
                            dve.wait_ge(rounded, ROUNDED[r])
                            nc.vector.tensor_tensor(k_hl[DH:P, par, cs], bank[DH:P, :], k_hl[DH:P, par, cs].bitcast(F32), ALU.subtract).then_inc(free, 1)
                        elif kind == "q":
                            dve.wait_ge(rounded, ROUNDED[r])
                            nc.vector.tensor_tensor(q_lo[:, par, cs], bank, q_hi[:, par, cs].bitcast(F32), ALU.subtract).then_inc(free, 1)
                        elif kind == "v":
                            tiles = slice(k * TPC, (k + 1) * TPC)
                            dve.wait_ge(w_ready, 3 * (targets.index(L) + 1))
                            m4 = mask_h[:, tiles].unsqueeze(2)
                            nc.vector.tensor_copy(va[:, par, tiles, DH:DH + 1], m4)
                            nc.vector.tensor_tensor(va[:, par, tiles, 0:DH], bank[:, 0:TPC * DH].rearrange("p (t d) -> p t d", d=DH),
                                                    m4.to_broadcast([P, TPC, DH]), ALU.mult).then_inc(free, 1)
                        elif kind == "max":
                            qt, kc, w_, _ = PASS1[k]
                            nc.vector.tensor_reduce(m_part[:, qt, kc:kc + 1], bank[:, 0:w_], axis=AX.X, op=ALU.max).then_inc(free, 1)
                            if k == N1 - 1:
                                wait_slot(dve, WHERE["max", L, N1 - 2])
                                wait_slot(dve, r)
                                maxima(L)
                        else:
                            nc.vector.tensor_copy(m_row[0:3, par, cs], ring[0:3, r % 2, :]).then_inc(free, 1)

                    def maxima(L):
                        st.run(nc.vector.tensor_reduce(m_neg[:, :], m_part[:, :, :], axis=AX.X, op=ALU.max, negate=True))
                        st.run(nc.vector.tensor_copy(m_split[:, :, 0], m_neg[:, :]))
                        st.run(nc.vector.tensor_tensor(m_rest[:, :], m_neg[:, :], m_split[:, :, 0], ALU.subtract))
                        st.run(nc.vector.tensor_copy(m_split[:, :, 1], m_rest[:, :]))
                        st.run(nc.vector.tensor_tensor(m_neg[:, :], m_rest[:, :], m_split[:, :, 1], ALU.subtract))
                        st.run(nc.vector.tensor_copy(m_split[:, :, 2], m_neg[:, :]))
                        dve.sem_inc(split_ready, 1)

                    def add_to_x(g):
                        dve.wait_ge(fin, g + 1)
                        nc.vector.reciprocal(rden[:, :].unsqueeze(2), psF[:, :, D:D + 1]).then_inc(recip, 1)
                        dve.wait_ge(recip, g + 1)
                        for j in range(TPC):
                            t = (g % NCH) * TPC + j
                            last = nc.vector.scalar_tensor_tensor(out=core.x[:, t, :], in0=psF[:, j, 0:D], scalar=rden[:, j:j + 1],
                                                                  in1=core.x[:, t, :], op0=ALU.mult, op1=ALU.add)
                        last.then_inc(added, 1)
                        dve.wait_ge(added, g + 1)

                    for n in range(*steps):
                        for r in AT.get(n, ()):
                            take(r)
                        if (g := due(n, 3)) is not None:
                            add_to_x(g)

        s.restart()
        heads(None, [0])
        with nc.Fori(0, H // HB) as i:
            s.restart()
            heads(i, list(range(1, HB + 1)))


def stage_rope_attention(nc, core, tag, WqkvT, WswapT, WoutT, cosT, sinT, before):
    H, DH, G, NPART = 16, 8, 4, 3
    NG = H // G
    SC = DH ** -0.5
    Q_ORDER, K_ORDER = (0, 1, 0, 1, 2, 0), (0, 0, 1, 1, 0, 2)
    PASS1 = [(qt, kc, min(CH, (qt + 1) * P - kc * CH), (qt // TPC) == kc) for qt in range(NT) for kc in range(qt // TPC + 1)]
    HEAD2 = [(qc, kb, max(0, kb * P - qc * CH)) for qc in range(NCH) for kb in range(TPC * (qc + 1))]
    N1, NH = len(PASS1), len(HEAD2)
    UNROLL = 2
    NPB, NR, MR = 2 * G, 3, 64
    LAG = 4
    with Stage(nc, tag) as s:
        o_all = s.sb("o_tokens", [P, NT, D])
        w_out = s.sb("w_out", [P, D])
        va = s.sb("v_aug", [P, NT, H + G, 32])
        qs, ks = s.sb("q_stack", [P, 2, G, T], BF16), s.sb("k_stack", [P, 2, G, T], BF16)
        scratch = {n: nc.dram_tensor(f"{tag}_{n}_parts", (NPART, P + G * DH, T), BF16, kind="Internal").ap() for n in "qk"}
        with Stage(nc, tag + "_in") as q:
            w, ws = q.sb("w_qkv", [P, 3 * D]), q.sb("w_swapped", [P, 2 * D])
            cos, sin = q.sb("cos", [P, T]), q.sb("sin", [P, T])
            loaded = q.sem("loaded")
            issue_loads(nc, [(dst[:, :], src) for dst, src in ((w, WqkvT), (ws, WswapT), (cos, cosT), (sin, sinT), (w_out, WoutT))], loaded)
            before()
            roped, rest = q.sb("roped", [P, T]), q.sb("rest", [P, T])
            parts = q.sb("parts", [P, 2, NPART, T], BF16)
            ps_a, ps_b = q.ps("ps_plain", [P, 2, CH]), q.ps("ps_swapped", [P, 2, CH])
            ps_v = q.ps("ps_v", [P, 2, TPC, D])
            stored, zeroed, dve_step = q.sem("stored"), q.sem("v_zeroed"), q.sem("dve_step")
            proj, a_used, b_used, v_done, v_out, split = (q.sem(n) for n in ("projected", "plain_used", "swapped_used", "v_done", "v_out", "split"))
            with nc.Block() as block:
                @block.sync
                def _(sp):
                    for n, name in enumerate("qk"):
                        for part in range(NPART):
                            sp.wait_ge(split, n * NPART + part + 1)
                            sp.dma_start(scratch[name][part, 0:P, :], parts[:, n, part, :]).then_inc(stored, 16)
                            sp.dma_start(scratch[name][part, P:P + G * DH, :], parts[0:G * DH, n, part, :]).then_inc(stored, 16)
                    sp.wait_ge(loaded, 80)
                    sp.wait_ge(stored, 16 * 4 * NPART)

                @block.gpsimd
                def _(pool):
                    nc.gpsimd.memset(va[:, :, :, :], 0.0).then_inc(zeroed, 1)
                    pool.wait_ge(zeroed, 1)
                    nc.gpsimd.memset(va[:, :, :, DH:DH + 1], 1.0).then_inc(zeroed, 1)
                    nc.gpsimd.memset(qs[:, :, :, :], 0.0).then_inc(zeroed, 1)
                    pool.wait_ge(zeroed, 3)

                @block.tensor
                def _(pe):
                    pe.wait_ge(loaded, 80)
                    for n in range(2 * NCH):
                        j, c = n // NCH, n % NCH
                        if n >= 2:
                            pe.wait_ge(a_used, n - 1)
                            pe.wait_ge(b_used, n - 1)
                        cols = core.xT[:, c * CH:(c + 1) * CH]
                        nc.tensor.matmul(ps_a[:, n % 2, :], w[:, j * D:(j + 1) * D], cols, start=True, stop=True)
                        nc.tensor.matmul(ps_b[:, n % 2, :], ws[:, j * D:(j + 1) * D], cols, start=True, stop=True).then_inc(proj, 1)
                    for c in range(NCH):
                        if c >= 2:
                            pe.wait_ge(v_out, c - 1)
                        for j in range(TPC):
                            t = c * TPC + j
                            last = nc.tensor.matmul(ps_v[:, c % 2, j, :], core.xT[:, t * P:(t + 1) * P], w[:, 2 * D:3 * D], start=True, stop=True)
                        last.then_inc(v_done, 1)

                @block.scalar
                def _(act):
                    act.wait_ge(zeroed, 2)
                    for c in range(NCH):
                        act.wait_ge(v_done, c + 1)
                        nc.scalar.activation(va[:, c * TPC:(c + 1) * TPC, 0:H, 0:DH],
                                             ps_v[:, c % 2, :, :].rearrange("p t (h d) -> p t h d", d=DH), ACT.Copy).then_inc(v_out, 1)

                @block.vector
                def _(dve):
                    st = Steps(dve, dve_step)
                    dve.wait_ge(loaded, 80)
                    for j in range(2):
                        for c in range(NCH):
                            n = j * NCH + c
                            cs = slice(c * CH, (c + 1) * CH)
                            dve.wait_ge(proj, n + 1)
                            nc.vector.tensor_tensor(roped[:, cs], ps_a[:, n % 2, :], cos[:, cs], ALU.mult).then_inc(a_used, 1)
                            nc.vector.tensor_tensor(rest[:, cs], ps_b[:, n % 2, :], sin[:, cs], ALU.mult).then_inc(b_used, 1)
                        dve.wait_ge(a_used, (j + 1) * NCH)
                        dve.wait_ge(b_used, (j + 1) * NCH)
                        st.run(nc.vector.tensor_tensor(roped[:, :], roped[:, :], rest[:, :], ALU.add))
                        for part in range(NPART):
                            nc.vector.tensor_copy(parts[:, j, part, :], roped[:, :]).then_inc(split, 1)
                            dve.wait_ge(split, j * NPART + part + 1)
                            if part < NPART - 1:
                                st.run(nc.vector.tensor_tensor(roped[:, :], roped[:, :], parts[:, j, part, :], ALU.subtract))

        with Stage(nc, tag + "_heads") as q:
            vg = q.sb("v_group", [P, 2, NT, G, 32])
            m_part = q.sb("max_part", [P, NT, NCH])
            m_neg, m_rest = q.sb("max_neg", [P, NT]), q.sb("max_rest", [P, NT])
            m_split = q.sb("max_split", [P, G, NT, 3], BF16)
            probs = q.sb("probs", [P, NPB, CH])
            oT, rden = q.sb("oT", [P, CH]), q.sb("rden", [P, TPC, G])
            ring, psS = q.ps("ps_ring", [P, NR, CH]), q.ps("ps_scores", [P, G, CH])
            ps_o = q.ps("ps_out", [P, CH])
            zeroed, dve_step = q.sem("zeroed"), q.sem("dve_step")
            stack_in, v_ready, cleared = [q.sem(f"stack_in{g}") for g in range(G)], q.sem("v_ready"), q.sem("max_rows_cleared")
            filled, slot_free = q.sem("ring_filled"), [q.sem(f"ring_free{b}") for b in range(NR)]
            split_ready = q.sem("max_split")
            sc2, exped, pv, oT_ready = q.sem("pass2_scored"), q.sem("exp_done"), q.sem("pv_done"), q.sem("oT_ready")
            recip = q.sem("recip")

            def groups(i, targets):
                main = i is not None
                steps = (0, UNROLL * NH + LAG) if main else (-NH, 0)
                NS = UNROLL * NH if main else 0
                at = lambda L, size, off=0, n=None: (bass.ds(i * (UNROLL * size) + (L * size + off), n or size) if main
                                                     else slice(off, off + (n or size)))
                ENDS = {L * NH + n: L * NCH + qc for L in range(UNROLL) for n, (qc, kb, _) in enumerate(HEAD2)
                        if kb == TPC * (qc + 1) - 1} if main else {}
                items = []
                for L in targets:
                    s0 = (L - 1) * NH
                    for g in range(G):
                        put = [s0 + 3 + (g * N1 + k) * (NH - 8) // (G * N1) for k in range(N1)]
                        items += [(put[k], "max", L, g, k) for k in range(N1)]
                        items += [(put[-1] + 2, "row", L, g, c) for c in range(NCH)]
                items += [(e + 2, "turn", chunk // NCH, 0, chunk) for e, chunk in ENDS.items()]
                items.sort(key=lambda item: item[0])
                AT = {}
                for r, item in enumerate(items):
                    AT.setdefault(item[0], []).append(r)
                TURNS = {it[4]: r for r, it in enumerate(items) if it[1] == "turn"}
                WHERE = {item[1:]: r for r, item in enumerate(items)}

                def pass2(n):
                    qc, kb, q0 = HEAD2[n % NH]
                    return n // NH, n // NH * NCH + qc, qc, kb, q0

                def due(n, lag):
                    return ENDS.get(n - lag)

                def wait_slot(eng, r):
                    eng.wait_ge(slot_free[r % NR], r // NR + 1)

                with nc.Block() as block:
                    @block.sync
                    def _(sp):
                        for n, L in enumerate(targets):
                            if L >= 2:
                                sp.wait_ge(pv, G * (L - 1) * NH)
                            for g in range(G):
                                for r in range(6):
                                    src, dst = at(L, G * DH, g * DH, DH), slice(r * DH, (r + 1) * DH)
                                    sp.dma_start(qs[dst, L % 2, g, :], scratch["q"][Q_ORDER[r], src, :]).then_inc(stack_in[g], 16)
                                    sp.dma_start(ks[dst, L % 2, g, :], scratch["k"][K_ORDER[r], src, :]).then_inc(stack_in[g], 16)
                            for g in range(G):
                                sp.wait_ge(stack_in[g], 16 * 12 * (n + 1))

                    @block.gpsimd
                    def _(pool):
                        for n, L in enumerate(targets):
                            if L >= 2:
                                pool.wait_ge(pv, G * (L - 1) * NH)
                            for g in range(G):
                                nc.gpsimd.memset(qs[MR:MR + 3, L % 2, g, :], 0.0).then_inc(cleared, 1)
                            pool.wait_ge(cleared, G * (n + 1))
                            nc.gpsimd.tensor_copy(vg[:, L % 2, :, :, :], va[:, :, at(L, G), :]).then_inc(v_ready, 1)
                            pool.wait_ge(v_ready, n + 1)

                    @block.tensor
                    def _(pe):
                        def fill(r):
                            _, kind, L, g, k = items[r]
                            n, par = (targets.index(L) if L in targets else 0), L % 2
                            if r >= NR:
                                pe.wait_ge(slot_free[r % NR], r // NR)
                            if kind == "max":
                                if k == 0:
                                    pe.wait_ge(cleared, G * n + g + 1)
                                    pe.wait_ge(stack_in[g], 16 * 12 * (n + 1))
                                qt, kc, w_, diag = PASS1[k]
                                last = nc.tensor.matmul(ring[:, r % NR, 0:w_], qs[:, par, g, qt * P:(qt + 1) * P],
                                                        ks[:, par, g, kc * CH:kc * CH + w_], start=True, stop=not diag)
                                if diag:
                                    last = nc.tensor.matmul(ring[:, r % NR, w_ - P:w_], core.ident_b[:, :], core.hide[:, :], start=False, stop=True)
                            elif kind == "turn":
                                pe.wait_ge(oT_ready, k + 1)
                                for j in range(TPC):
                                    last = nc.tensor.transpose(ring[:, r % NR, j * P:(j + 1) * P], oT[:, j * P:(j + 1) * P], core.ident[:, :])
                            else:
                                pe.wait_ge(split_ready, n * G + g + 1)
                                for j in range(TPC):
                                    last = nc.tensor.matmul(ring[MR:MR + 3, r % NR, j * P:(j + 1) * P], m_split[:, g, k * TPC + j, :],
                                                            core.ident_b[:, :], start=True, stop=True)
                            last.then_inc(filled, 1)

                        def scores(n, g):
                            L, _, qc, kb, q0 = pass2(n)
                            if n % NH == 0 and L in targets:
                                for c in range(NCH - NR, NCH - 1):
                                    wait_slot(pe, WHERE["row", L, g, c])
                                wait_slot(pe, WHERE["row", L, g, NCH - 1])
                            if n:
                                pe.wait_ge(exped, G * (n - 1) + g + 1)
                            q1, w_ = qc * CH + q0, CH - q0
                            diag = kb >= TPC * qc
                            mm = nc.tensor.matmul(psS[:, g, 0:w_], ks[:, L % 2, g, kb * P:(kb + 1) * P], qs[:, L % 2, g, q1:q1 + w_],
                                                  start=True, stop=not diag)
                            if diag:
                                mm = nc.tensor.matmul(psS[:, g, 0:P], core.ident_b[:, :], core.hideT[:, :], start=False, stop=True)
                            mm.then_inc(sc2, 1)

                        def values(n):
                            L, chunk, qc, kb, q0 = pass2(n)
                            if kb == 0 and chunk:
                                pe.wait_ge(oT_ready, chunk)
                            if n % NH == 0 and L in targets:
                                pe.wait_ge(v_ready, targets.index(L) + 1)
                            for g in range(G):
                                pe.wait_ge(exped, G * n + g + 1)
                                nc.tensor.matmul(ps_o[32 * g:32 * g + 32, q0:CH], vg[:, L % 2, kb, g, :], probs[:, (G * n + g) % NPB, 0:CH - q0],
                                                 start=kb == 0, stop=kb == TPC * (qc + 1) - 1).then_inc(pv, 1)

                        if main:
                            for g in range(G):
                                scores(0, g)
                        for n in range(*steps):
                            fills = AT.get(n, [])
                            for g in range(G):
                                if main and n + 1 < NS:
                                    scores(n + 1, g)
                                for r in fills[g * len(fills) // G:(g + 1) * len(fills) // G]:
                                    fill(r)
                            if main and n < NS:
                                values(n)

                    @block.scalar
                    def _(act):
                        def exponentials(n):
                            q0 = pass2(n)[4]
                            for g in range(G):
                                m = G * n + g
                                act.wait_ge(sc2, m + 1)
                                if m >= NPB:
                                    act.wait_ge(pv, m - NPB + 1)
                                nc.scalar.activation(probs[:, m % NPB, 0:CH - q0], psS[:, g, 0:CH - q0], ACT.Exp, scale=SC).then_inc(exped, 1)

                        if main:
                            exponentials(0)
                        for n in range(*steps):
                            if (chunk := due(n, 1)) is not None:
                                act.wait_ge(pv, G * n)
                                if chunk:
                                    act.wait_ge(filled, TURNS[chunk - 1] + 1)
                                nc.scalar.activation(oT[:, :], ps_o[:, :], ACT.Copy).then_inc(oT_ready, 1)
                            if main and n + 1 < NS:
                                exponentials(n + 1)

                    @block.vector
                    def _(dve):
                        st = Steps(dve, dve_step)

                        def maxima(g):
                            st.run(nc.vector.tensor_reduce(m_neg[:, :], m_part[:, :, :], axis=AX.X, op=ALU.max, negate=True))
                            st.run(nc.vector.tensor_copy(m_split[:, g, :, 0], m_neg[:, :]))
                            st.run(nc.vector.tensor_tensor(m_rest[:, :], m_neg[:, :], m_split[:, g, :, 0], ALU.subtract))
                            st.run(nc.vector.tensor_copy(m_split[:, g, :, 1], m_rest[:, :]))
                            st.run(nc.vector.tensor_tensor(m_neg[:, :], m_rest[:, :], m_split[:, g, :, 1], ALU.subtract))
                            st.run(nc.vector.tensor_copy(m_split[:, g, :, 2], m_neg[:, :]))
                            dve.sem_inc(split_ready, 1)

                        def take(r):
                            _, kind, L, g, k = items[r]
                            dve.wait_ge(filled, r + 1)
                            if kind == "turn":
                                output(r)
                                return
                            if kind == "row":
                                nc.vector.tensor_copy(qs[MR:MR + 3, L % 2, g, k * CH:(k + 1) * CH], ring[MR:MR + 3, r % NR, :]).then_inc(slot_free[r % NR], 1)
                                return
                            qt, kc, w_, _ = PASS1[k]
                            nc.vector.tensor_reduce(m_part[:, qt, kc:kc + 1], ring[:, r % NR, 0:w_], axis=AX.X, op=ALU.max).then_inc(slot_free[r % NR], 1)
                            if k == N1 - 1:
                                for kk in range(N1 - NR, N1 - 1):
                                    wait_slot(dve, WHERE["max", L, g, kk])
                                wait_slot(dve, r)
                                maxima(g)

                        def output(r):
                            _, _, L, _, chunk = items[r]
                            qc, turned = chunk % NCH, ring[:, r % NR, :].rearrange("p (t g d) -> p t g d", t=TPC, g=G)
                            nc.vector.reciprocal(rden[:, :, :].unsqueeze(3), turned[:, :, :, DH:DH + 1]).then_inc(recip, 1)
                            dve.wait_ge(recip, chunk + 1)
                            dst = o_all[:, qc * TPC:(qc + 1) * TPC, at(L, G * DH)].rearrange("p t (g d) -> p t g d", g=G)
                            nc.vector.tensor_tensor(dst, turned[:, :, :, 0:DH], rden[:, :, :].unsqueeze(3).to_broadcast([P, TPC, G, DH]), ALU.mult).then_inc(slot_free[r % NR], 1)
                            wait_slot(dve, r)

                        for n in range(*steps):
                            for r in AT.get(n, ()):
                                take(r)

            with nc.Block() as block:
                @block.gpsimd
                def _(pool):
                    nc.gpsimd.memset(ks[:, 1, :, :], 0.0).then_inc(zeroed, 1)
                    nc.gpsimd.memset(m_part[:, :, :], -3.0e38).then_inc(zeroed, 1)
                    pool.wait_ge(zeroed, 2)
                    nc.gpsimd.memset(ks[MR:MR + 3, 1, :, :], 1.0).then_inc(zeroed, 1)

                @block.vector
                def _(dve):
                    st = Steps(dve, dve_step)
                    st.run(nc.vector.memset(ks[:, 0, :, :], 0.0))
                    st.run(nc.vector.memset(ks[MR:MR + 3, 0, :, :], 1.0))
            q.restart()
            groups(None, [0])
            with nc.Fori(0, NG // UNROLL) as i:
                q.restart()
                groups(i, list(range(1, UNROLL + 1)))

        stage_project(nc, core, tag + "_out", o_all, w_out)


def stage_project(nc, core, tag, o_all, w_out):
    with Stage(nc, tag) as s:
        oT = s.sb("oT", [P, 2, CH])
        ps_t, ps_y = s.ps("ps_turned", [P, 2, CH]), s.ps("ps_y", [P, 2, TPC, D])
        turned, ready, done, added = s.sem("turned"), s.sem("oT_ready"), s.sem("y_done"), s.sem("x_added")
        with nc.Block() as block:
            @block.tensor
            def _(pe):
                def turn(c):
                    if c >= 2:
                        pe.wait_ge(ready, c - 1)
                    for j in range(TPC):
                        last = nc.tensor.transpose(ps_t[:, c % 2, j * P:(j + 1) * P], o_all[:, c * TPC + j, :], core.ident[:, :])
                    last.then_inc(turned, 1)

                turn(0)
                for c in range(NCH):
                    if c + 1 < NCH:
                        turn(c + 1)
                    pe.wait_ge(ready, c + 1)
                    if c >= 2:
                        pe.wait_ge(added, c - 1)
                    for j in range(TPC):
                        last = nc.tensor.matmul(ps_y[:, c % 2, j, :], oT[:, c % 2, j * P:(j + 1) * P], w_out[:, :], start=True, stop=True)
                    last.then_inc(done, 1)

            @block.scalar
            def _(act):
                for c in range(NCH):
                    act.wait_ge(turned, c + 1)
                    if c >= 2:
                        act.wait_ge(done, c - 1)
                    nc.scalar.activation(oT[:, c % 2, :], ps_t[:, c % 2, :], ACT.Copy).then_inc(ready, 1)

            @block.vector
            def _(dve):
                for c in range(NCH):
                    dve.wait_ge(done, c + 1)
                    tiles = slice(c * TPC, (c + 1) * TPC)
                    nc.vector.tensor_tensor(core.x[:, tiles, :], core.x[:, tiles, :], ps_y[:, c % 2, :, :], ALU.add).then_inc(added, 1)
                dve.wait_ge(added, NCH)


def stage_power_attention(nc, core, tag, Wq, WqS, Wk, WkS, Wv, Wg, Wp, lnw, cosT, sinT, before):
    HK, R, DH = 8, 2, 64
    SC = DH ** -0.5
    M = DH + 1
    TINY = 2.0 ** -60
    PASS1 = [(qt, kc, min(CH, (qt + 1) * P - kc * CH), (qt // TPC) == kc) for qt in range(NT) for kc in range(qt // TPC + 1)]
    HEAD2 = [(qc, kb, max(0, kb * P - qc * CH)) for qc in range(NCH) for kb in range(TPC * (qc + 1))]
    N1, NH = len(PASS1), len(HEAD2)
    NPB = 6
    NO = 1
    NR, NS = 3, 3
    LAG = 8
    FOFF = [0] + [CH + sum(CH - jj * P for jj in range(j)) for j in range(TPC)]
    FLEN = CH + sum(CH - j * P for j in range(TPC))
    NEXP = lambda g: TPC + (1 if g % NCH else 0)
    UNROLL = 2
    HB = UNROLL * R

    with Stage(nc, tag) as s:
        HP = HK + 1
        wq, wqs = s.sb("wq", [P, HP * R * DH]), s.sb("wq_swapped", [P, HP * R * DH])
        wk, wks, wv = s.sb("wk", [P, HP * DH]), s.sb("wk_swapped", [P, HP * DH]), s.sb("wv", [P, HP * DH])
        wp = s.sb("w_proj", [DH + 1, HK * R, D])
        lw = s.sb("ln_w", [DH, 1])
        cos, sin = s.sb("cos", [P, T]), s.sb("sin", [P, T])
        wg, loaded = s.sb("wg", [P, HK]), s.sem("loaded")
        issue_loads(nc, [(dst[:, 0:src.shape[1]], src) for dst, src in
                         ((wq, Wq), (wqs, WqS), (wk, Wk), (wks, WkS), (wv, Wv), (wg, Wg), (cos, cosT), (sin, sinT), (lw, lnw))], loaded)
        before()
        gcol, gend = s.sb("gate_col", [P, NT, HP]), s.sb("gate_tile_end", [P, NT, HP])
        later = s.sb("later_tiles", [P, NT, NT])
        tri = s.sb("tri_qk", [P, P])
        eps_col = s.sb("eps_decayed", [P, NT, HP])
        center = s.sb("center", [M, M])
        mean_col, den_bias = s.sb("mean_col", [M, 1]), s.sb("den_bias", [M, 1])
        f_dram = nc.dram_tensor(f"{tag}_decay", (HK + 1, T), F32, kind="Internal").ap()
        with Stage(nc, tag + "_in") as q:
            v, e, l, g = (q.sb(n, [HK, T]) for n in ("v", "e", "l", "g"))
            one, last_row = q.sb("one", [HK, T]), q.sb("last_row", [P, P])
            ps_z, ps_g, ps_e = q.ps("ps_z", [HK, 2, CH]), q.ps("ps_g", [P, NT, HK]), q.ps("ps_e", [P, NT, HP])
            dve_step, pool_step = q.sem("dve_step"), q.sem("pool_step")
            z_done, z_out, v_ready, abs_done, exp_done, ln_done = (q.sem(n) for n in ("z_done", "z_out", "v_ready", "abs_done", "exp_done", "ln_done"))
            g_ready, f_ready, f_exp, stored, g_turned, gcol_ready, e_done = (q.sem(n) for n in ("g_ready", "f_ready", "f_exp", "stored", "g_turned", "gcol_ready", "e_done"))
            eps_in, eps_exp = q.sem("eps_in"), q.sem("eps_exp")
            NLOAD = 10
            with nc.Block() as block:
                @block.sync
                def _(sp):
                    sp.wait_ge(pool_step, 1)
                    sp.dma_start(wp[0:DH, :, :], Wp.rearrange("(h d) n -> d h n", d=DH)).then_inc(loaded, 16)
                    sp.wait_ge(loaded, 16 * NLOAD)
                    sp.wait_ge(f_exp, 1)
                    sp.dma_start(f_dram[0:HK, :], e[:, :]).then_inc(stored, 16)
                    sp.dma_start(f_dram[HK:HK + 1, :], e[0:1, :]).then_inc(stored, 16)
                    sp.wait_ge(stored, 32)

                @block.gpsimd
                def _(pool):
                    st = Steps(pool, pool_step)
                    st.run(nc.gpsimd.memset(wp[:, :, :], 0.0))
                    st.run(nc.gpsimd.memset(one[:, :], 1.0))
                    st.run(nc.gpsimd.memset(later[:, :, :], 0.0))
                    st.run(nc.gpsimd.affine_select(out=later[:, :, :], in_=later[:, :, :], compare_op=ALU.is_ge, fill=MASKED, base=0,
                                                   pattern=[[1, NT], [-1, NT]], channel_multiplier=0))
                    st.run(nc.gpsimd.memset(tri[:, :], 1.0))
                    st.run(nc.gpsimd.affine_select(out=tri[:, :], in_=tri[:, :], compare_op=ALU.is_ge, fill=0.0, base=0,
                                                   pattern=[[-1, P]], channel_multiplier=1))
                    st.run(nc.gpsimd.memset(mean_col[0:DH, :], 1.0 / DH))
                    st.run(nc.gpsimd.memset(mean_col[DH:M, :], 1e-9))
                    for w, n in ((wq, R * DH), (wqs, R * DH), (wk, DH), (wks, DH), (wv, DH)):
                        st.run(nc.gpsimd.memset(w[:, HK * n:HP * n], 0.0))
                    st.run(nc.gpsimd.memset(gcol[:, :, HK:HP], 0.0))

                @block.tensor
                def _(pe):
                    pe.wait_ge(loaded, 16 * NLOAD)
                    for c in range(NCH):
                        if c >= 2:
                            pe.wait_ge(z_out, c - 1)
                        nc.tensor.matmul(ps_z[:, c % 2, :], wg[:, :], core.xT[:, c * CH:(c + 1) * CH], start=True, stop=True).then_inc(z_done, 1)
                    pe.wait_ge(g_ready, 1)
                    for t in range(NT):
                        last = nc.tensor.transpose(ps_g[:, t, :], g[:, t * P:(t + 1) * P], core.ident[0:HK, 0:HK])
                    last.then_inc(g_turned, 1)
                    pe.wait_ge(gcol_ready, 1)
                    nc.tensor.matmul(ps_e[:, :, :].rearrange("p t h -> p (t h)"), last_row[:, :], gcol[:, :, :].rearrange("p t h -> p (t h)"),
                                     start=True, stop=True).then_inc(e_done, 1)

                @block.scalar
                def _(act):
                    act.wait_ge(v_ready, 1)
                    nc.scalar.activation(l[:, :], v[:, :], ACT.Abs).then_inc(abs_done, 1)
                    act.wait_ge(abs_done, 1)
                    nc.scalar.activation(e[:, :], l[:, :], ACT.Exp, scale=-1.0).then_inc(exp_done, 1)
                    act.wait_ge(exp_done, 1)
                    nc.scalar.activation(l[:, :], e[:, :], ACT.Ln, bias=1.0).then_inc(ln_done, 1)
                    act.wait_ge(f_ready, 1)
                    nc.scalar.activation(e[:, :], e[:, :], ACT.Exp).then_inc(f_exp, 1)
                    act.wait_ge(eps_in, 1)
                    nc.scalar.activation(eps_col[:, :, :], eps_col[:, :, :], ACT.Exp).then_inc(eps_exp, 1)

                @block.vector
                def _(dve):
                    st = Steps(dve, dve_step)
                    dve.wait_ge(loaded, 16 * NLOAD)
                    dve.wait_ge(pool_step, 14)
                    st.add(nc.vector.tensor_scalar(wp[0:DH, :, :], wp[0:DH, :, :], lw[:, 0:1], None, ALU.mult))
                    st.add(nc.vector.tensor_copy(last_row[:, :], core.ident[:, P - 1:P].to_broadcast([P, P])))
                    st.add(nc.vector.tensor_scalar(den_bias[:, :], core.ident[0:M, DH:M], 1e-6, None, ALU.mult))
                    st.run(nc.vector.tensor_copy(center[:, :], core.ident[0:M, 0:M]))
                    st.add(nc.vector.tensor_scalar(center[0:DH, 0:DH], center[0:DH, 0:DH], -1.0 / DH, None, ALU.add))
                    for c in range(NCH):
                        dve.wait_ge(z_done, c + 1)
                        nc.vector.tensor_scalar(v[:, c * CH:(c + 1) * CH], ps_z[:, c % 2, :], 6.906768, None, ALU.add).then_inc(z_out, 1)
                    dve.wait_ge(z_out, NCH)
                    dve.sem_inc(v_ready, 1)
                    dve.wait_ge(exp_done, 1)
                    st.run(nc.vector.tensor_scalar(g[:, :], e[:, :], 1.0, -1.0, ALU.add, ALU.add))
                    st.run(nc.vector.tensor_tensor(g[:, :], e[:, :], g[:, :], ALU.subtract))
                    dve.wait_ge(ln_done, 1)
                    st.run(nc.vector.tensor_tensor(g[:, :], g[:, :], l[:, :], ALU.add))
                    st.run(nc.vector.scalar_tensor_tensor(out=v[:, :], in0=v[:, :], scalar=0.0, in1=g[:, :], op0=ALU.min, op1=ALU.subtract))
                    st.run(nc.vector.tensor_tensor_scan(l[:, :], one[:, :], v[:, :], 0.0, ALU.mult, ALU.add))
                    st.run(nc.vector.tensor_scalar(g[:, :], l[:, :], 0.5, None, ALU.mult))
                    dve.sem_inc(g_ready, 1)
                    by_tile = g[:, :].rearrange("h (t p) -> h t p", p=P)
                    nc.vector.tensor_tensor(e[:, :].rearrange("h (t p) -> h t p", p=P), by_tile[:, :, P - 1:P].to_broadcast([HK, NT, P]), by_tile,
                                            ALU.subtract).then_inc(f_ready, 1)
                    dve.wait_ge(g_turned, 1)
                    nc.vector.tensor_copy(gcol[:, :, 0:HK], ps_g[:, :, :]).then_inc(gcol_ready, 1)
                    dve.wait_ge(e_done, 1)
                    st.run(nc.vector.tensor_copy(gend[:, :, :], ps_e[:, :, :]))
                    nc.vector.tensor_tensor(eps_col[:, :, :], gend[:, :, :], gcol[:, :, :], ALU.subtract).then_inc(eps_in, 1)
                    dve.wait_ge(eps_exp, 1)
                    st.run(nc.vector.tensor_scalar(eps_col[:, :, :], eps_col[:, :, :], 1e-30, None, ALU.mult))

        with Stage(nc, tag + "_heads") as q:
            F32R = mybir.dt.float32r
            wq_h = [q.sb(f"wq_head{hh}", [P, 2, DH]) for hh in range(R)]
            wqs_h = [q.sb(f"wq_swapped_head{hh}", [P, 2, DH]) for hh in range(R)]
            wk_h, wks_h = q.sb("wk_head", [P, 2, DH]), q.sb("wk_swapped_head", [P, 2, DH])
            ge, nge, eps_d = (q.sb(n, [P, 2, NT]) for n in ("gate_end", "minus_gate_end", "eps_decayed_head"))
            c_col = q.sb("earlier_factor", [P, 2, NCH - 1, NT])
            c_eps = q.sb("earlier_eps", [P, 2, NCH - 1, NT])
            k_hl = q.sb("k_hi_lo", [P, 2, T], F32R)
            va = q.sb("v_aug", [P, 2, NT, M])
            decay, kd, k_hi = q.sb("decay", [P, T]), q.sb("k_decayed", [P, 2, CH]), q.sb("k_hi", [P, 2, CH], F32R)
            q_hi, q_lo = q.sb("q_hi", [P, R, T], F32R), q.sb("q_lo", [P, R, T], F32R)
            m_row = q.sb("max_row", [P, R, T], BF16)
            t1, t2, rot = (q.sb(n, [P, 2, CH]) for n in ("rope_plain", "rope_swapped", "rotated"))
            m_abs = q.sb("max_abs", [P, NT, NT])
            l1, l2 = q.sb("log_a", [P, NT, NT]), q.sb("log_b", [P, NT, NT])
            scrap = q.sb("masked_scores", [P, P])
            m_neg, m_rest = q.sb("max_neg", [P, NT]), q.sb("max_rest", [P, NT])
            m_split = q.sb("max_split", [P, NT, 3], BF16)
            fac = q.sb("factors", [P, 2, FLEN])
            sabs, probs = (q.sb(n, [P, NPB, CH]) for n in ("scores_abs", "probs"))
            oT, cT, sq = q.sb("oT", [M, CH]), q.sb("centered_T", [M, CH]), q.sb("squares_T", [M, CH])
            uu, rs, yy = (q.sb(n, [P, TPC]) for n in ("var", "rstd", "newton_term"))
            ring, psS, psO = q.ps("ps_ring", [P, NR, CH]), q.ps("ps_scores", [P, NS, CH]), q.ps("ps_out", [P, NO, CH])
            psC = q.ps("ps_center_final", [P, TPC, D])
            zeroed, dve_step, newton = q.sem("zeroed"), q.sem("dve_step"), q.sem("newton_step")
            w_ready, decay_in, t_done, rotated = (q.sem(n) for n in ("weights_ready", "decay_in", "rope_products", "rotated"))
            kd_out, rounded, split = (q.sem(n) for n in ("k_decayed", "rounded", "operand_split"))
            cols_in, c_exp, cols_ready = (q.sem(n) for n in ("cols_in", "c_exp", "cols_ready"))
            filled, slot_free = q.sem("ring_filled"), [q.sem(f"ring_free{b}") for b in range(NR)]
            max_done, ln_in, ln_out, split_ready = (q.sem(n) for n in ("pass1_max", "ln_in", "ln_out", "max_split"))
            f_done, f_masked = q.sem("factor_exp"), q.sem("factor_masked")
            sc2, abs_done, b_done, a_done, pv = (q.sem(n) for n in ("pass2_scored", "scores_abs", "product", "squared", "pv_done"))
            oT_ready, centered, cT_ready, added = (q.sem(n) for n in ("oT_ready", "centered", "cT_ready", "x_added"))
            u_ready, rs_ready = q.sem("var_ready"), q.sem("rstd_ready")

            def heads(i, targets):
                main = i is not None
                steps = (0, HB * NH + LAG) if main else (-NH, 0)
                N2 = HB * NH if main else 0
                at = lambda u, size, off=0, n=None: (bass.ds(i * (UNROLL * size) + (u * size + off), n or size) if main
                                                     else slice(off, off + (n or size)))
                START = {g: (g // NCH) * NH + HEAD2.index((g % NCH, 0, 0)) for g in range(-NCH, (HB + 1) * NCH)}
                ENDS = {START[g + 1] - 1: g for g in range(HB * NCH)} if main else {}
                cast_at = lambda g: max(steps[0], START[g] - (5 if g % NCH == 0 else 6))
                items, pairs = [], []
                for L in targets:
                    s0 = (L - 1) * NH
                    new_k = L % R == 0
                    todo = [(kind, c) for c in range(NCH) for kind in ("kq" if new_k else "q")]
                    for d, (kind, c) in enumerate(todo):
                        step = s0 + d * 12 // len(todo)
                        pairs.append((step, kind, L, c))
                        items += [(step, kind, L, c, 0), (step, kind, L, c, 1)]
                    if new_k:
                        items += [(s0 + 15 + 4 * c, "v", L, c, 0) for c in range(NCH)]
                    ready = {p[3]: p[0] + 3 for p in pairs if p[1:3] == ("q", L)}
                    items += [(max(s0 + 4 + k * (NH - 16) // N1, ready[PASS1[k][0] // TPC]), "max", L, k, 0) for k in range(N1)]
                    items += [(s0 + NH - 8, "row", L, c, 0) for c in range(NCH)]
                    items += [(cast_at(L * NCH), "bcast", L, 0, 0)]
                    if L < HB and main:
                        items += [(cast_at(L * NCH + c), "bcast", L, c, 0) for c in range(1, NCH)]
                if main:
                    items += [(cast_at(c), "bcast", 0, c, 0) for c in range(1, NCH)]
                items += [(e + 5, "fin", g // NCH, g, 0) for e, g in ENDS.items()]
                items.sort(key=lambda item: item[0])
                AT = {}
                for r, item in enumerate(items):
                    AT.setdefault(item[0], []).append(r)
                PAIR = {p[1:]: j for j, p in enumerate(pairs)}
                ROUNDS = [0]
                for p in pairs:
                    ROUNDS.append(ROUNDS[-1] + (2 if p[1] == "k" else 1))
                FINS = {it[3]: r for r, it in enumerate(items) if it[1] == "fin"}
                new_ks = [L for L in targets if L % R == 0]
                chunks = [it[2] * NCH + it[3] for it in items if it[1] == "bcast"]
                diagonals = [r for r, it in enumerate(items) if it[1] == "max" and PASS1[it[3]][3]]

                def pass2(n):
                    qc, kb, q0 = HEAD2[n % NH]
                    return n // NH, n // NH * NCH + qc, qc, kb, q0, kb >= TPC * qc

                def due(n, lag):
                    return ENDS.get(n - lag)

                def exps(g):
                    return sum(NEXP(gg) for gg in chunks[:chunks.index(g)])

                with nc.Block() as block:
                    @block.sync
                    def _(sp):
                        for n, L in enumerate(new_ks):
                            if n:
                                sp.wait_ge(kd_out, n * NCH)
                            sp.dma_start(decay[:, :], f_dram[at(L // R, 1), :].partition_broadcast(P)).then_inc(decay_in, 16)
                            sp.wait_ge(decay_in, 16 * (n + 1))

                    @block.gpsimd
                    def _(pool):
                        def head_weights(L):
                            u, used = L // R, [r for r, it in enumerate(items) if it[1] in "kq" and it[2] < L]
                            if used:
                                pool.wait_ge(filled, used[-1] + 1)
                            twice = lambda w, cols: w[:, cols].unsqueeze(1).to_broadcast([P, 2, DH])
                            nc.gpsimd.tensor_copy(wk_h[:, :, :], twice(wk, at(u, DH))).then_inc(w_ready, 1)
                            nc.gpsimd.tensor_copy(wks_h[:, :, :], twice(wks, at(u, DH))).then_inc(w_ready, 1)
                            for hh in range(R):
                                nc.gpsimd.tensor_copy(wq_h[hh][:, :, :], twice(wq, at(u, P, hh * DH, DH))).then_inc(w_ready, 1)
                                nc.gpsimd.tensor_copy(wqs_h[hh][:, :, :], twice(wqs, at(u, P, hh * DH, DH))).then_inc(w_ready, 1)

                        def rotate(j):
                            _, kind, L, c = pairs[j]
                            cs = slice(c * CH, (c + 1) * CH)
                            pool.wait_ge(t_done, 2 * j + 2)
                            if j >= 2:
                                pool.wait_ge(split, j - 1)
                            nc.gpsimd.tensor_tensor(rot[:, j % 2, :], t1[:, j % 2, :], t2[:, j % 2, :], ALU.add).then_inc(rotated, 1)
                            if kind == "k":
                                pool.wait_ge(rotated, j + 1)
                                pool.wait_ge(decay_in, 16 * (new_ks.index(L) + 1))
                                nc.gpsimd.tensor_tensor(kd[:, c % 2, :], rot[:, j % 2, :], decay[:, cs], ALU.mult).then_inc(kd_out, 1)

                        def low_half(j):
                            _, kind, L, c = pairs[j]
                            cs = slice(c * CH, (c + 1) * CH)
                            pool.wait_ge(rounded, ROUNDS[j + 1])
                            if kind == "k":
                                later_k = pairs[j + 1][1] == "k"
                                pool.wait_ge(rotated, j + 2)
                                pool.wait_ge(kd_out, new_ks.index(L) * NCH + c + (2 if later_k else 1))
                                out, whole, hi = k_hl[DH:P, L // R % 2, cs], kd[DH:P, c % 2, :], k_hi[DH:P, c % 2, :]
                            else:
                                out, whole, hi = q_lo[:, L % R, cs], rot[:, j % 2, :], q_hi[:, L % R, cs]
                            nc.gpsimd.tensor_tensor(out, whole, hi.bitcast(F32), ALU.subtract).then_inc(split, 1)
                            if kind == "k":
                                pool.wait_ge(split, j + 1)

                        def mask_factors(g):
                            for j in range(TPC):
                                pool.wait_ge(f_done, exps(g) + (1 if g % NCH else 0) + j + 1)
                                part = fac[:, g % 2, FOFF[1 + j]:FOFF[1 + j] + P]
                                nc.gpsimd.affine_select(out=part, in_=part, compare_op=ALU.is_ge, fill=0.0, base=0,
                                                        pattern=[[1, P]], channel_multiplier=-1).then_inc(f_masked, 1)

                        def root(g):
                            pool.wait_ge(u_ready, g + 1)
                            st = Steps(pool, newton, g * 12)
                            for _ in range(3):
                                st.run(nc.gpsimd.tensor_tensor(yy[:, :], rs[:, :], rs[:, :], ALU.mult))
                                st.run(nc.gpsimd.tensor_tensor(yy[:, :], yy[:, :], uu[:, :], ALU.mult))
                                st.run(nc.gpsimd.tensor_scalar(yy[:, :], yy[:, :], -0.5, 1.5, ALU.mult, ALU.add))
                                st.run(nc.gpsimd.tensor_tensor(rs[:, :], rs[:, :], yy[:, :], ALU.mult))
                            pool.sem_inc(rs_ready, 1)

                        todo = [((L - 1) * NH - 2, 0, head_weights, L) for L in new_ks]
                        todo += [(p[0], 1, rotate, j) for j, p in enumerate(pairs)]
                        todo += [(p[0] + 1, 2, low_half, j) for j, p in enumerate(pairs)]
                        todo += [(cast_at(g), 3, mask_factors, g) for g in chunks]
                        todo += [(e + 5.5, 4, root, g) for e, g in ENDS.items()]
                        for _, _, task, arg in sorted(todo, key=lambda t: t[:2]):
                            task(arg)

                    @block.tensor
                    def _(pe):
                        def fill(r):
                            _, kind, L, k, twin = items[r]
                            hh, u = L % R, L // R
                            out = ring[:, r % NR, :]
                            if r >= NR:
                                pe.wait_ge(slot_free[r % NR], r // NR)
                            if kind in "kq":
                                if kind == "k" and k == 0:
                                    pe.wait_ge(w_ready, (2 + 2 * R) * (new_ks.index(L) + 1))
                                w = ((wk_h, wks_h) if kind == "k" else (wq_h[hh], wqs_h[hh]))[twin]
                                last = nc.tensor.matmul(out, w[:, :, :].rearrange("p r d -> p (r d)"), core.xT[:, k * CH:(k + 1) * CH],
                                                        start=True, stop=True)
                            elif kind == "v":
                                for j in range(TPC):
                                    t = k * TPC + j
                                    last = nc.tensor.matmul(out[:, j * DH:(j + 1) * DH], core.xT[:, t * P:(t + 1) * P], wv[:, at(u, DH)],
                                                            start=True, stop=True)
                            elif kind == "max":
                                qt, kc, w_, _ = PASS1[k]
                                pe.wait_ge(split, PAIR["q", L, qt // TPC] + 1)
                                keys = k_hl[:, u % 2, kc * CH:kc * CH + w_]
                                last = nc.tensor.matmul(out[:, 0:w_], q_hi[:, hh, qt * P:(qt + 1) * P], keys, start=True, stop=True)
                            elif kind == "row":
                                pe.wait_ge(split_ready, targets.index(L) + 1)
                                for j in range(TPC):
                                    last = nc.tensor.matmul(out[0:3, j * P:(j + 1) * P], m_split[:, k * TPC + j, :], core.ident_b[:, :],
                                                            start=True, stop=True)
                            elif kind == "fin":
                                last = final(k, out)
                            else:
                                rows = [rr for rr in range(r) if items[rr][1] == "row" and items[rr][2] == L]
                                for rr in rows[-NR:]:
                                    pe.wait_ge(slot_free[rr % NR], rr // NR + 1)
                                last = nc.tensor.matmul(out, core.ones_b[:, :], m_row[:, hh, k * CH:(k + 1) * CH], start=True, stop=True)
                            last.then_inc(filled, 1)

                        def scores(n):
                            L, g, qc, kb, q0, _ = pass2(n)
                            if n >= NS:
                                pe.wait_ge(abs_done, n - NS + 1)
                            q1, w_ = qc * CH + q0, CH - q0
                            keys = k_hl[:, L // R % 2, kb * P:(kb + 1) * P]
                            nc.tensor.matmul(psS[:, n % NS, 0:w_], keys, q_hi[:, L % R, q1:q1 + w_], start=True, stop=False)
                            nc.tensor.matmul(psS[:, n % NS, 0:w_], keys, q_lo[:, L % R, q1:q1 + w_], start=False, stop=True).then_inc(sc2, 1)

                        def values(n):
                            L, g, qc, kb, q0, _ = pass2(n)
                            if kb == 0 and g >= NO:
                                pe.wait_ge(oT_ready, g - NO + 1)
                            pe.wait_ge(a_done, n + 1)
                            nc.tensor.matmul(psO[0:M, g % NO, q0:CH], va[:, L // R % 2, kb, :], probs[:, n % NPB, 0:CH - q0],
                                             start=kb == 0, stop=kb == TPC * (qc + 1) - 1).then_inc(pv, 1)

                        def center_values(g):
                            pe.wait_ge(oT_ready, g + 1)
                            pe.wait_ge(added, g)
                            nc.tensor.matmul(psC[0:M, :, :].rearrange("p t d -> p (t d)"), center[:, :], oT[:, :], start=True, stop=True).then_inc(centered, 1)

                        def final(g, columns):
                            pe.wait_ge(cT_ready, 2 * g + 2)
                            L = g // NCH
                            for j in range(TPC):
                                js = slice(j * P, (j + 1) * P)
                                nc.tensor.matmul(psC[:, j, :], cT[:, js], wp[:, at(L // R, R, L % R, 1), :], start=True, stop=True)
                                last = nc.tensor.matmul(columns[:, j:j + 1], sq[:, js], mean_col[:, :], start=True, stop=True)
                            return last

                        if main:
                            for n in range(NS):
                                scores(n)
                        for n in range(*steps):
                            if main and n + NS < N2:
                                scores(n + NS)
                            fills = AT.get(n, [])
                            for r in fills[:len(fills) // 2]:
                                fill(r)
                            if main and n < N2:
                                values(n)
                            for r in fills[len(fills) // 2:]:
                                fill(r)
                            if (g := due(n, 3)) is not None:
                                center_values(g)

                    @block.scalar
                    def _(act):
                        def key_factors(L):
                            kp = L // R % 2
                            act.wait_ge(cols_in, new_ks.index(L) + 1)
                            for qc in range(1, NCH):
                                nc.scalar.activation(c_col[:, kp, qc - 1, 0:qc * TPC], ge[:, kp, 0:qc * TPC], ACT.Exp, scale=-1.0,
                                                     bias=ge[:, kp, qc * TPC - 1:qc * TPC]).then_inc(c_exp, 1)

                        def high_half(j):
                            _, kind, L, c = pairs[j]
                            cs = slice(c * CH, (c + 1) * CH)
                            if kind == "k":
                                n = new_ks.index(L) * NCH + c
                                act.wait_ge(kd_out, n + 1)
                                if c >= 2:
                                    act.wait_ge(split, j - 1)
                                nc.scalar.activation(k_hi[:, c % 2, :], kd[:, c % 2, :], ACT.Copy).then_inc(rounded, 1)
                                nc.scalar.activation(k_hl[0:DH, L // R % 2, cs], kd[0:DH, c % 2, :], ACT.Copy).then_inc(rounded, 1)
                            else:
                                act.wait_ge(rotated, j + 1)
                                nc.scalar.activation(q_hi[:, L % R, cs], rot[:, j % 2, :], ACT.Copy).then_inc(rounded, 1)

                        def take_values(r):
                            _, _, L, c, _ = items[r]
                            act.wait_ge(filled, r + 1)
                            src = ring[:, r % NR, 0:TPC * DH].rearrange("p (t d) -> p t d", d=DH)
                            nc.scalar.activation(va[:, L // R % 2, c * TPC:(c + 1) * TPC, 0:DH], src, ACT.Copy).then_inc(slot_free[r % NR], 1)

                        def logarithms(L):
                            n = targets.index(L)
                            act.wait_ge(ln_in, 2 * n + 1)
                            nc.scalar.activation(l1[:, :, :], l1[:, :, :], ACT.Ln).then_inc(ln_out, 1)
                            act.wait_ge(ln_in, 2 * n + 2)
                            nc.scalar.activation(l2[:, :, :], l2[:, :, :], ACT.Ln).then_inc(ln_out, 1)

                        def factors(r):
                            _, _, L, qc, _ = items[r]
                            g, kp = L * NCH + qc, L // R % 2
                            act.wait_ge(filled, r + 1)
                            if main and g >= 2:
                                act.wait_ge(b_done, START[g - 1])
                                act.wait_ge(f_masked, TPC * chunks.index(g))
                            if qc:
                                nc.scalar.activation(fac[:, g % 2, 0:CH], ring[:, r % NR, :], ACT.Exp,
                                                     bias=nge[:, kp, qc * TPC - 1:qc * TPC]).then_inc(f_done, 1)
                            for j in range(TPC):
                                nc.scalar.activation(fac[:, g % 2, FOFF[1 + j]:FOFF[1 + j] + CH - j * P], ring[:, r % NR, j * P:CH], ACT.Exp,
                                                     bias=nge[:, kp, qc * TPC + j:qc * TPC + j + 1]).then_inc(f_done, 1)
                            act.wait_ge(f_done, exps(g) + NEXP(g))
                            act.sem_inc(slot_free[r % NR], 1)

                        def absolute(n):
                            L, g, qc, kb, q0, own = pass2(n)
                            w_, kp = CH - q0, L // R % 2
                            act.wait_ge(sc2, n + 1)
                            if L in new_ks and L < HB:
                                act.wait_ge(cols_ready, new_ks.index(L) + 1)
                            nc.scalar.activation(sabs[:, n % NPB, 0:w_], psS[:, n % NS, 0:w_], ACT.Abs,
                                                 scale=SC if own else c_col[:, kp, qc - 1, kb:kb + 1]).then_inc(abs_done, 1)

                        def square(n):
                            q0 = pass2(n)[4]
                            act.wait_ge(b_done, n + 1)
                            if n >= NPB:
                                act.wait_ge(pv, n - NPB + 1)
                            nc.scalar.activation(probs[:, n % NPB, 0:CH - q0], sabs[:, n % NPB, 0:CH - q0], ACT.Square).then_inc(a_done, 1)

                        if main:
                            for n in range(NS):
                                absolute(n)
                            square(0)
                        for n in range(*steps):
                            if (g := due(n, 1)) is not None:
                                act.wait_ge(pv, n)
                                act.wait_ge(centered, g)
                                nc.scalar.activation(oT[:, :], psO[0:M, g % NO, :], ACT.Copy).then_inc(oT_ready, 1)
                            if main and n + 1 < N2:
                                square(n + 1)
                            if main and n + NS < N2:
                                absolute(n + NS)
                            for L in new_ks:
                                if n == (L - 1) * NH + 1:
                                    key_factors(L)
                            for j, p in enumerate(pairs):
                                if p[0] + 1 == n:
                                    high_half(j)
                            for L in targets:
                                if n == L * NH - 10:
                                    logarithms(L)
                            for r in AT.get(n, ()):
                                if items[r][1] == "v":
                                    take_values(r)
                                if items[r][1] == "bcast":
                                    factors(r)
                            if (g := due(n, 4)) is not None:
                                act.wait_ge(centered, g + 1)
                                if g:
                                    act.wait_ge(filled, FINS[g - 1] + 1)
                                centred = psC[0:M, :, :].rearrange("p t d -> p (t d)")
                                nc.scalar.activation(cT[:, :], centred, ACT.Copy).then_inc(cT_ready, 1)
                                nc.scalar.activation(sq[:, :], centred, ACT.Square, bias=den_bias[:, :]).then_inc(cT_ready, 1)

                    @block.vector
                    def _(dve):
                        st = Steps(dve, dve_step)

                        def key_columns(L):
                            kp, col = L // R % 2, at(L // R, 1)
                            st.run(nc.vector.tensor_copy(ge[:, kp, :], gend[:, :, col].rearrange("p t h -> p (t h)")))
                            dve.sem_inc(cols_in, 1)
                            st.add(nc.vector.tensor_scalar(nge[:, kp, :], ge[:, kp, :], -1.0, None, ALU.mult))
                            st.run(nc.vector.tensor_copy(eps_d[:, kp, :], eps_col[:, :, col].rearrange("p t h -> p (t h)")))

                        def key_factor_columns(L):
                            kp = L // R % 2
                            dve.wait_ge(c_exp, (NCH - 1) * (new_ks.index(L) + 1))
                            for qc in range(1, NCH):
                                part = c_col[:, kp, qc - 1, 0:qc * TPC]
                                st.run(nc.vector.tensor_tensor(c_eps[:, kp, qc - 1, 0:qc * TPC], part, eps_d[:, kp, 0:qc * TPC], ALU.mult))
                                st.run(nc.vector.tensor_scalar(part, part, SC, None, ALU.mult))
                            dve.sem_inc(cols_ready, 1)

                        def rope_product(r):
                            _, kind, L, c, twin = items[r]
                            j = PAIR[kind, L, c]
                            if j >= 2:
                                dve.wait_ge(rotated, j - 1)
                            dve.wait_ge(filled, r + 1)
                            cs = slice(c * CH, (c + 1) * CH)
                            nc.vector.tensor_tensor((t1, t2)[twin][:, j % 2, :], ring[:, r % NR, :], (cos, sin)[twin][:, cs],
                                                    ALU.mult).then_inc(slot_free[r % NR], 1)
                            if twin:
                                for rr in (r - 1, r):
                                    dve.wait_ge(slot_free[rr % NR], rr // NR + 1)
                                dve.sem_inc(t_done, 2)

                        def take_max(r):
                            _, _, L, k, _ = items[r]
                            qt, kc, w_, diag = PASS1[k]
                            nb = w_ // P - (1 if diag else 0)
                            dve.wait_ge(filled, r + 1)
                            if diag:
                                nc.vector.tensor_tensor(scrap[:, :], ring[:, r % NR, w_ - P:w_], tri[:, :], ALU.mult).then_inc(max_done, 1)
                            if nb:
                                last = nc.vector.tensor_reduce(m_abs[:, qt, kc * TPC:kc * TPC + nb],
                                                               ring[:, r % NR, 0:nb * P].rearrange("p (b k) -> p b k", k=P),
                                                               axis=AX.X, op=ALU.max, apply_absolute_value=True)
                            if diag:
                                dve.wait_ge(max_done, diagonals.index(r) + 1)
                                last = nc.vector.tensor_reduce(m_abs[:, qt, qt:qt + 1], scrap[:, :], axis=AX.X, op=ALU.max, apply_absolute_value=True)
                            last.then_inc(slot_free[r % NR], 1)
                            if diag or k >= N1 - NR:
                                dve.wait_ge(slot_free[r % NR], r // NR + 1)

                        def take_row(r):
                            _, _, L, c, _ = items[r]
                            dve.wait_ge(filled, r + 1)
                            nc.vector.tensor_copy(m_row[0:3, L % R, c * CH:(c + 1) * CH], ring[0:3, r % NR, :]).then_inc(slot_free[r % NR], 1)

                        def logs_in(L):
                            n = targets.index(L)
                            st.run(nc.vector.tensor_scalar(l2[:, :, :], m_abs[:, :, :], SC, 1e-30, ALU.mult, ALU.add))
                            nc.vector.tensor_scalar(l1[:, :, :], l2[:, :, :], TINY, None, ALU.max).then_inc(ln_in, 1)
                            dve.wait_ge(ln_in, 2 * n + 1)
                            nc.vector.tensor_scalar(l2[:, :, :], l2[:, :, :], TINY, 1.0 / TINY, ALU.min, ALU.mult).then_inc(ln_in, 1)

                        def maxima(L):
                            n, kp = targets.index(L), L // R % 2
                            dve.wait_ge(ln_out, 2 * n + 2)
                            st.run(nc.vector.tensor_tensor(l1[:, :, :], l1[:, :, :], l2[:, :, :], ALU.add))
                            st.run(nc.vector.tensor_tensor(l1[:, :, :], l1[:, :, :], ge[:, kp, :].unsqueeze(1).to_broadcast([P, NT, NT]), ALU.subtract))
                            st.run(nc.vector.tensor_tensor(l1[:, :, :], l1[:, :, :], later[:, :, :], ALU.add))
                            st.run(nc.vector.tensor_reduce(m_neg[:, :], l1[:, :, :], axis=AX.X, op=ALU.max, negate=True))
                            st.run(nc.vector.tensor_copy(m_split[:, :, 0], m_neg[:, :]))
                            st.run(nc.vector.tensor_tensor(m_rest[:, :], m_neg[:, :], m_split[:, :, 0], ALU.subtract))
                            st.run(nc.vector.tensor_copy(m_split[:, :, 1], m_rest[:, :]))
                            st.run(nc.vector.tensor_tensor(m_neg[:, :], m_rest[:, :], m_split[:, :, 1], ALU.subtract))
                            st.run(nc.vector.tensor_copy(m_split[:, :, 2], m_neg[:, :]))
                            dve.sem_inc(split_ready, 1)

                        def product(n):
                            L, g, qc, kb, q0, own = pass2(n)
                            w_, kp = CH - q0, L // R % 2
                            if own:
                                j = kb - TPC * qc
                                f, eps = fac[:, g % 2, FOFF[1 + j]:FOFF[1 + j] + w_], eps_d[:, kp, kb:kb + 1]
                                if g in chunks:
                                    dve.wait_ge(f_masked, TPC * chunks.index(g) + j + 1)
                            else:
                                f, eps = fac[:, g % 2, 0:CH], c_eps[:, kp, qc - 1, kb:kb + 1]
                                if g in chunks:
                                    dve.wait_ge(f_done, exps(g) + 1)
                            dve.wait_ge(abs_done, n + 1)
                            nc.vector.scalar_tensor_tensor(out=sabs[:, n % NPB, 0:w_], in0=sabs[:, n % NPB, 0:w_], scalar=eps,
                                                           in1=f, op0=ALU.add, op1=ALU.mult).then_inc(b_done, 1)

                        def variance(r):
                            dve.wait_ge(filled, r + 1)
                            nc.vector.tensor_copy(uu[:, :], ring[:, r % NR, 0:TPC]).then_inc(slot_free[r % NR], 1)
                            dve.wait_ge(slot_free[r % NR], r // NR + 1)
                            nc.vector.tensor_scalar(rs[:, :].bitcast(I32), uu[:, :].bitcast(I32), -0.5, float(0x5F3759DF),
                                                    ALU.mult, ALU.add).then_inc(u_ready, 1)

                        def add_to_x(g):
                            dve.wait_ge(rs_ready, g + 1)
                            for j in range(TPC):
                                t = (g % NCH) * TPC + j
                                last = nc.vector.scalar_tensor_tensor(out=core.x[:, t, :], in0=psC[:, j, :], scalar=rs[:, j:j + 1],
                                                                      in1=core.x[:, t, :], op0=ALU.mult, op1=ALU.add)
                            last.then_inc(added, 1)
                            dve.wait_ge(added, g + 1)

                        if main:
                            product(0)
                            product(1)
                        for n in range(*steps):
                            if main and n + 2 < N2:
                                product(n + 2)
                            for L in new_ks:
                                if n == (L - 1) * NH:
                                    key_columns(L)
                                if n == (L - 1) * NH + 2:
                                    key_factor_columns(L)
                            for r in AT.get(n, ()):
                                kind, L, k = items[r][1:4]
                                if kind in ("k", "q"):
                                    rope_product(r)
                                if kind == "max":
                                    take_max(r)
                                if kind == "fin":
                                    variance(r)
                                if kind == "row":
                                    if k == 0:
                                        maxima(L)
                                    take_row(r)
                            for L in targets:
                                if n == L * NH - 11:
                                    logs_in(L)
                            if (g := due(n, 7)) is not None:
                                add_to_x(g)

            with nc.Block() as block:
                @block.gpsimd
                def _(pool):
                    for n, (buf, val) in enumerate(((m_row[:, :, :], 0.0), (m_abs[:, :, :], 0.0), (va[:, :, :, DH:M], 1.0))):
                        nc.gpsimd.memset(buf, val).then_inc(zeroed, 1)
                        pool.wait_ge(zeroed, n + 1)
            heads(None, [0])
            with nc.Fori(0, HK // UNROLL) as i:
                q.restart()
                heads(i, list(range(1, HB + 1)))


def hybrid_kernel(nc, a, out):
    with ExitStack() as ctx:
        core = Core(nc, ctx)
        stage_constants(nc, core, a["x"])
        with nc.sbuf_tensor("x_norm", [P, NT, D], F32) as xn:
            stage_mamba(nc, core, "mamba", xn, a, lambda: stage_norm(nc, core, "n0", xn))

        def gelu_ffn(tag):
            with nc.sbuf_tensor(tag + "_comb", [P, NT, 20], F32) as comb:
                def route():
                    stage_norm(nc, core, tag + "_n")
                    stage_route(nc, core, tag + "_r", 16, a["Wr"], a["br"], comb)

                stage_gelu_experts(nc, core, tag, comb, a["W1"], a["b1"], a["g1T"], a["be1T"], a["W2"], a["b2"], route)

        def silu_ffn(tag):
            with nc.sbuf_tensor(tag + "_comb", [P, NT, 8], F32) as comb:
                def route():
                    stage_norm(nc, core, tag + "_n")
                    stage_route(nc, core, tag + "_r", 8, a["gate_wT"], None, comb, capacity=int(1.25 * T / 8))

                stage_silu_experts(nc, core, tag, comb, a["gate_projT"], a["up_projT"], a["down_projT"], route)

        gelu_ffn("ffn0")
        stage_span_attention(nc, core, "span", a["Wq"], a["Wk"], a["Wv"], a["Wo"], a["span_val"], lambda: stage_norm(nc, core, "n2"))
        gelu_ffn("ffn1")
        stage_rope_attention(nc, core, "rope", a["W_qkvT"], a["W_qk_swapT"], a["W_outT"], a["cos8"], a["sin8"],
                             lambda: stage_norm(nc, core, "n4"))
        silu_ffn("moe0")
        stage_power_attention(nc, core, "power", a["pq"], a["pq_swap"], a["pk"], a["pk_swap"], a["pv"], a["pg"], a["w_proj"], a["ln_w"],
                              a["cos64"], a["sin64"], lambda: stage_norm(nc, core, "n6"))
        silu_ffn("moe1")
        stage_store(nc, core, out)


def _rotary_tables(np, angles, heads):
    cos, sin = np.cos(angles).astype(np.float32), np.sin(angles).astype(np.float32)
    pairs, t = angles.shape
    cos = np.tile(np.repeat(cos, 2, axis=0), (heads, 1))
    sin = np.tile(np.stack([-sin, sin], axis=1).reshape(2 * pairs, t), (heads, 1))
    return cos, sin


def kernel(**inputs):
    import numpy as np
    import concourse.bacc as bacc
    from concourse.bass_utils import run_bass_kernel_spmd

    w = {k: np.asarray(v) for k, v in inputs.items()}
    m = lambda name: w["L0_attn_a_" + name]
    halves = lambda v: v.reshape(-1, 128).T
    swapped = lambda v: v.reshape(v.shape[0], -1, 2)[:, :, ::-1].reshape(v.shape)
    times = np.arange(2048, dtype=np.float32)
    f8 = (1.0 / np.float32(10000.0) ** (np.arange(0, 8, 2, dtype=np.float32) / np.float32(8))).astype(np.float32)
    f64 = (2.0 * np.pi / float(2048) ** (np.arange(0, 64, 2, dtype=np.float32) / np.float32(64))).astype(np.float32)
    cos8, sin8 = _rotary_tables(np, np.outer(f8, times).astype(np.float32), 16)
    cos64, sin64 = _rotary_tables(np, np.outer(f64, times).astype(np.float32), 2)
    qkv, pa = w["L1_attn_a_W_qkv"], w["L1_attn_b_w_attn"]
    arrays = {
        "x": m("x"), "W_in": m("W_in"), "b_in": halves(m("b_in")), "conv_w": m("conv_w").reshape(2, 128, 4).transpose(1, 0, 2),
        "conv_b": halves(m("conv_b")), "W_xp": m("W_xp"), "b_xp": m("b_xp").reshape(32, 1), "W_dt": m("W_dt"), "b_dt": halves(m("b_dt")),
        "A_log": m("A_log"), "D_skip": halves(m("D_skip")), "W_out": m("W_out"), "b_out": m("b_out"), "alpha": m("alpha"), "beta": m("beta"),
        "Wq": w["L0_attn_b_Wq"], "Wk": w["L0_attn_b_Wk"], "Wv": w["L0_attn_b_Wv"], "Wo": w["L0_attn_b_Wo"], "span_val": w["L0_attn_b_span_val"],
        "Wr": w["L0_ffn_Wr"], "br": w["L0_ffn_br"], "W1": w["L0_ffn_W1"], "b1": w["L0_ffn_b1"], "g1T": w["L0_ffn_g1"].T, "be1T": w["L0_ffn_be1"].T,
        "W2": w["L0_ffn_W2"], "b2": w["L0_ffn_b2"],
        "W_qkvT": qkv.T, "W_qk_swapT": swapped(qkv[:256].T), "W_outT": w["L1_attn_a_W_out"].T, "cos8": cos8, "sin8": sin8,
        "pq": pa[:, :1024], "pq_swap": swapped(pa[:, :1024]), "pk": pa[:, 1024:1536], "pk_swap": swapped(pa[:, 1024:1536]),
        "pv": pa[:, 1536:2048], "pg": pa[:, 2048:], "w_proj": w["L1_attn_b_w_proj"], "ln_w": w["L1_attn_b_ln_w"].reshape(64, 1),
        "cos64": cos64, "sin64": sin64,
        "gate_wT": w["L1_ffn_gate_w"].T, "gate_projT": w["L1_ffn_gate_proj_w"].transpose(2, 0, 1),
        "up_projT": w["L1_ffn_up_proj_w"].transpose(2, 0, 1), "down_projT": w["L1_ffn_down_proj_w"].transpose(2, 0, 1),
    }
    arrays = {f"in_{k}": np.ascontiguousarray(v) for k, v in arrays.items()}
    nc = bacc.Bacc("TRN2", target_bir_lowering=False, num_devices=1)
    dram = {k[3:]: nc.dram_tensor(k, v.shape, mybir.dt.from_np(v.dtype), kind="ExternalInput").ap() for k, v in arrays.items()}
    out = nc.dram_tensor("out", (1, 2048, 128), F32, kind="ExternalOutput").ap()
    hybrid_kernel(nc, dram, out)
    return run_bass_kernel_spmd(nc, [arrays], core_ids=[0]).results[0]["out"]
```
